# Optimizing a Trainium2 kernel written in Bass

```python
import numpy as np
import jax
import jax.numpy as jnp

def _softmax(x, axis=-1):
    return jax.nn.softmax(x, axis=axis)

def _gelu(x):
    return jax.nn.gelu(x, approximate=True)

def _silu(x):
    return jax.nn.silu(x)

def _sigmoid(x):
    return jax.nn.sigmoid(x)

def _layernorm(x, axis=-1, eps=1e-05):
    m = jnp.mean(x, axis=axis, keepdims=True)
    v = jnp.var(x, axis=axis, keepdims=True)
    return (x - m) / jnp.sqrt(v + eps)

def _scatter_add(tgt, idx, src, axis=0):
    return tgt.at[idx].add(src)

def _segment_sum(src, seg, n):
    return jax.ops.segment_sum(src, seg, n)
kernel_name = 'mk_lm_tower_d4_tok_ids1024_r4_e44d9b'

def setup_inputs(seed: int=0):
    np.random.seed(seed)
    _w = jnp.asarray

    def _rec_inputs():
        import jax
        import jax.numpy as jnp
        _rk = jax.random.key(seed)
        x = jax.random.randint(jax.random.fold_in(_rk, 1), (8, 256), 0, 65532, jnp.int32)
        return x
    x = _rec_inputs()

    def _L0_tok_setup():
        import jax, jax.numpy as jnp
        import numpy as np
        A = 36313
        B = 27191
        key = jax.random.key(seed)
        k1, k2, k3 = jax.random.split(key, 3)
        vocab_size, bigram_dim, model_dim = (65536, 64, 256)
        tokens = jax.random.randint(k1, (4, 2048), 0, vocab_size - 1, dtype=jnp.int32)
        embed_weight = jax.random.normal(k2, (vocab_size, bigram_dim), dtype=jnp.float32) * 0.02
        proj_weight = jax.random.normal(k3, (model_dim, bigram_dim), dtype=jnp.float32) * 0.02
        scale = jnp.asarray(0.05, dtype=jnp.float32)
        return {'tokens': tokens, 'embed_weight': embed_weight, 'proj_weight': proj_weight, 'scale': scale}
    _L0_tok_all = _L0_tok_setup()
    _L0_tok_in = {k: v for k, v in _L0_tok_all.items() if k in ('embed_weight', 'proj_weight', 'scale')}
    del _L0_tok_all

    def _L0_attn_setup():
        import jax, jax.numpy as jnp
        import numpy as np
        B, T, D = (4, 256, 256)
        H, KVH = (16, 4)
        HD = D // H
        DFF = 1024
        WINDOW = 64
        EPS = 1e-05

        def _layernorm(x, g, b):
            mu = jnp.mean(x, axis=-1, keepdims=True)
            var = jnp.mean(jnp.square(x - mu), axis=-1, keepdims=True)
            return (x - mu) * jax.lax.rsqrt(var + EPS) * g + b

        def _rope(x):
            half = HD // 2
            theta = 1.0 / 10000.0 ** (jnp.arange(half, dtype=jnp.float32) / half)
            pos = jnp.arange(x.shape[2], dtype=jnp.float32)
            freqs = jnp.outer(pos, theta)
            cos_f, sin_f = (jnp.cos(freqs), jnp.sin(freqs))
            x1, x2 = (x[..., :half], x[..., half:])
            return jnp.concatenate([x1 * cos_f - x2 * sin_f, x2 * cos_f + x1 * sin_f], axis=-1)
        key = jax.random.key(seed)
        ks = jax.random.split(key, 16)
        s = 0.02
        d = {'x': jax.random.normal(ks[0], (B, T, D), dtype=jnp.float32), 'Wq': jax.random.normal(ks[1], (D, H * HD), dtype=jnp.float32) * s, 'bq': jnp.zeros((H * HD,), jnp.float32), 'Wk': jax.random.normal(ks[2], (D, KVH * HD), dtype=jnp.float32) * s, 'bk': jnp.zeros((KVH * HD,), jnp.float32), 'Wv': jax.random.normal(ks[3], (D, KVH * HD), dtype=jnp.float32) * s, 'bv': jnp.zeros((KVH * HD,), jnp.float32), 'Wo': jax.random.normal(ks[4], (D, D), dtype=jnp.float32) * s, 'bo': jnp.zeros((D,), jnp.float32), 'g1': jnp.ones((D,), jnp.float32), 'b1': jnp.zeros((D,), jnp.float32), 'Wf1': jax.random.normal(ks[5], (D, DFF), dtype=jnp.float32) * s, 'bf1': jnp.zeros((DFF,), jnp.float32), 'Wf2': jax.random.normal(ks[6], (DFF, D), dtype=jnp.float32) * s, 'bf2': jnp.zeros((D,), jnp.float32), 'g2': jnp.ones((D,), jnp.float32), 'b2': jnp.zeros((D,), jnp.float32)}
        return d
    _L0_attn_all = _L0_attn_setup()
    _L0_attn_in = {k: v for k, v in _L0_attn_all.items() if k in ('Wq', 'bq', 'Wk', 'bk', 'Wv', 'bv', 'Wo', 'bo', 'g1', 'b1', 'Wf1', 'bf1', 'Wf2', 'bf2', 'g2', 'b2')}
    del _L0_attn_all

    def _L0_ffn_setup():
        import jax, jax.numpy as jnp
        import numpy as np
        B, S, H, I, E, TOPK, KS = (4, 1024, 256, 128, 16, 2, 3)
        key = jax.random.key(seed)
        ks = jax.random.split(key, 9)
        sc = 0.02
        return {'hidden_states': jax.random.normal(ks[0], (B, S, H), dtype=jnp.float32), 'router_w': jax.random.normal(ks[1], (H, E), dtype=jnp.float32) * sc, 'router_bias': jnp.zeros((E,), dtype=jnp.float32), 'expert_gate_w': jax.random.normal(ks[2], (E - 1, H, I), dtype=jnp.float32) * sc, 'expert_up_w': jax.random.normal(ks[3], (E - 1, H, I), dtype=jnp.float32) * sc, 'expert_down_w': jax.random.normal(ks[4], (E - 1, I, H), dtype=jnp.float32) * sc, 'conv_w': jax.random.normal(ks[5], (I, H, KS), dtype=jnp.float32) * sc, 'shared_up_w': jax.random.normal(ks[6], (H, I), dtype=jnp.float32) * sc, 'shared_down_w': jax.random.normal(ks[7], (I, H), dtype=jnp.float32) * sc}
    _L0_ffn_all = _L0_ffn_setup()
    _L0_ffn_in = {k: v for k, v in _L0_ffn_all.items() if k in ('router_w', 'router_bias', 'expert_gate_w', 'expert_up_w', 'expert_down_w', 'conv_w', 'shared_up_w', 'shared_down_w')}
    del _L0_ffn_all

    def _L1_attn_setup():
        import jax, jax.numpy as jnp
        import numpy as np
        BATCH, SEQ, D_MODEL, STATE_DIM = (8, 512, 256, 256)

        def _cayley_circulant_eigenvalues(a_params, n):
            half_n = n // 2
            a_full = jnp.zeros((n,), dtype=a_params.dtype)
            a_full = a_full.at[1:half_n].set(a_params[:half_n - 1])
            a_full = a_full.at[half_n + 1:].set(-a_params[:half_n - 1][::-1])
            omega = jnp.fft.fft(a_full).imag
            w2 = omega * omega
            denom = 1.0 + w2
            return ((1.0 - w2) / denom + 1j * (-2.0 * omega / denom)).astype(jnp.complex64)
        key = jax.random.key(seed)
        k1, k2, k3, k4 = jax.random.split(key, 4)
        u = jax.random.normal(k1, (BATCH, SEQ, D_MODEL), dtype=jnp.float32)
        a_params = jax.random.normal(k2, (STATE_DIM // 2,), dtype=jnp.float32) * 0.1
        B_w = jax.random.normal(k3, (STATE_DIM, D_MODEL), dtype=jnp.float32) / np.sqrt(D_MODEL).astype(np.float32)
        C_w = jax.random.normal(k4, (D_MODEL, STATE_DIM), dtype=jnp.float32) / np.sqrt(STATE_DIM).astype(np.float32)
        D = jnp.zeros((D_MODEL,), dtype=jnp.float32)
        return {'u': u, 'a_params': a_params, 'B_w': B_w, 'C_w': C_w, 'D': D}
    _L1_attn_all = _L1_attn_setup()
    _L1_attn_in = {k: v for k, v in _L1_attn_all.items() if k in ('a_params', 'B_w', 'C_w', 'D')}
    del _L1_attn_all

    def _L1_ffn_setup():
        import jax, jax.numpy as jnp
        import numpy as np
        DIM = 256

        def _reference_tuple_inner(x, W_r, W_k, W_v, mu_r, mu_k):
            B, T, C = x.shape
            x_prev = jnp.concatenate([jnp.zeros((B, 1, C), x.dtype), x[:, :-1, :]], axis=1)
            xr = mu_r * x + (1.0 - mu_r) * x_prev
            xk = mu_k * x + (1.0 - mu_k) * x_prev
            r = jax.nn.sigmoid(jnp.einsum('btc,dc->btd', xr, W_r))
            k = jnp.einsum('btc,dc->btd', xk, W_k)
            k_act = jnp.square(jax.nn.relu(k))
            out = r * jnp.einsum('btc,dc->btd', k_act, W_v)
            new_state = x[:, -1, :]
            return (out, new_state)
        key = jax.random.key(seed)
        ks = jax.random.split(key, 6)
        B, T, C = (8, 512, DIM)
        x = jax.random.normal(ks[0], (B, T, C), dtype=jnp.float32)
        s = 1.0 / np.sqrt(C)
        W_r = jax.random.uniform(ks[1], (C, C), jnp.float32, -s, s)
        W_k = jax.random.uniform(ks[2], (C, C), jnp.float32, -s, s)
        W_v = jax.random.uniform(ks[3], (C, C), jnp.float32, -s, s)
        mu_r = jax.random.uniform(ks[4], (C,), jnp.float32)
        mu_k = jax.random.uniform(ks[5], (C,), jnp.float32)
        return {'x': x, 'W_r': W_r, 'W_k': W_k, 'W_v': W_v, 'mu_r': mu_r, 'mu_k': mu_k}
    _L1_ffn_all = _L1_ffn_setup()
    _L1_ffn_in = {k: v for k, v in _L1_ffn_all.items() if k in ('W_r', 'W_k', 'W_v', 'mu_r', 'mu_k')}
    del _L1_ffn_all

    def _L2_attn_setup():
        import jax, jax.numpy as jnp
        import numpy as np
        HID = 256
        NH = 16
        HD = HID // NH
        RANK = 16
        B, L = (2, 512)
        key = jax.random.key(seed)
        ks = jax.random.split(key, 9)
        s = 0.02
        return {'x': jax.random.normal(ks[0], (B, L, HID), dtype=jnp.float32), 'Wq': jax.random.normal(ks[1], (HID, HID), dtype=jnp.float32) * s, 'Wk': jax.random.normal(ks[2], (HID, HID), dtype=jnp.float32) * s, 'Wv': jax.random.normal(ks[3], (HID, HID), dtype=jnp.float32) * s, 'Wg': jax.random.normal(ks[4], (HID, HID), dtype=jnp.float32) * s, 'Wgk1': jax.random.normal(ks[5], (HID, RANK), dtype=jnp.float32) * s, 'Wgk2': jax.random.normal(ks[6], (RANK, HID), dtype=jnp.float32) * s, 'bgk2': jnp.zeros((HID,), dtype=jnp.float32), 'gamma': jnp.ones((HID,), dtype=jnp.float32), 'beta': jnp.zeros((HID,), dtype=jnp.float32), 'Wout': jax.random.normal(ks[7], (HID, HID), dtype=jnp.float32) * s}
    _L2_attn_all = _L2_attn_setup()
    _L2_attn_in = {k: v for k, v in _L2_attn_all.items() if k in ('Wq', 'Wk', 'Wv', 'Wg', 'Wgk1', 'Wgk2', 'bgk2', 'gamma', 'beta', 'Wout')}
    del _L2_attn_all

    def _L2_ffn_setup():
        import jax, jax.numpy as jnp
        import numpy as np
        QB = 127.0
        EPS = 1e-05

        def _ste(x, q):
            return x + jax.lax.stop_gradient(q - x)

        def bitlinear(x, W, b):
            w_scale = jnp.clip(jnp.mean(jnp.abs(W)), EPS, None)
            Wq = _ste(W, jnp.clip(jnp.round(W / w_scale), -1.0, 1.0) * w_scale)
            x_scale = jnp.clip(jnp.max(jnp.abs(x), axis=-1, keepdims=True), EPS, None)
            xq = _ste(x, jnp.clip(jnp.round(x * (QB / x_scale)), -QB - 1.0, QB) * (x_scale / QB))
            return jnp.einsum('bnd,hd->bnh', xq, Wq) + b
        key = jax.random.key(seed)
        k0, k1, k2 = jax.random.split(key, 3)
        B, N, D = (8, 1024, 256)
        H = int(D * 4.0)
        x = jax.random.normal(k0, (B, N, D), dtype=jnp.float32)
        W1 = jax.random.normal(k1, (H, D), dtype=jnp.float32) * 0.02
        b1 = jnp.zeros((H,), dtype=jnp.float32)
        W2 = jax.random.normal(k2, (D, H), dtype=jnp.float32) * 0.02
        b2 = jnp.zeros((D,), dtype=jnp.float32)
        return {'x': x, 'W1': W1, 'b1': b1, 'W2': W2, 'b2': b2}
    _L2_ffn_all = _L2_ffn_setup()
    _L2_ffn_in = {k: v for k, v in _L2_ffn_all.items() if k in ('W1', 'b1', 'W2', 'b2')}
    del _L2_ffn_all

    def _L3_attn_setup():
        import jax, jax.numpy as jnp
        import numpy as np
        B, T, C = (8, 512, 256)
        NL, LID = (12, 1)
        H = 4 * C

        def _ln(x, g, b):
            m = x.mean(-1, keepdims=True)
            v = ((x - m) ** 2).mean(-1, keepdims=True)
            return (x - m) * jax.lax.rsqrt(v + 1e-05) * g + b

        def _shift(x):
            return jnp.pad(x, ((0, 0), (1, 0), (0, 0)))[:, :-1]

        def _wkv(time_decay, time_first, k, v):
            w = -jnp.exp(time_decay)
            kt = jnp.moveaxis(k, 1, 0)
            vt = jnp.moveaxis(v, 1, 0)
            Bb, Cc = (k.shape[0], k.shape[2])
            init = (jnp.zeros((Bb, Cc), k.dtype), jnp.zeros((Bb, Cc), k.dtype), jnp.full((Bb, Cc), -1e+38, k.dtype))

            def step(carry, kv_t):
                aa, bb, pp = carry
                kk, vv = kv_t
                ww = time_first + kk
                p = jnp.maximum(pp, ww)
                e1 = jnp.exp(pp - p)
                e2 = jnp.exp(ww - p)
                out = (e1 * aa + e2 * vv) / (e1 * bb + e2)
                ww2 = pp + w
                p2 = jnp.maximum(ww2, kk)
                e1b = jnp.exp(ww2 - p2)
                e2b = jnp.exp(kk - p2)
                return ((e1b * aa + e2b * vv, e1b * bb + e2b, p2), out)
            _, out = jax.lax.scan(step, init, (kt, vt))
            return jnp.moveaxis(out, 0, 1)
        key = jax.random.key(seed)
        ks = jax.random.split(key, 8)
        f = lambda i, shape: 0.02 * jax.random.normal(ks[i], shape, jnp.float32)
        r01 = LID / (NL - 1)
        r10 = 1.0 - LID / NL
        h = np.arange(C, dtype=np.float64)
        decay = (-5 + 8 * (h / (C - 1)) ** (0.7 + 1.3 * r01)).astype(np.float32)
        zig = np.array([(i + 1) % 3 - 1 for i in range(C)]) * 0.5
        tfirst = (np.ones(C) * np.log(0.3) + zig).astype(np.float32)
        xpos = h / C
        tmk = (xpos ** r10).astype(np.float32)
        tmv = (xpos ** r10 + 0.3 * r01).astype(np.float32)
        tmr = (xpos ** (0.5 * r10)).astype(np.float32)
        cm = (xpos ** r10).astype(np.float32)
        return dict(x=jax.random.normal(ks[0], (B, T, C), jnp.float32), ln1_g=jnp.ones(C, jnp.float32), ln1_b=jnp.zeros(C, jnp.float32), ln2_g=jnp.ones(C, jnp.float32), ln2_b=jnp.zeros(C, jnp.float32), time_decay=jnp.asarray(decay), time_first=jnp.asarray(tfirst), time_mix_k=jnp.asarray(tmk), time_mix_v=jnp.asarray(tmv), time_mix_r=jnp.asarray(tmr), att_Wk=f(1, (C, C)), att_Wv=f(2, (C, C)), att_Wr=f(3, (C, C)), att_Wo=f(4, (C, C)), cm_k=jnp.asarray(cm), cm_r=jnp.asarray(cm), ffn_Wk=f(5, (H, C)), ffn_Wr=f(6, (C, C)), ffn_Wv=f(7, (C, H)))
    _L3_attn_all = _L3_attn_setup()
    _L3_attn_in = {k: v for k, v in _L3_attn_all.items() if k in ('ln1_g', 'ln1_b', 'ln2_g', 'ln2_b', 'time_decay', 'time_first', 'time_mix_k', 'time_mix_v', 'time_mix_r', 'att_Wk', 'att_Wv', 'att_Wr', 'att_Wo', 'cm_k', 'cm_r', 'ffn_Wk', 'ffn_Wr', 'ffn_Wv')}
    del _L3_attn_all

    def _L3_ffn_setup():
        import jax, jax.numpy as jnp
        import numpy as np
        H = 256
        F = 1024
        E = 8
        TOP_K = 2
        B, S = (1, 512)
        key = jax.random.key(seed)
        k0, k1, k2, k3 = jax.random.split(key, 4)
        hidden_states = jax.random.normal(k0, (B, S, H), dtype=jnp.float32)
        gate_w = jax.random.normal(k1, (E, H), dtype=jnp.float32) * 0.02
        gate_up_w = jax.random.normal(k2, (E, 2 * F, H), dtype=jnp.float32) * 0.02
        down_w = jax.random.normal(k3, (E, H, F), dtype=jnp.float32) * 0.02
        return {'hidden_states': hidden_states, 'gate_w': gate_w, 'gate_up_w': gate_up_w, 'down_w': down_w}
    _L3_ffn_all = _L3_ffn_setup()
    _L3_ffn_in = {k: v for k, v in _L3_ffn_all.items() if k in ('gate_w', 'gate_up_w', 'down_w')}
    del _L3_ffn_all
    return {'x': x, 'L0_tok_embed_weight': _L0_tok_in['embed_weight'], 'L0_tok_proj_weight': _L0_tok_in['proj_weight'], 'L0_tok_scale': _L0_tok_in['scale'], 'L0_attn_Wq': _L0_attn_in['Wq'], 'L0_attn_bq': _L0_attn_in['bq'], 'L0_attn_Wk': _L0_attn_in['Wk'], 'L0_attn_bk': _L0_attn_in['bk'], 'L0_attn_Wv': _L0_attn_in['Wv'], 'L0_attn_bv': _L0_attn_in['bv'], 'L0_attn_Wo': _L0_attn_in['Wo'], 'L0_attn_bo': _L0_attn_in['bo'], 'L0_attn_g1': _L0_attn_in['g1'], 'L0_attn_b1': _L0_attn_in['b1'], 'L0_attn_Wf1': _L0_attn_in['Wf1'], 'L0_attn_bf1': _L0_attn_in['bf1'], 'L0_attn_Wf2': _L0_attn_in['Wf2'], 'L0_attn_bf2': _L0_attn_in['bf2'], 'L0_attn_g2': _L0_attn_in['g2'], 'L0_attn_b2': _L0_attn_in['b2'], 'L0_ffn_router_w': _L0_ffn_in['router_w'], 'L0_ffn_router_bias': _L0_ffn_in['router_bias'], 'L0_ffn_expert_gate_w': _L0_ffn_in['expert_gate_w'], 'L0_ffn_expert_up_w': _L0_ffn_in['expert_up_w'], 'L0_ffn_expert_down_w': _L0_ffn_in['expert_down_w'], 'L0_ffn_conv_w': _L0_ffn_in['conv_w'], 'L0_ffn_shared_up_w': _L0_ffn_in['shared_up_w'], 'L0_ffn_shared_down_w': _L0_ffn_in['shared_down_w'], 'L1_attn_a_params': _L1_attn_in['a_params'], 'L1_attn_B_w': _L1_attn_in['B_w'], 'L1_attn_C_w': _L1_attn_in['C_w'], 'L1_attn_D': _L1_attn_in['D'], 'L1_ffn_W_r': _L1_ffn_in['W_r'], 'L1_ffn_W_k': _L1_ffn_in['W_k'], 'L1_ffn_W_v': _L1_ffn_in['W_v'], 'L1_ffn_mu_r': _L1_ffn_in['mu_r'], 'L1_ffn_mu_k': _L1_ffn_in['mu_k'], 'L2_attn_Wq': _L2_attn_in['Wq'], 'L2_attn_Wk': _L2_attn_in['Wk'], 'L2_attn_Wv': _L2_attn_in['Wv'], 'L2_attn_Wg': _L2_attn_in['Wg'], 'L2_attn_Wgk1': _L2_attn_in['Wgk1'], 'L2_attn_Wgk2': _L2_attn_in['Wgk2'], 'L2_attn_bgk2': _L2_attn_in['bgk2'], 'L2_attn_gamma': _L2_attn_in['gamma'], 'L2_attn_beta': _L2_attn_in['beta'], 'L2_attn_Wout': _L2_attn_in['Wout'], 'L2_ffn_W1': _L2_ffn_in['W1'], 'L2_ffn_b1': _L2_ffn_in['b1'], 'L2_ffn_W2': _L2_ffn_in['W2'], 'L2_ffn_b2': _L2_ffn_in['b2'], 'L3_attn_ln1_g': _L3_attn_in['ln1_g'], 'L3_attn_ln1_b': _L3_attn_in['ln1_b'], 'L3_attn_ln2_g': _L3_attn_in['ln2_g'], 'L3_attn_ln2_b': _L3_attn_in['ln2_b'], 'L3_attn_time_decay': _L3_attn_in['time_decay'], 'L3_attn_time_first': _L3_attn_in['time_first'], 'L3_attn_time_mix_k': _L3_attn_in['time_mix_k'], 'L3_attn_time_mix_v': _L3_attn_in['time_mix_v'], 'L3_attn_time_mix_r': _L3_attn_in['time_mix_r'], 'L3_attn_att_Wk': _L3_attn_in['att_Wk'], 'L3_attn_att_Wv': _L3_attn_in['att_Wv'], 'L3_attn_att_Wr': _L3_attn_in['att_Wr'], 'L3_attn_att_Wo': _L3_attn_in['att_Wo'], 'L3_attn_cm_k': _L3_attn_in['cm_k'], 'L3_attn_cm_r': _L3_attn_in['cm_r'], 'L3_attn_ffn_Wk': _L3_attn_in['ffn_Wk'], 'L3_attn_ffn_Wr': _L3_attn_in['ffn_Wr'], 'L3_attn_ffn_Wv': _L3_attn_in['ffn_Wv'], 'L3_ffn_gate_w': _L3_ffn_in['gate_w'], 'L3_ffn_gate_up_w': _L3_ffn_in['gate_up_w'], 'L3_ffn_down_w': _L3_ffn_in['down_w']}

def reference(x, L0_tok_embed_weight, L0_tok_proj_weight, L0_tok_scale, L0_attn_Wq, L0_attn_bq, L0_attn_Wk, L0_attn_bk, L0_attn_Wv, L0_attn_bv, L0_attn_Wo, L0_attn_bo, L0_attn_g1, L0_attn_b1, L0_attn_Wf1, L0_attn_bf1, L0_attn_Wf2, L0_attn_bf2, L0_attn_g2, L0_attn_b2, L0_ffn_router_w, L0_ffn_router_bias, L0_ffn_expert_gate_w, L0_ffn_expert_up_w, L0_ffn_expert_down_w, L0_ffn_conv_w, L0_ffn_shared_up_w, L0_ffn_shared_down_w, L1_attn_a_params, L1_attn_B_w, L1_attn_C_w, L1_attn_D, L1_ffn_W_r, L1_ffn_W_k, L1_ffn_W_v, L1_ffn_mu_r, L1_ffn_mu_k, L2_attn_Wq, L2_attn_Wk, L2_attn_Wv, L2_attn_Wg, L2_attn_Wgk1, L2_attn_Wgk2, L2_attn_bgk2, L2_attn_gamma, L2_attn_beta, L2_attn_Wout, L2_ffn_W1, L2_ffn_b1, L2_ffn_W2, L2_ffn_b2, L3_attn_ln1_g, L3_attn_ln1_b, L3_attn_ln2_g, L3_attn_ln2_b, L3_attn_time_decay, L3_attn_time_first, L3_attn_time_mix_k, L3_attn_time_mix_v, L3_attn_time_mix_r, L3_attn_att_Wk, L3_attn_att_Wv, L3_attn_att_Wr, L3_attn_att_Wo, L3_attn_cm_k, L3_attn_cm_r, L3_attn_ffn_Wk, L3_attn_ffn_Wr, L3_attn_ffn_Wv, L3_ffn_gate_w, L3_ffn_gate_up_w, L3_ffn_down_w):
    import jax
    import jax.numpy as jnp

    def _L0_tok_ref(tokens, embed_weight, proj_weight, scale):
        import jax, jax.numpy as jnp
        import numpy as np
        A = 36313
        B = 27191
        t = tokens.astype(jnp.int32)
        mod = embed_weight.shape[0] - 1
        h_rest = jnp.mod(jnp.bitwise_xor(A * t[..., 1:], B * t[..., :-1]), mod)
        h_first = jnp.full(t.shape[:-1] + (1,), mod, dtype=jnp.int32)
        idx = jnp.concatenate([h_first, h_rest], axis=-1)
        h = embed_weight[idx]
        out = jnp.einsum('bsd,md->bsm', h, proj_weight)
        return out * scale.astype(out.dtype)

    def _L0_attn_ref(x, Wq, bq, Wk, bk, Wv, bv, Wo, bo, g1, b1, Wf1, bf1, Wf2, bf2, g2, b2):
        import jax, jax.numpy as jnp
        import numpy as np
        B, T, D = (4, 256, 256)
        H, KVH = (16, 4)
        HD = D // H
        DFF = 1024
        WINDOW = 64
        EPS = 1e-05

        def _layernorm(x, g, b):
            mu = jnp.mean(x, axis=-1, keepdims=True)
            var = jnp.mean(jnp.square(x - mu), axis=-1, keepdims=True)
            return (x - mu) * jax.lax.rsqrt(var + EPS) * g + b

        def _rope(x):
            half = HD // 2
            theta = 1.0 / 10000.0 ** (jnp.arange(half, dtype=jnp.float32) / half)
            pos = jnp.arange(x.shape[2], dtype=jnp.float32)
            freqs = jnp.outer(pos, theta)
            cos_f, sin_f = (jnp.cos(freqs), jnp.sin(freqs))
            x1, x2 = (x[..., :half], x[..., half:])
            return jnp.concatenate([x1 * cos_f - x2 * sin_f, x2 * cos_f + x1 * sin_f], axis=-1)
        Bt, Tt, _ = x.shape
        h = _layernorm(x, g1, b1)
        q = (h @ Wq + bq).reshape(Bt, Tt, H, HD).transpose(0, 2, 1, 3)
        k = (h @ Wk + bk).reshape(Bt, Tt, KVH, HD).transpose(0, 2, 1, 3)
        v = (h @ Wv + bv).reshape(Bt, Tt, KVH, HD).transpose(0, 2, 1, 3)
        group = H // KVH
        k = jnp.repeat(k, group, axis=1)
        v = jnp.repeat(v, group, axis=1)
        q, k = (_rope(q), _rope(k))
        scores = jnp.einsum('bhqd,bhkd->bhqk', q, k) / jnp.sqrt(jnp.float32(HD))
        row = jnp.arange(Tt)[:, None]
        col = jnp.arange(Tt)[None, :]
        valid = (col <= row) & (row - col < WINDOW)
        scores = jnp.where(valid, scores, jnp.float32(-1000000000.0))
        attn = jax.nn.softmax(scores, axis=-1)
        out = jnp.einsum('bhqk,bhkd->bhqd', attn, v)
        out = out.transpose(0, 2, 1, 3).reshape(Bt, Tt, D)
        x = x + (out @ Wo + bo)
        h2 = _layernorm(x, g2, b2)
        ff = jax.nn.gelu(h2 @ Wf1 + bf1, approximate=False) @ Wf2 + bf2
        return x + ff

    def _L0_ffn_ref(hidden_states, router_w, router_bias, expert_gate_w, expert_up_w, expert_down_w, conv_w, shared_up_w, shared_down_w):
        import jax, jax.numpy as jnp
        import numpy as np
        B, S, H, I, E, TOPK, KS = (4, 1024, 256, 128, 16, 2, 3)
        b, s, h = hidden_states.shape
        flat = hidden_states.reshape(b * s, h)
        logits = (flat @ router_w).astype(jnp.float32) + router_bias
        probs = jax.nn.softmax(logits, axis=-1)
        top_w, top_i = jax.lax.top_k(probs, TOPK)
        norm_w = top_w / (jnp.sum(top_w, axis=-1, keepdims=True) + 1e-06)
        norm_w = norm_w.astype(hidden_states.dtype)
        combine = jnp.sum(jax.nn.one_hot(top_i, E, dtype=norm_w.dtype) * norm_w[..., None], axis=1)
        routed = combine[:, E - 1:E] * flat
        for e in range(E - 1):
            y = jax.nn.silu(flat @ expert_gate_w[e]) * (flat @ expert_up_w[e]) @ expert_down_w[e]
            routed = routed + combine[:, e:e + 1] * y
        routed = routed.reshape(b, s, h)
        x_ncw = jnp.transpose(hidden_states, (0, 2, 1))
        gate = jax.lax.conv_general_dilated(x_ncw, conv_w, window_strides=(1,), padding=[(KS - 1, 0)], dimension_numbers=('NCW', 'OIW', 'NCW'))
        gate = jnp.transpose(gate, (0, 2, 1))
        shared = jax.nn.silu(gate) * (hidden_states @ shared_up_w) @ shared_down_w
        return shared + routed

    def _L1_attn_ref(u, a_params, B_w, C_w, D):
        import jax, jax.numpy as jnp
        import numpy as np
        BATCH, SEQ, D_MODEL, STATE_DIM = (8, 512, 256, 256)

        def _cayley_circulant_eigenvalues(a_params, n):
            half_n = n // 2
            a_full = jnp.zeros((n,), dtype=a_params.dtype)
            a_full = a_full.at[1:half_n].set(a_params[:half_n - 1])
            a_full = a_full.at[half_n + 1:].set(-a_params[:half_n - 1][::-1])
            omega = jnp.fft.fft(a_full).imag
            w2 = omega * omega
            denom = 1.0 + w2
            return ((1.0 - w2) / denom + 1j * (-2.0 * omega / denom)).astype(jnp.complex64)
        n = B_w.shape[0]
        lambdas = _cayley_circulant_eigenvalues(a_params, n)
        Bu = jnp.einsum('bsd,nd->bsn', u, B_w)

        def step(h, bu_t):
            Wh = jnp.fft.ifft(lambdas * jnp.fft.fft(h.astype(jnp.float32))).real.astype(h.dtype)
            h_new = Wh + bu_t
            return (h_new, h_new)
        h0 = jnp.zeros((u.shape[0], n), dtype=u.dtype)
        _, hs = jax.lax.scan(step, h0, jnp.swapaxes(Bu, 0, 1))
        y = jnp.einsum('sbn,dn->bsd', hs, C_w) + D * u
        return y

    def _L1_ffn_ref(x, W_r, W_k, W_v, mu_r, mu_k):
        import jax, jax.numpy as jnp
        import numpy as np
        DIM = 256

        def _reference_tuple_inner(x, W_r, W_k, W_v, mu_r, mu_k):
            B, T, C = x.shape
            x_prev = jnp.concatenate([jnp.zeros((B, 1, C), x.dtype), x[:, :-1, :]], axis=1)
            xr = mu_r * x + (1.0 - mu_r) * x_prev
            xk = mu_k * x + (1.0 - mu_k) * x_prev
            r = jax.nn.sigmoid(jnp.einsum('btc,dc->btd', xr, W_r))
            k = jnp.einsum('btc,dc->btd', xk, W_k)
            k_act = jnp.square(jax.nn.relu(k))
            out = r * jnp.einsum('btc,dc->btd', k_act, W_v)
            new_state = x[:, -1, :]
            return (out, new_state)
        return _reference_tuple_inner(x, W_r, W_k, W_v, mu_r, mu_k)[0]

    def _L2_attn_ref(x, Wq, Wk, Wv, Wg, Wgk1, Wgk2, bgk2, gamma, beta, Wout):
        import jax, jax.numpy as jnp
        import numpy as np
        HID = 256
        NH = 16
        HD = HID // NH
        RANK = 16
        B, L = (2, 512)
        Bb, Ll, Hid = x.shape
        H, Dh = (NH, HD)
        q = (x @ Wq).reshape(Bb, Ll, H, Dh)
        k = (x @ Wk).reshape(Bb, Ll, H, Dh)
        v = (x @ Wv).reshape(Bb, Ll, H, Dh)
        gk = (jax.nn.log_sigmoid(x @ Wgk1 @ Wgk2 + bgk2) / 16.0).reshape(Bb, Ll, H, Dh)
        qT = jnp.transpose(q, (1, 0, 2, 3))
        kT = jnp.transpose(k, (1, 0, 2, 3))
        vT = jnp.transpose(v, (1, 0, 2, 3))
        gT = jnp.transpose(gk, (1, 0, 2, 3))

        def step(state, inp):
            qt, kt, vt, gt = inp
            gate = jnp.exp(gt)
            state = state * gate[..., None] + vt[..., None] * kt[..., None, :]
            out_t = jnp.einsum('bhvk,bhk->bhv', state, qt)
            return (state, out_t)
        state0 = jnp.zeros((Bb, H, Dh, Dh), dtype=x.dtype)
        _, outs = jax.lax.scan(step, state0, (qT, kT, vT, gT))
        out = jnp.transpose(outs, (1, 0, 2, 3)).reshape(Bb, Ll, Hid)
        mu = out.mean(-1, keepdims=True)
        var = out.var(-1, keepdims=True)
        out = (out - mu) / jnp.sqrt(var + 1e-05) * gamma + beta
        out = out * jax.nn.silu(x @ Wg)
        return out @ Wout

    def _L2_ffn_ref(x, W1, b1, W2, b2):
        import jax, jax.numpy as jnp
        import numpy as np
        QB = 127.0
        EPS = 1e-05

        def _ste(x, q):
            return x + jax.lax.stop_gradient(q - x)

        def bitlinear(x, W, b):
            w_scale = jnp.clip(jnp.mean(jnp.abs(W)), EPS, None)
            Wq = _ste(W, jnp.clip(jnp.round(W / w_scale), -1.0, 1.0) * w_scale)
            x_scale = jnp.clip(jnp.max(jnp.abs(x), axis=-1, keepdims=True), EPS, None)
            xq = _ste(x, jnp.clip(jnp.round(x * (QB / x_scale)), -QB - 1.0, QB) * (x_scale / QB))
            return jnp.einsum('bnd,hd->bnh', xq, Wq) + b
        h = bitlinear(x, W1, b1)
        h = jax.nn.gelu(h, approximate=False)
        return bitlinear(h, W2, b2)

    def _L3_attn_ref(x, ln1_g, ln1_b, ln2_g, ln2_b, time_decay, time_first, time_mix_k, time_mix_v, time_mix_r, att_Wk, att_Wv, att_Wr, att_Wo, cm_k, cm_r, ffn_Wk, ffn_Wr, ffn_Wv):
        import jax, jax.numpy as jnp
        import numpy as np
        B, T, C = (8, 512, 256)
        NL, LID = (12, 1)
        H = 4 * C

        def _ln(x, g, b):
            m = x.mean(-1, keepdims=True)
            v = ((x - m) ** 2).mean(-1, keepdims=True)
            return (x - m) * jax.lax.rsqrt(v + 1e-05) * g + b

        def _shift(x):
            return jnp.pad(x, ((0, 0), (1, 0), (0, 0)))[:, :-1]

        def _wkv(time_decay, time_first, k, v):
            w = -jnp.exp(time_decay)
            kt = jnp.moveaxis(k, 1, 0)
            vt = jnp.moveaxis(v, 1, 0)
            Bb, Cc = (k.shape[0], k.shape[2])
            init = (jnp.zeros((Bb, Cc), k.dtype), jnp.zeros((Bb, Cc), k.dtype), jnp.full((Bb, Cc), -1e+38, k.dtype))

            def step(carry, kv_t):
                aa, bb, pp = carry
                kk, vv = kv_t
                ww = time_first + kk
                p = jnp.maximum(pp, ww)
                e1 = jnp.exp(pp - p)
                e2 = jnp.exp(ww - p)
                out = (e1 * aa + e2 * vv) / (e1 * bb + e2)
                ww2 = pp + w
                p2 = jnp.maximum(ww2, kk)
                e1b = jnp.exp(ww2 - p2)
                e2b = jnp.exp(kk - p2)
                return ((e1b * aa + e2b * vv, e1b * bb + e2b, p2), out)
            _, out = jax.lax.scan(step, init, (kt, vt))
            return jnp.moveaxis(out, 0, 1)
        xa = _ln(x, ln1_g, ln1_b)
        xx = _shift(xa)
        xk = xa * time_mix_k + xx * (1 - time_mix_k)
        xv = xa * time_mix_v + xx * (1 - time_mix_v)
        xr = xa * time_mix_r + xx * (1 - time_mix_r)
        k = jnp.einsum('btc,oc->bto', xk, att_Wk)
        v = jnp.einsum('btc,oc->bto', xv, att_Wv)
        r = jnp.einsum('btc,oc->bto', xr, att_Wr)
        rwkv = jax.nn.sigmoid(r) * _wkv(time_decay, time_first, k, v)
        x = x + jnp.einsum('bto,co->btc', rwkv, att_Wo)
        xc = _ln(x, ln2_g, ln2_b)
        xx2 = _shift(xc)
        xk2 = xc * cm_k + xx2 * (1 - cm_k)
        xr2 = xc * cm_r + xx2 * (1 - cm_r)
        kk = jnp.square(jax.nn.relu(jnp.einsum('btc,hc->bth', xk2, ffn_Wk)))
        kv = jnp.einsum('bth,ch->btc', kk, ffn_Wv)
        rkv = jax.nn.sigmoid(jnp.einsum('btc,oc->bto', xr2, ffn_Wr)) * kv
        return x + rkv

    def _L3_ffn_ref(hidden_states, gate_w, gate_up_w, down_w):
        import jax, jax.numpy as jnp
        import numpy as np
        H = 256
        F = 1024
        E = 8
        TOP_K = 2
        B, S = (1, 512)
        b, s, h = hidden_states.shape
        x = hidden_states.reshape(-1, h)
        router_logits = x @ gate_w.T
        probs = jax.nn.softmax(router_logits.astype(jnp.float32), axis=-1)
        topw, sel = jax.lax.top_k(probs, TOP_K)
        topw = topw / jnp.sum(topw, axis=-1, keepdims=True)
        topw = topw.astype(x.dtype)
        combine = jnp.sum(jax.nn.one_hot(sel, E, dtype=x.dtype) * topw[..., None], axis=1)
        gu = jnp.einsum('th,efh->etf', x, gate_up_w)
        gate, up = (gu[..., :F], gu[..., F:])
        hact = up * jax.nn.gelu(gate, approximate=False)
        expert_out = jnp.einsum('etf,ehf->eth', hact, down_w)
        out = jnp.einsum('eth,te->th', expert_out, combine)
        return out.reshape(b, s, h)
    h = _L0_tok_ref(x, L0_tok_embed_weight, L0_tok_proj_weight, L0_tok_scale)
    h = h + _L0_attn_ref(_layernorm(h, axis=-1), L0_attn_Wq, L0_attn_bq, L0_attn_Wk, L0_attn_bk, L0_attn_Wv, L0_attn_bv, L0_attn_Wo, L0_attn_bo, L0_attn_g1, L0_attn_b1, L0_attn_Wf1, L0_attn_bf1, L0_attn_Wf2, L0_attn_bf2, L0_attn_g2, L0_attn_b2)
    h = h + _L0_ffn_ref(_layernorm(h, axis=-1), L0_ffn_router_w, L0_ffn_router_bias, L0_ffn_expert_gate_w, L0_ffn_expert_up_w, L0_ffn_expert_down_w, L0_ffn_conv_w, L0_ffn_shared_up_w, L0_ffn_shared_down_w)
    h = h + _L1_attn_ref(_layernorm(h, axis=-1), L1_attn_a_params, L1_attn_B_w, L1_attn_C_w, L1_attn_D)
    h = h + _L1_ffn_ref(_layernorm(h, axis=-1), L1_ffn_W_r, L1_ffn_W_k, L1_ffn_W_v, L1_ffn_mu_r, L1_ffn_mu_k)
    h = h + _L2_attn_ref(_layernorm(h, axis=-1), L2_attn_Wq, L2_attn_Wk, L2_attn_Wv, L2_attn_Wg, L2_attn_Wgk1, L2_attn_Wgk2, L2_attn_bgk2, L2_attn_gamma, L2_attn_beta, L2_attn_Wout)
    h = h + _L2_ffn_ref(_layernorm(h, axis=-1), L2_ffn_W1, L2_ffn_b1, L2_ffn_W2, L2_ffn_b2)
    h = h + _L3_attn_ref(_layernorm(h, axis=-1), L3_attn_ln1_g, L3_attn_ln1_b, L3_attn_ln2_g, L3_attn_ln2_b, L3_attn_time_decay, L3_attn_time_first, L3_attn_time_mix_k, L3_attn_time_mix_v, L3_attn_time_mix_r, L3_attn_att_Wk, L3_attn_att_Wv, L3_attn_att_Wr, L3_attn_att_Wo, L3_attn_cm_k, L3_attn_cm_r, L3_attn_ffn_Wk, L3_attn_ffn_Wr, L3_attn_ffn_Wv)
    h = h + _L3_ffn_ref(_layernorm(h, axis=-1), L3_ffn_gate_w, L3_ffn_gate_up_w, L3_ffn_down_w)
    return h

_drawn_inputs = setup_inputs


def setup_inputs(seed=0):
    import zlib

    import numpy as np

    out = dict(_drawn_inputs(seed))
    spreads = {'L0_attn_bq': (0.0, 0.8),
     'L0_attn_bk': (0.0, 0.8),
     'L0_attn_bv': (0.0, 0.1),
     'L0_attn_bo': (0.0, 0.1),
     'L0_attn_g1': (1.0, 0.6),
     'L0_attn_b1': (0.0, 0.1),
     'L0_attn_bf1': (0.0, 0.1),
     'L0_attn_bf2': (0.0, 0.1),
     'L0_attn_g2': (1.0, 0.2),
     'L0_attn_b2': (0.0, 0.1),
     'L0_ffn_router_bias': (0.0, 0.419),
     'L1_attn_D': (0.0, 0.8),
     'L2_attn_bgk2': (0.0, 0.8),
     'L2_attn_gamma': (1.0, 0.6),
     'L2_attn_beta': (0.0, 0.8),
     'L2_ffn_b1': (0.0, 0.8),
     'L2_ffn_b2': (0.0, 2.0),
     'L3_attn_ln1_g': (1.0, 0.6),
     'L3_attn_ln1_b': (0.0, 0.8),
     'L3_attn_ln2_g': (1.0, 0.6),
     'L3_attn_ln2_b': (0.0, 0.8)}
    factors = {'L0_ffn_expert_up_w': 3.156,
     'L1_ffn_W_r': 8.0,
     'L1_ffn_W_k': 8.0,
     'L1_ffn_W_v': 8.0,
     'L1_ffn_mu_r': 8.0,
     'L1_ffn_mu_k': 8.0,
     'L2_attn_Wq': 8.0,
     'L2_attn_Wk': 8.0,
     'L2_attn_Wv': 8.0,
     'L2_attn_Wg': 8.0,
     'L2_attn_Wgk1': 8.0,
     'L2_attn_Wgk2': 8.0,
     'L2_attn_Wout': 8.0,
     'L2_ffn_W1': 8.0,
     'L2_ffn_W2': 8.0,
     'L3_attn_time_decay': 8.0,
     'L3_attn_time_first': 8.0,
     'L3_attn_time_mix_k': 8.0,
     'L3_attn_time_mix_v': 8.0,
     'L3_attn_time_mix_r': 8.0,
     'L3_attn_att_Wk': 8.0,
     'L3_attn_att_Wv': 8.0,
     'L3_attn_att_Wr': 8.0,
     'L3_attn_att_Wo': 8.0,
     'L3_attn_cm_k': 8.0,
     'L3_attn_cm_r': 8.0,
     'L3_attn_ffn_Wk': 8.0,
     'L3_attn_ffn_Wr': 8.0,
     'L3_attn_ffn_Wv': 8.0,
     'L3_ffn_gate_w': 51.804,
     'L3_ffn_gate_up_w': 46.603,
     'L3_ffn_down_w': 46.677}
    for name, (base, spread) in spreads.items():
        noise = np.random.default_rng([zlib.crc32(name.encode()), seed]).standard_normal(out[name].shape)
        drawn = base * np.exp(spread * noise) if base else spread * noise
        out[name] = jnp.asarray(drawn.astype(out[name].dtype))
    for name, factor in factors.items():
        out[name] = (out[name] * factor).astype(out[name].dtype)
    return out
```

```python
from contextlib import ExitStack

import numpy as np
import concourse.bass as bass
from concourse import mybir

F32 = mybir.dt.float32
BF16 = mybir.dt.bfloat16
I32 = mybir.dt.int32
U32 = mybir.dt.uint32
ACT = mybir.ActivationFunctionType
ALU = mybir.AluOpType
AX = mybir.AxisListType

P = 128
D = 256
NH = D // P
B, T = 8, 256
N = B * T
TN = 512
TILES = N // TN
SPT = TN // T
PAD = 2
EPS = 1e-5
ROUND = 12582912.0

NORMS = {f"n{j}": j for j in range(13)}
WITH_BIAS = ["n1", "n2", "n7", "n10", "n11"]
NORM_COUNT = {"mean": TILES, "var": TILES, "std": TILES, "rstd": TILES, "centred": 2 * TILES, "squared": 2 * TILES,
              "scaled": 2 * TILES, "done": 2 * TILES}

VECS = ["bq", "bk", "bo", "g1", "b1", "g2", "b2", "bf2", "D", "mu_r", "mu_k", "bgk2", "gamma", "beta",
        "ln1_g", "ln1_b", "ln2_g", "ln2_b", "decay", "first", "mix_k", "mix_v", "mix_r", "cm_k", "cm_r"]
VCOL = {n: 2 * i for i, n in enumerate(VECS)}
NV = 2 * len(VECS)
BF1 = NV
NVEC = NV + 8


PRIMED = [
    "att+kv_turned+y_turned", "att_out+softplus2+exps+cm_sig+w3_copied", "cos_done+moe_h+summed+gate_sums+x_clip+pp",
    "emb_copied+qk_copied+moe_silu+before+qkv_read+xq_copied+befo",
    "emb_proj+qk_ready+moe_in+fourier_in+qkv_ready+x_turned+mix_r",
    "emb_turned+swapped+moe_down+ssm_out+gate_ready+xq_turned+wkv", "exp_done+rk_read+gate_read+h_gelu+kvr_read",
    "expert_in", "expert_in0", "expert_in1", "factors", "ff1+g_ready", "ff2+l2a_ready",
    "ff_read+l2a_read+hid_127+ffv_read+l3f_done", "g_read", "gelu_done+softplus3+before4+gelu3", "h0_done",
    "h_quantised+l3a_done+scaled3", "h_shifted+x3_done+hact", "keys_spread+state+hid_clip+ratio", "kv_copied",
    "l0a_done", "masked+moe_own_in+ssm_read+gate_to_mid+x_scale+p_max", "norm_centred", "norm_done", "norm_mean",
    "norm_rstd", "norm_scaled", "norm_squared", "norm_std", "norm_var", "picked", "probs+v_spread+hid_max+den_inv",
    "probs_copied+softplus1+hq_copied+ffk_relu", "probs_turned+v_ready+gla_att+hq_turned+ffk_ready+gu_ready",
    "rotated+moe_own+turned_out+to_mid+x_inv+pp_prev", "row_inv+l1f_done+gla_masked+h_scaled+den",
    "row_max+moe_out+l1a_done+clamped+x_127+exp_args", "row_sum+v_read+decayed+x_quantised+num",
    "scores+rk_ready+gla_scores+h_ready+cm_ready+w3_spread", "seq_staged+sum_in+k_squared+keys_staged+tile_staged",
    "shifted+mixed+to_end+x_shifted+sums", "swap_used+moe_up+turned_in+log_gate+x_max+mixed3+ffk_squared",
    "values+v_turned+y_ready+ffv_ready+down_ready", "values_spread+gla_out+hid_inv+mixed4",
    "wo_done+gated+hid_scale+wkv", "wo_ready+state_sum", "x3_added", "y_added", "y_scaled",
    "z_ready+q_spread+wkv_pool",
]

SHARED = [
    [("emb_proj", 8), ("qk_ready", 12), ("moe_in", 64), ("fourier_in", 8), ("qkv_ready", 28), ("x_turned", 16), ("mix_ready", 24)],
    [("emb_turned", 4), ("swapped", 12), ("moe_down", 64), ("ssm_out", 8), ("gate_ready", 8), ("xq_turned", 16), ("wkv_out", 8)],
    [("scores", 32), ("rk_ready", 16), ("gla_scores", 32), ("h_ready", 16), ("cm_ready", 8), ("w3_spread", 32)],
    [("probs_turned", 32), ("v_ready", 8), ("gla_att", 32), ("hq_turned", 16), ("ffk_ready", 32), ("gu_ready", 256)],
    [("values", 8), ("v_turned", 8), ("y_ready", 16), ("ffv_ready", 8), ("down_ready", 64)],
    [("att", 32), ("kv_turned", 8), ("y_turned", 16)],
    [("wo_ready", 8), ("state_sum", 8)],
    [("ff1", 32), ("g_ready", 8)],
    [("ff2", 8), ("l2a_ready", 8)],
    [("emb_copied", 4), ("qk_copied", 12), ("moe_silu", 64), ("before", 16), ("qkv_read", 28), ("xq_copied", 16), ("before3", 24)],
    [("exp_done", 32), ("rk_read", 16), ("gate_read", 8), ("h_gelu", 16), ("kvr_read", 24)],
    [("probs_copied", 32), ("softplus1", 8), ("hq_copied", 16), ("ffk_relu", 32)],
    [("att_out", 32), ("softplus2", 8), ("exps", 32), ("cm_sig", 8), ("w3_copied", 32)],
    [("gelu_done", 32), ("softplus3", 8), ("before4", 16), ("gelu3", 256)],
    [("factors", 24)], [("kv_copied", 8)], [("g_read", 8)],
    [("swap_used", 12), ("moe_up", 60), ("turned_in", 16), ("log_gate", 8), ("x_max", 16), ("mixed3", 24), ("ffk_squared", 32)],
    [("cos_done", 12), ("moe_h", 64), ("summed", 8), ("gate_sums", 8), ("x_clip", 16), ("pp", 8)],
    [("rotated", 12), ("moe_own", 8), ("turned_out", 16), ("to_mid", 8), ("x_inv", 16), ("pp_prev", 8)],
    [("masked", 32), ("moe_own_in", 8), ("ssm_read", 8), ("gate_to_mid", 8), ("x_scale", 16), ("p_max", 8)],
    [("row_max", 32), ("moe_out", 8), ("l1a_done", 8), ("clamped", 8), ("x_127", 16), ("exp_args", 32)],
    [("shifted", 32), ("mixed", 16), ("to_end", 8), ("x_shifted", 16), ("sums", 16)],
    [("row_sum", 32), ("v_read", 8), ("decayed", 16), ("x_quantised", 16), ("num", 8)],
    [("row_inv", 32), ("l1f_done", 8), ("gla_masked", 32), ("h_scaled", 16), ("den", 8)],
    [("probs", 32), ("v_spread", 8), ("hid_max", 16), ("den_inv", 8)],
    [("keys_spread", 8), ("state", 8), ("hid_clip", 16), ("ratio", 8)],
    [("values_spread", 16), ("gla_out", 32), ("hid_inv", 16), ("mixed4", 16)],
    [("wo_done", 8), ("gated", 8), ("hid_scale", 16), ("wkv", 8)],
    [("ff_read", 8), ("l2a_read", 8), ("hid_127", 16), ("ffv_read", 8), ("l3f_done", 64)],
    [("h_shifted", 16), ("x3_done", 8), ("hact", 256)], [("h_quantised", 16), ("l3a_done", 8), ("scaled3", 64)],
    [("seq_staged", 16), ("sum_in", 8), ("k_squared", 8), ("keys_staged", 8), ("tile_staged", 4)],
    [("z_ready", 8), ("q_spread", 32), ("wkv_pool", 32)],
]
PLACE = {}
for _row in SHARED:
    _base = 0
    for _name, _count in _row:
        PLACE[_name] = ("+".join(n for n, _ in _row)[:60], _base)
        _base += _count


class Kernel:

    def __init__(self, nc, ctx, ins, out):
        self.nc, self.ctx, self.ins, self.out = nc, ctx, ins, out
        self.sems = {}
        self.unprimed = set()

    def sem(self, name):
        if name.split("_")[0] in NORMS:
            name = "norm_" + name.split("_")[1]
        name = PLACE.get(name, (name, 0))[0]
        if name not in self.sems:
            self.sems[name] = self.ctx.enter_context(self.nc.semaphore(name))
        return self.sems[name]

    def at(self, name, count):
        norm, _, what = name.partition("_")
        if norm in NORMS:
            name = "norm_" + what
            count = count + NORM_COUNT[what] * (NORMS[norm] if what != "done" else WITH_BIAS.index(norm))
        name, before = PLACE.get(name, (name, 0))
        count = count + before
        if type(count) is not int and name not in PRIMED:
            self.unprimed.add(name)
        return self.sem(name), count + (1 if name in PRIMED else 0)

    def sb(self, name, cols, dt=F32, parts=P):
        return self.ctx.enter_context(self.nc.sbuf_tensor(name, [parts, cols], dt))


def seqs(buf):
    return buf[:, 0:NH * N].rearrange("p (h s t) -> p h s t", h=NH, s=B)


def tile(view, h, t):
    return view[:, h, bass.ds(t * SPT, SPT), :]


def blocks(ap, k):
    return ap.rearrange("p (k m) -> p k m", k=k)


def allocate(k):
    nc = k.nc
    k.H = seqs(k.sb("residual", NH * N))
    k.Ybuf = k.sb("normed", NH * B * (T + PAD))
    k.Y = k.Ybuf[:, :].rearrange("p (h s t) -> p h s t", h=NH, s=B)
    for n in "ABCDEQ":
        k.raw = k.sb("buf" + n, NH * N)
        if n == "A": k.A = k.raw
        if n == "B": k.B = k.raw
        if n == "C": k.C = k.raw
        if n == "D": k.D = k.raw
        if n == "E": k.E = k.raw
        if n == "Q": k.Q = k.raw
    k.R = k.sb("rstd", 2 * TN)
    k.W = k.sb("weights0", 9344)
    k.V = k.sb("weights1", 5504)
    k.ident = k.sb("ident", P)
    k.identb = k.sb("identb", P, BF16)
    k.mean_w = k.sb("mean_w", P)
    k.vec = k.sb("vec", NVEC)
    k.vec2 = k.sb("vec2", 24)
    k.rope = k.sb("rope", 2 * T)
    k.attc = k.sb("attc", 4 * P + 4 + 8 + 16)
    k.perm = k.attc[:, 0:P]
    k.band = k.attc[:, P:3 * P].rearrange("p (m k) -> p m k", m=2)
    k.causal = k.attc[:, 3 * P:4 * P]
    k.groupmask = k.attc[:, 4 * P:4 * P + 4]
    k.headmask = k.attc[:, 4 * P + 4:4 * P + 12]
    k.small = k.sb("small", 1024)
    k.PS = k.ctx.enter_context(nc.psum_tensor("banks", [P, 8, 512], F32))
    k.eps = k.small[:, 1023:1024]


def yt(k, h, t, shift=0):
    return k.Y[:, h, bass.ds(t * SPT, SPT), PAD - shift:PAD - shift + T]


def bank(k, b):
    return k.PS[:, b, :]


def bank_seq(k, b):
    return k.PS[:, b, :].rearrange("p (s t) -> p s t", s=SPT)


def rstd(k, p):
    return k.R[:, p * TN:(p + 1) * TN].rearrange("p (s t) -> p s t", s=SPT)


def vcol(k, name, h=0):
    return k.vec[:, VCOL[name] + h:VCOL[name] + h + 1]



def norm_pe(k, pe, n, src, ready, per_tile, free=()):
    for s, v in free:
        pe.wait_ge(*k.at(s, v))
    with pe.Fori(0, TILES // 2) as i:
        for par in range(2):
            t = 2 * i + par
            pe.wait_ge(*k.at(ready, per_tile * (t + 1)))
            pe.wait_ge(*k.at(n + "_centred", 4 * i))
            for h in range(NH):
                mm = pe.matmul(bank(k, par), k.mean_w[:, :], tile(src, h, t), start=h == 0, stop=h == 1)
            mm.then_inc(k.sem(n + "_mean"), 1)
    with pe.Fori(0, TILES // 2) as i:
        for par in range(2):
            t = 2 * i + par
            pe.wait_ge(*k.at(n + "_squared", 2 * (t + 1)))
            pe.wait_ge(*k.at(n + "_std", 2 * i))
            for h in range(NH):
                mm = pe.matmul(bank(k, 2 + par), k.mean_w[:, :], tile(seqs(k.Q), h, t), start=h == 0, stop=h == 1)
            mm.then_inc(k.sem(n + "_var"), 1)


def norm_act(k, act, n, bias=None, dst=None, free=()):
    for s, v in free:
        act.wait_ge(*k.at(s, v))
    with act.Fori(0, TILES) as t:
        for h in range(NH):
            act.wait_ge(*k.at(n + "_centred", 2 * t + h + 1))
            act.activation(tile(seqs(k.Q), h, t), tile(seqs(k.D), h, t), ACT.Square).then_inc(k.sem(n + "_squared"), 1)
    with act.Fori(0, TILES // 2) as i:
        for par in range(2):
            t = 2 * i + par
            act.wait_ge(*k.at(n + "_var", t + 1))
            act.wait_ge(*k.at(n + "_scaled", 4 * i))
            act.activation(k.R[:, par * TN:(par + 1) * TN], bank(k, 2 + par), ACT.Sqrt, bias=k.eps).then_inc(k.sem(n + "_std"), 1)
    if bias is not None:
        with act.Fori(0, TILES) as t:
            for h in range(NH):
                act.wait_ge(*k.at(n + "_scaled", 2 * t + h + 1))
                act.activation(dst(h, t), tile(seqs(k.D), h, t), ACT.Identity, bias=vcol(k, bias, h)).then_inc(k.sem(n + "_done"), 1)


def norm_dve(k, dve, n, src, gain=None, dst=None, free=()):
    for s, v in free:
        dve.wait_ge(*k.at(s, v))
    with dve.Fori(0, TILES // 2) as i:
        for par in range(2):
            t = 2 * i + par
            dve.wait_ge(*k.at(n + "_mean", t + 1))
            for h in range(NH):
                dve.tensor_tensor(tile(seqs(k.D), h, t), tile(src, h, t), bank_seq(k, par), ALU.subtract).then_inc(k.sem(n + "_centred"), 1)
    with dve.Fori(0, TILES // 2) as i:
        for par in range(2):
            t = 2 * i + par
            dve.wait_ge(*k.at(n + "_std", t + 1))
            dve.reciprocal(k.R[:, par * TN:(par + 1) * TN], k.R[:, par * TN:(par + 1) * TN]).then_inc(k.sem(n + "_rstd"), 1)
            dve.wait_ge(*k.at(n + "_rstd", t + 1))
            for h in range(NH):
                dve.wait_ge(*k.at(n + "_squared", 2 * t + h + 1))
                if gain is None:
                    dve.tensor_tensor(dst(h, t), tile(seqs(k.D), h, t), rstd(k, par), ALU.mult).then_inc(k.sem(n + "_scaled"), 1)
                else:
                    dve.scalar_tensor_tensor(tile(seqs(k.D), h, t), tile(seqs(k.D), h, t), vcol(k, gain, h), rstd(k, par), ALU.mult, ALU.mult).then_inc(k.sem(n + "_scaled"), 1)



def load_constants(k, sp):
    i = k.ins
    for dst, name in ((k.ident, "c_ident"), (k.mean_w, "c_mean"), (k.vec, "vecs"), (k.rope, "c_rope"), (k.attc, "c_att")):
        sp.dma_start(dst[:, :], i[name]).then_inc(k.sem("constants"), 16)
    sp.dma_start(k.identb[:, :], i["c_identb"]).then_inc(k.sem("constants"), 16)


CONST = 6 * 16


def load(k, sp, dst, src, sem):
    sp.dma_start(dst, src).then_inc(k.sem(sem), 16)



def hash_views(k):
    s = k.small[:, :].bitcast(I32)
    return [s[:, 16 * j:16 * j + 16] for j in range(20)]


def tok_load(k, sp):
    i = k.ins
    v = hash_views(k)
    sp.dma_start(v[0], i["tok"]).then_inc(k.sem("tok_in"), 16)
    sp.dma_start(v[1], i["tok_prev"]).then_inc(k.sem("tok_in"), 16)
    sp.dma_start(k.small[:, 320:336], i["c_first"]).then_inc(k.sem("tok_in"), 16)
    sp.dma_start(k.small[:, 336:337], i["scale"].to_broadcast([P, 1])).then_inc(k.sem("tok_in"), 16)
    sp.dma_start(k.W[0:64, 0:256], i["projT"]).then_inc(k.sem("tok_in"), 16)


def tok_dve(k, dve):
    v = hash_views(k)
    f = k.small
    done = [0]

    def chain(ins):
        done[0] += 1
        ins.then_inc(k.sem("hash_step"), 1)
        dve.wait_ge(*k.at("hash_step", done[0]))
    dve.memset(k.eps, EPS).then_inc(k.sem("eps_set"), 1)
    dve.memset(k.Y[:, :, :, 0:PAD], 0.0).then_inc(k.sem("pad_set"), 1)
    dve.wait_ge(*k.at("constants", CONST))
    for j, name in enumerate(["mu_r", "mu_k", "mix_k", "mix_v", "mix_r", "cm_k", "cm_r"]):
        dve.tensor_scalar(k.vec2[:, 2 * j:2 * j + 2], k.vec[:, VCOL[name]:VCOL[name] + 2], -1.0, 1.0, ALU.mult, ALU.add).then_inc(k.sem("rest_ready"), 1)
    dve.wait_ge(*k.at("tok_in", 80))
    limbs = []
    for src, mul, o in ((0, 36313, 2), (1, 27191, 9)):
        lo, hi, p0, p1, mid, a, b = v[o:o + 7]
        chain(dve.tensor_scalar(lo, v[src], 255, None, ALU.bitwise_and))
        chain(dve.tensor_scalar(hi, v[src], 8, None, ALU.logical_shift_right))
        chain(dve.tensor_scalar(p0, lo, float(mul), None, ALU.mult))
        chain(dve.tensor_scalar(p1, hi, float(mul), None, ALU.mult))
        chain(dve.tensor_scalar(mid, p1, 255, 8, ALU.bitwise_and, ALU.logical_shift_left))
        chain(dve.tensor_tensor(p0, p0, mid, ALU.add))
        chain(dve.tensor_scalar(a, p0, 65535, None, ALU.bitwise_and))
        chain(dve.tensor_scalar(b, p0, 16, None, ALU.logical_shift_right))
        chain(dve.tensor_scalar(p1, p1, 8, None, ALU.logical_shift_right))
        chain(dve.tensor_tensor(b, b, p1, ALU.add))
        limbs.append((a, b))
    (a0, b0), (a1, b1) = limbs
    chain(dve.tensor_tensor(a0, a0, a1, ALU.bitwise_xor))
    chain(dve.tensor_tensor(b0, b0, b1, ALU.bitwise_xor))
    sm, neg, big = f[:, 352:368], f[:, 368:384], f[:, 384:400]
    chain(dve.tensor_tensor(sm, a0, b0, ALU.add))
    chain(dve.tensor_scalar(neg, b0, 32768.0, None, ALU.is_ge))
    chain(dve.tensor_tensor(sm, sm, neg, ALU.subtract))
    chain(dve.tensor_scalar(big, sm, 65535.0, -65535.0, ALU.is_ge, ALU.mult))
    chain(dve.tensor_tensor(sm, sm, big, ALU.add))
    first = f[:, 320:336]
    chain(dve.scalar_tensor_tensor(neg, sm, -65535.0, first, ALU.add, ALU.mult))
    chain(dve.tensor_tensor(sm, sm, neg, ALU.subtract))
    dve.tensor_copy(f[:, 400:416].bitcast(U32), sm).then_inc(k.sem("rows_known"), 1)


def tok_pool(k, pool):
    pool.wait_ge(*k.at("rows_known", 1))
    idx = k.small[:, 400:416].bitcast(U32)
    for j in range(N // P):
        pool.indirect_dma_start(k.B[:, 64 * j:64 * j + 64], None, k.ins["embed"],
                                bass.IndirectOffsetOnAxis(ap=idx[:, j:j + 1], axis=0)).then_inc(k.sem("gathered"), 16)


def tok_pe(k, pe):
    pe.wait_ge(*k.at("constants", CONST))
    pe.wait_ge(*k.at("gathered", 16 * (N // P)))
    for t in range(TILES):
        if t >= 2:
            pe.wait_ge(*k.at("emb_copied", t - 1))
        for j in range(TN // P):
            mm = pe.transpose(k.PS[0:64, t % 2, j * P:(j + 1) * P], k.B[:, 64 * (4 * t + j):64 * (4 * t + j) + 64], k.ident[:, :])
        mm.then_inc(k.sem("emb_turned"), 1)
    pe.wait_ge(*k.at("tok_in", 80))
    for t in range(TILES):
        pe.wait_ge(*k.at("emb_copied", t + 1))
        if t >= 2:
            pe.wait_ge(*k.at("h0_done", 2 * (t - 1)))
        for m in range(NH):
            pe.matmul(bank(k, 2 + 2 * (t % 2) + m), k.W[0:64, m * P:(m + 1) * P],
                      k.A[0:64, t * TN:(t + 1) * TN], start=True, stop=True).then_inc(k.sem("emb_proj"), 1)


def tok_act(k, act):
    act.wait_ge(*k.at("tok_in", 80))
    for t in range(TILES):
        act.wait_ge(*k.at("emb_turned", t + 1))
        act.activation(k.A[0:64, t * TN:(t + 1) * TN], k.PS[0:64, t % 2, :], ACT.Copy).then_inc(k.sem("emb_copied"), 1)
    for t in range(TILES):
        for m in range(NH):
            act.wait_ge(*k.at("emb_proj", 2 * t + m + 1))
            act.activation(tile(k.H, m, t), bank_seq(k, 2 + 2 * (t % 2) + m), ACT.Copy, scale=k.small[:, 336:337]).then_inc(k.sem("h0_done"), 1)



QB = T // 64
WINDOW0 = [max(0, 64 * q - 64) for q in range(QB)]
L0 = {"wq": 0, "wk": 512, "wv": 768, "wo": 896, "wf1": 1408, "wf2": 3456}


def l0a_w(k, name, cols, nk=NH):
    return blocks(k.V[:, L0[name]:L0[name] + nk * cols], nk)


def l0a_load(k, sp):
    sp.dma_start(k.V[:, 0:5504], k.ins["l0a_w"]).then_inc(k.sem("l0a_weights"), 16)
    sp.dma_start(k.small[:, 448:512], k.ins["bv"].to_broadcast([P, 64])).then_inc(k.sem("l0a_weights"), 16)


def att_views(k):
    a = {}
    a["qs"] = k.E[:, 2048:2560]
    a["ys"] = k.E[:, 2560:3072].rearrange("p (h t) -> p h t", h=2)
    a["sm"] = [k.E[:, 3072:4096].rearrange("p (a k) -> p a k", a=8), k.C[:, 3072:4096].rearrange("p (a k) -> p a k", a=8)]
    a["pt"] = [k.E[:, 0:1024].rearrange("p (a k) -> p a k", a=8), k.E[:, 1024:2048].rearrange("p (a k) -> p a k", a=8)]
    a["kz"] = k.C[:, 2048:3072].rearrange("p (g t) -> p g t", g=4)
    a["k"] = k.C[:, 0:2048].rearrange("p (s t) -> p s t", s=B)
    a["vz"] = k.Q[:, :].rearrange("p (w a m) -> p w a m", w=4, a=8)
    a["mx"] = k.small[:, 512:528]
    a["sum"] = k.small[:, 528:544]
    return a


QKB = [(0, 1, 4), (5, 6, 7)]


def l0a_pe(k, pe):
    a = att_views(k)
    norm_pe(k, pe, "n0", k.H, "h0_done", 2, free=(("h0_done", 2 * TILES),))
    norm_pe(k, pe, "n1", seqs(k.A), "n0_scaled", 2)
    pe.wait_ge(*k.at("l0a_weights", 32))
    wq, wk = l0a_w(k, "wq", D), l0a_w(k, "wk", P)
    with pe.Fori(0, TILES // 2) as i:
        for par in range(2):
            t = 2 * i + par
            pe.wait_ge(*k.at("n1_done", 2 * (t + 1)))
            pe.wait_ge(*k.at("qk_copied", 6 * i))
            for o in range(3):
                for h in range(NH):
                    w = wk[:, h, :] if o == 2 else wq[:, h, o * P:(o + 1) * P]
                    mm = pe.matmul(bank(k, QKB[par][o]), w, yt(k, h, t), start=h == 0, stop=h == 1)
                mm.then_inc(k.sem("qk_ready"), 1)
    with pe.Fori(0, TILES // 2) as i:
        for m in range(6):
            t = 2 * i + m // 3
            pe.wait_ge(*k.at("qk_copied", 6 * i + m + 1))
            pe.wait_ge(*k.at("swap_used", 6 * i + max(m - 1, 0)))
            src = a["k"][:, bass.ds(t * SPT, SPT), :] if m % 3 == 2 else tile(seqs(k.B), m % 3, t)
            pe.matmul(bank(k, 2 + m % 2), k.perm, src, start=True, stop=True).then_inc(k.sem("swapped"), 1)

    wv = l0a_w(k, "wv", 64)
    with pe.Fori(0, B) as b:

        def scores(qb):
            if qb == 0:
                pe.wait_ge(*k.at("keys_spread", b + 1))
            if qb >= 2:
                pe.wait_ge(*k.at("masked", 4 * b + qb - 1))
            for j2 in range(2):
                mm = pe.matmul(bank(k, 1 + 2 * (qb % 2) + j2), a["qs"][64 * j2:64 * j2 + 64, P * qb:P * qb + P],
                               a["kz"][64 * j2:64 * j2 + 64, :, WINDOW0[qb]:WINDOW0[qb] + P], start=True, stop=True)
            mm.then_inc(k.sem("scores"), 1)

        def values(qb):
            pe.wait_ge(*k.at("probs", 4 * b + qb + 1))
            pe.wait_ge(*k.at("probs_copied", 4 * b + qb))
            for x in range(8):
                mm = pe.transpose(k.PS[:, 5 + x // 4, (x % 4) * P:(x % 4 + 1) * P], a["sm"][qb % 2][:, x, :], k.ident[:, :])
            mm.then_inc(k.sem("probs_turned"), 1)
            if qb == 0:
                pe.wait_ge(*k.at("values_spread", 2 * b + 2))
            pe.wait_ge(*k.at("probs_copied", 4 * b + qb + 1))
            pe.wait_ge(*k.at("att_out", 4 * b + qb))
            for x in range(8):
                mm = pe.matmul(k.PS[:, 7, 0:P], a["vz"][:, qb, x, :], a["pt"][qb % 2][:, x, :], start=x == 0, stop=x == 7)
            mm.then_inc(k.sem("att"), 1)

        pe.wait_ge(*k.at("seq_staged", 2 * b + 2))
        pe.wait_ge(*k.at("values_spread", 2 * b))
        for w in range(4):
            for h in range(NH):
                mm = pe.matmul(k.PS[:, 0, 64 * w:64 * w + 64], a["ys"][:, h, WINDOW0[w]:WINDOW0[w] + P], wv[:, h, :],
                               start=h == 0, stop=h == 1)
        mm.then_inc(k.sem("values"), 1)
        pe.wait_ge(*k.at("masked", 4 * b))
        scores(0)
        scores(1)
        for qb in range(QB):
            values(qb)
            if qb + 2 < QB:
                scores(qb + 2)

    wo = l0a_w(k, "wo", D)
    pe.wait_ge(*k.at("att_out", 4 * B))
    with pe.Fori(0, TILES // 2) as i:
        for par in range(2):
            t = 2 * i + par
            pe.wait_ge(*k.at("wo_done", 4 * i))
            for m in range(NH):
                for j in range(2):
                    mm = pe.matmul(bank(k, 4 + 2 * par + m), wo[:, j, m * P:(m + 1) * P], tile(seqs(k.D), j, t), start=j == 0, stop=j == 1)
                mm.then_inc(k.sem("wo_ready"), 1)
    norm_pe(k, pe, "n2", seqs(k.A), "wo_done", 2)
    wf1, wf2 = l0a_w(k, "wf1", 1024), l0a_w(k, "wf2", D, 8)
    with pe.Fori(0, TILES // 2) as i:
        for par in range(2):
            t = 2 * i + par
            pe.wait_ge(*k.at("n2_done", 2 * (t + 1)))
            for m in range(8):
                pe.wait_ge(*k.at("gelu_done", 16 * i + max(8 * par + m - 3, 0)))
                for h in range(NH):
                    mm = pe.matmul(bank(k, 4 + m % 4), wf1[:, h, m * P:(m + 1) * P], yt(k, h, t), start=h == 0, stop=h == 1)
                mm.then_inc(k.sem("ff1"), 1)
        for par in range(2):
            f = (k.B, k.C)[par][:, :].rearrange("p (m n) -> p m n", m=8)
            pe.wait_ge(*k.at("gelu_done", 16 * i + 8 * (par + 1)))
            pe.wait_ge(*k.at("ff_read", 4 * i))
            for m in range(NH):
                for x in range(8):
                    mm = pe.matmul(bank(k, 2 * par + m), wf2[:, x, m * P:(m + 1) * P], f[:, x, :], start=x == 0, stop=x == 7)
                mm.then_inc(k.sem("ff2"), 1)


def l0a_act(k, act):
    a = att_views(k)
    act.wait_ge(*k.at("constants", CONST))
    act.wait_ge(*k.at("eps_set", 1))
    norm_act(k, act, "n0")
    norm_act(k, act, "n1", "b1", lambda h, t: yt(k, h, t))
    with act.Fori(0, TILES // 2) as i:
        for par in range(2):
            t = 2 * i + par
            for o in range(3):
                act.wait_ge(*k.at("qk_ready", 6 * i + 3 * par + o + 1))
                dst = a["k"][:, bass.ds(t * SPT, SPT), :] if o == 2 else tile(seqs(k.B), o, t)
                bias = vcol(k, "bk") if o == 2 else vcol(k, "bq", o)
                act.activation(dst, bank_seq(k, QKB[par][o]), ACT.Identity, bias=bias).then_inc(k.sem("qk_copied"), 1)
    with act.Fori(0, B) as b:

        def outputs(qb):
            act.wait_ge(*k.at("probs_turned", 4 * b + qb + 1))
            act.wait_ge(*k.at("att", 4 * b + max(qb - 1, 0)))
            act.activation(a["pt"][qb % 2], k.PS[:, 5:7, :].rearrange("p b (x k) -> p (b x) k", x=4), ACT.Copy).then_inc(k.sem("probs_copied"), 1)
            act.wait_ge(*k.at("att", 4 * b + qb + 1))
            act.activation(seqs(k.D)[:, :, b, 64 * qb:64 * qb + 64], k.PS[:, 7, 0:P].rearrange("p (j q) -> p j q", j=2), ACT.Copy).then_inc(k.sem("att_out"), 1)

        for qb in range(QB):
            act.wait_ge(*k.at("shifted", 4 * b + qb + 1))
            act.activation(a["sm"][qb % 2], a["sm"][qb % 2], ACT.Exp, scale=0.25).then_inc(k.sem("exp_done"), 1)
            if qb:
                outputs(qb - 1)
        outputs(QB - 1)
    norm_act(k, act, "n2", "b2", lambda h, t: yt(k, h, t))
    with act.Fori(0, TILES // 2) as i:
        for par in range(2):
            f = (k.B, k.C)[par][:, :].rearrange("p (m n) -> p m n", m=8)
            act.wait_ge(*k.at("ff2", 4 * i))
            for m in range(8):
                act.wait_ge(*k.at("ff1", 16 * i + 8 * par + m + 1))
                act.activation(f[:, m, :], bank(k, 4 + m % 4), ACT.Gelu, bias=k.vec[:, BF1 + m:BF1 + m + 1]).then_inc(k.sem("gelu_done"), 1)


def l0a_pool(k, pool):
    a = att_views(k)
    pool.wait_ge(*k.at("n1_var", TILES))
    pool.memset(k.Q[:, :], 0.0).then_inc(k.sem("vz_zero"), 1)
    with pool.Fori(0, B) as b:
        pool.wait_ge(*k.at("rotated", 3 * TILES))
        pool.wait_ge(*k.at("scores", 4 * b))
        pool.tensor_copy(a["qs"].rearrange("p (q j t) -> p j q t", q=QB, j=2),
                         seqs(k.B)[:, :, b, :].rearrange("p j (q t) -> p j q t", q=QB)).then_inc(k.sem("seq_staged"), 1)
        pool.tensor_copy(a["ys"], k.Y[:, :, b, PAD:PAD + T]).then_inc(k.sem("seq_staged"), 1)


def l0a_dve(k, dve):
    a = att_views(k)
    cos = k.rope[:, 0:T].unsqueeze(1).to_broadcast([P, SPT, T])
    sin = k.rope[:, T:2 * T].unsqueeze(1).to_broadcast([P, SPT, T])
    norm_dve(k, dve, "n0", k.H, dst=lambda h, t: tile(seqs(k.A), h, t))
    norm_dve(k, dve, "n1", seqs(k.A), gain="g1")
    tmp = k.E[:, 0:1024].rearrange("p (m s t) -> p m s t", m=2, s=SPT)
    with dve.Fori(0, TILES // 2) as i:
        for m in range(6):
            t = 2 * i + m // 3
            x = a["k"][:, bass.ds(t * SPT, SPT), :] if m % 3 == 2 else tile(seqs(k.B), m % 3, t)
            dve.wait_ge(*k.at("swapped", 6 * i + m + 1))
            dve.tensor_tensor(tmp[:, m % 2], bank_seq(k, 2 + m % 2), sin, ALU.mult).then_inc(k.sem("swap_used"), 1)
            dve.tensor_tensor(x, x, cos, ALU.mult).then_inc(k.sem("cos_done"), 1)
            dve.wait_ge(*k.at("swap_used", 6 * i + m + 1))
            dve.wait_ge(*k.at("cos_done", 6 * i + m + 1))
            dve.tensor_tensor(x, x, tmp[:, m % 2], ALU.add).then_inc(k.sem("rotated"), 1)
    bv = k.small[:, 448:512].rearrange("p (g d) -> p g d", g=4).unsqueeze(1).to_broadcast([P, 4, 4, 16])
    dve.wait_ge(*k.at("l0a_weights", 32))
    dve.wait_ge(*k.at("vz_zero", 1))
    with dve.Fori(0, B) as b:

        def soften(qb):
            sm = a["sm"][qb % 2]
            mx = a["mx"][:, 8 * (qb % 2):8 * (qb % 2) + 8]
            mask = k.band[:, min(qb, 1), :].unsqueeze(1).to_broadcast([P, 8, P])
            dve.wait_ge(*k.at("scores", 4 * b + qb + 1))
            dve.wait_ge(*k.at("probs_turned", 4 * b + max(qb - 1, 0)))
            src = k.PS[:, 1 + 2 * (qb % 2):3 + 2 * (qb % 2), :].rearrange("p b (g k) -> p (b g) k", g=4)
            dve.tensor_tensor(sm, src, mask, ALU.add).then_inc(k.sem("masked"), 1)
            dve.wait_ge(*k.at("masked", 4 * b + qb + 1))
            dve.tensor_reduce(mx, sm, AX.X, ALU.max).then_inc(k.sem("row_max"), 1)
            dve.wait_ge(*k.at("row_max", 4 * b + qb + 1))
            dve.tensor_tensor(sm, sm, mx.unsqueeze(2).to_broadcast([P, 8, P]), ALU.subtract).then_inc(k.sem("shifted"), 1)

        def normalise(qb):
            sm = a["sm"][qb % 2]
            s = a["sum"][:, 8 * (qb % 2):8 * (qb % 2) + 8]
            dve.wait_ge(*k.at("exp_done", 4 * b + qb + 1))
            dve.tensor_reduce(s, sm, AX.X, ALU.add).then_inc(k.sem("row_sum"), 1)
            dve.wait_ge(*k.at("row_sum", 4 * b + qb + 1))
            dve.reciprocal(s, s).then_inc(k.sem("row_inv"), 1)
            dve.wait_ge(*k.at("row_inv", 4 * b + qb + 1))
            dve.tensor_tensor(sm, sm, s.unsqueeze(2).to_broadcast([P, 8, P]), ALU.mult).then_inc(k.sem("probs"), 1)

        dve.wait_ge(*k.at("scores", 4 * b))
        dve.tensor_tensor(a["kz"], a["k"][:, b, :].unsqueeze(1).to_broadcast([P, 4, T]),
                          k.groupmask.unsqueeze(2).to_broadcast([P, 4, T]), ALU.mult).then_inc(k.sem("keys_spread"), 1)
        dve.wait_ge(*k.at("values", b + 1))
        dve.wait_ge(*k.at("att", 4 * b))
        for j2 in range(2):
            base = k.Q[:, 4 * j2 * 144:4 * j2 * 144 + 16]
            dst = bass.AP(tensor=base.tensor, offset=base.offset, ap=[base.ap[0], [1024, 4], [144, 4], [1, 16]])
            src = k.PS[:, 0, 0:256].rearrange("p (w g d) -> p w g d", w=4, g=4)
            dve.tensor_tensor(dst, src, bv, ALU.add).then_inc(k.sem("values_spread"), 1)
        soften(0)
        soften(1)
        for qb in range(QB):
            normalise(qb)
            if qb + 2 < QB:
                soften(qb + 2)
    with dve.Fori(0, TILES // 2) as i:
        for par in range(2):
            t = 2 * i + par
            for m in range(NH):
                dve.wait_ge(*k.at("wo_ready", 2 * t + m + 1))
                x = tile(seqs(k.A), m, t)
                dve.scalar_tensor_tensor(x, bank_seq(k, 4 + 2 * par + m), vcol(k, "bo", m), x, ALU.add, ALU.add).then_inc(k.sem("wo_done"), 1)
    norm_dve(k, dve, "n2", seqs(k.A), gain="g2")
    with dve.Fori(0, TILES // 2) as i:
        for par in range(2):
            t = 2 * i + par
            for m in range(NH):
                dve.wait_ge(*k.at("ff2", 2 * t + m + 1))
                x = tile(seqs(k.A), m, t)
                dve.scalar_tensor_tensor(x, bank_seq(k, 2 * par + m), vcol(k, "bf2", m), x, ALU.add, ALU.add).then_inc(k.sem("ff_read"), 1)
                dve.wait_ge(*k.at("ff_read", 2 * t + m + 1))
                dve.tensor_tensor(tile(k.H, m, t), tile(k.H, m, t), x, ALU.add).then_inc(k.sem("l0a_done"), 1)



def logits_pe(k, pe, n, ready, w, E, b):
    for g in range(N // P):
        if g % 4 == 0:
            pe.wait_ge(*k.at(ready, 2 * (g // 4 + 1)))
        for h in range(NH):
            mm = pe.matmul(k.PS[:, b, E * g:E * g + E], k.Y[:, h, g // 2, PAD + g % 2 * P:PAD + g % 2 * P + P], w[:, h, :],
                           start=h == 0, stop=h == 1)
    mm.then_inc(k.sem(n + "_logits"), 1)


def route_dve(k, dve, n, E, b, norm_eps, bias, lo):
    G = N // P
    buf = [k.A[:, lo + 256 * j:lo + 256 * j + G * E].rearrange("p (g e) -> p g e", g=G) for j in range(4)]
    col = [k.A[:, lo + 1024 + 16 * j:lo + 1040 + 16 * j] for j in range(4)]
    wide = lambda c: c.unsqueeze(2).to_broadcast([P, G, E])
    rev = k.attc[:, 4 * P + 12:4 * P + 12 + E].unsqueeze(1).to_broadcast([P, G, E])
    x, y, one, w = buf
    c, m1, m2, s = col
    done = [0]

    def chain(ins):
        done[0] += 1
        ins.then_inc(k.sem(n + "_route"), 1)
        dve.wait_ge(*k.at(n + "_route", done[0]))

    logits = k.PS[:, b, 0:G * E].rearrange("p (g e) -> p g e", g=G)
    dve.wait_ge(*k.at(n + "_logits", 1))
    if bias is not None:
        chain(dve.tensor_tensor(x, logits, bias.unsqueeze(1).to_broadcast([P, G, E]), ALU.add))
    else:
        chain(dve.tensor_copy(x, logits))
    chain(dve.tensor_reduce(c, x, AX.X, ALU.max))
    chain(dve.tensor_tensor(x, x, wide(c), ALU.subtract))
    dve.sem_inc(k.sem(n + "_exp_in"), 1)
    dve.wait_ge(*k.at(n + "_exp", 1))
    chain(dve.tensor_reduce(s, x, AX.X, ALU.add))
    chain(dve.reciprocal(s, s))
    chain(dve.tensor_tensor(x, x, wide(s), ALU.mult))
    for step, m in ((0, m1), (1, m2)):
        pick = one if step == 0 else y
        chain(dve.tensor_reduce(m, x, AX.X, ALU.max))
        chain(dve.tensor_tensor(pick, x, wide(m), ALU.is_equal))
        chain(dve.tensor_tensor(pick, pick, rev, ALU.mult))
        chain(dve.tensor_reduce(c, pick, AX.X, ALU.max))
        chain(dve.tensor_tensor(pick, pick, wide(c), ALU.is_equal))
        if step == 0:
            chain(dve.scalar_tensor_tensor(x, pick, -2.0, x, ALU.mult, ALU.add))
    chain(dve.tensor_tensor(s, m1, m2, ALU.add))
    if norm_eps:
        chain(dve.tensor_scalar(s, s, norm_eps, None, ALU.add))
    chain(dve.reciprocal(s, s))
    chain(dve.tensor_tensor(m1, m1, s, ALU.mult))
    chain(dve.tensor_tensor(m2, m2, s, ALU.mult))
    chain(dve.tensor_tensor(one, one, wide(m1), ALU.mult))
    chain(dve.tensor_tensor(y, y, wide(m2), ALU.mult))
    dve.tensor_tensor(w, one, y, ALU.add).then_inc(k.sem(n + "_combine"), 1)


def route_act(k, act, n, E, lo):
    x = k.A[:, lo:lo + N // P * E]
    act.wait_ge(*k.at(n + "_exp_in", 1))
    act.activation(x, x, ACT.Exp).then_inc(k.sem(n + "_exp"), 1)
    for q in range(4):
        act.wait_ge(*k.at(n + "_cw_turned", q + 1))
        act.activation(k.A[0:E, 2048 + q * TN:2048 + (q + 1) * TN], k.PS[0:E, 4 + q, :], ACT.Copy).then_inc(k.sem(n + "_cw"), 1)


def combine_pe(k, pe, n, E, lo):
    pe.wait_ge(*k.at(n + "_combine", 1))
    w = k.A[:, lo + 768:lo + 768 + N // P * E]
    for g in range(N // P):
        mm = pe.transpose(k.PS[0:E, 4 + g // 4, (g % 4) * P:(g % 4 + 1) * P], w[:, E * g:E * g + E], k.ident[:, :])
        if g % 4 == 3:
            mm.then_inc(k.sem(n + "_cw_turned"), 1)


def spread_weight(k, pe, b, E, e, t):
    return pe.matmul(bank(k, b), k.ident[0:E, e:e + 1].to_broadcast([E, P]), k.A[0:E, bass.ds(t * TN + 2048, TN)], start=True, stop=True)



E0 = 16
W0 = {"up": 0, "down": 3840, "conv": 7680, "sup": 8448, "sdown": 8704, "router": 8960}


def l0f_inputs(ins, a):
    gate, up, down = a["L0_ffn_expert_gate_w"], a["L0_ffn_expert_up_w"], a["L0_ffn_expert_down_w"]
    ins["l0f_gate"] = np.concatenate([halves(gate[e]) for e in range(E0 - 1)], axis=1)
    conv = a["L0_ffn_conv_w"].transpose(2, 1, 0)
    ins["l0f_w"] = np.concatenate([halves(up[e]) for e in range(E0 - 1)] + [down[e] for e in range(E0 - 1)]
                                  + [halves(conv[j]) for j in range(3)]
                                  + [halves(a["L0_ffn_shared_up_w"]), a["L0_ffn_shared_down_w"], halves(a["L0_ffn_router_w"])], axis=1)
    ins["router_bias"] = a["L0_ffn_router_bias"].reshape(1, E0)


def l0f_load(k, sp):
    sp.wait_ge(*k.at("emb_proj", 8))
    sp.dma_start(k.W[:, 0:8992], k.ins["l0f_w"]).then_inc(k.sem("l0f_weights"), 16)
    sp.dma_start(k.small[:, 544:560], k.ins["router_bias"].to_broadcast([P, E0])).then_inc(k.sem("l0f_weights"), 16)
    sp.wait_ge(*k.at("att", 4 * B))
    sp.dma_start(k.E[:, 0:3840], k.ins["l0f_gate"]).then_inc(k.sem("l0f_weights"), 16)


def l0f_pe(k, pe):
    wt = lambda name, i, n: blocks(k.W[:, W0[name] + i * n:W0[name] + (i + 1) * n], n // P if name != "router" else 2)
    norm_pe(k, pe, "n3", k.H, "l0a_done", 2, free=(("ff_read", 2 * TILES),))
    pe.wait_ge(*k.at("l0f_weights", 48))
    logits_pe(k, pe, "l0f", "n3_scaled", blocks(k.W[:, 8960:8992], 2), E0, 1)
    combine_pe(k, pe, "l0f", E0, 0)
    l1_prep_pe(k, pe)
    pe.wait_ge(*k.at("folded_copied", 2))
    pe.wait_ge(*k.at("eigen", 1))
    pe.wait_ge(*k.at("l0f_cw", 4))
    with pe.Fori(0, TILES) as t:

        def first(x):
            p = 3 * (x % 2)
            pe.wait_ge(*k.at("moe_h", E0 * t + max(x - 1, 0)))
            if x < E0 - 1:
                g, u = blocks(k.E[:, 256 * x:256 * x + 256], 2), wt("up", x, 256)
                for h in range(NH):
                    pe.matmul(bank(k, p), g[:, h, :], yt(k, h, t), start=h == 0, stop=h == 1)
            else:
                u = wt("sup", 0, 256)
                for j in range(3):
                    cv = wt("conv", j, 256)
                    for h in range(NH):
                        pe.matmul(bank(k, p), cv[:, h, :], yt(k, h, t, 2 - j), start=j + h == 0, stop=j + h == 3)
            for h in range(NH):
                pe.matmul(bank(k, p + 1), u[:, h, :], yt(k, h, t), start=h == 0, stop=h == 1)
            spread_weight(k, pe, p + 2, E0, x, t).then_inc(k.sem("moe_in"), 1)

        def second(x):
            w = k.W[:, W0["down"] + 256 * x:W0["down"] + 256 * x + 256] if x < E0 - 1 else k.W[:, W0["sdown"]:W0["sdown"] + 256]
            if x == 0:
                pe.wait_ge(*k.at("moe_out", 2 * t))
            pe.wait_ge(*k.at("moe_h", E0 * t + x + 1))
            for m in range(NH):
                mm = pe.matmul(bank(k, 6 + m), w[:, m * P:(m + 1) * P], k.B[:, 1024 + TN * (x % 2):1024 + TN * (x % 2 + 1)],
                               start=x == 0, stop=x == E0 - 1)
            mm.then_inc(k.sem("moe_down"), 1)

        for x in range(E0):
            first(x)
            if x:
                second(x - 1)
        second(E0 - 1)


def l0f_act(k, act):
    norm_act(k, act, "n3")
    route_act(k, act, "l0f", E0, 0)
    l1_prep_act(k, act)
    with act.Fori(0, TILES) as t:
        for x in range(E0):
            act.wait_ge(*k.at("moe_in", E0 * t + x + 1))
            act.wait_ge(*k.at("moe_h", E0 * t + max(x - 1, 0)))
            act.activation(k.B[:, TN * (x % 2):TN * (x % 2 + 1)], bank(k, 3 * (x % 2)), ACT.Silu).then_inc(k.sem("moe_silu"), 1)


def l0f_dve(k, dve):
    norm_dve(k, dve, "n3", k.H, dst=lambda h, t: yt(k, h, t))
    route_dve(k, dve, "l0f", E0, 1, 1e-6, k.small[:, 544:560], 0)
    l1_prep_dve(k, dve)
    own = k.B[:, 2048:3072].rearrange("p (h s t) -> p h s t", h=2, s=SPT)
    with dve.Fori(0, TILES) as t:
        for x in range(E0):
            s, hid = k.B[:, TN * (x % 2):TN * (x % 2 + 1)], k.B[:, 1024 + TN * (x % 2):1024 + TN * (x % 2 + 1)]
            p = 3 * (x % 2)
            dve.wait_ge(*k.at("moe_silu", E0 * t + x + 1))
            dve.wait_ge(*k.at("moe_down", E0 * t + max(x - 1, 0)))
            if x < E0 - 1:
                dve.tensor_tensor(s, s, bank(k, p + 1), ALU.mult).then_inc(k.sem("moe_up"), 1)
                dve.wait_ge(*k.at("moe_up", (E0 - 1) * t + x + 1))
                dve.tensor_tensor(hid, s, bank(k, p + 2), ALU.mult).then_inc(k.sem("moe_h"), 1)
            else:
                for h in range(NH):
                    dve.tensor_tensor(own[:, h], yt(k, h, t), bank_seq(k, p + 2), ALU.mult).then_inc(k.sem("moe_own"), 1)
                dve.tensor_tensor(hid, s, bank(k, p + 1), ALU.mult).then_inc(k.sem("moe_h"), 1)
        dve.wait_ge(*k.at("moe_own", 2 * t + 2))
        for m in range(NH):
            dve.tensor_tensor(tile(k.H, m, t), tile(k.H, m, t), own[:, m], ALU.add).then_inc(k.sem("moe_own_in"), 1)
        dve.wait_ge(*k.at("moe_down", E0 * t + E0))
        dve.wait_ge(*k.at("moe_own_in", 2 * t + 2))
        for m in range(NH):
            dve.tensor_tensor(tile(k.H, m, t), tile(k.H, m, t), bank_seq(k, 6 + m), ALU.add).then_inc(k.sem("moe_out"), 1)



V1 = {"B": 0, "F": 512, "G": 1024, "C": 1536, "S": 2048, "a": 2176, "ER": 2304, "EI": 2560, "keep": 2816, "BF": 3328, "CG": 3840}


def l1a_inputs(ins, a):
    n, f = np.arange(D)[:, None].astype(np.float64), np.arange(P)[None, :]
    w = 2 * np.pi / D
    ft = np.concatenate([np.cos(w * n * f), -np.sin(w * n * f)], axis=1)
    ft[:, P] = np.cos(np.pi * n[:, 0])
    g = 2 * ft / D
    g[:, 0] /= 2
    g[:, P] /= 2
    s = -2 * np.sin(w * (np.arange(P)[:, None] + 1) * f)
    s[P - 1] = 0.0
    ft, g, s = (x.astype(np.float32) for x in (ft, g, s))
    ins["l1_w"] = np.concatenate([halves(a["L1_attn_B_w"]), halves(ft), halves(g), halves(a["L1_attn_C_w"].T), s,
                                  a["L1_attn_a_params"].reshape(P, 1)], axis=1)


def l1a_load(k, sp):
    sp.wait_ge(*k.at("ff2", 2 * TILES))
    sp.dma_start(k.V[:, 0:2177], k.ins["l1_w"]).then_inc(k.sem("l1_weights"), 16)


def l1w(k, name):
    return blocks(k.V[:, V1[name]:V1[name] + 512], 2)


def l1_prep_pe(k, pe):
    pe.wait_ge(*k.at("l1_weights", 16))
    pe.matmul(k.PS[:, 0, 0:1], k.V[:, V1["S"]:V1["S"] + P], k.V[:, V1["a"]:V1["a"] + 1], start=True, stop=True).then_inc(k.sem("omega"), 1)
    for b, lhs, rhs in ((2, "B", "F"), (3, "G", "C")):
        for m in range(NH):
            for h in range(NH):
                mm = pe.matmul(k.PS[:, b, m * D:(m + 1) * D], l1w(k, lhs)[:, h, m * P:(m + 1) * P], l1w(k, rhs)[:, h, :], start=h == 0, stop=h == 1)
        mm.then_inc(k.sem("folded"), 1)


def l1_prep_act(k, act):
    for j, name in enumerate(("BF", "CG")):
        act.wait_ge(*k.at("folded", j + 1))
        act.activation(k.V[:, V1[name]:V1[name] + 512], bank(k, 2 + j), ACT.Copy).then_inc(k.sem("folded_copied"), 1)


def l1_prep_dve(k, dve):
    s = k.vec2
    done = [0]

    def chain(ins):
        done[0] += 1
        ins.then_inc(k.sem("eigen_step"), 1)
        dve.wait_ge(*k.at("eigen_step", done[0]))
    w, w2, den, lr, li = (s[:, 14 + j:15 + j] for j in range(5))
    dve.wait_ge(*k.at("omega", 1))
    chain(dve.tensor_copy(w, k.PS[:, 0, 0:1]))
    chain(dve.tensor_tensor(w2, w, w, ALU.mult))
    chain(dve.tensor_scalar(den, w2, 1.0, None, ALU.add))
    chain(dve.reciprocal(den, den))
    chain(dve.tensor_scalar(w2, w2, -1.0, 1.0, ALU.mult, ALU.add))
    chain(dve.tensor_tensor(lr, w2, den, ALU.mult))
    chain(dve.tensor_scalar(w, w, -2.0, None, ALU.mult))
    dve.tensor_tensor(li, w, den, ALU.mult).then_inc(k.sem("eigen"), 1)
    keep = k.V[:, V1["keep"]:V1["keep"] + TN]
    chain(dve.memset(keep, 1.0))
    dve.memset(keep.rearrange("p (s t) -> p s t", s=SPT)[:, :, 0:1], 0.0).then_inc(k.sem("keep_set"), 1)


def l1a_tables_pool(k, pool):
    s = k.vec2
    lr, li, sq, c0 = (s[:, 17 + j:18 + j] for j in range(4))
    done = [0]

    def chain(ins):
        done[0] += 1
        ins.then_inc(k.sem("power_step"), 1)
        pool.wait_ge(*k.at("power_step", done[0]))
    ER, EI = k.V[:, V1["ER"]:V1["ER"] + T], k.V[:, V1["EI"]:V1["EI"] + T]
    tmp = k.D[:, 0:2 * P]
    pool.wait_ge(*k.at("n3_scaled", 2 * TILES))
    pool.wait_ge(*k.at("eigen", 1))
    chain(pool.memset(ER[:, 0:1], 1.0))
    chain(pool.memset(EI[:, 0:1], 0.0))
    n = 1
    while n < T:
        a, b = tmp[:, 0:n], tmp[:, P:P + n]
        chain(pool.tensor_scalar(a, ER[:, 0:n], lr, None, ALU.mult))
        chain(pool.tensor_scalar(b, EI[:, 0:n], li, None, ALU.mult))
        chain(pool.tensor_tensor(ER[:, n:2 * n], a, b, ALU.subtract))
        chain(pool.tensor_scalar(a, ER[:, 0:n], li, None, ALU.mult))
        chain(pool.tensor_scalar(b, EI[:, 0:n], lr, None, ALU.mult))
        chain(pool.tensor_tensor(EI[:, n:2 * n], a, b, ALU.add))
        chain(pool.tensor_tensor(sq, lr, lr, ALU.mult))
        chain(pool.tensor_tensor(c0, li, li, ALU.mult))
        chain(pool.tensor_tensor(li, li, lr, ALU.mult))
        chain(pool.tensor_tensor(li, li, li, ALU.add))
        chain(pool.tensor_tensor(lr, sq, c0, ALU.subtract))
        n *= 2
    pool.sem_inc(k.sem("powers"), 1)


def l1a_pe(k, pe):
    norm_pe(k, pe, "n4", k.H, "moe_out", 2, free=(("moe_h", E0 * TILES),))
    bf, cg = l1w(k, "BF"), l1w(k, "CG")
    with pe.Fori(0, TILES // 2) as i:
        for par in range(2):
            t = 2 * i + par
            pe.wait_ge(*k.at("n4_scaled", 2 * (t + 1)))
            pe.wait_ge(*k.at("turned_in", 8 * i))
            for m in range(NH):
                for h in range(NH):
                    mm = pe.matmul(bank(k, 4 + 2 * par + m), bf[:, h, m * P:(m + 1) * P], yt(k, h, t), start=h == 0, stop=h == 1)
                mm.then_inc(k.sem("fourier_in"), 1)
    with pe.Fori(0, TILES // 2) as i:
        for par in range(2):
            t = 2 * i + par
            pe.wait_ge(*k.at("z_ready", 2 * (t + 1)))
            pe.wait_ge(*k.at("ssm_read", 4 * i))
            for m in range(NH):
                for h in range(NH):
                    mm = pe.matmul(bank(k, 2 * par + m), cg[:, h, m * P:(m + 1) * P], tile(seqs(k.C), h, t), start=h == 0, stop=h == 1)
                mm.then_inc(k.sem("ssm_out"), 1)


def l1a_act(k, act):
    norm_act(k, act, "n4")


def powers(k, name):
    return k.V[:, V1[name]:V1[name] + T].unsqueeze(1).to_broadcast([P, SPT, T])


def l1a_pool(k, pool):
    l1a_tables_pool(k, pool)
    A, Bv, C, Dv = seqs(k.A), seqs(k.B), seqs(k.C), seqs(k.D)
    pool.wait_ge(*k.at("ff2", 2 * TILES))
    with pool.Fori(0, TILES) as t:
        pool.wait_ge(*k.at("turned_in", 4 * t + 2))
        pool.tensor_tensor(tile(C, 0, t), tile(A, 0, t), tile(A, 1, t), ALU.add).then_inc(k.sem("sum_in"), 1)
        pool.wait_ge(*k.at("turned_in", 4 * t + 4))
        pool.tensor_tensor(tile(C, 1, t), tile(Bv, 0, t), tile(Bv, 1, t), ALU.subtract).then_inc(k.sem("sum_in"), 1)
    with pool.Fori(0, TILES) as t:
        pool.wait_ge(*k.at("turned_out", 4 * t + 2))
        pool.tensor_tensor(tile(C, 0, t), tile(A, 0, t), tile(A, 1, t), ALU.subtract).then_inc(k.sem("z_ready"), 1)
        pool.wait_ge(*k.at("turned_out", 4 * t + 4))
        pool.tensor_tensor(tile(C, 1, t), tile(Bv, 0, t), tile(Bv, 1, t), ALU.add).then_inc(k.sem("z_ready"), 1)


def flat(buf, h, t):
    return buf[:, bass.ds(t * TN + h * N, TN)]


def l1a_dve(k, dve):
    A, Bv, Dv = seqs(k.A), seqs(k.B), seqs(k.D)
    norm_dve(k, dve, "n4", k.H, dst=lambda h, t: yt(k, h, t), free=(("powers", 1),))
    dve.wait_ge(*k.at("powers", 1))
    dve.wait_ge(*k.at("keep_set", 1))
    with dve.Fori(0, TILES // 2) as i:
        for par in range(2):
            t = 2 * i + par
            re, im = bank_seq(k, 4 + 2 * par), bank_seq(k, 5 + 2 * par)
            dve.wait_ge(*k.at("fourier_in", 2 * t + 2))
            for dst, src, e in ((tile(A, 0, t), re, "ER"), (tile(A, 1, t), im, "EI"), (tile(Bv, 0, t), im, "ER"), (tile(Bv, 1, t), re, "EI")):
                dve.tensor_tensor(dst, src, powers(k, e), ALU.mult).then_inc(k.sem("turned_in"), 1)
    with dve.Fori(0, TILES) as t:
        for h in range(NH):
            dve.wait_ge(*k.at("sum_in", 2 * t + h + 1))
            dve.tensor_tensor_scan(flat(k.D, h, t), k.V[:, V1["keep"]:V1["keep"] + TN], flat(k.C, h, t), 0.0, ALU.mult, ALU.add).then_inc(k.sem("summed"), 1)
        dve.wait_ge(*k.at("summed", 2 * t + 2))
        for dst, h, e in ((tile(A, 0, t), 0, "ER"), (tile(A, 1, t), 1, "EI"), (tile(Bv, 0, t), 1, "ER"), (tile(Bv, 1, t), 0, "EI")):
            dve.tensor_tensor(dst, tile(Dv, h, t), powers(k, e), ALU.mult).then_inc(k.sem("turned_out"), 1)
    with dve.Fori(0, TILES // 2) as i:
        for par in range(2):
            t = 2 * i + par
            dve.wait_ge(*k.at("z_ready", 2 * t + 2))
            for m in range(NH):
                dve.wait_ge(*k.at("ssm_out", 2 * t + m + 1))
                dve.scalar_tensor_tensor(tile(A, m, t), yt(k, m, t), vcol(k, "D", m), bank_seq(k, 2 * par + m), ALU.mult, ALU.add).then_inc(k.sem("ssm_read"), 1)
                dve.wait_ge(*k.at("ssm_read", 2 * t + m + 1))
                dve.tensor_tensor(tile(k.H, m, t), tile(k.H, m, t), tile(A, m, t), ALU.add).then_inc(k.sem("l1a_done"), 1)



def l1f_inputs(ins, a):
    ins["l1f_w"] = np.concatenate([halves(a["L1_ffn_W_" + n].T) for n in "rkv"], axis=1)


def l1f_load(k, sp):
    sp.wait_ge(*k.at("moe_down", E0 * TILES))
    sp.dma_start(k.W[:, 0:1536], k.ins["l1f_w"]).then_inc(k.sem("l1f_weights"), 16)


def l1f_pe(k, pe):
    wr, wk, wv = (blocks(k.W[:, 512 * j:512 * j + 512], 2) for j in range(3))
    norm_pe(k, pe, "n5", k.H, "l1a_done", 2, free=(("ssm_read", 2 * TILES),))
    pe.wait_ge(*k.at("l1f_weights", 16))
    pe.wait_ge(*k.at("n5_std", TILES))
    with pe.Fori(0, TILES // 2) as i:
        for par in range(2):
            t = 2 * i + par
            pe.wait_ge(*k.at("rk_read", 8 * i))
            pe.wait_ge(*k.at("mixed", 4 * t + 4))
            for o, (w, x) in enumerate(((wr, k.B), (wk, k.C))):
                for m in range(NH):
                    for h in range(NH):
                        mm = pe.matmul(bank(k, 4 * par + 2 * o + m), w[:, h, m * P:(m + 1) * P], tile(seqs(x), h, t), start=h == 0, stop=h == 1)
                    mm.then_inc(k.sem("rk_ready"), 1)
    with pe.Fori(0, TILES // 2) as i:
        for par in range(2):
            t = 2 * i + par
            pe.wait_ge(*k.at("k_squared", 2 * t + 2))
            pe.wait_ge(*k.at("rk_read", 4 * TILES))
            pe.wait_ge(*k.at("v_read", 4 * i))
            for m in range(NH):
                for h in range(NH):
                    mm = pe.matmul(bank(k, 4 * par + m), wv[:, h, m * P:(m + 1) * P], tile(seqs(k.D), h, t), start=h == 0, stop=h == 1)
                mm.then_inc(k.sem("v_ready"), 1)


def l1f_act(k, act):
    norm_act(k, act, "n5")
    act.wait_ge(*k.at("rest_ready", 7))
    with act.Fori(0, TILES) as t:
        act.wait_ge(*k.at("n5_scaled", 2 * t + 2))
        for o, x in enumerate((k.B, k.C)):
            for h in range(NH):
                act.activation(tile(seqs(x), h, t), yt(k, h, t, 1), ACT.Copy, scale=k.vec2[:, 2 * o + h:2 * o + h + 1]).then_inc(k.sem("before"), 1)
    with act.Fori(0, TILES // 2) as i:
        for par in range(2):
            t = 2 * i + par
            for m in range(NH):
                act.wait_ge(*k.at("rk_ready", 4 * t + m + 1))
                act.activation(tile(seqs(k.A), m, t), bank_seq(k, 4 * par + m), ACT.Sigmoid).then_inc(k.sem("rk_read"), 1)
            for m in range(NH):
                act.wait_ge(*k.at("rk_ready", 4 * t + 2 + m + 1))
                act.activation(tile(seqs(k.D), m, t), bank_seq(k, 4 * par + 2 + m), ACT.Relu).then_inc(k.sem("rk_read"), 1)


def l1f_pool(k, pool):
    with pool.Fori(0, TILES) as t:
        for h in range(NH):
            pool.wait_ge(*k.at("rk_read", 4 * t + 2 + h + 1))
            pool.tensor_tensor(tile(seqs(k.D), h, t), tile(seqs(k.D), h, t), tile(seqs(k.D), h, t), ALU.mult).then_inc(k.sem("k_squared"), 1)


def l1f_dve(k, dve):
    norm_dve(k, dve, "n5", k.H, dst=lambda h, t: yt(k, h, t))
    with dve.Fori(0, TILES) as t:
        for o, (x, mu) in enumerate(((k.B, "mu_r"), (k.C, "mu_k"))):
            for h in range(NH):
                dve.wait_ge(*k.at("before", 4 * t + 2 * o + h + 1))
                v = tile(seqs(x), h, t)
                dve.scalar_tensor_tensor(v, yt(k, h, t), vcol(k, mu, h), v, ALU.mult, ALU.add).then_inc(k.sem("mixed"), 1)
    with dve.Fori(0, TILES // 2) as i:
        for par in range(2):
            t = 2 * i + par
            for m in range(NH):
                a = tile(seqs(k.A), m, t)
                dve.wait_ge(*k.at("v_ready", 2 * t + m + 1))
                dve.tensor_tensor(a, a, bank_seq(k, 4 * par + m), ALU.mult).then_inc(k.sem("v_read"), 1)
                dve.wait_ge(*k.at("v_read", 2 * t + m + 1))
                dve.tensor_tensor(tile(k.H, m, t), tile(k.H, m, t), a, ALU.add).then_inc(k.sem("l1f_done"), 1)



CH = 128
W2 = {"q": 1536, "k": 2048, "g": 2560, "out": 3072, "v": 3584, "gk1": 4096, "gk2": 4352}
FAR = 16 * 85.0


def l2a_inputs(ins, a):
    w = {n: a["L2_attn_" + n] for n in ("Wq", "Wk", "Wg", "Wout", "Wv", "Wgk1")}
    w["Wgk1"] = np.pad(w["Wgk1"], ((0, 0), (0, P - 16)))
    ins["l2a_w"] = np.concatenate([halves(w[n]) for n in ("Wq", "Wk", "Wg", "Wout", "Wv", "Wgk1")], axis=1)
    ins["gk2"] = np.pad(a["L2_attn_Wgk2"], ((0, P - 16), (0, 0)))


def l2a_load(k, sp):
    sp.dma_start(k.W[:, 1536:4352], k.ins["l2a_w"]).then_inc(k.sem("l2a_weights"), 16)
    sp.dma_start(k.W[:, 4352:4608], k.ins["gk2"]).then_inc(k.sem("l2a_weights"), 16)


def l2w(k, name):
    return blocks(k.W[:, W2[name]:W2[name] + 512], 2)


def gla_views(k):
    v = {"keep": k.V[:, 0:512], "gsum": k.V[:, 4096:4098]}
    for name, a in (("dm", 512), ("eo", 1024), ("vi", 1536)):
        v[name] = k.V[:, a:a + 512].rearrange("p (h c t) -> p h c t", h=2, c=2)
    v["ve"] = k.V[:, 2048:2304].rearrange("p (h t) -> p h t", h=2)
    v["ks"] = k.V[:, 2560:3072].rearrange("p (h t) -> p h t", h=2)
    v["turned"] = k.V[:, 3072:3584]
    v["veT"] = k.V[:, 3072:3328].rearrange("p (h m) -> p h m", h=2)
    v["kT"] = k.V[:, 3328:3584].rearrange("p (h m) -> p h m", h=2)
    v["st"] = k.V[:, 3584:3840].rearrange("p (h m) -> p h m", h=2)
    v["qz"] = [k.A[:, 1024 * j:1024 * j + 1024].rearrange("p (a t) -> p a t", a=8) for j in range(2)]
    v["am"] = [k.A[:, 2048 + 1024 * j:3072 + 1024 * j].rearrange("p (a t) -> p a t", a=8) for j in range(2)]
    v["vz"] = k.Q[:, :].rearrange("p (u a m) -> p u a m", u=4, a=8)
    return v


def l2a_pe(k, pe):
    v = gla_views(k)
    norm_pe(k, pe, "n6", k.H, "l1f_done", 2, free=(("v_read", 2 * TILES),))
    pe.wait_ge(*k.at("l2a_weights", 32))
    pe.wait_ge(*k.at("n6_std", TILES))
    with pe.Fori(0, TILES // 2) as i:
        for par in range(2):
            t = 2 * i + par
            pe.wait_ge(*k.at("n6_scaled", 2 * t + 2))
            for n in range(7):
                pe.wait_ge(*k.at("qkv_read", 14 * i + (par and n + 1)))
                w = l2w(k, "qkv"[n // 2])[:, :, (n % 2) * P:(n % 2 + 1) * P] if n < 6 else blocks(k.W[:, W2["gk1"]:W2["gk1"] + 256], 2)
                for h in range(NH):
                    mm = pe.matmul(bank(k, n), w[:, h, :], yt(k, h, t), start=h == 0, stop=h == 1)
                mm.then_inc(k.sem("qkv_ready"), 1)
    pe.wait_ge(*k.at("qkv_read", 7 * TILES))
    with pe.Fori(0, TILES // 2) as i:
        for par in range(2):
            pe.wait_ge(*k.at("gate_read", 4 * i))
            for m in range(NH):
                pe.matmul(bank(k, 2 * par + m), k.W[:, W2["gk2"] + m * P:W2["gk2"] + (m + 1) * P], k.Q[:, bass.ds((2 * i + par) * TN, TN)],
                          start=True, stop=True).then_inc(k.sem("gate_ready"), 1)
    pe.wait_ge(*k.at("gate_read", 2 * TILES))
    with pe.Fori(0, B) as b:

        def scores(u):
            c, h = u // 2, u % 2
            pe.wait_ge(*k.at("q_spread", 4 * b + u + 1))
            pe.wait_ge(*k.at("gla_masked", 4 * b + max(u - 1, 0)))
            for x in range(2):
                mm = pe.matmul(bank(k, 2 + 2 * (u % 2) + x), v["ks"][:, h, CH * c:CH * c + CH], v["qz"][u % 2][:, 4 * x:4 * x + 4, :], start=True, stop=True)
            mm.then_inc(k.sem("gla_scores"), 1)

        def outputs(u):
            c, h = u // 2, u % 2
            pe.wait_ge(*k.at("gla_masked", 4 * b + u + 1))
            pe.wait_ge(*k.at("gla_out", 4 * b + max(u - 1, 0)))
            for x in range(8):
                mm = pe.matmul(k.PS[:, 6 + u % 2, 0:P], v["vz"][:, u, x, :], v["am"][u % 2][:, x, :], start=x == 0, stop=x == 7 and c == 0)
            if c:
                if u == 2:
                    pe.wait_ge(*k.at("state", b + 1))
                mm = pe.matmul(k.PS[:, 6 + u % 2, 0:P], v["st"][:, h, :], seqs(k.B)[:, h, b, CH:2 * CH], start=False, stop=True)
            mm.then_inc(k.sem("gla_att"), 1)

        pe.wait_ge(*k.at("keys_staged", b + 1))
        scores(0)
        scores(1)
        pe.wait_ge(*k.at("decayed", 2 * b + 2))
        pe.wait_ge(*k.at("v_spread", b))
        pe.wait_ge(*k.at("state", b))
        for u in range(4):
            mm = pe.transpose(k.PS[:, 0, P * u:P * u + P], v["vi"][:, u % 2, u // 2, :], k.ident[:, :])
        mm.then_inc(k.sem("v_turned"), 1)
        for h in range(NH):
            pe.transpose(k.PS[:, 1, P * h:P * h + P], v["ve"][:, h, :], k.ident[:, :])
            mm = pe.transpose(k.PS[:, 1, D + P * h:D + P * h + P], v["ks"][:, h, 0:CH], k.ident[:, :])
        mm.then_inc(k.sem("kv_turned"), 1)
        pe.wait_ge(*k.at("v_spread", b + 1))
        outputs(0)
        scores(2)
        pe.wait_ge(*k.at("kv_copied", b + 1))
        for h in range(NH):
            mm = pe.matmul(k.PS[:, 1, P * h:P * h + P], v["kT"][:, h, :], v["veT"][:, h, :], start=True, stop=True)
        mm.then_inc(k.sem("state_sum"), 1)
        outputs(1)
        scores(3)
        outputs(2)
        outputs(3)
    norm_pe(k, pe, "n7", seqs(k.E), "gla_out", 8, free=(("gla_out", 4 * B),))
    pe.wait_ge(*k.at("n7_std", TILES))
    with pe.Fori(0, TILES // 2) as i:
        for par in range(2):
            pe.wait_ge(*k.at("g_read", 4 * i))
            for m in range(NH):
                for h in range(NH):
                    mm = pe.matmul(bank(k, 2 * par + m), l2w(k, "g")[:, h, m * P:(m + 1) * P], yt(k, h, 2 * i + par), start=h == 0, stop=h == 1)
                mm.then_inc(k.sem("g_ready"), 1)
    with pe.Fori(0, TILES // 2) as i:
        for par in range(2):
            t = 2 * i + par
            pe.wait_ge(*k.at("gated", 2 * t + 2))
            pe.wait_ge(*k.at("l2a_read", 4 * i))
            for m in range(NH):
                for h in range(NH):
                    mm = pe.matmul(bank(k, 4 + 2 * par + m), l2w(k, "out")[:, h, m * P:(m + 1) * P], tile(seqs(k.A), h, t), start=h == 0, stop=h == 1)
                mm.then_inc(k.sem("l2a_ready"), 1)


def l2a_act(k, act):
    v = gla_views(k)
    norm_act(k, act, "n6")
    with act.Fori(0, TILES // 2) as i:
        for par in range(2):
            t = 2 * i + par
            for n in range(7):
                dst = tile(seqs((k.B, k.C, k.E)[n // 2]), n % 2, t) if n < 6 else tile(seqs(k.Q), 0, t)
                act.wait_ge(*k.at("qkv_ready", 7 * t + n + 1))
                act.activation(dst, bank_seq(k, n), ACT.Copy).then_inc(k.sem("qkv_read"), 1)
    with act.Fori(0, TILES // 2) as i:
        for par in range(2):
            t = 2 * i + par
            for m in range(NH):
                act.wait_ge(*k.at("gate_ready", 2 * t + m + 1))
                act.activation(tile(seqs(k.A), m, t), bank_seq(k, 2 * par + m), ACT.Identity, bias=vcol(k, "bgk2", m)).then_inc(k.sem("gate_read"), 1)
    for n, (f, src, dst) in enumerate(((ACT.Abs, k.A, k.Q), (ACT.Exp, k.Q, k.Q), (ACT.Ln, k.Q, k.Q))):
        with act.Fori(0, TILES) as t:
            for m in range(NH):
                act.wait_ge(*k.at("gate_read" if n == 0 else f"softplus{n}", 2 * t + m + 1))
                act.activation(tile(seqs(dst), m, t), tile(seqs(src), m, t), f, bias=1.0 if n == 2 else 0.0, scale=-1.0 if n == 1 else 1.0).then_inc(k.sem(f"softplus{n + 1}"), 1)
    with act.Fori(0, B) as b:
        act.wait_ge(*k.at("clamped", b + 1))
        act.wait_ge(*k.at("gla_out", 4 * b))
        act.activation(v["vi"], v["dm"], ACT.Exp, scale=-1 / 16).then_inc(k.sem("factors"), 1)
        act.wait_ge(*k.at("to_end", b + 1))
        act.activation(v["ve"], v["ve"], ACT.Exp, scale=1 / 16).then_inc(k.sem("factors"), 1)
        act.activation(v["eo"], v["dm"], ACT.Exp, scale=1 / 16).then_inc(k.sem("factors"), 1)
        act.wait_ge(*k.at("kv_turned", b + 1))
        act.wait_ge(*k.at("state_sum", b))
        act.activation(v["turned"], bank(k, 1), ACT.Copy).then_inc(k.sem("kv_copied"), 1)
    norm_act(k, act, "n7", "beta", lambda h, t: tile(seqs(k.A), h, t))
    with act.Fori(0, TILES // 2) as i:
        for par in range(2):
            for m in range(NH):
                act.wait_ge(*k.at("g_ready", 4 * i + 2 * par + m + 1))
                act.activation(tile(seqs(k.B), m, 2 * i + par), bank_seq(k, 2 * par + m), ACT.Silu).then_inc(k.sem("g_read"), 1)


def l2a_pool(k, pool):
    v = gla_views(k)
    pool.wait_ge(*k.at("gate_sums", 2 * TILES))
    pool.memset(k.Q[:, :], 0.0).then_inc(k.sem("vz2_zero"), 1)
    pool.wait_ge(*k.at("qkv_read", 7 * TILES))
    with pool.Fori(0, B) as b:
        pool.wait_ge(*k.at("state_sum", b))
        pool.wait_ge(*k.at("gla_scores", 4 * b))
        pool.tensor_copy(v["ks"], seqs(k.C)[:, :, b, :]).then_inc(k.sem("keys_staged"), 1)
        for u in range(4):
            pool.wait_ge(*k.at("gla_scores", 4 * b + max(u - 1, 0)))
            pool.tensor_tensor(v["qz"][u % 2], seqs(k.B)[:, u % 2, b, CH * (u // 2):CH * (u // 2) + CH].unsqueeze(1).to_broadcast([P, 8, CH]),
                               k.headmask.unsqueeze(2).to_broadcast([P, 8, CH]), ALU.mult).then_inc(k.sem("q_spread"), 1)


def l2a_dve(k, dve):
    v = gla_views(k)
    norm_dve(k, dve, "n6", k.H, dst=lambda h, t: yt(k, h, t))
    dve.wait_ge(*k.at("ssm_out", 2 * TILES))
    dve.memset(v["keep"], 1.0).then_inc(k.sem("keep2"), 1)
    dve.wait_ge(*k.at("keep2", 1))
    dve.memset(v["keep"].rearrange("p (c t) -> p c t", t=CH)[:, :, 0:1], 0.0).then_inc(k.sem("keep2"), 1)
    dve.wait_ge(*k.at("keep2", 2))
    with dve.Fori(0, TILES) as t:
        for m in range(NH):
            dve.wait_ge(*k.at("softplus3", 2 * t + m + 1))
            g = tile(seqs(k.A), m, t)
            dve.scalar_tensor_tensor(g, g, 0.0, tile(seqs(k.Q), m, t), ALU.min, ALU.subtract).then_inc(k.sem("log_gate"), 1)
            dve.wait_ge(*k.at("log_gate", 2 * t + m + 1))
            dve.tensor_tensor_scan(flat(k.D, m, t), v["keep"], flat(k.A, m, t), 0.0, ALU.mult, ALU.add).then_inc(k.sem("gate_sums"), 1)
    dve.wait_ge(*k.at("gate_sums", 2 * TILES))
    dve.wait_ge(*k.at("vz2_zero", 1))
    G = seqs(k.D)
    with dve.Fori(0, B) as b:
        g = G[:, :, b, :].rearrange("p h (c t) -> p h c t", c=2)
        dve.wait_ge(*k.at("factors", 3 * b))
        dve.wait_ge(*k.at("kv_turned", b))
        dve.tensor_tensor(v["dm"], g, g[:, :, :, CH // 2 - 1:CH // 2].to_broadcast([P, 2, 2, CH]), ALU.subtract).then_inc(k.sem("to_mid"), 1)
        dve.tensor_tensor(v["gsum"].unsqueeze(2), g[:, :, 0, CH - 1:CH], g[:, :, 1, CH // 2 - 1:CH // 2], ALU.add).then_inc(k.sem("gate_to_mid"), 1)
        dve.wait_ge(*k.at("to_mid", b + 1))
        dve.tensor_scalar(v["dm"], v["dm"], FAR, -FAR, ALU.min, ALU.max).then_inc(k.sem("clamped"), 1)
        dve.wait_ge(*k.at("gate_to_mid", b + 1))
        dve.tensor_tensor(v["ve"], v["gsum"].unsqueeze(2).to_broadcast([P, 2, CH]), g[:, :, 0, :], ALU.subtract).then_inc(k.sem("to_end"), 1)
        vals = seqs(k.E)[:, :, b, :]
        dve.wait_ge(*k.at("factors", 3 * b + 1))
        dve.tensor_tensor(v["vi"], v["vi"], vals.rearrange("p h (c t) -> p h c t", c=2), ALU.mult).then_inc(k.sem("decayed"), 1)
        dve.wait_ge(*k.at("factors", 3 * b + 2))
        dve.tensor_tensor(v["ve"], v["ve"], vals[:, :, 0:CH], ALU.mult).then_inc(k.sem("decayed"), 1)

        def mask(u):
            dve.wait_ge(*k.at("gla_scores", 4 * b + u + 1))
            dve.wait_ge(*k.at("gla_att", 4 * b + max(u - 1, 0)))
            src = k.PS[:, 2 + 2 * (u % 2):4 + 2 * (u % 2), :].rearrange("p b (a t) -> p (b a) t", a=4)
            dve.tensor_tensor(v["am"][u % 2], src, k.causal.unsqueeze(1).to_broadcast([P, 8, CH]), ALU.mult).then_inc(k.sem("gla_masked"), 1)

        def output(u):
            c, h = u // 2, u % 2
            dve.wait_ge(*k.at("gla_att", 4 * b + u + 1))
            dve.tensor_tensor(seqs(k.E)[:, h, b, CH * c:CH * c + CH], k.PS[:, 6 + u % 2, 0:P], v["eo"][:, h, c, :], ALU.mult).then_inc(k.sem("gla_out"), 1)

        mask(0)
        mask(1)
        dve.wait_ge(*k.at("v_turned", b + 1))
        base = k.Q[:, 0:16]
        dst = bass.AP(tensor=base.tensor, offset=base.offset, ap=[base.ap[0], [1024, 4], [144, 8], [1, 16]])
        dve.tensor_copy(dst, k.PS[:, 0, :].rearrange("p (u a d) -> p u a d", u=4, a=8)).then_inc(k.sem("v_spread"), 1)
        dve.wait_ge(*k.at("factors", 3 * b + 3))
        dve.wait_ge(*k.at("decayed", 2 * b + 2))
        output(0)
        mask(2)
        dve.wait_ge(*k.at("state_sum", b + 1))
        dve.tensor_tensor(v["st"].rearrange("p h (a d) -> p h a d", a=8), k.PS[:, 1, 0:D].rearrange("p (h a d) -> p h a d", h=2, a=8),
                          k.headmask.unsqueeze(1).unsqueeze(3).to_broadcast([P, 2, 8, 16]), ALU.mult).then_inc(k.sem("state"), 1)
        output(1)
        mask(3)
        output(2)
        output(3)
    norm_dve(k, dve, "n7", seqs(k.E), gain="gamma")
    with dve.Fori(0, TILES) as t:
        for m in range(NH):
            dve.wait_ge(*k.at("g_read", 2 * t + m + 1))
            dve.wait_ge(*k.at("n7_done", 2 * t + m + 1))
            x = tile(seqs(k.A), m, t)
            dve.tensor_tensor(x, x, tile(seqs(k.B), m, t), ALU.mult).then_inc(k.sem("gated"), 1)
    with dve.Fori(0, TILES // 2) as i:
        for par in range(2):
            t = 2 * i + par
            for m in range(NH):
                dve.wait_ge(*k.at("l2a_ready", 2 * t + m + 1))
                dve.tensor_tensor(tile(k.H, m, t), tile(k.H, m, t), bank_seq(k, 4 + 2 * par + m), ALU.add).then_inc(k.sem("l2a_read"), 1)



W6 = {"b1": 6656, "b2": 7680}
GPT = TN // P


def l2f_inputs(ins, a):
    ins["l2f_w"] = np.concatenate([halves(a["L2_ffn_W1"].T), halves(a["L2_ffn_W2"].T)], axis=1)
    ins["l2f_b"] = np.concatenate([a["L2_ffn_b1"], a["L2_ffn_b2"]]).reshape(1, 1280)


def l2f_load(k, sp):
    sp.dma_start(k.W[:, 6656:7936], k.ins["l2f_b"].to_broadcast([P, 1280])).then_inc(k.sem("l2f_bias"), 16)
    sp.wait_ge(*k.at("state_sum", B))
    sp.dma_start(k.C[:, :], k.ins["l2f_w"]).then_inc(k.sem("l2f_weights"), 16)


def ffq_views(k):
    v = {"w1": k.W[:, 4608:5632].bitcast(BF16).rearrange("p (k m) -> p k m", k=2),
         "w2": k.W[:, 5632:6656].bitcast(BF16).rearrange("p (k m) -> p k m", k=8),
         "b1": k.W[:, 6656:7680], "b2": k.W[:, 7680:7936], "wsum": k.vec2[:, 22:24], "wscale": k.vec2[:, 20:22], "winv": k.vec2[:, 14:16],
         "xs": k.A[:, 0:1024].rearrange("p (h t) -> p h t", h=2),
         "out": k.B[:, 3072:3328], "hq": k.B[:, 2048:2560].bitcast(BF16), "ht": k.B[:, 2560:3072].bitcast(BF16).rearrange("p (k t) -> p k t", k=8)}
    for j in range(2):
        v["x", j] = k.A[:, 1024 + 256 * j:1280 + 256 * j]
        v["xq", j] = k.A[:, 1536 + 128 * j:1664 + 128 * j].bitcast(BF16)
        v["xt", j] = k.A[:, 1792 + 128 * j:1920 + 128 * j].bitcast(BF16).rearrange("p (k t) -> p k t", k=2)
        v["h", j] = k.B[:, 1024 * j:1024 * j + 1024]
        v["sx", j] = k.small[:, 560 + 4 * j:564 + 4 * j]
        v["sh", j] = k.small[:, 568 + 4 * j:572 + 4 * j]
    return v


def l2f_pe(k, pe):
    v = ffq_views(k)
    norm_pe(k, pe, "n8", k.H, "l2a_read", 2, free=(("gated", 2 * TILES),))
    pe.wait_ge(*k.at("w_sums", 2))
    pe.matmul(k.PS[:, 4, 0:2], k.mean_w[:, :], v["wsum"], start=True, stop=True).then_inc(k.sem("w_means"), 1)
    pe.wait_ge(*k.at("w_quantised", 2))
    with pe.Fori(0, TILES) as t:

        def phase1(g):
            n = GPT * t + g
            if g == 0:
                pe.wait_ge(*k.at("tile_staged", t + 1))
            pe.wait_ge(*k.at("x_shifted", n))
            for h in range(NH):
                mm = pe.transpose(k.PS[:, 0, P * h:P * h + P], v["xs"][:, h, P * g:P * g + P], k.ident[:, :])
            mm.then_inc(k.sem("x_turned"), 1)
            pe.wait_ge(*k.at("x_quantised", n + 1))
            pe.wait_ge(*k.at("xq_copied", n))
            for h in range(NH):
                mm = pe.transpose(k.PS[:, 2, 64 * h:64 * h + 64].bitcast(BF16), v["xq", g % 2][:, P * h:P * h + P], k.identb[:, :])
            mm.then_inc(k.sem("xq_turned"), 1)

        def phase2(g):
            n = GPT * t + g
            pe.wait_ge(*k.at("xq_copied", n + 1))
            pe.wait_ge(*k.at("h_scaled", n))
            for c in range(2):
                for h in range(NH):
                    mm = pe.matmul(bank(k, 3 + c), v["xt", g % 2][:, h, :], v["w1"][:, h, TN * c:TN * c + TN], start=h == 0, stop=h == 1)
            mm.then_inc(k.sem("h_ready"), 1)

        def phase3(g):
            n = GPT * t + g
            pe.wait_ge(*k.at("h_quantised", n + 1))
            pe.wait_ge(*k.at("hq_copied", n))
            for x in range(8):
                mm = pe.transpose(k.PS[:, 5, 64 * x:64 * x + 64].bitcast(BF16), v["hq"][:, P * x:P * x + P], k.identb[:, :])
            mm.then_inc(k.sem("hq_turned"), 1)
            pe.wait_ge(*k.at("hq_copied", n + 1))
            pe.wait_ge(*k.at("y_scaled", n))
            for x in range(8):
                mm = pe.matmul(k.PS[:, 6, 0:D], v["ht"][:, x, :], v["w2"][:, x, :], start=x == 0, stop=x == 7)
            mm.then_inc(k.sem("y_ready"), 1)
            pe.wait_ge(*k.at("y_scaled", n + 1))
            pe.wait_ge(*k.at("y_added", n))
            for h in range(NH):
                mm = pe.transpose(k.PS[:, 7, P * h:P * h + P], v["out"][:, P * h:P * h + P], k.ident[:, :])
            mm.then_inc(k.sem("y_turned"), 1)

        for s in range(GPT + 2):
            if s < GPT:
                phase1(s)
            if 1 <= s <= GPT:
                phase2(s - 1)
            if s >= 2:
                phase3(s - 2)


def l2f_act(k, act):
    v = ffq_views(k)
    norm_act(k, act, "n8")
    with act.Fori(0, TILES) as t:

        def phase1(g):
            n = GPT * t + g
            act.wait_ge(*k.at("xq_turned", n + 1))
            act.wait_ge(*k.at("h_ready", GPT * t + max(g - 1, 0)))
            act.activation(v["xt", g % 2], k.PS[:, 2, 0:P].bitcast(BF16).rearrange("p (k t) -> p k t", k=2), ACT.Copy).then_inc(k.sem("xq_copied"), 1)

        def phase2(g):
            n = GPT * t + g
            act.wait_ge(*k.at("h_scaled", n + 1))
            act.activation(v["h", g % 2], v["h", g % 2], ACT.Gelu).then_inc(k.sem("h_gelu"), 1)

        def phase3(g):
            n = GPT * t + g
            act.wait_ge(*k.at("hq_turned", n + 1))
            act.wait_ge(*k.at("y_ready", n))
            act.activation(v["ht"], bank(k, 5).bitcast(BF16).rearrange("p (k t) -> p k t", k=8), ACT.Copy).then_inc(k.sem("hq_copied"), 1)

        for s in range(GPT + 2):
            if s < GPT:
                phase1(s)
            if 1 <= s <= GPT:
                phase2(s - 1)
            if s >= 2:
                phase3(s - 2)


def l2f_pool(k, pool):
    v = ffq_views(k)
    pool.wait_ge(*k.at("l2a_ready", 2 * TILES))
    with pool.Fori(0, TILES) as t:
        pool.wait_ge(*k.at("n8_scaled", 2 * t + 2))
        pool.wait_ge(*k.at("x_turned", GPT * t))
        pool.tensor_copy(v["xs"].rearrange("p h (s t) -> p h s t", s=SPT), k.Y[:, :, bass.ds(SPT * t, SPT), PAD:PAD + T]).then_inc(k.sem("tile_staged"), 1)


def l2f_dve(k, dve):
    v = ffq_views(k)
    norm_dve(k, dve, "n8", k.H, dst=lambda h, t: yt(k, h, t))
    done = [0]

    def chain(ins):
        done[0] += 1
        ins.then_inc(k.sem("w_step"), 1)
        dve.wait_ge(*k.at("w_step", done[0]))
    raw = [k.C[:, 0:2048], k.C[:, 2048:4096]]
    dve.wait_ge(*k.at("l2f_weights", 16))
    for j in range(2):
        dve.tensor_reduce(v["wsum"][:, j:j + 1], raw[j], AX.X, ALU.add, apply_absolute_value=True).then_inc(k.sem("w_sums"), 1)
    dve.wait_ge(*k.at("w_means", 1))
    chain(dve.tensor_scalar(v["wscale"], k.PS[:, 4, 0:2], 1 / 1024, EPS, ALU.mult, ALU.max))
    chain(dve.reciprocal(v["winv"], v["wscale"]))
    chain(dve.tensor_scalar(v["wscale"], v["wscale"], 1 / 127, None, ALU.mult))
    for j, w in enumerate(("w1", "w2")):
        flatw = v[w].rearrange("p k m -> p (k m)")
        chain(dve.tensor_scalar(raw[j], raw[j], v["winv"][:, j:j + 1], ROUND, ALU.mult, ALU.add))
        chain(dve.tensor_scalar(raw[j], raw[j], ROUND, 1.0, ALU.subtract, ALU.min))
        dve.tensor_scalar(flatw, raw[j], -1.0, None, ALU.max).then_inc(k.sem("w_quantised"), 1)
    dve.wait_ge(*k.at("l2f_bias", 16))
    with dve.Fori(0, TILES) as t:

        def row_scale(src, s, n, what, j):
            dve.tensor_reduce(s[:, 0:1], src, AX.X, ALU.max, apply_absolute_value=True).then_inc(k.sem(what + "_max"), 1)
            dve.wait_ge(*k.at(what + "_max", n + 1))
            dve.tensor_scalar(s[:, 0:1], s[:, 0:1], EPS, None, ALU.max).then_inc(k.sem(what + "_clip"), 1)
            dve.wait_ge(*k.at(what + "_clip", n + 1))
            dve.reciprocal(s[:, 1:2], s[:, 0:1]).then_inc(k.sem(what + "_inv"), 1)
            dve.tensor_scalar(s[:, 2:3], s[:, 0:1], v["wscale"][:, j:j + 1], None, ALU.mult).then_inc(k.sem(what + "_scale"), 1)
            dve.wait_ge(*k.at(what + "_inv", n + 1))
            dve.tensor_scalar(s[:, 1:2], s[:, 1:2], 127.0, None, ALU.mult).then_inc(k.sem(what + "_127"), 1)
            dve.wait_ge(*k.at(what + "_127", n + 1))

        def phase1(g):
            n = GPT * t + g
            x, s = v["x", g % 2], v["sx", g % 2]
            dve.wait_ge(*k.at("x_turned", n + 1))
            row_scale(k.PS[:, 0, 0:D], s, n, "x", 0)
            dve.tensor_scalar(x, k.PS[:, 0, 0:D], s[:, 1:2], ROUND, ALU.mult, ALU.add).then_inc(k.sem("x_shifted"), 1)
            dve.wait_ge(*k.at("x_shifted", n + 1))
            dve.wait_ge(*k.at("xq_turned", GPT * t + max(g - 1, 0)))
            dve.tensor_scalar(v["xq", g % 2], x, ROUND, 127.0, ALU.subtract, ALU.min).then_inc(k.sem("x_quantised"), 1)

        def phase2(g):
            n = GPT * t + g
            dve.wait_ge(*k.at("h_ready", n + 1))
            dve.wait_ge(*k.at("x_scale", n + 1))
            dve.wait_ge(*k.at("h_quantised", GPT * t + max(g - 1, 0)))
            dve.scalar_tensor_tensor(v["h", g % 2], k.PS[:, 3:5, :].rearrange("p b n -> p (b n)"), v["sx", g % 2][:, 2:3], v["b1"],
                                     ALU.mult, ALU.add).then_inc(k.sem("h_scaled"), 1)

        def phase3(g):
            n = GPT * t + g
            x, s = v["h", g % 2], v["sh", g % 2]
            dve.wait_ge(*k.at("h_gelu", n + 1))
            row_scale(x, s, n, "hid", 1)
            dve.tensor_scalar(x, x, s[:, 1:2], ROUND, ALU.mult, ALU.add).then_inc(k.sem("h_shifted"), 1)
            dve.wait_ge(*k.at("h_shifted", n + 1))
            dve.wait_ge(*k.at("hq_turned", n))
            dve.tensor_scalar(v["hq"], x, ROUND, 127.0, ALU.subtract, ALU.min).then_inc(k.sem("h_quantised"), 1)

        def phase4(g):
            n = GPT * t + g
            dve.wait_ge(*k.at("y_ready", n + 1))
            dve.wait_ge(*k.at("y_turned", n))
            dve.wait_ge(*k.at("hid_scale", n + 1))
            dve.scalar_tensor_tensor(v["out"], k.PS[:, 6, 0:D], v["sh", g % 2][:, 2:3], v["b2"], ALU.mult, ALU.add).then_inc(k.sem("y_scaled"), 1)
            dve.wait_ge(*k.at("y_turned", n + 1))
            pos = P * (g % 2)
            dst = k.H[:, :, bass.ds(SPT * t + g // 2, 1), pos:pos + P].rearrange("p h s t -> p h (s t)")
            dve.tensor_tensor(dst, dst, k.PS[:, 7, 0:D].rearrange("p (h t) -> p h t", h=2), ALU.add).then_inc(k.sem("y_added"), 1)

        for s in range(GPT + 2):
            if s < GPT:
                phase1(s)
            if 1 <= s <= GPT:
                phase2(s - 1)
            if s >= 2:
                phase3(s - 2)
                phase4(s - 2)



V3 = {"k": 0, "v": 512, "r": 1024, "o": 1536}
FIRST = -1e38


def l3a_inputs(ins, a):
    w = {n: a["L3_attn_" + n].T for n in ("att_Wk", "att_Wv", "att_Wr", "att_Wo", "ffn_Wk", "ffn_Wr", "ffn_Wv")}
    ins["l3a_w"] = np.concatenate([halves(w[n]) for n in ("att_Wk", "att_Wv", "att_Wr", "att_Wo", "ffn_Wk")], axis=1)
    ins["l3a_w2"] = np.concatenate([halves(w["ffn_Wv"]), halves(w["ffn_Wr"])], axis=1)


def l3a_load(k, sp):
    sp.wait_ge(*k.at("gla_out", 4 * B))
    sp.dma_start(k.V[:, 0:4096], k.ins["l3a_w"]).then_inc(k.sem("l3a_weights"), 16)
    sp.wait_ge(*k.at("y_ready", N // P))
    sp.wait_ge(*k.at("y_scaled", N // P))
    sp.dma_start(k.W[:, 6144:8704], k.ins["l3a_w2"]).then_inc(k.sem("l3a_weights"), 16)


def wkv_views(k, h):
    s = (k.B, k.C)[h]
    v = {"pp": s[:, 0:513], "aa": s[:, 520:1033], "bb": s[:, 1040:1553], "p": k.R[:, TN * h:TN * h + TN],
         "step": (k.W[:, 8704:9216], k.rope[:, :])[h], "first": k.V[:, 4608:5120]}
    for j, name in enumerate(("e1b", "e2b", "e1", "e2")):
        v[name] = s[:, 2048 + TN * j:2560 + TN * j]
    return v


def l3a_pe(k, pe):
    norm_pe(k, pe, "n9", k.H, "y_added", 4, free=(("y_added", N // P), ("h_scaled", N // P)))
    norm_pe(k, pe, "n10", seqs(k.A), "n9_scaled", 2)
    pe.wait_ge(*k.at("l3a_weights", 32))
    pe.wait_ge(*k.at("n10_std", TILES))
    wb = lambda name: blocks(k.V[:, V3[name]:V3[name] + 512], 2)
    with pe.Fori(0, TILES // 2) as i:
        for par in range(2):
            t = 2 * i + par
            for n in range(6):
                pe.wait_ge(*k.at("mixed3", 6 * t + 2 * (n // 2) + 2))
                pe.wait_ge(*k.at("kvr_read", 12 * i + (par and n + 1)))
                for h in range(NH):
                    mm = pe.matmul(bank(k, n), wb("kvr"[n // 2])[:, h, (n % 2) * P:(n % 2 + 1) * P], tile(seqs((k.B, k.C, k.E)[n // 2]), h, t), start=h == 0, stop=h == 1)
                mm.then_inc(k.sem("mix_ready"), 1)
    pe.wait_ge(*k.at("kvr_read", 6 * TILES))
    with pe.Fori(0, TILES // 2) as i:
        for par in range(2):
            t = 2 * i + par
            pe.wait_ge(*k.at("wkv", 2 * t + 2))
            pe.wait_ge(*k.at("x3_done", 4 * i))
            for m in range(NH):
                for h in range(NH):
                    mm = pe.matmul(bank(k, 4 + 2 * par + m), wb("o")[:, h, m * P:(m + 1) * P], tile(seqs(k.E), h, t), start=h == 0, stop=h == 1)
                mm.then_inc(k.sem("wkv_out"), 1)
    norm_pe(k, pe, "n11", seqs(k.A), "x3_done", 2)
    pe.wait_ge(*k.at("n11_std", TILES))
    wr = blocks(k.W[:, 8192:8704], 2)
    with pe.Fori(0, TILES // 2) as i:
        for par in range(2):
            t = 2 * i + par
            pe.wait_ge(*k.at("mixed4", 4 * t + 4))
            pe.wait_ge(*k.at("cm_sig", 4 * i))
            for m in range(NH):
                for h in range(NH):
                    mm = pe.matmul(bank(k, 2 * par + m), wr[:, h, m * P:(m + 1) * P], tile(seqs(k.C), h, t), start=h == 0, stop=h == 1)
                mm.then_inc(k.sem("cm_ready"), 1)
    pe.wait_ge(*k.at("cm_sig", 2 * TILES))
    wk, wv = blocks(k.V[:, 2048:4096], 2), blocks(k.W[:, 6144:8192], 8)
    with pe.Fori(0, TILES // 2) as i:
        for par in range(2):
            t = 2 * i + par
            for m in range(8):
                pe.wait_ge(*k.at("ffk_relu", 16 * i + max(8 * par + m - 3, 0)))
                for h in range(NH):
                    mm = pe.matmul(bank(k, 4 + m % 4), wk[:, h, m * P:(m + 1) * P], tile(seqs(k.B), h, t), start=h == 0, stop=h == 1)
                mm.then_inc(k.sem("ffk_ready"), 1)
        for par in range(2):
            f = (k.E, k.Q)[par][:, :].rearrange("p (m n) -> p m n", m=8)
            pe.wait_ge(*k.at("ffk_squared", 16 * i + 8 * (par + 1)))
            pe.wait_ge(*k.at("ffv_read", 4 * i))
            for m in range(NH):
                for x in range(8):
                    mm = pe.matmul(bank(k, 2 * par + m), wv[:, x, m * P:(m + 1) * P], f[:, x, :], start=x == 0, stop=x == 7)
                mm.then_inc(k.sem("ffv_ready"), 1)


def l3a_act(k, act):
    norm_act(k, act, "n9")
    act.activation(k.small[:, 576:578], k.vec[:, VCOL["decay"]:VCOL["decay"] + 2], ACT.Exp).then_inc(k.sem("decay_exp"), 1)
    norm_act(k, act, "n10", "ln1_b", lambda h, t: yt(k, h, t))
    with act.Fori(0, TILES) as t:
        act.wait_ge(*k.at("n10_done", 2 * t + 2))
        for o, x in enumerate((k.B, k.C, k.E)):
            for h in range(NH):
                act.activation(tile(seqs(x), h, t), yt(k, h, t, 1), ACT.Copy, scale=k.vec2[:, 4 + 2 * o + h:5 + 2 * o + h]).then_inc(k.sem("before3"), 1)
    with act.Fori(0, TILES) as t:
        for n in range(6):
            act.wait_ge(*k.at("mix_ready", 6 * t + max(n, 5 if n == 4 else 0) + 1))
            dst = tile(seqs((k.D, k.Q, k.E)[n // 2]), n % 2, t)
            act.activation(dst, bank_seq(k, n), ACT.Sigmoid if n >= 4 else ACT.Copy).then_inc(k.sem("kvr_read"), 1)
    with act.Fori(0, TILES) as t:
        for h in range(NH):
            v = wkv_views(k, h)
            for j, name in enumerate(("e1b", "e2b", "e1", "e2")):
                act.wait_ge(*k.at("exp_args", 8 * t + 4 * h + j + 1))
                act.activation(v[name], v[name], ACT.Exp).then_inc(k.sem("exps"), 1)
    norm_act(k, act, "n11", "ln2_b", lambda h, t: yt(k, h, t))
    with act.Fori(0, TILES) as t:
        act.wait_ge(*k.at("n11_done", 2 * t + 2))
        for o, x in enumerate((k.B, k.C)):
            for h in range(NH):
                act.activation(tile(seqs(x), h, t), yt(k, h, t, 1), ACT.Copy, scale=k.vec2[:, 10 + 2 * o + h:11 + 2 * o + h]).then_inc(k.sem("before4"), 1)
    with act.Fori(0, TILES // 2) as i:
        for par in range(2):
            t = 2 * i + par
            act.wait_ge(*k.at("cm_ready", 2 * t + 2))
            for m in range(NH):
                act.activation(tile(seqs(k.C), m, t), bank_seq(k, 2 * par + m), ACT.Sigmoid).then_inc(k.sem("cm_sig"), 1)
    with act.Fori(0, TILES // 2) as i:
        for par in range(2):
            f = (k.E, k.Q)[par][:, :].rearrange("p (m n) -> p m n", m=8)
            act.wait_ge(*k.at("ffv_ready", 4 * i))
            for m in range(8):
                act.wait_ge(*k.at("ffk_ready", 16 * i + 8 * par + m + 1))
                act.activation(f[:, m, :], bank(k, 4 + m % 4), ACT.Relu).then_inc(k.sem("ffk_relu"), 1)


def l3a_pool(k, pool):
    with pool.Fori(0, TILES) as t:
        for h in range(NH):
            v = wkv_views(k, h)
            val = flat(k.Q, h, t)
            pool.wait_ge(*k.at("exps", 8 * t + 4 * h + 4))
            pool.tensor_tensor(v["pp"][:, 1:TN + 1], v["e2b"], val, ALU.mult).then_inc(k.sem("wkv_pool"), 1)
            pool.tensor_tensor(v["p"], v["e2"], val, ALU.mult).then_inc(k.sem("wkv_pool"), 1)
            pool.wait_ge(*k.at("sums", 4 * t + 2 * h + 2))
            pool.tensor_tensor(v["e1b"], v["e1"], v["aa"][:, 0:TN], ALU.mult).then_inc(k.sem("wkv_pool"), 1)
            pool.wait_ge(*k.at("wkv_pool", 8 * t + 4 * h + 3))
            pool.tensor_tensor(v["e1"], v["e1"], v["bb"][:, 0:TN], ALU.mult).then_inc(k.sem("wkv_pool"), 1)


def l3a_dve(k, dve):
    norm_dve(k, dve, "n9", k.H, dst=lambda h, t: tile(seqs(k.A), h, t))
    done = [0]

    def chain(ins):
        done[0] += 1
        ins.then_inc(k.sem("wkv_step"), 1)
        dve.wait_ge(*k.at("wkv_step", done[0]))
    vs = [wkv_views(k, h) for h in range(NH)]
    w = k.small[:, 576:578]
    first = vs[0]["first"]
    dve.wait_ge(*k.at("decay_exp", 1))
    chain(dve.tensor_scalar(w, w, -1.0, None, ALU.mult))
    chain(dve.memset(first, 0.0))
    chain(dve.memset(first.rearrange("p (s t) -> p s t", s=SPT)[:, :, 0:1], FIRST))
    for h in range(NH):
        chain(dve.tensor_scalar(vs[h]["step"], first, w[:, h:h + 1], None, ALU.add))
    norm_dve(k, dve, "n10", seqs(k.A), gain="ln1_g")
    with dve.Fori(0, TILES) as t:
        for o, (x, mu) in enumerate(((k.B, "mix_k"), (k.C, "mix_v"), (k.E, "mix_r"))):
            for h in range(NH):
                dve.wait_ge(*k.at("before3", 6 * t + 2 * o + h + 1))
                y = tile(seqs(x), h, t)
                dve.scalar_tensor_tensor(y, yt(k, h, t), vcol(k, mu, h), y, ALU.mult, ALU.add).then_inc(k.sem("mixed3"), 1)
    dve.wait_ge(*k.at("mix_ready", 6 * TILES))
    for h in range(NH):
        for name in ("pp", "aa", "bb"):
            chain(dve.memset(vs[h][name][:, 0:1], 0.0))
    with dve.Fori(0, TILES) as t:
        for h in range(NH):
            v, n = vs[h], 2 * t + h
            key, u = flat(k.D, h, t), vcol(k, "first", h)
            dve.wait_ge(*k.at("kvr_read", 6 * t + 6))
            dve.wait_ge(*k.at("wkv", 2 * t))
            dve.tensor_tensor_scan(v["pp"][:, 1:TN + 1], v["step"], key, 0.0, ALU.add, ALU.max).then_inc(k.sem("pp"), 1)
            dve.wait_ge(*k.at("pp", n + 1))
            dve.tensor_tensor(v["e1"], v["pp"][:, 0:TN], v["first"], ALU.add).then_inc(k.sem("pp_prev"), 1)
            dve.wait_ge(*k.at("pp_prev", n + 1))
            dve.scalar_tensor_tensor(v["p"], key, u, v["e1"], ALU.add, ALU.max).then_inc(k.sem("p_max"), 1)
            dve.scalar_tensor_tensor(v["e1b"], v["e1"], w[:, h:h + 1], v["pp"][:, 1:TN + 1], ALU.add, ALU.subtract).then_inc(k.sem("exp_args"), 1)
            dve.tensor_tensor(v["e2b"], key, v["pp"][:, 1:TN + 1], ALU.subtract).then_inc(k.sem("exp_args"), 1)
            dve.wait_ge(*k.at("p_max", n + 1))
            dve.tensor_tensor(v["e1"], v["e1"], v["p"], ALU.subtract).then_inc(k.sem("exp_args"), 1)
            dve.scalar_tensor_tensor(v["e2"], key, u, v["p"], ALU.add, ALU.subtract).then_inc(k.sem("exp_args"), 1)
        for h in range(NH):
            v = vs[h]
            dve.wait_ge(*k.at("exps", 8 * t + 4 * h + 2))
            dve.tensor_tensor_scan(v["bb"][:, 1:TN + 1], v["e1b"], v["e2b"], 0.0, ALU.mult, ALU.add).then_inc(k.sem("sums"), 1)
            dve.wait_ge(*k.at("wkv_pool", 8 * t + 4 * h + 1))
            dve.tensor_tensor_scan(v["aa"][:, 1:TN + 1], v["e1b"], v["pp"][:, 1:TN + 1], 0.0, ALU.mult, ALU.add).then_inc(k.sem("sums"), 1)
        for h in range(NH):
            v, n = vs[h], 2 * t + h
            dve.wait_ge(*k.at("wkv_pool", 8 * t + 4 * h + 3))
            dve.tensor_tensor(v["e1b"], v["e1b"], v["p"], ALU.add).then_inc(k.sem("num"), 1)
            dve.wait_ge(*k.at("wkv_pool", 8 * t + 4 * h + 4))
            dve.tensor_tensor(v["e1"], v["e1"], v["e2"], ALU.add).then_inc(k.sem("den"), 1)
            dve.wait_ge(*k.at("den", n + 1))
            dve.reciprocal(v["e1"], v["e1"]).then_inc(k.sem("den_inv"), 1)
            dve.wait_ge(*k.at("num", n + 1))
            dve.wait_ge(*k.at("den_inv", n + 1))
            dve.tensor_tensor(v["e1"], v["e1"], v["e1b"], ALU.mult).then_inc(k.sem("ratio"), 1)
            dve.wait_ge(*k.at("ratio", n + 1))
            dve.tensor_tensor(flat(k.E, h, t), flat(k.E, h, t), v["e1"], ALU.mult).then_inc(k.sem("wkv"), 1)
    with dve.Fori(0, TILES // 2) as i:
        for par in range(2):
            t = 2 * i + par
            for m in range(NH):
                dve.wait_ge(*k.at("wkv_out", 2 * t + m + 1))
                dve.tensor_tensor(tile(seqs(k.A), m, t), tile(seqs(k.A), m, t), bank_seq(k, 4 + 2 * par + m), ALU.add).then_inc(k.sem("x3_done"), 1)
    norm_dve(k, dve, "n11", seqs(k.A), gain="ln2_g")
    with dve.Fori(0, TILES) as t:
        for o, (x, mu) in enumerate(((k.B, "cm_k"), (k.C, "cm_r"))):
            for h in range(NH):
                dve.wait_ge(*k.at("before4", 4 * t + 2 * o + h + 1))
                y = tile(seqs(x), h, t)
                dve.scalar_tensor_tensor(y, yt(k, h, t), vcol(k, mu, h), y, ALU.mult, ALU.add).then_inc(k.sem("mixed4"), 1)
    with dve.Fori(0, TILES // 2) as i:
        for par in range(2):
            f = (k.E, k.Q)[par][:, :].rearrange("p (m n) -> p m n", m=8)
            for m in range(8):
                dve.wait_ge(*k.at("ffk_relu", 16 * i + 8 * par + m + 1))
                dve.tensor_tensor(f[:, m, :], f[:, m, :], f[:, m, :], ALU.mult).then_inc(k.sem("ffk_squared"), 1)
        for par in range(2):
            t = 2 * i + par
            for m in range(NH):
                c, x = tile(seqs(k.C), m, t), tile(seqs(k.A), m, t)
                dve.wait_ge(*k.at("ffv_ready", 2 * t + m + 1))
                dve.tensor_tensor(c, c, bank_seq(k, 2 * par + m), ALU.mult).then_inc(k.sem("ffv_read"), 1)
                dve.tensor_tensor(tile(k.H, m, t), tile(k.H, m, t), x, ALU.add).then_inc(k.sem("x3_added"), 1)
                dve.wait_ge(*k.at("ffv_read", 2 * t + m + 1))
                dve.wait_ge(*k.at("x3_added", 2 * t + m + 1))
                dve.tensor_tensor(tile(k.H, m, t), tile(k.H, m, t), c, ALU.add).then_inc(k.sem("l3a_done"), 1)



E3, FF3 = 8, 1024


def l3f_inputs(ins, a):
    gu, down = a["L3_ffn_gate_up_w"], a["L3_ffn_down_w"]
    ins["l3f_gu"] = gu.transpose(0, 2, 1).reshape(E3, 2, P, 2 * FF3).transpose(0, 2, 1, 3).reshape(E3, P, 4 * FF3)
    ins["l3f_down"] = down.transpose(0, 2, 1).reshape(E3, 8, P, D).transpose(0, 2, 1, 3).reshape(E3, P, 8 * D)
    ins["l3f_gate"] = halves(a["L3_ffn_gate_w"].T)


def expert_bufs(k, j):
    gu = (k.W[:, 0:4096], k.B[:, :])[j]
    down = (k.W[:, 4096:6144], k.C[:, 0:2048])[j]
    return gu, down


def l3f_load(k, sp):
    sp.dma_start(k.small[:, 600:616], k.ins["l3f_gate"]).then_inc(k.sem("l3f_router"), 16)
    for e in range(2):
        if e == 1:
            sp.wait_ge(*k.at("l3a_done", 2 * TILES))
        gu, down = expert_bufs(k, e)
        sp.dma_start(gu, k.ins["l3f_gu"][e]).then_inc(k.sem(f"expert_in{e}"), 16)
        sp.dma_start(down, k.ins["l3f_down"][e]).then_inc(k.sem(f"expert_in{e}"), 16)
    with sp.Fori(1, E3 // 2) as i:
        for j in range(2):
            gu, down = expert_bufs(k, j)
            sp.wait_ge(*k.at("down_ready", 16 * i + 8 * j - 8))
            sp.dma_start(gu.unsqueeze(1), k.ins["l3f_gu"][bass.ds(2 * i + j, 1)].rearrange("e p n -> p e n")).then_inc(k.sem(f"expert_in{j}"), 16)
            sp.dma_start(down.unsqueeze(1), k.ins["l3f_down"][bass.ds(2 * i + j, 1)].rearrange("e p n -> p e n")).then_inc(k.sem(f"expert_in{j}"), 16)


def moe3_views(k):
    return {"pick": [k.E[0:E3, 2048 + P * j:2048 + P * (j + 1)] for j in range(2)], "s": [k.C[:, 2048 + TN * j:2560 + TN * j] for j in range(2)], "w": [k.C[:, 3072 + TN * j:3584 + TN * j] for j in range(2)],
            "out": [k.E[:, TN * j:TN * j + TN] for j in range(4)], "f": [k.D[:, :].rearrange("p (m n) -> p m n", m=8), k.Q[:, :].rearrange("p (m n) -> p m n", m=8)]}


def l3f_pe(k, pe):
    v = moe3_views(k)
    norm_pe(k, pe, "n12", k.H, "l3a_done", 2, free=(("ffv_read", 2 * TILES),))
    pe.wait_ge(*k.at("l3f_router", 16))
    logits_pe(k, pe, "l3f", "n12_scaled", blocks(k.small[:, 600:616], 2), E3, 1)
    combine_pe(k, pe, "l3f", E3, 0)
    pe.wait_ge(*k.at("l3f_cw", 4))
    with pe.Fori(0, E3 // 2) as i:
        for j in range(2):
            gu, down = (blocks(b, n) for b, n in zip(expert_bufs(k, j), (2, 8)))
            with pe.Fori(0, TILES // 2) as q:
                n = 8 * i + 4 * j + 2 * q
                pe.wait_ge(*k.at(f"expert_in{j}", 32 * i + 32))
                pe.wait_ge(*k.at("picked", 2 * i + j + 1))
                for par in range(2):
                    t = 2 * q + par
                    for m in range(8):
                        pe.wait_ge(*k.at("hact", 8 * n + max(8 * par + m - 1, 0)))
                        for o in range(2):
                            for h in range(NH):
                                mm = pe.matmul(bank(k, 2 * (m % 2) + o), gu[:, h, FF3 * o + m * P:FF3 * o + (m + 1) * P], yt(k, h, t), start=h == 0, stop=h == 1)
                        mm.then_inc(k.sem("gu_ready"), 1)
                    pe.wait_ge(*k.at("scaled3", 2 * n))
                    pe.matmul(bank(k, 4 + 2 * par), v["pick"][j],
                              k.A[0:E3, bass.ds(t * TN + 2048, TN)], start=True, stop=True).then_inc(k.sem("w3_spread"), 1)
                for par in range(2):
                    pe.wait_ge(*k.at("hact", 8 * n + 8 * (par + 1)))
                    pe.wait_ge(*k.at("w3_copied", n + par + 1))
                    for m in range(NH):
                        for x in range(8):
                            mm = pe.matmul(bank(k, 4 + 2 * par + m), down[:, x, m * P:(m + 1) * P], v["f"][par][:, x, :], start=x == 0, stop=x == 7)
                        mm.then_inc(k.sem("down_ready"), 1)


def l3f_act(k, act):
    v = moe3_views(k)
    norm_act(k, act, "n12")
    route_act(k, act, "l3f", E3, 0)
    with act.Fori(0, E3 * TILES // 2) as q:
        n = 2 * q
        for par in range(2):
            for m in range(8):
                act.wait_ge(*k.at("gu_ready", 8 * n + 8 * par + m + 1))
                act.wait_ge(*k.at("hact", 8 * n + max(8 * par + m - 1, 0)))
                act.activation(v["s"][m % 2], bank(k, 2 * (m % 2)), ACT.Gelu).then_inc(k.sem("gelu3"), 1)
            act.wait_ge(*k.at("w3_spread", n + par + 1))
            act.wait_ge(*k.at("scaled3", 2 * n))
            act.activation(v["w"][par], bank(k, 4 + 2 * par), ACT.Copy).then_inc(k.sem("w3_copied"), 1)


def l3f_dve(k, dve):
    v = moe3_views(k)
    norm_dve(k, dve, "n12", k.H, dst=lambda h, t: yt(k, h, t))
    route_dve(k, dve, "l3f", E3, 1, 0.0, None, 0)
    dve.wait_ge(*k.at("ffv_ready", 2 * TILES))
    with dve.Fori(0, E3 // 2) as i:
        for j in range(2):
            dve.wait_ge(*k.at("w3_spread", 8 * i))
            e = 2 * i + j
            dve.tensor_copy(v["pick"][j], k.ident[0:E3, bass.ds(e, 1)].to_broadcast([E3, P])).then_inc(k.sem("picked"), 1)
            with dve.Fori(0, TILES // 2) as q:
                n = 8 * i + 4 * j + 2 * q
                for par in range(2):
                    f = v["f"][par]
                    dve.wait_ge(*k.at("down_ready", 2 * n))
                    for m in range(8):
                        dve.wait_ge(*k.at("gelu3", 8 * n + 8 * par + m + 1))
                        dve.tensor_tensor(f[:, m, :], v["s"][m % 2], bank(k, 2 * (m % 2) + 1), ALU.mult).then_inc(k.sem("hact"), 1)
                for par in range(2):
                    t = 2 * q + par
                    for m in range(NH):
                        o = v["out"][2 * par + m]
                        dve.wait_ge(*k.at("down_ready", 2 * n + 2 * par + m + 1))
                        dve.tensor_tensor(o, bank(k, 4 + 2 * par + m), v["w"][par], ALU.mult).then_inc(k.sem("scaled3"), 1)
                        dve.wait_ge(*k.at("scaled3", 2 * n + 2 * par + m + 1))
                        dve.tensor_tensor(tile(k.H, m, t), tile(k.H, m, t), o.rearrange("p (s t) -> p s t", s=SPT), ALU.add).then_inc(k.sem("l3f_done"), 1)


def more_inputs(ins, a):
    l0f_inputs(ins, a)
    l1a_inputs(ins, a)
    l1f_inputs(ins, a)
    l2a_inputs(ins, a)
    l2f_inputs(ins, a)
    l3a_inputs(ins, a)
    l3f_inputs(ins, a)
    return


SP_STAGES = [l0a_load, l0f_load, l1a_load, l1f_load, l2a_load, l2f_load, l3a_load, l3f_load]
POOL_STAGES = [l0a_pool, l1a_pool, l1f_pool, l2a_pool, l2f_pool, l3a_pool]
PE_STAGES = [l0a_pe, l0f_pe, l1a_pe, l1f_pe, l2a_pe, l2f_pe, l3a_pe, l3f_pe]
ACT_STAGES = [l0a_act, l0f_act, l1a_act, l1f_act, l2a_act, l2f_act, l3a_act, l3f_act]
DVE_STAGES = [l0a_dve, l0f_dve, l1a_dve, l1f_dve, l2a_dve, l2f_dve, l3a_dve, l3f_dve]
LAST, LAST_PER = "l3f_done", 16



def build(nc, ins, out):
    with ExitStack() as ctx:
        k = Kernel(nc, ctx, ins, out)
        allocate(k)
        block = ctx.enter_context(nc.Block())

        @block.sync
        def _(sp):
            for name in PRIMED:
                sp.sem_inc(k.sem(name), 1)
            load_constants(k, sp)
            tok_load(k, sp)
            for f in SP_STAGES:
                f(k, sp)
            for h in range(NH):
                if LAST_PER:
                    sp.wait_ge(*k.at(LAST, LAST_PER * TILES))
                sp.dma_start(out[h].rearrange("p (s t) -> p s t", s=B), k.H[:, h]).then_inc(k.sem("stored"), 16)
            sp.wait_ge(*k.at("stored", 16 * NH))

        @block.gpsimd
        def _(pool):
            tok_pool(k, pool)
            for f in POOL_STAGES:
                f(k, pool)

        @block.tensor
        def _(pe):
            tok_pe(k, pe)
            for f in PE_STAGES:
                f(k, pe)

        @block.scalar
        def _(act):
            tok_act(k, act)
            for f in ACT_STAGES:
                f(k, act)

        @block.vector
        def _(dve):
            tok_dve(k, dve)
            for f in DVE_STAGES:
                f(k, dve)
        assert not k.unprimed, sorted(k.unprimed)



def halves(a):
    r, m = a.shape
    return a.reshape(r // P, P, m).transpose(1, 0, 2).reshape(P, -1)


def constants():
    f = np.float32
    c = {}
    c["c_ident"] = np.eye(P, dtype=f)
    c["c_mean"] = np.full((P, P), 1.0 / D, f)
    p = np.arange(P)
    theta = f(1.0) / np.power(f(10000.0), np.arange(8, dtype=f) / f(8))
    ang = np.outer(np.arange(T, dtype=f), theta).astype(f)
    cos, sin = np.cos(ang).astype(f), np.sin(ang).astype(f)
    sign = np.where(p % 16 < 8, f(-1), f(1))
    c["c_rope"] = np.concatenate([cos[:, p % 8].T, (sin[:, p % 8] * sign).T], axis=1).astype(f)
    perm = np.zeros((P, P), f)
    perm[p ^ 8, p] = 1.0
    q, key = np.arange(64)[:, None], np.arange(P)[None, :]
    first = np.where(key <= q, 0.0, -4e9)
    later = np.where((key - 64 <= q) & (q - (key - 64) < 64), 0.0, -4e9)
    band = np.concatenate([np.tile(first, (2, 1)), np.tile(later, (2, 1))], axis=1)
    causal = (p[:, None] <= p[None, :]).astype(f)
    gm = (p[:, None] // 16 % 4 == np.arange(4)[None, :]).astype(f)
    hm = (p[:, None] // 16 == np.arange(8)[None, :]).astype(f)
    rev = np.tile(16.0 - np.arange(16), (P, 1))
    c["c_att"] = np.concatenate([perm, band, causal, gm, hm, rev], axis=1).astype(f)
    fi = np.zeros((P, N // P), f)
    fi[0, ::2] = 1.0
    c["c_first"] = fi
    return c


def kernel(**x):
    import concourse.bacc as _bacc
    from concourse.bass_utils import run_bass_kernel_spmd as _run
    import ml_dtypes

    a = {n: np.ascontiguousarray(v) for n, v in x.items()}
    ins = constants()
    ins["c_identb"] = np.eye(P, dtype=ml_dtypes.bfloat16)
    tok = a["x"]
    ins["tok"] = tok.reshape(N // P, P).T
    ins["tok_prev"] = np.concatenate([np.zeros((B, 1), tok.dtype), tok[:, :-1]], axis=1).reshape(N // P, P).T
    ins["scale"] = a["L0_tok_scale"].reshape(1, 1)
    ins["embed"] = a["L0_tok_embed_weight"]
    ins["projT"] = a["L0_tok_proj_weight"].T
    jt, j2, g, d = np.meshgrid(np.arange(2), np.arange(2), np.arange(4), np.arange(16), indexing="ij")
    order = ((4 * g + 2 * jt + j2) * 16 + d).reshape(-1)
    dup = np.tile(np.arange(64), 2)
    v = {"bq": a["L0_attn_bq"][order], "bk": np.concatenate([a["L0_attn_bk"][dup], a["L0_attn_bk"][dup]]),
         "bo": a["L0_attn_bo"], "g1": a["L0_attn_g1"],
         "b1": a["L0_attn_b1"], "g2": a["L0_attn_g2"], "b2": a["L0_attn_b2"], "bf2": a["L0_attn_bf2"],
         "D": a["L1_attn_D"], "mu_r": a["L1_ffn_mu_r"], "mu_k": a["L1_ffn_mu_k"], "bgk2": a["L2_attn_bgk2"],
         "gamma": a["L2_attn_gamma"], "beta": a["L2_attn_beta"], "ln1_g": a["L3_attn_ln1_g"],
         "ln1_b": a["L3_attn_ln1_b"], "ln2_g": a["L3_attn_ln2_g"], "ln2_b": a["L3_attn_ln2_b"],
         "decay": a["L3_attn_time_decay"], "first": a["L3_attn_time_first"], "mix_k": a["L3_attn_time_mix_k"],
         "mix_v": a["L3_attn_time_mix_v"], "mix_r": a["L3_attn_time_mix_r"], "cm_k": a["L3_attn_cm_k"],
         "cm_r": a["L3_attn_cm_r"]}
    ins["vecs"] = np.concatenate([v[n].reshape(NH, P).T for n in VECS] + [a["L0_attn_bf1"].reshape(8, P).T], axis=1)
    ins["l0a_w"] = np.concatenate([halves(a["L0_attn_Wq"][:, order]), halves(a["L0_attn_Wk"][:, dup]), halves(a["L0_attn_Wv"]),
                                   halves(a["L0_attn_Wo"][order]), halves(a["L0_attn_Wf1"]), halves(a["L0_attn_Wf2"])], axis=1)
    ins["bv"] = a["L0_attn_bv"].reshape(1, 64)
    more_inputs(ins, a)

    nc = _bacc.Bacc("TRN2", target_bir_lowering=False, num_devices=1)
    arrays, aps = {}, {}
    for name, arr in ins.items():
        arr = np.ascontiguousarray(arr)
        arrays["in_" + name] = arr
        aps[name] = nc.dram_tensor("in_" + name, arr.shape, mybir.dt.from_np(arr.dtype), kind="ExternalInput").ap()
    out = nc.dram_tensor("out_0", (NH, P, N), F32, kind="ExternalOutput").ap()
    build(nc, aps, out)
    r = _run(nc, [arrays], core_ids=[0])
    got = r.results[0]["out_0"]
    return got.reshape(D, N).T.reshape(B, T, D)
```

```python
from contextlib import ExitStack

import numpy as np
import concourse.bass as bass
from concourse import mybir

F32 = mybir.dt.float32
BF16 = mybir.dt.bfloat16
I32 = mybir.dt.int32
U32 = mybir.dt.uint32
ACT = mybir.ActivationFunctionType
ALU = mybir.AluOpType
AX = mybir.AxisListType

P = 128
D = 256
NH = D // P
B, T = 8, 256
N = B * T
TN = 512
TILES = N // TN
SPT = TN // T
PAD = 2
EPS = 1e-5
ROUND = 12582912.0

NORMS = {f"n{j}": j for j in range(13)}
WITH_BIAS = ["n1", "n2", "n7", "n10", "n11"]
NORM_COUNT = {"mean": TILES, "var": TILES, "std": TILES, "rstd": TILES, "centred": 2 * TILES, "squared": 2 * TILES,
              "scaled": 2 * TILES, "done": 2 * TILES}

VECS = ["bq", "bk", "bo", "g1", "b1", "g2", "b2", "bf2", "D", "mu_r", "mu_k", "bgk2", "gamma", "beta",
        "ln1_g", "ln1_b", "ln2_g", "ln2_b", "decay", "first", "mix_k", "mix_v", "mix_r", "cm_k", "cm_r"]
VCOL = {n: 2 * i for i, n in enumerate(VECS)}
NV = 2 * len(VECS)
BF1 = NV
NVEC = NV + 8


PRIMED = [
    "att+kv_turned+y_turned+ranks+rows_turned+slots_turned+out_tu", "att_out+softplus2+exps+cm_sig+rows_copied",
    "cos_done+moe_h+summed+gate_sums+x_clip+pp", "emb_copied+qk_copied+moe_silu+before+qkv_read+xq_copied+befo",
    "emb_proj+qk_ready+moe_in+fourier_in+qkv_ready+x_turned+mix_r",
    "emb_turned+swapped+moe_down+ssm_out+gate_ready+xq_turned+wkv", "exp_done+rk_read+gate_read+h_gelu+kvr_read",
    "factors", "ff1+g_ready", "ff2+l2a_ready", "ff_read+l2a_read+hid_127+ffv_read+l3f_done", "g_read",
    "gelu_done+softplus3+before4+gelu3", "h0_done", "h_quantised+l3a_done+o_copied", "h_shifted+x3_done+hact",
    "kv_copied", "l0a_done", "mask_ready+keys_spread+state+hid_clip+ratio", "max_scaled+mixed+to_end+x_shifted+sums",
    "moe_own_in+ssm_read+gate_to_mid+x_scale+p_max", "norm_centred", "norm_done", "norm_mean", "norm_rstd",
    "norm_scaled", "norm_squared", "norm_std", "norm_var", "o_out0", "o_out1", "probs+v_spread+hid_max+den_inv",
    "probs_copied+softplus1+hq_copied+ffk_relu+slots_copied",
    "probs_turned+v_ready+gla_att+hq_turned+ffk_ready+gu_ready", "rotated+moe_own+turned_out+to_mid+x_inv+pp_prev",
    "row_inv+l1f_done+gla_masked+h_scaled+den", "row_max+moe_out+l1a_done+clamped+x_127+exp_args",
    "row_sum+v_read+decayed+x_quantised+num", "scores+rk_ready+gla_scores+h_ready+cm_ready",
    "seq_staged+sum_in+k_squared+keys_staged+tile_staged",
    "swap_used+moe_up+turned_in+log_gate+x_max+mixed3+ffk_squared", "values+v_turned+y_ready+ffv_ready+down_ready",
    "values_spread+gla_out+hid_inv+mixed4", "wo_done+gated+hid_scale+wkv+row_staged+second_in", "wo_ready+state_sum",
    "x3_added", "x_in0", "x_in1", "y_added", "y_scaled", "z_ready+q_spread+wkv_pool",
]

SHARED = [
    [("emb_proj", 8), ("qk_ready", 12), ("moe_in", 64), ("fourier_in", 8), ("qkv_ready", 28), ("x_turned", 16), ("mix_ready", 24)],
    [("emb_turned", 4), ("swapped", 12), ("moe_down", 64), ("ssm_out", 8), ("gate_ready", 8), ("xq_turned", 16), ("wkv_out", 8)],
    [("scores", 32), ("rk_ready", 16), ("gla_scores", 32), ("h_ready", 16), ("cm_ready", 8)],
    [("probs_turned", 64), ("v_ready", 8), ("gla_att", 32), ("hq_turned", 16), ("ffk_ready", 32), ("gu_ready", 192)],
    [("values", 8), ("v_turned", 8), ("y_ready", 16), ("ffv_ready", 8), ("down_ready", 24)],
    [("att", 32), ("kv_turned", 8), ("y_turned", 16), ("ranks", 1), ("rows_turned", 8), ("slots_turned", 24), ("out_turned", 8)],
    [("wo_ready", 8), ("state_sum", 8)],
    [("ff1", 32), ("g_ready", 8)],
    [("ff2", 8), ("l2a_ready", 8)],
    [("emb_copied", 4), ("qk_copied", 12), ("moe_silu", 64), ("before", 16), ("qkv_read", 28), ("xq_copied", 16), ("before3", 24)],
    [("exp_done", 32), ("rk_read", 16), ("gate_read", 8), ("h_gelu", 16), ("kvr_read", 24)],
    [("probs_copied", 64), ("softplus1", 8), ("hq_copied", 16), ("ffk_relu", 32), ("slots_copied", 24)],
    [("att_out", 32), ("softplus2", 8), ("exps", 32), ("cm_sig", 8), ("rows_copied", 8)],
    [("gelu_done", 32), ("softplus3", 8), ("before4", 16), ("gelu3", 192)],
    [("factors", 24)], [("kv_copied", 8)], [("g_read", 8)],
    [("swap_used", 12), ("moe_up", 60), ("turned_in", 16), ("log_gate", 8), ("x_max", 16), ("mixed3", 24), ("ffk_squared", 32)],
    [("cos_done", 12), ("moe_h", 64), ("summed", 8), ("gate_sums", 8), ("x_clip", 16), ("pp", 8)],
    [("rotated", 12), ("moe_own", 8), ("turned_out", 16), ("to_mid", 8), ("x_inv", 16), ("pp_prev", 8)],
    [("moe_own_in", 8), ("ssm_read", 8), ("gate_to_mid", 8), ("x_scale", 16), ("p_max", 8)],
    [("row_max", 32), ("moe_out", 8), ("l1a_done", 8), ("clamped", 8), ("x_127", 16), ("exp_args", 32)],
    [("max_scaled", 32), ("mixed", 16), ("to_end", 8), ("x_shifted", 16), ("sums", 16)],
    [("row_sum", 32), ("v_read", 8), ("decayed", 16), ("x_quantised", 16), ("num", 8)],
    [("row_inv", 32), ("l1f_done", 8), ("gla_masked", 32), ("h_scaled", 16), ("den", 8)],
    [("probs", 32), ("v_spread", 8), ("hid_max", 16), ("den_inv", 8)],
    [("mask_ready", 1), ("keys_spread", 8), ("state", 8), ("hid_clip", 16), ("ratio", 8)],
    [("values_spread", 16), ("gla_out", 32), ("hid_inv", 16), ("mixed4", 16)],
    [("wo_done", 8), ("gated", 8), ("hid_scale", 16), ("wkv", 8), ("row_staged", 24), ("second_in", 16)],
    [("ff_read", 8), ("l2a_read", 8), ("hid_127", 16), ("ffv_read", 8), ("l3f_done", 16)],
    [("h_shifted", 16), ("x3_done", 8), ("hact", 192)], [("h_quantised", 16), ("l3a_done", 8), ("o_copied", 24)],
    [("seq_staged", 16), ("sum_in", 8), ("k_squared", 8), ("keys_staged", 8), ("tile_staged", 4)],
    [("z_ready", 8), ("q_spread", 32), ("wkv_pool", 32)],
]
PLACE = {}
for _row in SHARED:
    _base = 0
    for _name, _count in _row:
        PLACE[_name] = ("+".join(n for n, _ in _row)[:60], _base)
        _base += _count


class Kernel:

    def __init__(self, nc, ctx, ins, out):
        self.nc, self.ctx, self.ins, self.out = nc, ctx, ins, out
        self.sems = {}
        self.unprimed = set()

    def sem(self, name):
        if name.split("_")[0] in NORMS:
            name = "norm_" + name.split("_")[1]
        name = PLACE.get(name, (name, 0))[0]
        if name not in self.sems:
            self.sems[name] = self.ctx.enter_context(self.nc.semaphore(name))
        return self.sems[name]

    def at(self, name, count, positive=False):
        norm, _, what = name.partition("_")
        if norm in NORMS:
            name = "norm_" + what
            count = count + NORM_COUNT[what] * (NORMS[norm] if what != "done" else WITH_BIAS.index(norm))
        name, before = PLACE.get(name, (name, 0))
        count = count + before
        if type(count) is not int and name not in PRIMED and not positive:
            self.unprimed.add(name)
        return self.sem(name), count + (1 if name in PRIMED else 0)

    def sb(self, name, cols, dt=F32, parts=P):
        return self.ctx.enter_context(self.nc.sbuf_tensor(name, [parts, cols], dt))


def seqs(buf):
    return buf[:, 0:NH * N].rearrange("p (h s t) -> p h s t", h=NH, s=B)


def tile(view, h, t):
    return view[:, h, bass.ds(t * SPT, SPT), :]


def blocks(ap, k):
    return ap.rearrange("p (k m) -> p k m", k=k)


def allocate(k):
    nc = k.nc
    k.H = seqs(k.sb("residual", NH * N))
    k.Ybuf = k.sb("normed", NH * B * (T + PAD))
    k.Y = k.Ybuf[:, :].rearrange("p (h s t) -> p h s t", h=NH, s=B)
    for n in "ABCDEQ":
        k.raw = k.sb("buf" + n, NH * N)
        if n == "A": k.A = k.raw
        if n == "B": k.B = k.raw
        if n == "C": k.C = k.raw
        if n == "D": k.D = k.raw
        if n == "E": k.E = k.raw
        if n == "Q": k.Q = k.raw
    k.R = k.sb("rstd", 2 * TN)
    k.W = k.sb("weights0", 9344)
    k.V = k.sb("weights1", 5504)
    k.ident = k.sb("ident", P)
    k.identb = k.sb("identb", P, BF16)
    k.mean_w = k.sb("mean_w", P)
    k.vec = k.sb("vec", NVEC)
    k.vec2 = k.sb("vec2", 24)
    k.rope = k.sb("rope", 2 * T)
    k.attc = k.sb("attc", 4 * P + 4 + 8 + 16 + 27)
    k.perm = k.attc[:, 0:P]
    k.band = k.attc[:, P:3 * P].rearrange("p (m k) -> p m k", m=2)
    k.causal = k.attc[:, 3 * P:4 * P]
    k.groupmask = k.attc[:, 4 * P:4 * P + 4]
    k.headmask = k.attc[:, 4 * P + 4:4 * P + 12]
    k.small = k.sb("small", 1024)
    k.PS = k.ctx.enter_context(nc.psum_tensor("banks", [P, 8, 512], F32))
    k.eps = k.small[:, 1023:1024]


def yt(k, h, t, shift=0):
    return k.Y[:, h, bass.ds(t * SPT, SPT), PAD - shift:PAD - shift + T]


def bank(k, b):
    return k.PS[:, b, :]


def bank_seq(k, b):
    return k.PS[:, b, :].rearrange("p (s t) -> p s t", s=SPT)


def rstd(k, p):
    return k.R[:, p * TN:(p + 1) * TN].rearrange("p (s t) -> p s t", s=SPT)


def vcol(k, name, h=0):
    return k.vec[:, VCOL[name] + h:VCOL[name] + h + 1]



def norm_pe(k, pe, n, src, ready, per_tile, free=()):
    for s, v in free:
        pe.wait_ge(*k.at(s, v))
    with pe.Fori(0, TILES // 2) as i:
        for par in range(2):
            t = 2 * i + par
            pe.wait_ge(*k.at(ready, per_tile * (t + 1)))
            pe.wait_ge(*k.at(n + "_centred", 4 * i))
            for h in range(NH):
                mm = pe.matmul(bank(k, par), k.mean_w[:, :], tile(src, h, t), start=h == 0, stop=h == 1)
            mm.then_inc(k.sem(n + "_mean"), 1)
    with pe.Fori(0, TILES // 2) as i:
        for par in range(2):
            t = 2 * i + par
            pe.wait_ge(*k.at(n + "_squared", 2 * (t + 1)))
            pe.wait_ge(*k.at(n + "_std", 2 * i))
            for h in range(NH):
                mm = pe.matmul(bank(k, 2 + par), k.mean_w[:, :], tile(seqs(k.Q), h, t), start=h == 0, stop=h == 1)
            mm.then_inc(k.sem(n + "_var"), 1)


def norm_act(k, act, n, bias=None, dst=None, free=()):
    for s, v in free:
        act.wait_ge(*k.at(s, v))
    with act.Fori(0, TILES) as t:
        for h in range(NH):
            act.wait_ge(*k.at(n + "_centred", 2 * t + h + 1))
            act.activation(tile(seqs(k.Q), h, t), tile(seqs(k.D), h, t), ACT.Square).then_inc(k.sem(n + "_squared"), 1)
    with act.Fori(0, TILES // 2) as i:
        for par in range(2):
            t = 2 * i + par
            act.wait_ge(*k.at(n + "_var", t + 1))
            act.wait_ge(*k.at(n + "_scaled", 4 * i))
            act.activation(k.R[:, par * TN:(par + 1) * TN], bank(k, 2 + par), ACT.Sqrt, bias=k.eps).then_inc(k.sem(n + "_std"), 1)
    if bias is not None:
        with act.Fori(0, TILES) as t:
            for h in range(NH):
                act.wait_ge(*k.at(n + "_scaled", 2 * t + h + 1))
                act.activation(dst(h, t), tile(seqs(k.D), h, t), ACT.Identity, bias=vcol(k, bias, h)).then_inc(k.sem(n + "_done"), 1)


def norm_dve(k, dve, n, src, gain=None, dst=None, free=()):
    for s, v in free:
        dve.wait_ge(*k.at(s, v))
    with dve.Fori(0, TILES // 2) as i:
        for par in range(2):
            t = 2 * i + par
            dve.wait_ge(*k.at(n + "_mean", t + 1))
            for h in range(NH):
                dve.tensor_tensor(tile(seqs(k.D), h, t), tile(src, h, t), bank_seq(k, par), ALU.subtract).then_inc(k.sem(n + "_centred"), 1)
    with dve.Fori(0, TILES // 2) as i:
        for par in range(2):
            t = 2 * i + par
            dve.wait_ge(*k.at(n + "_std", t + 1))
            dve.reciprocal(k.R[:, par * TN:(par + 1) * TN], k.R[:, par * TN:(par + 1) * TN]).then_inc(k.sem(n + "_rstd"), 1)
            dve.wait_ge(*k.at(n + "_rstd", t + 1))
            for h in range(NH):
                dve.wait_ge(*k.at(n + "_squared", 2 * t + h + 1))
                if gain is None:
                    dve.tensor_tensor(dst(h, t), tile(seqs(k.D), h, t), rstd(k, par), ALU.mult).then_inc(k.sem(n + "_scaled"), 1)
                else:
                    dve.scalar_tensor_tensor(tile(seqs(k.D), h, t), tile(seqs(k.D), h, t), vcol(k, gain, h), rstd(k, par), ALU.mult, ALU.mult).then_inc(k.sem(n + "_scaled"), 1)



def load_constants(k, sp):
    i = k.ins
    for dst, name in ((k.ident, "c_ident"), (k.mean_w, "c_mean"), (k.vec, "vecs"), (k.rope, "c_rope"), (k.attc, "c_att")):
        sp.dma_start(dst[:, :], i[name]).then_inc(k.sem("constants"), 16)
    sp.dma_start(k.identb[:, :], i["c_identb"]).then_inc(k.sem("constants"), 16)


CONST = 6 * 16


def load(k, sp, dst, src, sem):
    sp.dma_start(dst, src).then_inc(k.sem(sem), 16)



def hash_views(k):
    s = k.small[:, :].bitcast(I32)
    return [s[:, 16 * j:16 * j + 16] for j in range(20)]


def tok_load(k, sp):
    i = k.ins
    v = hash_views(k)
    sp.dma_start(v[0], i["tok"]).then_inc(k.sem("tok_in"), 16)
    sp.dma_start(v[1], i["tok_prev"]).then_inc(k.sem("tok_in"), 16)
    sp.dma_start(k.small[:, 320:336], i["c_first"]).then_inc(k.sem("tok_in"), 16)
    sp.dma_start(k.small[:, 336:337], i["scale"].to_broadcast([P, 1])).then_inc(k.sem("tok_in"), 16)
    sp.dma_start(k.W[0:64, 0:256], i["projT"]).then_inc(k.sem("tok_in"), 16)


def tok_dve(k, dve):
    v = hash_views(k)
    f = k.small
    done = [0]

    def chain(ins):
        done[0] += 1
        ins.then_inc(k.sem("hash_step"), 1)
        dve.wait_ge(*k.at("hash_step", done[0]))
    dve.memset(k.eps, EPS).then_inc(k.sem("eps_set"), 1)
    dve.memset(k.Y[:, :, :, 0:PAD], 0.0).then_inc(k.sem("pad_set"), 1)
    dve.wait_ge(*k.at("constants", CONST))
    for j, name in enumerate(["mu_r", "mu_k", "mix_k", "mix_v", "mix_r", "cm_k", "cm_r"]):
        dve.tensor_scalar(k.vec2[:, 2 * j:2 * j + 2], k.vec[:, VCOL[name]:VCOL[name] + 2], -1.0, 1.0, ALU.mult, ALU.add).then_inc(k.sem("rest_ready"), 1)
    dve.wait_ge(*k.at("tok_in", 80))
    limbs = []
    for src, mul, o in ((0, 36313, 2), (1, 27191, 9)):
        lo, hi, p0, p1, mid, a, b = v[o:o + 7]
        chain(dve.tensor_scalar(lo, v[src], 255, None, ALU.bitwise_and))
        chain(dve.tensor_scalar(hi, v[src], 8, None, ALU.logical_shift_right))
        chain(dve.tensor_scalar(p0, lo, float(mul), None, ALU.mult))
        chain(dve.tensor_scalar(p1, hi, float(mul), None, ALU.mult))
        chain(dve.tensor_scalar(mid, p1, 255, 8, ALU.bitwise_and, ALU.logical_shift_left))
        chain(dve.tensor_tensor(p0, p0, mid, ALU.add))
        chain(dve.tensor_scalar(a, p0, 65535, None, ALU.bitwise_and))
        chain(dve.tensor_scalar(b, p0, 16, None, ALU.logical_shift_right))
        chain(dve.tensor_scalar(p1, p1, 8, None, ALU.logical_shift_right))
        chain(dve.tensor_tensor(b, b, p1, ALU.add))
        limbs.append((a, b))
    (a0, b0), (a1, b1) = limbs
    chain(dve.tensor_tensor(a0, a0, a1, ALU.bitwise_xor))
    chain(dve.tensor_tensor(b0, b0, b1, ALU.bitwise_xor))
    sm, neg, big = f[:, 352:368], f[:, 368:384], f[:, 384:400]
    chain(dve.tensor_tensor(sm, a0, b0, ALU.add))
    chain(dve.tensor_scalar(neg, b0, 32768.0, None, ALU.is_ge))
    chain(dve.tensor_tensor(sm, sm, neg, ALU.subtract))
    chain(dve.tensor_scalar(big, sm, 65535.0, -65535.0, ALU.is_ge, ALU.mult))
    chain(dve.tensor_tensor(sm, sm, big, ALU.add))
    first = f[:, 320:336]
    chain(dve.scalar_tensor_tensor(neg, sm, -65535.0, first, ALU.add, ALU.mult))
    chain(dve.tensor_tensor(sm, sm, neg, ALU.subtract))
    dve.tensor_copy(f[:, 400:416].bitcast(U32), sm).then_inc(k.sem("rows_known"), 1)


def tok_pool(k, pool):
    pool.wait_ge(*k.at("rows_known", 1))
    idx = k.small[:, 400:416].bitcast(U32)
    for j in range(N // P):
        pool.indirect_dma_start(k.B[:, 64 * j:64 * j + 64], None, k.ins["embed"],
                                bass.IndirectOffsetOnAxis(ap=idx[:, j:j + 1], axis=0)).then_inc(k.sem("gathered"), 16)


def tok_pe(k, pe):
    pe.wait_ge(*k.at("constants", CONST))
    pe.wait_ge(*k.at("gathered", 16 * (N // P)))
    for t in range(TILES):
        if t >= 2:
            pe.wait_ge(*k.at("emb_copied", t - 1))
        for j in range(TN // P):
            mm = pe.transpose(k.PS[0:64, t % 2, j * P:(j + 1) * P], k.B[:, 64 * (4 * t + j):64 * (4 * t + j) + 64], k.ident[:, :])
        mm.then_inc(k.sem("emb_turned"), 1)
    pe.wait_ge(*k.at("tok_in", 80))
    for t in range(TILES):
        pe.wait_ge(*k.at("emb_copied", t + 1))
        if t >= 2:
            pe.wait_ge(*k.at("h0_done", 2 * (t - 1)))
        for m in range(NH):
            pe.matmul(bank(k, 2 + 2 * (t % 2) + m), k.W[0:64, m * P:(m + 1) * P],
                      k.A[0:64, t * TN:(t + 1) * TN], start=True, stop=True).then_inc(k.sem("emb_proj"), 1)


def tok_act(k, act):
    act.wait_ge(*k.at("tok_in", 80))
    for t in range(TILES):
        act.wait_ge(*k.at("emb_turned", t + 1))
        act.activation(k.A[0:64, t * TN:(t + 1) * TN], k.PS[0:64, t % 2, :], ACT.Copy).then_inc(k.sem("emb_copied"), 1)
    for t in range(TILES):
        for m in range(NH):
            act.wait_ge(*k.at("emb_proj", 2 * t + m + 1))
            act.activation(tile(k.H, m, t), bank_seq(k, 2 + 2 * (t % 2) + m), ACT.Copy, scale=k.small[:, 336:337]).then_inc(k.sem("h0_done"), 1)



QB = T // 64
WINDOW0 = [max(0, 64 * q - 64) for q in range(QB)]
L0 = {"wq": 0, "wk": 512, "wv": 768, "wo": 896, "wf1": 1408, "wf2": 3456}


def l0a_w(k, name, cols, nk=NH):
    return blocks(k.V[:, L0[name]:L0[name] + nk * cols], nk)


def l0a_load(k, sp):
    sp.dma_start(k.V[:, 0:5504], k.ins["l0a_w"]).then_inc(k.sem("l0a_weights"), 16)
    sp.dma_start(k.small[:, 448:512], k.ins["bv"].to_broadcast([P, 64])).then_inc(k.sem("l0a_weights"), 16)


def att_views(k):
    a = {}
    a["qs"] = k.E[:, 2048:2560]
    a["ys"] = k.E[:, 2560:3072].rearrange("p (h t) -> p h t", h=2)
    a["sm"] = [k.E[:, 3072:4096].rearrange("p (a k) -> p a k", a=8), k.C[:, 3072:4096].rearrange("p (a k) -> p a k", a=8)]
    a["pt"] = [k.E[:, 0:1024].rearrange("p (a k) -> p a k", a=8), k.E[:, 1024:2048].rearrange("p (a k) -> p a k", a=8)]
    a["kz"] = k.C[:, 2048:3072].rearrange("p (g t) -> p g t", g=4)
    a["k"] = k.C[:, 0:2048].rearrange("p (s t) -> p s t", s=B)
    a["vz"] = k.Q[:, :].rearrange("p (w a m) -> p w a m", w=4, a=8)
    a["mask"] = k.R[:, 0:P].bitcast(BF16).rearrange("p (m k) -> p m k", m=2)
    a["mx"] = k.small[:, 512:528]
    a["sum"] = k.small[:, 528:544]
    return a


QKB = [(0, 1, 4), (5, 6, 7)]


def l0a_pe(k, pe):
    a = att_views(k)
    norm_pe(k, pe, "n0", k.H, "h0_done", 2, free=(("h0_done", 2 * TILES),))
    norm_pe(k, pe, "n1", seqs(k.A), "n0_scaled", 2)
    pe.wait_ge(*k.at("l0a_weights", 32))
    wq, wk = l0a_w(k, "wq", D), l0a_w(k, "wk", P)
    with pe.Fori(0, TILES // 2) as i:
        for par in range(2):
            t = 2 * i + par
            pe.wait_ge(*k.at("n1_done", 2 * (t + 1)))
            pe.wait_ge(*k.at("qk_copied", 6 * i))
            for o in range(3):
                for h in range(NH):
                    w = wk[:, h, :] if o == 2 else wq[:, h, o * P:(o + 1) * P]
                    mm = pe.matmul(bank(k, QKB[par][o]), w, yt(k, h, t), start=h == 0, stop=h == 1)
                mm.then_inc(k.sem("qk_ready"), 1)
    with pe.Fori(0, TILES // 2) as i:
        for m in range(6):
            t = 2 * i + m // 3
            pe.wait_ge(*k.at("qk_copied", 6 * i + m + 1))
            pe.wait_ge(*k.at("swap_used", 6 * i + max(m - 1, 0)))
            src = a["k"][:, bass.ds(t * SPT, SPT), :] if m % 3 == 2 else tile(seqs(k.B), m % 3, t)
            pe.matmul(bank(k, 2 + m % 2), k.perm, src, start=True, stop=True).then_inc(k.sem("swapped"), 1)

    wv = l0a_w(k, "wv", 64)

    def scores(b, q, n):
        if q == 0:
            pe.wait_ge(*k.at("keys_spread", b + 1))
            pe.wait_ge(*k.at("seq_staged", 2 * b + 1))
        if type(n) is not int or n >= 2:
            pe.wait_ge(*k.at("exp_done", n - 1, positive=True))
        for j2 in range(2):
            out = bank(k, 1 + 2 * (q % 2) + j2)
            pe.matmul(out, k.identb[:, :], a["mask"][:, min(q, 1), :].unsqueeze(1).to_broadcast([P, 4, P]), start=True, stop=False)
            mm = pe.matmul(out, a["qs"][64 * j2:64 * j2 + 64, P * q:P * q + P],
                           a["kz"][64 * j2:64 * j2 + 64, :, WINDOW0[q]:WINDOW0[q] + P], start=False, stop=True)
        mm.then_inc(k.sem("scores"), 1)

    def turn_probs(b, q):
        pe.wait_ge(*k.at("probs", 4 * b + q + 1))
        for half in range(2):
            pe.wait_ge(*k.at("probs_copied", 8 * b + max(2 * q + half - 1, 0)))
            for x in range(4):
                mm = pe.transpose(k.PS[:, 5 + half, x * P:(x + 1) * P], a["sm"][q % 2][:, 4 * half + x, :], k.ident[:, :])
            mm.then_inc(k.sem("probs_turned"), 1)

    def attend(b, q):
        if q == 0:
            pe.wait_ge(*k.at("values_spread", 2 * b + 2))
        pe.wait_ge(*k.at("probs_copied", 8 * b + 2 * q + 2))
        pe.wait_ge(*k.at("att_out", 4 * b + q))
        for x in range(8):
            mm = pe.matmul(k.PS[:, 7, 0:P], a["vz"][:, q, x, :], a["pt"][q % 2][:, x, :], start=x == 0, stop=x == 7)
        mm.then_inc(k.sem("att"), 1)

    def values(b):
        pe.wait_ge(*k.at("seq_staged", 2 * b + 2))
        pe.wait_ge(*k.at("values_spread", 2 * b))
        for w in range(4):
            for h in range(NH):
                mm = pe.matmul(k.PS[:, 0, 64 * w:64 * w + 64], a["ys"][:, h, WINDOW0[w]:WINDOW0[w] + P], wv[:, h, :],
                               start=h == 0, stop=h == 1)
        mm.then_inc(k.sem("values"), 1)

    def sequence(b, last):
        for q in range(QB):
            if not last or q < 2:
                scores(b + (q + 2) // QB, (q + 2) % QB, 4 * b + q + 2)
            turn_probs(b, q)
            if q:
                attend(b, q - 1)
        if not last:
            values(b + 1)
        attend(b, QB - 1)

    pe.wait_ge(*k.at("mask_ready", 1))
    scores(0, 0, 0)
    scores(0, 1, 1)
    values(0)
    with pe.Fori(0, B - 1) as b:
        sequence(b, False)
    sequence(B - 1, True)

    wo = l0a_w(k, "wo", D)
    pe.wait_ge(*k.at("att_out", 4 * B))
    with pe.Fori(0, TILES // 2) as i:
        for par in range(2):
            t = 2 * i + par
            pe.wait_ge(*k.at("wo_done", 4 * i))
            for m in range(NH):
                for j in range(2):
                    mm = pe.matmul(bank(k, 4 + 2 * par + m), wo[:, j, m * P:(m + 1) * P], tile(seqs(k.D), j, t), start=j == 0, stop=j == 1)
                mm.then_inc(k.sem("wo_ready"), 1)
    norm_pe(k, pe, "n2", seqs(k.A), "wo_done", 2)
    wf1, wf2 = l0a_w(k, "wf1", 1024), l0a_w(k, "wf2", D, 8)
    with pe.Fori(0, TILES // 2) as i:
        for par in range(2):
            t = 2 * i + par
            pe.wait_ge(*k.at("n2_done", 2 * (t + 1)))
            for m in range(8):
                pe.wait_ge(*k.at("gelu_done", 16 * i + max(8 * par + m - 3, 0)))
                for h in range(NH):
                    mm = pe.matmul(bank(k, 4 + m % 4), wf1[:, h, m * P:(m + 1) * P], yt(k, h, t), start=h == 0, stop=h == 1)
                mm.then_inc(k.sem("ff1"), 1)
        for par in range(2):
            f = (k.B, k.C)[par][:, :].rearrange("p (m n) -> p m n", m=8)
            pe.wait_ge(*k.at("gelu_done", 16 * i + 8 * (par + 1)))
            pe.wait_ge(*k.at("ff_read", 4 * i))
            for m in range(NH):
                for x in range(8):
                    mm = pe.matmul(bank(k, 2 * par + m), wf2[:, x, m * P:(m + 1) * P], f[:, x, :], start=x == 0, stop=x == 7)
                mm.then_inc(k.sem("ff2"), 1)


def l0a_act(k, act):
    a = att_views(k)
    act.wait_ge(*k.at("constants", CONST))
    act.wait_ge(*k.at("eps_set", 1))
    norm_act(k, act, "n0")
    norm_act(k, act, "n1", "b1", lambda h, t: yt(k, h, t))
    with act.Fori(0, TILES // 2) as i:
        for par in range(2):
            t = 2 * i + par
            for o in range(3):
                act.wait_ge(*k.at("qk_ready", 6 * i + 3 * par + o + 1))
                dst = a["k"][:, bass.ds(t * SPT, SPT), :] if o == 2 else tile(seqs(k.B), o, t)
                bias = vcol(k, "bk") if o == 2 else vcol(k, "bq", o)
                act.activation(dst, bank_seq(k, QKB[par][o]), ACT.Identity, bias=bias).then_inc(k.sem("qk_copied"), 1)

    def exps(q, n):
        act.wait_ge(*k.at("max_scaled", n + 1))
        if type(n) is not int or n >= 2:
            act.wait_ge(*k.at("probs_turned", 2 * n - 2, positive=True))
        for x in range(8):
            ex = act.activation(a["sm"][q % 2][:, x, :], k.PS[:, 1 + 2 * (q % 2) + x // 4, x % 4 * P:x % 4 * P + P], ACT.Exp,
                                bias=a["mx"][:, 8 * (q % 2) + x:8 * (q % 2) + x + 1], scale=0.25)
        ex.then_inc(k.sem("exp_done"), 1)

    def copies(b, q):
        act.wait_ge(*k.at("att", 4 * b + max(q - 1, 0)))
        for half in range(2):
            act.wait_ge(*k.at("probs_turned", 8 * b + 2 * q + half + 1))
            act.activation(a["pt"][q % 2][:, 4 * half:4 * half + 4, :], bank(k, 5 + half).rearrange("p (x k) -> p x k", x=4), ACT.Copy).then_inc(k.sem("probs_copied"), 1)

    def output(b, q):
        act.wait_ge(*k.at("att", 4 * b + q + 1))
        act.activation(seqs(k.D)[:, :, b, 64 * q:64 * q + 64] if type(b) is int else seqs(k.D)[:, :, bass.ds(b, 1), 64 * q:64 * q + 64].rearrange("p j b q -> p j (b q)"),
                       k.PS[:, 7, 0:P].rearrange("p (j q) -> p j q", j=2), ACT.Copy).then_inc(k.sem("att_out"), 1)

    def sequence(b, last):
        for q in range(QB):
            if not last or q < 2:
                exps(q, 4 * b + q + 2)
            copies(b, q)
            if q:
                output(b, q - 1)
        output(b, QB - 1)

    exps(0, 0)
    exps(1, 1)
    with act.Fori(0, B - 1) as b:
        sequence(b, False)
    sequence(B - 1, True)
    norm_act(k, act, "n2", "b2", lambda h, t: yt(k, h, t))
    with act.Fori(0, TILES // 2) as i:
        for par in range(2):
            f = (k.B, k.C)[par][:, :].rearrange("p (m n) -> p m n", m=8)
            act.wait_ge(*k.at("ff2", 4 * i))
            for m in range(8):
                act.wait_ge(*k.at("ff1", 16 * i + 8 * par + m + 1))
                act.activation(f[:, m, :], bank(k, 4 + m % 4), ACT.Gelu, bias=k.vec[:, BF1 + m:BF1 + m + 1]).then_inc(k.sem("gelu_done"), 1)


def l0a_pool(k, pool):
    a = att_views(k)
    pool.wait_ge(*k.at("n1_var", TILES))
    pool.memset(k.Q[:, :], 0.0).then_inc(k.sem("vz_zero"), 1)
    with pool.Fori(0, B) as b:
        pool.wait_ge(*k.at("rotated", 3 * TILES))
        pool.wait_ge(*k.at("scores", 4 * b))
        pool.tensor_copy(a["qs"].rearrange("p (q j t) -> p j q t", q=QB, j=2),
                         seqs(k.B)[:, :, b, :].rearrange("p j (q t) -> p j q t", q=QB)).then_inc(k.sem("seq_staged"), 1)
        pool.wait_ge(*k.at("values", b))
        pool.tensor_copy(a["ys"], k.Y[:, :, b, PAD:PAD + T]).then_inc(k.sem("seq_staged"), 1)


def l0a_dve(k, dve):
    a = att_views(k)
    cos = k.rope[:, 0:T].unsqueeze(1).to_broadcast([P, SPT, T])
    sin = k.rope[:, T:2 * T].unsqueeze(1).to_broadcast([P, SPT, T])
    norm_dve(k, dve, "n0", k.H, dst=lambda h, t: tile(seqs(k.A), h, t))
    norm_dve(k, dve, "n1", seqs(k.A), gain="g1")
    tmp = k.E[:, 0:1024].rearrange("p (m s t) -> p m s t", m=2, s=SPT)
    with dve.Fori(0, TILES // 2) as i:
        for m in range(6):
            t = 2 * i + m // 3
            x = a["k"][:, bass.ds(t * SPT, SPT), :] if m % 3 == 2 else tile(seqs(k.B), m % 3, t)
            dve.wait_ge(*k.at("swapped", 6 * i + m + 1))
            dve.tensor_tensor(tmp[:, m % 2], bank_seq(k, 2 + m % 2), sin, ALU.mult).then_inc(k.sem("swap_used"), 1)
            dve.tensor_tensor(x, x, cos, ALU.mult).then_inc(k.sem("cos_done"), 1)
            dve.wait_ge(*k.at("swap_used", 6 * i + m + 1))
            dve.wait_ge(*k.at("cos_done", 6 * i + m + 1))
            dve.tensor_tensor(x, x, tmp[:, m % 2], ALU.add).then_inc(k.sem("rotated"), 1)
    dve.tensor_copy(a["mask"], k.band).then_inc(k.sem("mask_ready"), 1)
    bv = k.small[:, 448:512].rearrange("p (g d) -> p g d", g=4).unsqueeze(1).to_broadcast([P, 4, 4, 16])
    dve.wait_ge(*k.at("l0a_weights", 32))
    dve.wait_ge(*k.at("vz_zero", 1))

    def largest(q, n):
        mx = a["mx"][:, 8 * (q % 2):8 * (q % 2) + 8]
        dve.wait_ge(*k.at("scores", n + 1))
        src = k.PS[:, 1 + 2 * (q % 2):3 + 2 * (q % 2), :].rearrange("p b (g k) -> p (b g) k", g=4)
        dve.tensor_reduce(mx, src, AX.X, ALU.max).then_inc(k.sem("row_max"), 1)
        dve.wait_ge(*k.at("row_max", n + 1))
        dve.tensor_scalar(mx, mx, -0.25, None, ALU.mult).then_inc(k.sem("max_scaled"), 1)

    def normalise(q, n):
        sm = a["sm"][q % 2]
        s = a["sum"][:, 8 * (q % 2):8 * (q % 2) + 8]
        dve.wait_ge(*k.at("exp_done", n + 1))
        dve.tensor_reduce(s, sm, AX.X, ALU.add).then_inc(k.sem("row_sum"), 1)
        dve.wait_ge(*k.at("row_sum", n + 1))
        dve.reciprocal(s, s).then_inc(k.sem("row_inv"), 1)
        dve.wait_ge(*k.at("row_inv", n + 1))
        dve.tensor_tensor(sm, sm, s.unsqueeze(2).to_broadcast([P, 8, P]), ALU.mult).then_inc(k.sem("probs"), 1)

    def spread_keys(b):
        key = a["k"][:, b, :].unsqueeze(1) if type(b) is int else a["k"][:, bass.ds(b, 1), :]
        if type(b) is not int:
            dve.wait_ge(*k.at("scores", 4 * b, positive=True))
        dve.tensor_tensor(a["kz"], key.to_broadcast([P, 4, T]),
                          k.groupmask.unsqueeze(2).to_broadcast([P, 4, T]), ALU.mult).then_inc(k.sem("keys_spread"), 1)

    def spread_values(b):
        dve.wait_ge(*k.at("values", b + 1))
        dve.wait_ge(*k.at("att", 4 * b))
        for j2 in range(2):
            base = k.Q[:, 4 * j2 * 144:4 * j2 * 144 + 16]
            dst = bass.AP(tensor=base.tensor, offset=base.offset, ap=[base.ap[0], [1024, 4], [144, 4], [1, 16]])
            src = k.PS[:, 0, 0:256].rearrange("p (w g d) -> p w g d", w=4, g=4)
            dve.tensor_tensor(dst, src, bv, ALU.add).then_inc(k.sem("values_spread"), 1)

    def sequence(b, last):
        for q in range(QB):
            n = 4 * b + q
            if not last or q < 2:
                largest(q, n + 2)
            if not last or q < 3:
                normalise((q + 1) % QB, n + 1)
            if q == 0:
                spread_values(b)
            if q == 1 and not last:
                spread_keys(b + 1)

    spread_keys(0)
    largest(0, 0)
    largest(1, 1)
    normalise(0, 0)
    with dve.Fori(0, B - 1) as b:
        sequence(b, False)
    sequence(B - 1, True)
    with dve.Fori(0, TILES // 2) as i:
        for par in range(2):
            t = 2 * i + par
            for m in range(NH):
                dve.wait_ge(*k.at("wo_ready", 2 * t + m + 1))
                x = tile(seqs(k.A), m, t)
                dve.scalar_tensor_tensor(x, bank_seq(k, 4 + 2 * par + m), vcol(k, "bo", m), x, ALU.add, ALU.add).then_inc(k.sem("wo_done"), 1)
    norm_dve(k, dve, "n2", seqs(k.A), gain="g2")
    with dve.Fori(0, TILES // 2) as i:
        for par in range(2):
            t = 2 * i + par
            for m in range(NH):
                dve.wait_ge(*k.at("ff2", 2 * t + m + 1))
                x = tile(seqs(k.A), m, t)
                dve.scalar_tensor_tensor(x, bank_seq(k, 2 * par + m), vcol(k, "bf2", m), x, ALU.add, ALU.add).then_inc(k.sem("ff_read"), 1)
                dve.wait_ge(*k.at("ff_read", 2 * t + m + 1))
                dve.tensor_tensor(tile(k.H, m, t), tile(k.H, m, t), x, ALU.add).then_inc(k.sem("l0a_done"), 1)



def logits_pe(k, pe, n, ready, w, E, b):
    for g in range(N // P):
        if g % 4 == 0:
            pe.wait_ge(*k.at(ready, 2 * (g // 4 + 1)))
        for h in range(NH):
            mm = pe.matmul(k.PS[:, b, E * g:E * g + E], k.Y[:, h, g // 2, PAD + g % 2 * P:PAD + g % 2 * P + P], w[:, h, :],
                           start=h == 0, stop=h == 1)
    mm.then_inc(k.sem(n + "_logits"), 1)


def route_dve(k, dve, n, E, b, norm_eps, bias, lo, sparse=False):
    G = N // P
    buf = [k.A[:, lo + 256 * j:lo + 256 * j + G * E].rearrange("p (g e) -> p g e", g=G) for j in range(4)]
    col = [k.A[:, lo + 1024 + 16 * j:lo + 1040 + 16 * j] for j in range(4)]
    wide = lambda c: c.unsqueeze(2).to_broadcast([P, G, E])
    rev = k.attc[:, 4 * P + 12:4 * P + 12 + E].unsqueeze(1).to_broadcast([P, G, E])
    x, y, one, w = buf
    c, m1, m2, s = col
    done = [0]

    def chain(ins):
        done[0] += 1
        ins.then_inc(k.sem(n + "_route"), 1)
        dve.wait_ge(*k.at(n + "_route", done[0]))

    logits = k.PS[:, b, 0:G * E].rearrange("p (g e) -> p g e", g=G)
    dve.wait_ge(*k.at(n + "_logits", 1))
    if bias is not None:
        chain(dve.tensor_tensor(x, logits, bias.unsqueeze(1).to_broadcast([P, G, E]), ALU.add))
    else:
        chain(dve.tensor_copy(x, logits))
    chain(dve.tensor_reduce(c, x, AX.X, ALU.max))
    chain(dve.tensor_tensor(x, x, wide(c), ALU.subtract))
    dve.sem_inc(k.sem(n + "_exp_in"), 1)
    dve.wait_ge(*k.at(n + "_exp", 1))
    chain(dve.tensor_reduce(s, x, AX.X, ALU.add))
    chain(dve.reciprocal(s, s))
    chain(dve.tensor_tensor(x, x, wide(s), ALU.mult))
    for step, m in ((0, m1), (1, m2)):
        pick = one if step == 0 else y
        chain(dve.tensor_reduce(m, x, AX.X, ALU.max))
        chain(dve.tensor_tensor(pick, x, wide(m), ALU.is_equal))
        chain(dve.tensor_tensor(pick, pick, rev, ALU.mult))
        chain(dve.tensor_reduce(c, pick, AX.X, ALU.max))
        chain(dve.tensor_tensor(pick, pick, wide(c), ALU.is_equal))
        if step == 0:
            chain(dve.scalar_tensor_tensor(x, pick, -2.0, x, ALU.mult, ALU.add))
    if sparse:
        chain(dve.tensor_tensor(w, one, y, ALU.add))
        dve.sem_inc(k.sem(n + "_chosen"), 1)
    chain(dve.tensor_tensor(s, m1, m2, ALU.add))
    if norm_eps:
        chain(dve.tensor_scalar(s, s, norm_eps, None, ALU.add))
    chain(dve.reciprocal(s, s))
    chain(dve.tensor_tensor(m1, m1, s, ALU.mult))
    chain(dve.tensor_tensor(m2, m2, s, ALU.mult))
    if sparse:
        return chain
    chain(dve.tensor_tensor(one, one, wide(m1), ALU.mult))
    chain(dve.tensor_tensor(y, y, wide(m2), ALU.mult))
    dve.tensor_tensor(w, one, y, ALU.add).then_inc(k.sem(n + "_combine"), 1)


def route_act(k, act, n, E, lo):
    x = k.A[:, lo:lo + N // P * E]
    act.wait_ge(*k.at(n + "_exp_in", 1))
    act.activation(x, x, ACT.Exp).then_inc(k.sem(n + "_exp"), 1)


def combine_act(k, act, n, E):
    for q in range(4):
        act.wait_ge(*k.at(n + "_cw_turned", q + 1))
        act.activation(k.A[0:E, 2048 + q * TN:2048 + (q + 1) * TN], k.PS[0:E, 4 + q, :], ACT.Copy).then_inc(k.sem(n + "_cw"), 1)


def combine_pe(k, pe, n, E, lo):
    pe.wait_ge(*k.at(n + "_combine", 1))
    w = k.A[:, lo + 768:lo + 768 + N // P * E]
    for g in range(N // P):
        mm = pe.transpose(k.PS[0:E, 4 + g // 4, (g % 4) * P:(g % 4 + 1) * P], w[:, E * g:E * g + E], k.ident[:, :])
        if g % 4 == 3:
            mm.then_inc(k.sem(n + "_cw_turned"), 1)


def spread_weight(k, pe, b, E, e, t):
    return pe.matmul(bank(k, b), k.ident[0:E, e:e + 1].to_broadcast([E, P]), k.A[0:E, bass.ds(t * TN + 2048, TN)], start=True, stop=True)



E0 = 16
W0 = {"up": 0, "down": 3840, "conv": 7680, "sup": 8448, "sdown": 8704, "router": 8960}


def l0f_inputs(ins, a):
    gate, up, down = a["L0_ffn_expert_gate_w"], a["L0_ffn_expert_up_w"], a["L0_ffn_expert_down_w"]
    ins["l0f_gate"] = np.concatenate([halves(gate[e]) for e in range(E0 - 1)], axis=1)
    conv = a["L0_ffn_conv_w"].transpose(2, 1, 0)
    ins["l0f_w"] = np.concatenate([halves(up[e]) for e in range(E0 - 1)] + [down[e] for e in range(E0 - 1)]
                                  + [halves(conv[j]) for j in range(3)]
                                  + [halves(a["L0_ffn_shared_up_w"]), a["L0_ffn_shared_down_w"], halves(a["L0_ffn_router_w"])], axis=1)
    ins["router_bias"] = a["L0_ffn_router_bias"].reshape(1, E0)


def l0f_load(k, sp):
    sp.wait_ge(*k.at("emb_proj", 8))
    sp.dma_start(k.W[:, 0:8992], k.ins["l0f_w"]).then_inc(k.sem("l0f_weights"), 16)
    sp.dma_start(k.small[:, 544:560], k.ins["router_bias"].to_broadcast([P, E0])).then_inc(k.sem("l0f_weights"), 16)
    sp.wait_ge(*k.at("att", 4 * B))
    sp.dma_start(k.E[:, 0:3840], k.ins["l0f_gate"]).then_inc(k.sem("l0f_weights"), 16)


def l0f_pe(k, pe):
    wt = lambda name, i, n: blocks(k.W[:, W0[name] + i * n:W0[name] + (i + 1) * n], n // P if name != "router" else 2)
    norm_pe(k, pe, "n3", k.H, "l0a_done", 2, free=(("ff_read", 2 * TILES),))
    pe.wait_ge(*k.at("l0f_weights", 48))
    logits_pe(k, pe, "l0f", "n3_scaled", blocks(k.W[:, 8960:8992], 2), E0, 1)
    combine_pe(k, pe, "l0f", E0, 0)
    l1_prep_pe(k, pe)
    pe.wait_ge(*k.at("folded_copied", 2))
    pe.wait_ge(*k.at("eigen", 1))
    pe.wait_ge(*k.at("l0f_cw", 4))
    with pe.Fori(0, TILES) as t:

        def first(x):
            p = 3 * (x % 2)
            pe.wait_ge(*k.at("moe_h", E0 * t + max(x - 1, 0)))
            if x < E0 - 1:
                g, u = blocks(k.E[:, 256 * x:256 * x + 256], 2), wt("up", x, 256)
                for h in range(NH):
                    pe.matmul(bank(k, p), g[:, h, :], yt(k, h, t), start=h == 0, stop=h == 1)
            else:
                u = wt("sup", 0, 256)
                for j in range(3):
                    cv = wt("conv", j, 256)
                    for h in range(NH):
                        pe.matmul(bank(k, p), cv[:, h, :], yt(k, h, t, 2 - j), start=j + h == 0, stop=j + h == 3)
            for h in range(NH):
                pe.matmul(bank(k, p + 1), u[:, h, :], yt(k, h, t), start=h == 0, stop=h == 1)
            spread_weight(k, pe, p + 2, E0, x, t).then_inc(k.sem("moe_in"), 1)

        def second(x):
            w = k.W[:, W0["down"] + 256 * x:W0["down"] + 256 * x + 256] if x < E0 - 1 else k.W[:, W0["sdown"]:W0["sdown"] + 256]
            if x == 0:
                pe.wait_ge(*k.at("moe_out", 2 * t))
            pe.wait_ge(*k.at("moe_h", E0 * t + x + 1))
            for m in range(NH):
                mm = pe.matmul(bank(k, 6 + m), w[:, m * P:(m + 1) * P], k.B[:, 1024 + TN * (x % 2):1024 + TN * (x % 2 + 1)],
                               start=x == 0, stop=x == E0 - 1)
            mm.then_inc(k.sem("moe_down"), 1)

        for x in range(E0):
            first(x)
            if x:
                second(x - 1)
        second(E0 - 1)


def l0f_act(k, act):
    norm_act(k, act, "n3")
    route_act(k, act, "l0f", E0, 0)
    combine_act(k, act, "l0f", E0)
    l1_prep_act(k, act)
    with act.Fori(0, TILES) as t:
        for x in range(E0):
            act.wait_ge(*k.at("moe_in", E0 * t + x + 1))
            act.wait_ge(*k.at("moe_h", E0 * t + max(x - 1, 0)))
            act.activation(k.B[:, TN * (x % 2):TN * (x % 2 + 1)], bank(k, 3 * (x % 2)), ACT.Silu).then_inc(k.sem("moe_silu"), 1)


def l0f_dve(k, dve):
    norm_dve(k, dve, "n3", k.H, dst=lambda h, t: yt(k, h, t))
    route_dve(k, dve, "l0f", E0, 1, 1e-6, k.small[:, 544:560], 0)
    l1_prep_dve(k, dve)
    own = k.B[:, 2048:3072].rearrange("p (h s t) -> p h s t", h=2, s=SPT)
    with dve.Fori(0, TILES) as t:
        for x in range(E0):
            s, hid = k.B[:, TN * (x % 2):TN * (x % 2 + 1)], k.B[:, 1024 + TN * (x % 2):1024 + TN * (x % 2 + 1)]
            p = 3 * (x % 2)
            dve.wait_ge(*k.at("moe_silu", E0 * t + x + 1))
            dve.wait_ge(*k.at("moe_down", E0 * t + max(x - 1, 0)))
            if x < E0 - 1:
                dve.tensor_tensor(s, s, bank(k, p + 1), ALU.mult).then_inc(k.sem("moe_up"), 1)
                dve.wait_ge(*k.at("moe_up", (E0 - 1) * t + x + 1))
                dve.tensor_tensor(hid, s, bank(k, p + 2), ALU.mult).then_inc(k.sem("moe_h"), 1)
            else:
                for h in range(NH):
                    dve.tensor_tensor(own[:, h], yt(k, h, t), bank_seq(k, p + 2), ALU.mult).then_inc(k.sem("moe_own"), 1)
                dve.tensor_tensor(hid, s, bank(k, p + 1), ALU.mult).then_inc(k.sem("moe_h"), 1)
        dve.wait_ge(*k.at("moe_own", 2 * t + 2))
        for m in range(NH):
            dve.tensor_tensor(tile(k.H, m, t), tile(k.H, m, t), own[:, m], ALU.add).then_inc(k.sem("moe_own_in"), 1)
        dve.wait_ge(*k.at("moe_down", E0 * t + E0))
        dve.wait_ge(*k.at("moe_own_in", 2 * t + 2))
        for m in range(NH):
            dve.tensor_tensor(tile(k.H, m, t), tile(k.H, m, t), bank_seq(k, 6 + m), ALU.add).then_inc(k.sem("moe_out"), 1)



V1 = {"B": 0, "F": 512, "G": 1024, "C": 1536, "S": 2048, "a": 2176, "ER": 2304, "EI": 2560, "keep": 2816, "BF": 3328, "CG": 3840}


def l1a_inputs(ins, a):
    n, f = np.arange(D)[:, None].astype(np.float64), np.arange(P)[None, :]
    w = 2 * np.pi / D
    ft = np.concatenate([np.cos(w * n * f), -np.sin(w * n * f)], axis=1)
    ft[:, P] = np.cos(np.pi * n[:, 0])
    g = 2 * ft / D
    g[:, 0] /= 2
    g[:, P] /= 2
    s = -2 * np.sin(w * (np.arange(P)[:, None] + 1) * f)
    s[P - 1] = 0.0
    ft, g, s = (x.astype(np.float32) for x in (ft, g, s))
    ins["l1_w"] = np.concatenate([halves(a["L1_attn_B_w"]), halves(ft), halves(g), halves(a["L1_attn_C_w"].T), s,
                                  a["L1_attn_a_params"].reshape(P, 1)], axis=1)


def l1a_load(k, sp):
    sp.wait_ge(*k.at("ff2", 2 * TILES))
    sp.dma_start(k.V[:, 0:2177], k.ins["l1_w"]).then_inc(k.sem("l1_weights"), 16)


def l1w(k, name):
    return blocks(k.V[:, V1[name]:V1[name] + 512], 2)


def l1_prep_pe(k, pe):
    pe.wait_ge(*k.at("l1_weights", 16))
    pe.matmul(k.PS[:, 0, 0:1], k.V[:, V1["S"]:V1["S"] + P], k.V[:, V1["a"]:V1["a"] + 1], start=True, stop=True).then_inc(k.sem("omega"), 1)
    for b, lhs, rhs in ((2, "B", "F"), (3, "G", "C")):
        for m in range(NH):
            for h in range(NH):
                mm = pe.matmul(k.PS[:, b, m * D:(m + 1) * D], l1w(k, lhs)[:, h, m * P:(m + 1) * P], l1w(k, rhs)[:, h, :], start=h == 0, stop=h == 1)
        mm.then_inc(k.sem("folded"), 1)


def l1_prep_act(k, act):
    for j, name in enumerate(("BF", "CG")):
        act.wait_ge(*k.at("folded", j + 1))
        act.activation(k.V[:, V1[name]:V1[name] + 512], bank(k, 2 + j), ACT.Copy).then_inc(k.sem("folded_copied"), 1)


def l1_prep_dve(k, dve):
    s = k.vec2
    done = [0]

    def chain(ins):
        done[0] += 1
        ins.then_inc(k.sem("eigen_step"), 1)
        dve.wait_ge(*k.at("eigen_step", done[0]))
    w, w2, den, lr, li = (s[:, 14 + j:15 + j] for j in range(5))
    dve.wait_ge(*k.at("omega", 1))
    chain(dve.tensor_copy(w, k.PS[:, 0, 0:1]))
    chain(dve.tensor_tensor(w2, w, w, ALU.mult))
    chain(dve.tensor_scalar(den, w2, 1.0, None, ALU.add))
    chain(dve.reciprocal(den, den))
    chain(dve.tensor_scalar(w2, w2, -1.0, 1.0, ALU.mult, ALU.add))
    chain(dve.tensor_tensor(lr, w2, den, ALU.mult))
    chain(dve.tensor_scalar(w, w, -2.0, None, ALU.mult))
    dve.tensor_tensor(li, w, den, ALU.mult).then_inc(k.sem("eigen"), 1)
    keep = k.V[:, V1["keep"]:V1["keep"] + TN]
    chain(dve.memset(keep, 1.0))
    dve.memset(keep.rearrange("p (s t) -> p s t", s=SPT)[:, :, 0:1], 0.0).then_inc(k.sem("keep_set"), 1)


def l1a_tables_pool(k, pool):
    s = k.vec2
    lr, li, sq, c0 = (s[:, 17 + j:18 + j] for j in range(4))
    done = [0]

    def chain(ins):
        done[0] += 1
        ins.then_inc(k.sem("power_step"), 1)
        pool.wait_ge(*k.at("power_step", done[0]))
    ER, EI = k.V[:, V1["ER"]:V1["ER"] + T], k.V[:, V1["EI"]:V1["EI"] + T]
    tmp = k.D[:, 0:2 * P]
    pool.wait_ge(*k.at("n3_scaled", 2 * TILES))
    pool.wait_ge(*k.at("eigen", 1))
    chain(pool.memset(ER[:, 0:1], 1.0))
    chain(pool.memset(EI[:, 0:1], 0.0))
    n = 1
    while n < T:
        a, b = tmp[:, 0:n], tmp[:, P:P + n]
        chain(pool.tensor_scalar(a, ER[:, 0:n], lr, None, ALU.mult))
        chain(pool.tensor_scalar(b, EI[:, 0:n], li, None, ALU.mult))
        chain(pool.tensor_tensor(ER[:, n:2 * n], a, b, ALU.subtract))
        chain(pool.tensor_scalar(a, ER[:, 0:n], li, None, ALU.mult))
        chain(pool.tensor_scalar(b, EI[:, 0:n], lr, None, ALU.mult))
        chain(pool.tensor_tensor(EI[:, n:2 * n], a, b, ALU.add))
        chain(pool.tensor_tensor(sq, lr, lr, ALU.mult))
        chain(pool.tensor_tensor(c0, li, li, ALU.mult))
        chain(pool.tensor_tensor(li, li, lr, ALU.mult))
        chain(pool.tensor_tensor(li, li, li, ALU.add))
        chain(pool.tensor_tensor(lr, sq, c0, ALU.subtract))
        n *= 2
    pool.sem_inc(k.sem("powers"), 1)


def l1a_pe(k, pe):
    norm_pe(k, pe, "n4", k.H, "moe_out", 2, free=(("moe_h", E0 * TILES),))
    bf, cg = l1w(k, "BF"), l1w(k, "CG")
    with pe.Fori(0, TILES // 2) as i:
        for par in range(2):
            t = 2 * i + par
            pe.wait_ge(*k.at("n4_scaled", 2 * (t + 1)))
            pe.wait_ge(*k.at("turned_in", 8 * i))
            for m in range(NH):
                for h in range(NH):
                    mm = pe.matmul(bank(k, 4 + 2 * par + m), bf[:, h, m * P:(m + 1) * P], yt(k, h, t), start=h == 0, stop=h == 1)
                mm.then_inc(k.sem("fourier_in"), 1)
    with pe.Fori(0, TILES // 2) as i:
        for par in range(2):
            t = 2 * i + par
            pe.wait_ge(*k.at("z_ready", 2 * (t + 1)))
            pe.wait_ge(*k.at("ssm_read", 4 * i))
            for m in range(NH):
                for h in range(NH):
                    mm = pe.matmul(bank(k, 2 * par + m), cg[:, h, m * P:(m + 1) * P], tile(seqs(k.C), h, t), start=h == 0, stop=h == 1)
                mm.then_inc(k.sem("ssm_out"), 1)


def l1a_act(k, act):
    norm_act(k, act, "n4")


def powers(k, name):
    return k.V[:, V1[name]:V1[name] + T].unsqueeze(1).to_broadcast([P, SPT, T])


def l1a_pool(k, pool):
    l1a_tables_pool(k, pool)
    A, Bv, C, Dv = seqs(k.A), seqs(k.B), seqs(k.C), seqs(k.D)
    pool.wait_ge(*k.at("ff2", 2 * TILES))
    with pool.Fori(0, TILES) as t:
        pool.wait_ge(*k.at("turned_in", 4 * t + 2))
        pool.tensor_tensor(tile(C, 0, t), tile(A, 0, t), tile(A, 1, t), ALU.add).then_inc(k.sem("sum_in"), 1)
        pool.wait_ge(*k.at("turned_in", 4 * t + 4))
        pool.tensor_tensor(tile(C, 1, t), tile(Bv, 0, t), tile(Bv, 1, t), ALU.subtract).then_inc(k.sem("sum_in"), 1)
    with pool.Fori(0, TILES) as t:
        pool.wait_ge(*k.at("turned_out", 4 * t + 2))
        pool.tensor_tensor(tile(C, 0, t), tile(A, 0, t), tile(A, 1, t), ALU.subtract).then_inc(k.sem("z_ready"), 1)
        pool.wait_ge(*k.at("turned_out", 4 * t + 4))
        pool.tensor_tensor(tile(C, 1, t), tile(Bv, 0, t), tile(Bv, 1, t), ALU.add).then_inc(k.sem("z_ready"), 1)


def flat(buf, h, t):
    return buf[:, bass.ds(t * TN + h * N, TN)]


def l1a_dve(k, dve):
    A, Bv, Dv = seqs(k.A), seqs(k.B), seqs(k.D)
    norm_dve(k, dve, "n4", k.H, dst=lambda h, t: yt(k, h, t), free=(("powers", 1),))
    dve.wait_ge(*k.at("powers", 1))
    dve.wait_ge(*k.at("keep_set", 1))
    with dve.Fori(0, TILES // 2) as i:
        for par in range(2):
            t = 2 * i + par
            re, im = bank_seq(k, 4 + 2 * par), bank_seq(k, 5 + 2 * par)
            dve.wait_ge(*k.at("fourier_in", 2 * t + 2))
            for dst, src, e in ((tile(A, 0, t), re, "ER"), (tile(A, 1, t), im, "EI"), (tile(Bv, 0, t), im, "ER"), (tile(Bv, 1, t), re, "EI")):
                dve.tensor_tensor(dst, src, powers(k, e), ALU.mult).then_inc(k.sem("turned_in"), 1)
    with dve.Fori(0, TILES) as t:
        for h in range(NH):
            dve.wait_ge(*k.at("sum_in", 2 * t + h + 1))
            dve.tensor_tensor_scan(flat(k.D, h, t), k.V[:, V1["keep"]:V1["keep"] + TN], flat(k.C, h, t), 0.0, ALU.mult, ALU.add).then_inc(k.sem("summed"), 1)
        dve.wait_ge(*k.at("summed", 2 * t + 2))
        for dst, h, e in ((tile(A, 0, t), 0, "ER"), (tile(A, 1, t), 1, "EI"), (tile(Bv, 0, t), 1, "ER"), (tile(Bv, 1, t), 0, "EI")):
            dve.tensor_tensor(dst, tile(Dv, h, t), powers(k, e), ALU.mult).then_inc(k.sem("turned_out"), 1)
    with dve.Fori(0, TILES // 2) as i:
        for par in range(2):
            t = 2 * i + par
            dve.wait_ge(*k.at("z_ready", 2 * t + 2))
            for m in range(NH):
                dve.wait_ge(*k.at("ssm_out", 2 * t + m + 1))
                dve.scalar_tensor_tensor(tile(A, m, t), yt(k, m, t), vcol(k, "D", m), bank_seq(k, 2 * par + m), ALU.mult, ALU.add).then_inc(k.sem("ssm_read"), 1)
                dve.wait_ge(*k.at("ssm_read", 2 * t + m + 1))
                dve.tensor_tensor(tile(k.H, m, t), tile(k.H, m, t), tile(A, m, t), ALU.add).then_inc(k.sem("l1a_done"), 1)



def l1f_inputs(ins, a):
    ins["l1f_w"] = np.concatenate([halves(a["L1_ffn_W_" + n].T) for n in "rkv"], axis=1)


def l1f_load(k, sp):
    sp.wait_ge(*k.at("moe_down", E0 * TILES))
    sp.dma_start(k.W[:, 0:1536], k.ins["l1f_w"]).then_inc(k.sem("l1f_weights"), 16)


def l1f_pe(k, pe):
    wr, wk, wv = (blocks(k.W[:, 512 * j:512 * j + 512], 2) for j in range(3))
    norm_pe(k, pe, "n5", k.H, "l1a_done", 2, free=(("ssm_read", 2 * TILES),))
    pe.wait_ge(*k.at("l1f_weights", 16))
    pe.wait_ge(*k.at("n5_std", TILES))
    with pe.Fori(0, TILES // 2) as i:
        for par in range(2):
            t = 2 * i + par
            pe.wait_ge(*k.at("rk_read", 8 * i))
            pe.wait_ge(*k.at("mixed", 4 * t + 4))
            for o, (w, x) in enumerate(((wr, k.B), (wk, k.C))):
                for m in range(NH):
                    for h in range(NH):
                        mm = pe.matmul(bank(k, 4 * par + 2 * o + m), w[:, h, m * P:(m + 1) * P], tile(seqs(x), h, t), start=h == 0, stop=h == 1)
                    mm.then_inc(k.sem("rk_ready"), 1)
    with pe.Fori(0, TILES // 2) as i:
        for par in range(2):
            t = 2 * i + par
            pe.wait_ge(*k.at("k_squared", 2 * t + 2))
            pe.wait_ge(*k.at("rk_read", 4 * TILES))
            pe.wait_ge(*k.at("v_read", 4 * i))
            for m in range(NH):
                for h in range(NH):
                    mm = pe.matmul(bank(k, 4 * par + m), wv[:, h, m * P:(m + 1) * P], tile(seqs(k.D), h, t), start=h == 0, stop=h == 1)
                mm.then_inc(k.sem("v_ready"), 1)


def l1f_act(k, act):
    norm_act(k, act, "n5")
    act.wait_ge(*k.at("rest_ready", 7))
    with act.Fori(0, TILES) as t:
        act.wait_ge(*k.at("n5_scaled", 2 * t + 2))
        for o, x in enumerate((k.B, k.C)):
            for h in range(NH):
                act.activation(tile(seqs(x), h, t), yt(k, h, t, 1), ACT.Copy, scale=k.vec2[:, 2 * o + h:2 * o + h + 1]).then_inc(k.sem("before"), 1)
    with act.Fori(0, TILES // 2) as i:
        for par in range(2):
            t = 2 * i + par
            for m in range(NH):
                act.wait_ge(*k.at("rk_ready", 4 * t + m + 1))
                act.activation(tile(seqs(k.A), m, t), bank_seq(k, 4 * par + m), ACT.Sigmoid).then_inc(k.sem("rk_read"), 1)
            for m in range(NH):
                act.wait_ge(*k.at("rk_ready", 4 * t + 2 + m + 1))
                act.activation(tile(seqs(k.D), m, t), bank_seq(k, 4 * par + 2 + m), ACT.Relu).then_inc(k.sem("rk_read"), 1)


def l1f_pool(k, pool):
    with pool.Fori(0, TILES) as t:
        for h in range(NH):
            pool.wait_ge(*k.at("rk_read", 4 * t + 2 + h + 1))
            pool.tensor_tensor(tile(seqs(k.D), h, t), tile(seqs(k.D), h, t), tile(seqs(k.D), h, t), ALU.mult).then_inc(k.sem("k_squared"), 1)


def l1f_dve(k, dve):
    norm_dve(k, dve, "n5", k.H, dst=lambda h, t: yt(k, h, t))
    with dve.Fori(0, TILES) as t:
        for o, (x, mu) in enumerate(((k.B, "mu_r"), (k.C, "mu_k"))):
            for h in range(NH):
                dve.wait_ge(*k.at("before", 4 * t + 2 * o + h + 1))
                v = tile(seqs(x), h, t)
                dve.scalar_tensor_tensor(v, yt(k, h, t), vcol(k, mu, h), v, ALU.mult, ALU.add).then_inc(k.sem("mixed"), 1)
    with dve.Fori(0, TILES // 2) as i:
        for par in range(2):
            t = 2 * i + par
            for m in range(NH):
                a = tile(seqs(k.A), m, t)
                dve.wait_ge(*k.at("v_ready", 2 * t + m + 1))
                dve.tensor_tensor(a, a, bank_seq(k, 4 * par + m), ALU.mult).then_inc(k.sem("v_read"), 1)
                dve.wait_ge(*k.at("v_read", 2 * t + m + 1))
                dve.tensor_tensor(tile(k.H, m, t), tile(k.H, m, t), a, ALU.add).then_inc(k.sem("l1f_done"), 1)



CH = 128
W2 = {"q": 1536, "k": 2048, "g": 2560, "out": 3072, "v": 3584, "gk1": 4096, "gk2": 4352}
FAR = 16 * 85.0


def l2a_inputs(ins, a):
    w = {n: a["L2_attn_" + n] for n in ("Wq", "Wk", "Wg", "Wout", "Wv", "Wgk1")}
    w["Wgk1"] = np.pad(w["Wgk1"], ((0, 0), (0, P - 16)))
    ins["l2a_w"] = np.concatenate([halves(w[n]) for n in ("Wq", "Wk", "Wg", "Wout", "Wv", "Wgk1")], axis=1)
    ins["gk2"] = np.pad(a["L2_attn_Wgk2"], ((0, P - 16), (0, 0)))


def l2a_load(k, sp):
    sp.dma_start(k.W[:, 1536:4352], k.ins["l2a_w"]).then_inc(k.sem("l2a_weights"), 16)
    sp.dma_start(k.W[:, 4352:4608], k.ins["gk2"]).then_inc(k.sem("l2a_weights"), 16)


def l2w(k, name):
    return blocks(k.W[:, W2[name]:W2[name] + 512], 2)


def gla_views(k):
    v = {"keep": k.V[:, 0:512], "gsum": k.V[:, 4096:4098]}
    for name, a in (("dm", 512), ("eo", 1024), ("vi", 1536)):
        v[name] = k.V[:, a:a + 512].rearrange("p (h c t) -> p h c t", h=2, c=2)
    v["ve"] = k.V[:, 2048:2304].rearrange("p (h t) -> p h t", h=2)
    v["ks"] = k.V[:, 2560:3072].rearrange("p (h t) -> p h t", h=2)
    v["turned"] = k.V[:, 3072:3584]
    v["veT"] = k.V[:, 3072:3328].rearrange("p (h m) -> p h m", h=2)
    v["kT"] = k.V[:, 3328:3584].rearrange("p (h m) -> p h m", h=2)
    v["st"] = k.V[:, 3584:3840].rearrange("p (h m) -> p h m", h=2)
    v["qz"] = [k.A[:, 1024 * j:1024 * j + 1024].rearrange("p (a t) -> p a t", a=8) for j in range(2)]
    v["am"] = [k.A[:, 2048 + 1024 * j:3072 + 1024 * j].rearrange("p (a t) -> p a t", a=8) for j in range(2)]
    v["vz"] = k.Q[:, :].rearrange("p (u a m) -> p u a m", u=4, a=8)
    return v


def l2a_pe(k, pe):
    v = gla_views(k)
    norm_pe(k, pe, "n6", k.H, "l1f_done", 2, free=(("v_read", 2 * TILES),))
    pe.wait_ge(*k.at("l2a_weights", 32))
    pe.wait_ge(*k.at("n6_std", TILES))
    with pe.Fori(0, TILES // 2) as i:
        for par in range(2):
            t = 2 * i + par
            pe.wait_ge(*k.at("n6_scaled", 2 * t + 2))
            for n in range(7):
                pe.wait_ge(*k.at("qkv_read", 14 * i + (par and n + 1)))
                w = l2w(k, "qkv"[n // 2])[:, :, (n % 2) * P:(n % 2 + 1) * P] if n < 6 else blocks(k.W[:, W2["gk1"]:W2["gk1"] + 256], 2)
                for h in range(NH):
                    mm = pe.matmul(bank(k, n), w[:, h, :], yt(k, h, t), start=h == 0, stop=h == 1)
                mm.then_inc(k.sem("qkv_ready"), 1)
    pe.wait_ge(*k.at("qkv_read", 7 * TILES))
    with pe.Fori(0, TILES // 2) as i:
        for par in range(2):
            pe.wait_ge(*k.at("gate_read", 4 * i))
            for m in range(NH):
                pe.matmul(bank(k, 2 * par + m), k.W[:, W2["gk2"] + m * P:W2["gk2"] + (m + 1) * P], k.Q[:, bass.ds((2 * i + par) * TN, TN)],
                          start=True, stop=True).then_inc(k.sem("gate_ready"), 1)
    pe.wait_ge(*k.at("gate_read", 2 * TILES))
    with pe.Fori(0, B) as b:

        def scores(u):
            c, h = u // 2, u % 2
            pe.wait_ge(*k.at("q_spread", 4 * b + u + 1))
            pe.wait_ge(*k.at("gla_masked", 4 * b + max(u - 1, 0)))
            for x in range(2):
                mm = pe.matmul(bank(k, 2 + 2 * (u % 2) + x), v["ks"][:, h, CH * c:CH * c + CH], v["qz"][u % 2][:, 4 * x:4 * x + 4, :], start=True, stop=True)
            mm.then_inc(k.sem("gla_scores"), 1)

        def outputs(u):
            c, h = u // 2, u % 2
            pe.wait_ge(*k.at("gla_masked", 4 * b + u + 1))
            pe.wait_ge(*k.at("gla_out", 4 * b + max(u - 1, 0)))
            for x in range(8):
                mm = pe.matmul(k.PS[:, 6 + u % 2, 0:P], v["vz"][:, u, x, :], v["am"][u % 2][:, x, :], start=x == 0, stop=x == 7 and c == 0)
            if c:
                if u == 2:
                    pe.wait_ge(*k.at("state", b + 1))
                mm = pe.matmul(k.PS[:, 6 + u % 2, 0:P], v["st"][:, h, :], seqs(k.B)[:, h, b, CH:2 * CH], start=False, stop=True)
            mm.then_inc(k.sem("gla_att"), 1)

        pe.wait_ge(*k.at("keys_staged", b + 1))
        scores(0)
        scores(1)
        pe.wait_ge(*k.at("decayed", 2 * b + 2))
        pe.wait_ge(*k.at("v_spread", b))
        pe.wait_ge(*k.at("state", b))
        for u in range(4):
            mm = pe.transpose(k.PS[:, 0, P * u:P * u + P], v["vi"][:, u % 2, u // 2, :], k.ident[:, :])
        mm.then_inc(k.sem("v_turned"), 1)
        for h in range(NH):
            pe.transpose(k.PS[:, 1, P * h:P * h + P], v["ve"][:, h, :], k.ident[:, :])
            mm = pe.transpose(k.PS[:, 1, D + P * h:D + P * h + P], v["ks"][:, h, 0:CH], k.ident[:, :])
        mm.then_inc(k.sem("kv_turned"), 1)
        pe.wait_ge(*k.at("v_spread", b + 1))
        outputs(0)
        scores(2)
        pe.wait_ge(*k.at("kv_copied", b + 1))
        for h in range(NH):
            mm = pe.matmul(k.PS[:, 1, P * h:P * h + P], v["kT"][:, h, :], v["veT"][:, h, :], start=True, stop=True)
        mm.then_inc(k.sem("state_sum"), 1)
        outputs(1)
        scores(3)
        outputs(2)
        outputs(3)
    norm_pe(k, pe, "n7", seqs(k.E), "gla_out", 8, free=(("gla_out", 4 * B),))
    pe.wait_ge(*k.at("n7_std", TILES))
    with pe.Fori(0, TILES // 2) as i:
        for par in range(2):
            pe.wait_ge(*k.at("g_read", 4 * i))
            for m in range(NH):
                for h in range(NH):
                    mm = pe.matmul(bank(k, 2 * par + m), l2w(k, "g")[:, h, m * P:(m + 1) * P], yt(k, h, 2 * i + par), start=h == 0, stop=h == 1)
                mm.then_inc(k.sem("g_ready"), 1)
    with pe.Fori(0, TILES // 2) as i:
        for par in range(2):
            t = 2 * i + par
            pe.wait_ge(*k.at("gated", 2 * t + 2))
            pe.wait_ge(*k.at("l2a_read", 4 * i))
            for m in range(NH):
                for h in range(NH):
                    mm = pe.matmul(bank(k, 4 + 2 * par + m), l2w(k, "out")[:, h, m * P:(m + 1) * P], tile(seqs(k.A), h, t), start=h == 0, stop=h == 1)
                mm.then_inc(k.sem("l2a_ready"), 1)


def l2a_act(k, act):
    v = gla_views(k)
    norm_act(k, act, "n6")
    with act.Fori(0, TILES // 2) as i:
        for par in range(2):
            t = 2 * i + par
            for n in range(7):
                dst = tile(seqs((k.B, k.C, k.E)[n // 2]), n % 2, t) if n < 6 else tile(seqs(k.Q), 0, t)
                act.wait_ge(*k.at("qkv_ready", 7 * t + n + 1))
                act.activation(dst, bank_seq(k, n), ACT.Copy).then_inc(k.sem("qkv_read"), 1)
    with act.Fori(0, TILES // 2) as i:
        for par in range(2):
            t = 2 * i + par
            for m in range(NH):
                act.wait_ge(*k.at("gate_ready", 2 * t + m + 1))
                act.activation(tile(seqs(k.A), m, t), bank_seq(k, 2 * par + m), ACT.Identity, bias=vcol(k, "bgk2", m)).then_inc(k.sem("gate_read"), 1)
    for n, (f, src, dst) in enumerate(((ACT.Abs, k.A, k.Q), (ACT.Exp, k.Q, k.Q), (ACT.Ln, k.Q, k.Q))):
        with act.Fori(0, TILES) as t:
            for m in range(NH):
                act.wait_ge(*k.at("gate_read" if n == 0 else f"softplus{n}", 2 * t + m + 1))
                act.activation(tile(seqs(dst), m, t), tile(seqs(src), m, t), f, bias=1.0 if n == 2 else 0.0, scale=-1.0 if n == 1 else 1.0).then_inc(k.sem(f"softplus{n + 1}"), 1)
    with act.Fori(0, B) as b:
        act.wait_ge(*k.at("clamped", b + 1))
        act.wait_ge(*k.at("gla_out", 4 * b))
        act.activation(v["vi"], v["dm"], ACT.Exp, scale=-1 / 16).then_inc(k.sem("factors"), 1)
        act.wait_ge(*k.at("to_end", b + 1))
        act.activation(v["ve"], v["ve"], ACT.Exp, scale=1 / 16).then_inc(k.sem("factors"), 1)
        act.activation(v["eo"], v["dm"], ACT.Exp, scale=1 / 16).then_inc(k.sem("factors"), 1)
        act.wait_ge(*k.at("kv_turned", b + 1))
        act.wait_ge(*k.at("state_sum", b))
        act.activation(v["turned"], bank(k, 1), ACT.Copy).then_inc(k.sem("kv_copied"), 1)
    norm_act(k, act, "n7", "beta", lambda h, t: tile(seqs(k.A), h, t))
    with act.Fori(0, TILES // 2) as i:
        for par in range(2):
            for m in range(NH):
                act.wait_ge(*k.at("g_ready", 4 * i + 2 * par + m + 1))
                act.activation(tile(seqs(k.B), m, 2 * i + par), bank_seq(k, 2 * par + m), ACT.Silu).then_inc(k.sem("g_read"), 1)


def l2a_pool(k, pool):
    v = gla_views(k)
    pool.wait_ge(*k.at("gate_sums", 2 * TILES))
    pool.memset(k.Q[:, :], 0.0).then_inc(k.sem("vz2_zero"), 1)
    pool.wait_ge(*k.at("qkv_read", 7 * TILES))
    with pool.Fori(0, B) as b:
        pool.wait_ge(*k.at("state_sum", b))
        pool.wait_ge(*k.at("gla_scores", 4 * b))
        pool.tensor_copy(v["ks"], seqs(k.C)[:, :, b, :]).then_inc(k.sem("keys_staged"), 1)
        for u in range(4):
            pool.wait_ge(*k.at("gla_scores", 4 * b + max(u - 1, 0)))
            pool.tensor_tensor(v["qz"][u % 2], seqs(k.B)[:, u % 2, b, CH * (u // 2):CH * (u // 2) + CH].unsqueeze(1).to_broadcast([P, 8, CH]),
                               k.headmask.unsqueeze(2).to_broadcast([P, 8, CH]), ALU.mult).then_inc(k.sem("q_spread"), 1)


def l2a_dve(k, dve):
    v = gla_views(k)
    norm_dve(k, dve, "n6", k.H, dst=lambda h, t: yt(k, h, t))
    dve.wait_ge(*k.at("ssm_out", 2 * TILES))
    dve.memset(v["keep"], 1.0).then_inc(k.sem("keep2"), 1)
    dve.wait_ge(*k.at("keep2", 1))
    dve.memset(v["keep"].rearrange("p (c t) -> p c t", t=CH)[:, :, 0:1], 0.0).then_inc(k.sem("keep2"), 1)
    dve.wait_ge(*k.at("keep2", 2))
    with dve.Fori(0, TILES) as t:
        for m in range(NH):
            dve.wait_ge(*k.at("softplus3", 2 * t + m + 1))
            g = tile(seqs(k.A), m, t)
            dve.scalar_tensor_tensor(g, g, 0.0, tile(seqs(k.Q), m, t), ALU.min, ALU.subtract).then_inc(k.sem("log_gate"), 1)
            dve.wait_ge(*k.at("log_gate", 2 * t + m + 1))
            dve.tensor_tensor_scan(flat(k.D, m, t), v["keep"], flat(k.A, m, t), 0.0, ALU.mult, ALU.add).then_inc(k.sem("gate_sums"), 1)
    dve.wait_ge(*k.at("gate_sums", 2 * TILES))
    dve.wait_ge(*k.at("vz2_zero", 1))
    G = seqs(k.D)
    with dve.Fori(0, B) as b:
        g = G[:, :, b, :].rearrange("p h (c t) -> p h c t", c=2)
        dve.wait_ge(*k.at("factors", 3 * b))
        dve.wait_ge(*k.at("kv_turned", b))
        dve.tensor_tensor(v["dm"], g, g[:, :, :, CH // 2 - 1:CH // 2].to_broadcast([P, 2, 2, CH]), ALU.subtract).then_inc(k.sem("to_mid"), 1)
        dve.tensor_tensor(v["gsum"].unsqueeze(2), g[:, :, 0, CH - 1:CH], g[:, :, 1, CH // 2 - 1:CH // 2], ALU.add).then_inc(k.sem("gate_to_mid"), 1)
        dve.wait_ge(*k.at("to_mid", b + 1))
        dve.tensor_scalar(v["dm"], v["dm"], FAR, -FAR, ALU.min, ALU.max).then_inc(k.sem("clamped"), 1)
        dve.wait_ge(*k.at("gate_to_mid", b + 1))
        dve.tensor_tensor(v["ve"], v["gsum"].unsqueeze(2).to_broadcast([P, 2, CH]), g[:, :, 0, :], ALU.subtract).then_inc(k.sem("to_end"), 1)
        vals = seqs(k.E)[:, :, b, :]
        dve.wait_ge(*k.at("factors", 3 * b + 1))
        dve.tensor_tensor(v["vi"], v["vi"], vals.rearrange("p h (c t) -> p h c t", c=2), ALU.mult).then_inc(k.sem("decayed"), 1)
        dve.wait_ge(*k.at("factors", 3 * b + 2))
        dve.tensor_tensor(v["ve"], v["ve"], vals[:, :, 0:CH], ALU.mult).then_inc(k.sem("decayed"), 1)

        def mask(u):
            dve.wait_ge(*k.at("gla_scores", 4 * b + u + 1))
            dve.wait_ge(*k.at("gla_att", 4 * b + max(u - 1, 0)))
            src = k.PS[:, 2 + 2 * (u % 2):4 + 2 * (u % 2), :].rearrange("p b (a t) -> p (b a) t", a=4)
            dve.tensor_tensor(v["am"][u % 2], src, k.causal.unsqueeze(1).to_broadcast([P, 8, CH]), ALU.mult).then_inc(k.sem("gla_masked"), 1)

        def output(u):
            c, h = u // 2, u % 2
            dve.wait_ge(*k.at("gla_att", 4 * b + u + 1))
            dve.tensor_tensor(seqs(k.E)[:, h, b, CH * c:CH * c + CH], k.PS[:, 6 + u % 2, 0:P], v["eo"][:, h, c, :], ALU.mult).then_inc(k.sem("gla_out"), 1)

        mask(0)
        mask(1)
        dve.wait_ge(*k.at("v_turned", b + 1))
        base = k.Q[:, 0:16]
        dst = bass.AP(tensor=base.tensor, offset=base.offset, ap=[base.ap[0], [1024, 4], [144, 8], [1, 16]])
        dve.tensor_copy(dst, k.PS[:, 0, :].rearrange("p (u a d) -> p u a d", u=4, a=8)).then_inc(k.sem("v_spread"), 1)
        dve.wait_ge(*k.at("factors", 3 * b + 3))
        dve.wait_ge(*k.at("decayed", 2 * b + 2))
        output(0)
        mask(2)
        dve.wait_ge(*k.at("state_sum", b + 1))
        dve.tensor_tensor(v["st"].rearrange("p h (a d) -> p h a d", a=8), k.PS[:, 1, 0:D].rearrange("p (h a d) -> p h a d", h=2, a=8),
                          k.headmask.unsqueeze(1).unsqueeze(3).to_broadcast([P, 2, 8, 16]), ALU.mult).then_inc(k.sem("state"), 1)
        output(1)
        mask(3)
        output(2)
        output(3)
    norm_dve(k, dve, "n7", seqs(k.E), gain="gamma")
    with dve.Fori(0, TILES) as t:
        for m in range(NH):
            dve.wait_ge(*k.at("g_read", 2 * t + m + 1))
            dve.wait_ge(*k.at("n7_done", 2 * t + m + 1))
            x = tile(seqs(k.A), m, t)
            dve.tensor_tensor(x, x, tile(seqs(k.B), m, t), ALU.mult).then_inc(k.sem("gated"), 1)
    with dve.Fori(0, TILES // 2) as i:
        for par in range(2):
            t = 2 * i + par
            for m in range(NH):
                dve.wait_ge(*k.at("l2a_ready", 2 * t + m + 1))
                dve.tensor_tensor(tile(k.H, m, t), tile(k.H, m, t), bank_seq(k, 4 + 2 * par + m), ALU.add).then_inc(k.sem("l2a_read"), 1)



W6 = {"b1": 6656, "b2": 7680}
GPT = TN // P


def l2f_inputs(ins, a):
    ins["l2f_w"] = np.concatenate([halves(a["L2_ffn_W1"].T), halves(a["L2_ffn_W2"].T)], axis=1)
    ins["l2f_b"] = np.concatenate([a["L2_ffn_b1"], a["L2_ffn_b2"]]).reshape(1, 1280)


def l2f_load(k, sp):
    sp.dma_start(k.W[:, 6656:7936], k.ins["l2f_b"].to_broadcast([P, 1280])).then_inc(k.sem("l2f_bias"), 16)
    sp.wait_ge(*k.at("state_sum", B))
    sp.dma_start(k.C[:, :], k.ins["l2f_w"]).then_inc(k.sem("l2f_weights"), 16)


def ffq_views(k):
    v = {"w1": k.W[:, 4608:5632].bitcast(BF16).rearrange("p (k m) -> p k m", k=2),
         "w2": k.W[:, 5632:6656].bitcast(BF16).rearrange("p (k m) -> p k m", k=8),
         "b1": k.W[:, 6656:7680], "b2": k.W[:, 7680:7936], "wsum": k.vec2[:, 22:24], "wscale": k.vec2[:, 20:22], "winv": k.vec2[:, 14:16],
         "xs": k.A[:, 0:1024].rearrange("p (h t) -> p h t", h=2),
         "out": k.B[:, 3072:3328], "hq": k.B[:, 2048:2560].bitcast(BF16), "ht": k.B[:, 2560:3072].bitcast(BF16).rearrange("p (k t) -> p k t", k=8)}
    for j in range(2):
        v["x", j] = k.A[:, 1024 + 256 * j:1280 + 256 * j]
        v["xq", j] = k.A[:, 1536 + 128 * j:1664 + 128 * j].bitcast(BF16)
        v["xt", j] = k.A[:, 1792 + 128 * j:1920 + 128 * j].bitcast(BF16).rearrange("p (k t) -> p k t", k=2)
        v["h", j] = k.B[:, 1024 * j:1024 * j + 1024]
        v["sx", j] = k.small[:, 560 + 4 * j:564 + 4 * j]
        v["sh", j] = k.small[:, 568 + 4 * j:572 + 4 * j]
    return v


def over_groups(engine, work):
    def steps(tile_of_step):
        for u in range(GPT):
            for f, lag in work:
                t, g = tile_of_step + (u - lag) // GPT, (u - lag) % GPT
                if type(t) is not int or 0 <= t < TILES:
                    f(t, GPT * t + g, g)
    steps(0)
    with engine.Fori(1, TILES) as t:
        steps(t)
    steps(TILES)


def two_back(n):
    return n - 1 if type(n) is not int else max(n - 1, 0)


def l2f_pe(k, pe):
    v = ffq_views(k)
    norm_pe(k, pe, "n8", k.H, "l2a_read", 2, free=(("gated", 2 * TILES),))
    pe.wait_ge(*k.at("w_sums", 2))
    pe.matmul(k.PS[:, 4, 0:2], k.mean_w[:, :], v["wsum"], start=True, stop=True).then_inc(k.sem("w_means"), 1)
    pe.wait_ge(*k.at("w_quantised", 2))

    def turn_x(t, n, g):
        if g == 0:
            pe.wait_ge(*k.at("tile_staged", t + 1))
        pe.wait_ge(*k.at("x_shifted", n))
        for h in range(NH):
            mm = pe.transpose(k.PS[:, 0, P * h:P * h + P], v["xs"][:, h, P * g:P * g + P], k.ident[:, :])
        mm.then_inc(k.sem("x_turned"), 1)

    def turn_xq(t, n, g):
        pe.wait_ge(*k.at("x_quantised", n + 1, positive=True))
        pe.wait_ge(*k.at("xq_copied", n))
        for h in range(NH):
            mm = pe.transpose(k.PS[:, 2, 64 * h:64 * h + 64].bitcast(BF16), v["xq", g % 2][:, P * h:P * h + P], k.identb[:, :])
        mm.then_inc(k.sem("xq_turned"), 1)

    def turn_hidden(t, n, g):
        pe.wait_ge(*k.at("h_quantised", n + 1))
        pe.wait_ge(*k.at("hq_copied", n))
        for x in range(8):
            mm = pe.transpose(k.PS[:, 5, 64 * x:64 * x + 64].bitcast(BF16), v["hq"][:, P * x:P * x + P], k.identb[:, :])
        mm.then_inc(k.sem("hq_turned"), 1)

    def first_product(t, n, g):
        pe.wait_ge(*k.at("xq_copied", n + 1))
        pe.wait_ge(*k.at("h_scaled", n))
        for c in range(2):
            for h in range(NH):
                mm = pe.matmul(bank(k, 3 + c), v["xt", g % 2][:, h, :], v["w1"][:, h, TN * c:TN * c + TN], start=h == 0, stop=h == 1)
        mm.then_inc(k.sem("h_ready"), 1)

    def turn_out(t, n, g):
        pe.wait_ge(*k.at("y_scaled", n + 1))
        pe.wait_ge(*k.at("y_added", n))
        for h in range(NH):
            mm = pe.transpose(k.PS[:, 7, P * h:P * h + P], v["out"][:, P * h:P * h + P], k.ident[:, :])
        mm.then_inc(k.sem("y_turned"), 1)

    def second_product(t, n, g):
        pe.wait_ge(*k.at("hq_copied", n + 1))
        pe.wait_ge(*k.at("y_scaled", n))
        for x in range(8):
            mm = pe.matmul(k.PS[:, 6, 0:D], v["ht"][:, x, :], v["w2"][:, x, :], start=x == 0, stop=x == 7)
        mm.then_inc(k.sem("y_ready"), 1)

    over_groups(pe, [(turn_x, 0), (turn_xq, 1), (turn_hidden, 3), (turn_out, 4), (first_product, 1), (second_product, 3)])


def l2f_act(k, act):
    v = ffq_views(k)
    norm_act(k, act, "n8")

    def copy_x(t, n, g):
        act.wait_ge(*k.at("xq_turned", n + 1))
        act.wait_ge(*k.at("h_ready", two_back(n)))
        act.activation(v["xt", g % 2], k.PS[:, 2, 0:P].bitcast(BF16).rearrange("p (k t) -> p k t", k=2), ACT.Copy).then_inc(k.sem("xq_copied"), 1)

    def copy_hidden(t, n, g):
        act.wait_ge(*k.at("hq_turned", n + 1))
        act.wait_ge(*k.at("y_ready", n))
        act.activation(v["ht"], bank(k, 5).bitcast(BF16).rearrange("p (k t) -> p k t", k=8), ACT.Copy).then_inc(k.sem("hq_copied"), 1)

    def gelu(t, n, g):
        act.wait_ge(*k.at("h_scaled", n + 1))
        act.activation(v["h", g % 2], v["h", g % 2], ACT.Gelu).then_inc(k.sem("h_gelu"), 1)

    over_groups(act, [(copy_x, 1), (copy_hidden, 3), (gelu, 1)])


def l2f_pool(k, pool):
    v = ffq_views(k)
    pool.wait_ge(*k.at("l2a_ready", 2 * TILES))
    with pool.Fori(0, TILES) as t:
        pool.wait_ge(*k.at("n8_scaled", 2 * t + 2))
        pool.wait_ge(*k.at("x_turned", GPT * t))
        pool.tensor_copy(v["xs"].rearrange("p h (s t) -> p h s t", s=SPT), k.Y[:, :, bass.ds(SPT * t, SPT), PAD:PAD + T]).then_inc(k.sem("tile_staged"), 1)


def l2f_dve(k, dve):
    v = ffq_views(k)
    norm_dve(k, dve, "n8", k.H, dst=lambda h, t: yt(k, h, t))
    done = [0]

    def chain(ins):
        done[0] += 1
        ins.then_inc(k.sem("w_step"), 1)
        dve.wait_ge(*k.at("w_step", done[0]))
    raw = [k.C[:, 0:2048], k.C[:, 2048:4096]]
    dve.wait_ge(*k.at("l2f_weights", 16))
    for j in range(2):
        dve.tensor_reduce(v["wsum"][:, j:j + 1], raw[j], AX.X, ALU.add, apply_absolute_value=True).then_inc(k.sem("w_sums"), 1)
    dve.wait_ge(*k.at("w_means", 1))
    chain(dve.tensor_scalar(v["wscale"], k.PS[:, 4, 0:2], 1 / 1024, EPS, ALU.mult, ALU.max))
    chain(dve.reciprocal(v["winv"], v["wscale"]))
    chain(dve.tensor_scalar(v["wscale"], v["wscale"], 1 / 127, None, ALU.mult))
    for j, w in enumerate(("w1", "w2")):
        flatw = v[w].rearrange("p k m -> p (k m)")
        chain(dve.tensor_scalar(raw[j], raw[j], v["winv"][:, j:j + 1], ROUND, ALU.mult, ALU.add))
        chain(dve.tensor_scalar(raw[j], raw[j], ROUND, 1.0, ALU.subtract, ALU.min))
        dve.tensor_scalar(flatw, raw[j], -1.0, None, ALU.max).then_inc(k.sem("w_quantised"), 1)
    dve.wait_ge(*k.at("l2f_bias", 16))

    def row_scale(src, s, n, what, j):
        dve.tensor_reduce(s[:, 0:1], src, AX.X, ALU.max, apply_absolute_value=True).then_inc(k.sem(what + "_max"), 1)
        dve.wait_ge(*k.at(what + "_max", n + 1))
        dve.tensor_scalar(s[:, 0:1], s[:, 0:1], EPS, None, ALU.max).then_inc(k.sem(what + "_clip"), 1)
        dve.wait_ge(*k.at(what + "_clip", n + 1))
        dve.reciprocal(s[:, 1:2], s[:, 0:1]).then_inc(k.sem(what + "_inv"), 1)
        dve.tensor_scalar(s[:, 2:3], s[:, 0:1], v["wscale"][:, j:j + 1], None, ALU.mult).then_inc(k.sem(what + "_scale"), 1)
        dve.wait_ge(*k.at(what + "_inv", n + 1))
        dve.tensor_scalar(s[:, 1:2], s[:, 1:2], 127.0, None, ALU.mult).then_inc(k.sem(what + "_127"), 1)
        dve.wait_ge(*k.at(what + "_127", n + 1))

    def quantise_x(t, n, g):
        x, s = v["x", g % 2], v["sx", g % 2]
        dve.wait_ge(*k.at("x_turned", n + 1))
        row_scale(k.PS[:, 0, 0:D], s, n, "x", 0)
        dve.tensor_scalar(x, k.PS[:, 0, 0:D], s[:, 1:2], ROUND, ALU.mult, ALU.add).then_inc(k.sem("x_shifted"), 1)
        dve.wait_ge(*k.at("x_shifted", n + 1))
        dve.wait_ge(*k.at("xq_turned", two_back(n)))
        dve.tensor_scalar(v["xq", g % 2], x, ROUND, 127.0, ALU.subtract, ALU.min).then_inc(k.sem("x_quantised"), 1)

    def scale_hidden(t, n, g):
        dve.wait_ge(*k.at("h_ready", n + 1))
        dve.wait_ge(*k.at("x_scale", n + 1))
        dve.wait_ge(*k.at("h_quantised", two_back(n)))
        dve.scalar_tensor_tensor(v["h", g % 2], k.PS[:, 3:5, :].rearrange("p b n -> p (b n)"), v["sx", g % 2][:, 2:3], v["b1"],
                                 ALU.mult, ALU.add).then_inc(k.sem("h_scaled"), 1)

    def quantise_hidden(t, n, g):
        x, s = v["h", g % 2], v["sh", g % 2]
        dve.wait_ge(*k.at("h_gelu", n + 1))
        row_scale(x, s, n, "hid", 1)
        dve.tensor_scalar(x, x, s[:, 1:2], ROUND, ALU.mult, ALU.add).then_inc(k.sem("h_shifted"), 1)
        dve.wait_ge(*k.at("h_shifted", n + 1))
        dve.wait_ge(*k.at("hq_turned", n))
        dve.tensor_scalar(v["hq"], x, ROUND, 127.0, ALU.subtract, ALU.min).then_inc(k.sem("h_quantised"), 1)

    def add_out(t, n, g):
        dve.wait_ge(*k.at("y_turned", n + 1))
        seq = bass.ds(SPT * t + g // 2, 1)
        dst = k.H[:, :, seq, P * (g % 2):P * (g % 2) + P].rearrange("p h s t -> p h (s t)")
        dve.tensor_tensor(dst, dst, k.PS[:, 7, 0:D].rearrange("p (h t) -> p h t", h=2), ALU.add).then_inc(k.sem("y_added"), 1)

    def scale_out(t, n, g):
        dve.wait_ge(*k.at("y_ready", n + 1))
        dve.wait_ge(*k.at("y_turned", n))
        dve.wait_ge(*k.at("hid_scale", n + 1))
        dve.scalar_tensor_tensor(v["out"], k.PS[:, 6, 0:D], v["sh", g % 2][:, 2:3], v["b2"], ALU.mult, ALU.add).then_inc(k.sem("y_scaled"), 1)

    over_groups(dve, [(quantise_x, 0), (scale_hidden, 1), (add_out, 4), (quantise_hidden, 2), (scale_out, 3)])



V3 = {"k": 0, "v": 512, "r": 1024, "o": 1536}
FIRST = -1e38


def l3a_inputs(ins, a):
    w = {n: a["L3_attn_" + n].T for n in ("att_Wk", "att_Wv", "att_Wr", "att_Wo", "ffn_Wk", "ffn_Wr", "ffn_Wv")}
    ins["l3a_w"] = np.concatenate([halves(w[n]) for n in ("att_Wk", "att_Wv", "att_Wr", "att_Wo", "ffn_Wk")], axis=1)
    ins["l3a_w2"] = np.concatenate([halves(w["ffn_Wv"]), halves(w["ffn_Wr"])], axis=1)


def l3a_load(k, sp):
    sp.wait_ge(*k.at("gla_out", 4 * B))
    sp.dma_start(k.V[:, 0:4096], k.ins["l3a_w"]).then_inc(k.sem("l3a_weights"), 16)
    sp.wait_ge(*k.at("y_ready", N // P))
    sp.wait_ge(*k.at("y_scaled", N // P))
    sp.dma_start(k.W[:, 6144:8704], k.ins["l3a_w2"]).then_inc(k.sem("l3a_weights"), 16)


def wkv_views(k, h):
    s = (k.B, k.C)[h]
    v = {"pp": s[:, 0:513], "aa": s[:, 520:1033], "bb": s[:, 1040:1553], "p": k.R[:, TN * h:TN * h + TN],
         "step": (k.W[:, 8704:9216], k.rope[:, :])[h], "first": k.V[:, 4608:5120]}
    for j, name in enumerate(("e1b", "e2b", "e1", "e2")):
        v[name] = s[:, 2048 + TN * j:2560 + TN * j]
    return v


def l3a_pe(k, pe):
    norm_pe(k, pe, "n9", k.H, "y_added", 4, free=(("y_added", N // P), ("h_scaled", N // P)))
    norm_pe(k, pe, "n10", seqs(k.A), "n9_scaled", 2)
    pe.wait_ge(*k.at("l3a_weights", 32))
    pe.wait_ge(*k.at("n10_std", TILES))
    wb = lambda name: blocks(k.V[:, V3[name]:V3[name] + 512], 2)
    with pe.Fori(0, TILES // 2) as i:
        for par in range(2):
            t = 2 * i + par
            for n in range(6):
                pe.wait_ge(*k.at("mixed3", 6 * t + 2 * (n // 2) + 2))
                pe.wait_ge(*k.at("kvr_read", 12 * i + (par and n + 1)))
                for h in range(NH):
                    mm = pe.matmul(bank(k, n), wb("kvr"[n // 2])[:, h, (n % 2) * P:(n % 2 + 1) * P], tile(seqs((k.B, k.C, k.E)[n // 2]), h, t), start=h == 0, stop=h == 1)
                mm.then_inc(k.sem("mix_ready"), 1)
    pe.wait_ge(*k.at("kvr_read", 6 * TILES))
    with pe.Fori(0, TILES // 2) as i:
        for par in range(2):
            t = 2 * i + par
            pe.wait_ge(*k.at("wkv", 2 * t + 2))
            pe.wait_ge(*k.at("x3_done", 4 * i))
            for m in range(NH):
                for h in range(NH):
                    mm = pe.matmul(bank(k, 4 + 2 * par + m), wb("o")[:, h, m * P:(m + 1) * P], tile(seqs(k.E), h, t), start=h == 0, stop=h == 1)
                mm.then_inc(k.sem("wkv_out"), 1)
    norm_pe(k, pe, "n11", seqs(k.A), "x3_done", 2)
    pe.wait_ge(*k.at("n11_std", TILES))
    wr = blocks(k.W[:, 8192:8704], 2)
    with pe.Fori(0, TILES // 2) as i:
        for par in range(2):
            t = 2 * i + par
            pe.wait_ge(*k.at("mixed4", 4 * t + 4))
            pe.wait_ge(*k.at("cm_sig", 4 * i))
            for m in range(NH):
                for h in range(NH):
                    mm = pe.matmul(bank(k, 2 * par + m), wr[:, h, m * P:(m + 1) * P], tile(seqs(k.C), h, t), start=h == 0, stop=h == 1)
                mm.then_inc(k.sem("cm_ready"), 1)
    pe.wait_ge(*k.at("cm_sig", 2 * TILES))
    wk, wv = blocks(k.V[:, 2048:4096], 2), blocks(k.W[:, 6144:8192], 8)
    with pe.Fori(0, TILES // 2) as i:
        for par in range(2):
            t = 2 * i + par
            for m in range(8):
                pe.wait_ge(*k.at("ffk_relu", 16 * i + max(8 * par + m - 3, 0)))
                for h in range(NH):
                    mm = pe.matmul(bank(k, 4 + m % 4), wk[:, h, m * P:(m + 1) * P], tile(seqs(k.B), h, t), start=h == 0, stop=h == 1)
                mm.then_inc(k.sem("ffk_ready"), 1)
        for par in range(2):
            f = (k.E, k.Q)[par][:, :].rearrange("p (m n) -> p m n", m=8)
            pe.wait_ge(*k.at("ffk_squared", 16 * i + 8 * (par + 1)))
            pe.wait_ge(*k.at("ffv_read", 4 * i))
            for m in range(NH):
                for x in range(8):
                    mm = pe.matmul(bank(k, 2 * par + m), wv[:, x, m * P:(m + 1) * P], f[:, x, :], start=x == 0, stop=x == 7)
                mm.then_inc(k.sem("ffv_ready"), 1)


def l3a_act(k, act):
    norm_act(k, act, "n9")
    act.activation(k.small[:, 576:578], k.vec[:, VCOL["decay"]:VCOL["decay"] + 2], ACT.Exp).then_inc(k.sem("decay_exp"), 1)
    norm_act(k, act, "n10", "ln1_b", lambda h, t: yt(k, h, t))
    with act.Fori(0, TILES) as t:
        act.wait_ge(*k.at("n10_done", 2 * t + 2))
        for o, x in enumerate((k.B, k.C, k.E)):
            for h in range(NH):
                act.activation(tile(seqs(x), h, t), yt(k, h, t, 1), ACT.Copy, scale=k.vec2[:, 4 + 2 * o + h:5 + 2 * o + h]).then_inc(k.sem("before3"), 1)
    with act.Fori(0, TILES) as t:
        for n in range(6):
            act.wait_ge(*k.at("mix_ready", 6 * t + max(n, 5 if n == 4 else 0) + 1))
            dst = tile(seqs((k.D, k.Q, k.E)[n // 2]), n % 2, t)
            act.activation(dst, bank_seq(k, n), ACT.Sigmoid if n >= 4 else ACT.Copy).then_inc(k.sem("kvr_read"), 1)
    with act.Fori(0, TILES) as t:
        for h in range(NH):
            v = wkv_views(k, h)
            for j, name in enumerate(("e1b", "e2b", "e1", "e2")):
                act.wait_ge(*k.at("exp_args", 8 * t + 4 * h + j + 1))
                act.activation(v[name], v[name], ACT.Exp).then_inc(k.sem("exps"), 1)
    norm_act(k, act, "n11", "ln2_b", lambda h, t: yt(k, h, t))
    with act.Fori(0, TILES) as t:
        act.wait_ge(*k.at("n11_done", 2 * t + 2))
        for o, x in enumerate((k.B, k.C)):
            for h in range(NH):
                act.activation(tile(seqs(x), h, t), yt(k, h, t, 1), ACT.Copy, scale=k.vec2[:, 10 + 2 * o + h:11 + 2 * o + h]).then_inc(k.sem("before4"), 1)
    with act.Fori(0, TILES // 2) as i:
        for par in range(2):
            t = 2 * i + par
            act.wait_ge(*k.at("cm_ready", 2 * t + 2))
            for m in range(NH):
                act.activation(tile(seqs(k.C), m, t), bank_seq(k, 2 * par + m), ACT.Sigmoid).then_inc(k.sem("cm_sig"), 1)
    with act.Fori(0, TILES // 2) as i:
        for par in range(2):
            f = (k.E, k.Q)[par][:, :].rearrange("p (m n) -> p m n", m=8)
            act.wait_ge(*k.at("ffv_ready", 4 * i))
            for m in range(8):
                act.wait_ge(*k.at("ffk_ready", 16 * i + 8 * par + m + 1))
                act.activation(f[:, m, :], bank(k, 4 + m % 4), ACT.Relu).then_inc(k.sem("ffk_relu"), 1)


def l3a_pool(k, pool):
    with pool.Fori(0, TILES) as t:
        for h in range(NH):
            v = wkv_views(k, h)
            val = flat(k.Q, h, t)
            pool.wait_ge(*k.at("exps", 8 * t + 4 * h + 4))
            pool.tensor_tensor(v["pp"][:, 1:TN + 1], v["e2b"], val, ALU.mult).then_inc(k.sem("wkv_pool"), 1)
            pool.tensor_tensor(v["p"], v["e2"], val, ALU.mult).then_inc(k.sem("wkv_pool"), 1)
            pool.wait_ge(*k.at("sums", 4 * t + 2 * h + 2))
            pool.tensor_tensor(v["e1b"], v["e1"], v["aa"][:, 0:TN], ALU.mult).then_inc(k.sem("wkv_pool"), 1)
            pool.wait_ge(*k.at("wkv_pool", 8 * t + 4 * h + 3))
            pool.tensor_tensor(v["e1"], v["e1"], v["bb"][:, 0:TN], ALU.mult).then_inc(k.sem("wkv_pool"), 1)


def l3a_dve(k, dve):
    norm_dve(k, dve, "n9", k.H, dst=lambda h, t: tile(seqs(k.A), h, t))
    done = [0]

    def chain(ins):
        done[0] += 1
        ins.then_inc(k.sem("wkv_step"), 1)
        dve.wait_ge(*k.at("wkv_step", done[0]))
    vs = [wkv_views(k, h) for h in range(NH)]
    w = k.small[:, 576:578]
    first = vs[0]["first"]
    dve.wait_ge(*k.at("decay_exp", 1))
    chain(dve.tensor_scalar(w, w, -1.0, None, ALU.mult))
    chain(dve.memset(first, 0.0))
    chain(dve.memset(first.rearrange("p (s t) -> p s t", s=SPT)[:, :, 0:1], FIRST))
    for h in range(NH):
        chain(dve.tensor_scalar(vs[h]["step"], first, w[:, h:h + 1], None, ALU.add))
    norm_dve(k, dve, "n10", seqs(k.A), gain="ln1_g")
    with dve.Fori(0, TILES) as t:
        for o, (x, mu) in enumerate(((k.B, "mix_k"), (k.C, "mix_v"), (k.E, "mix_r"))):
            for h in range(NH):
                dve.wait_ge(*k.at("before3", 6 * t + 2 * o + h + 1))
                y = tile(seqs(x), h, t)
                dve.scalar_tensor_tensor(y, yt(k, h, t), vcol(k, mu, h), y, ALU.mult, ALU.add).then_inc(k.sem("mixed3"), 1)
    dve.wait_ge(*k.at("mix_ready", 6 * TILES))
    for h in range(NH):
        for name in ("pp", "aa", "bb"):
            chain(dve.memset(vs[h][name][:, 0:1], 0.0))
    with dve.Fori(0, TILES) as t:
        for h in range(NH):
            v, n = vs[h], 2 * t + h
            key, u = flat(k.D, h, t), vcol(k, "first", h)
            dve.wait_ge(*k.at("kvr_read", 6 * t + 6))
            dve.wait_ge(*k.at("wkv", 2 * t))
            dve.tensor_tensor_scan(v["pp"][:, 1:TN + 1], v["step"], key, 0.0, ALU.add, ALU.max).then_inc(k.sem("pp"), 1)
            dve.wait_ge(*k.at("pp", n + 1))
            dve.tensor_tensor(v["e1"], v["pp"][:, 0:TN], v["first"], ALU.add).then_inc(k.sem("pp_prev"), 1)
            dve.wait_ge(*k.at("pp_prev", n + 1))
            dve.scalar_tensor_tensor(v["p"], key, u, v["e1"], ALU.add, ALU.max).then_inc(k.sem("p_max"), 1)
            dve.scalar_tensor_tensor(v["e1b"], v["e1"], w[:, h:h + 1], v["pp"][:, 1:TN + 1], ALU.add, ALU.subtract).then_inc(k.sem("exp_args"), 1)
            dve.tensor_tensor(v["e2b"], key, v["pp"][:, 1:TN + 1], ALU.subtract).then_inc(k.sem("exp_args"), 1)
            dve.wait_ge(*k.at("p_max", n + 1))
            dve.tensor_tensor(v["e1"], v["e1"], v["p"], ALU.subtract).then_inc(k.sem("exp_args"), 1)
            dve.scalar_tensor_tensor(v["e2"], key, u, v["p"], ALU.add, ALU.subtract).then_inc(k.sem("exp_args"), 1)
        for h in range(NH):
            v = vs[h]
            dve.wait_ge(*k.at("exps", 8 * t + 4 * h + 2))
            dve.tensor_tensor_scan(v["bb"][:, 1:TN + 1], v["e1b"], v["e2b"], 0.0, ALU.mult, ALU.add).then_inc(k.sem("sums"), 1)
            dve.wait_ge(*k.at("wkv_pool", 8 * t + 4 * h + 1))
            dve.tensor_tensor_scan(v["aa"][:, 1:TN + 1], v["e1b"], v["pp"][:, 1:TN + 1], 0.0, ALU.mult, ALU.add).then_inc(k.sem("sums"), 1)
        for h in range(NH):
            v, n = vs[h], 2 * t + h
            dve.wait_ge(*k.at("wkv_pool", 8 * t + 4 * h + 3))
            dve.tensor_tensor(v["e1b"], v["e1b"], v["p"], ALU.add).then_inc(k.sem("num"), 1)
            dve.wait_ge(*k.at("wkv_pool", 8 * t + 4 * h + 4))
            dve.tensor_tensor(v["e1"], v["e1"], v["e2"], ALU.add).then_inc(k.sem("den"), 1)
            dve.wait_ge(*k.at("den", n + 1))
            dve.reciprocal(v["e1"], v["e1"]).then_inc(k.sem("den_inv"), 1)
            dve.wait_ge(*k.at("num", n + 1))
            dve.wait_ge(*k.at("den_inv", n + 1))
            dve.tensor_tensor(v["e1"], v["e1"], v["e1b"], ALU.mult).then_inc(k.sem("ratio"), 1)
            dve.wait_ge(*k.at("ratio", n + 1))
            dve.tensor_tensor(flat(k.E, h, t), flat(k.E, h, t), v["e1"], ALU.mult).then_inc(k.sem("wkv"), 1)
    with dve.Fori(0, TILES // 2) as i:
        for par in range(2):
            t = 2 * i + par
            for m in range(NH):
                dve.wait_ge(*k.at("wkv_out", 2 * t + m + 1))
                dve.tensor_tensor(tile(seqs(k.A), m, t), tile(seqs(k.A), m, t), bank_seq(k, 4 + 2 * par + m), ALU.add).then_inc(k.sem("x3_done"), 1)
    norm_dve(k, dve, "n11", seqs(k.A), gain="ln2_g")
    with dve.Fori(0, TILES) as t:
        for o, (x, mu) in enumerate(((k.B, "cm_k"), (k.C, "cm_r"))):
            for h in range(NH):
                dve.wait_ge(*k.at("before4", 4 * t + 2 * o + h + 1))
                y = tile(seqs(x), h, t)
                dve.scalar_tensor_tensor(y, yt(k, h, t), vcol(k, mu, h), y, ALU.mult, ALU.add).then_inc(k.sem("mixed4"), 1)
    with dve.Fori(0, TILES // 2) as i:
        for par in range(2):
            f = (k.E, k.Q)[par][:, :].rearrange("p (m n) -> p m n", m=8)
            for m in range(8):
                dve.wait_ge(*k.at("ffk_relu", 16 * i + 8 * par + m + 1))
                dve.tensor_tensor(f[:, m, :], f[:, m, :], f[:, m, :], ALU.mult).then_inc(k.sem("ffk_squared"), 1)
        for par in range(2):
            t = 2 * i + par
            for m in range(NH):
                c, x = tile(seqs(k.C), m, t), tile(seqs(k.A), m, t)
                dve.wait_ge(*k.at("ffv_ready", 2 * t + m + 1))
                dve.tensor_tensor(c, c, bank_seq(k, 2 * par + m), ALU.mult).then_inc(k.sem("ffv_read"), 1)
                dve.tensor_tensor(tile(k.H, m, t), tile(k.H, m, t), x, ALU.add).then_inc(k.sem("x3_added"), 1)
                dve.wait_ge(*k.at("ffv_read", 2 * t + m + 1))
                dve.wait_ge(*k.at("x3_added", 2 * t + m + 1))
                dve.tensor_tensor(tile(k.H, m, t), tile(k.H, m, t), c, ALU.add).then_inc(k.sem("l3a_done"), 1)



E3, FF3 = 8, 1024
TS = 256
TILES3 = (2 * N + E3 * (TS - 1)) // TS
TILES3 += TILES3 % 2
GROUPS = N // P


def l3f_inputs(ins, a):
    gu, down = a["L3_ffn_gate_up_w"], a["L3_ffn_down_w"]
    ins["l3f_gu"] = gu.transpose(0, 2, 1).reshape(E3, 2, P, 2 * FF3).transpose(0, 2, 1, 3).reshape(E3 * P, 4 * FF3)
    ins["l3f_down"] = down.transpose(0, 2, 1).reshape(E3, 8, P, D).transpose(0, 2, 1, 3).reshape(E3 * P, 8 * D)
    ins["l3f_gate"] = halves(a["L3_ffn_gate_w"].T)


def moe3_views(k):
    two = lambda ap: [ap[:, 512 * j:512 * j + 512].rearrange("p (s d) -> p s d", s=2) for j in range(2)]
    A = k.A
    v = {"gu": [k.W[:, 0:4096], k.B[:, :]], "down": [k.W[:, 4096:6144], k.C[:, 0:2048]],
         "rows": k.Q[:, :].rearrange("p (g d) -> p g d", g=GROUPS),
         "x": two(k.C[:, 2048:3072]), "xt": two(k.C[:, 3072:4096]), "o": two(k.V[:, 1024:2048]),
         "f": [k.D[:, 2048 * j:2048 * j + 2048].rearrange("p (m n) -> p m n", m=8) for j in range(2)],
         "gelu": [k.V[:, TS * j:TS * j + TS] for j in range(4)],
         "first": k.E[:, :].rearrange("p (g d) -> p g d", g=GROUPS), "second": k.Q[:, :].rearrange("p (g d) -> p g d", g=GROUPS),
         "out": k.B[:, :].rearrange("p (g d) -> p g d", g=GROUPS)}
    ge = lambda ap: ap.rearrange("p (g e) -> p g e", e=E3)
    v["pick2"], v["pick1"], v["tmp"] = ge(A[:, 256:384]), ge(A[:, 512:640]), ge(A[:, 0:128])
    v["m1"], v["m2"] = A[:, 1040:1056], A[:, 1056:1072]
    v["base"] = ge(A[:, 1088:1088 + 17 * E3])
    v["tiles"] = A[:, 1232:1240]
    v["start"] = A[:, 1240:1249]
    v["place"] = ge(A[:, 1280:1408])
    v["sum"] = A[:, 1408:1424]
    v["slot"] = [A[:, 1424 + 16 * j:1440 + 16 * j].bitcast(U32) for j in range(2)]
    n = TILES3 + 2
    v["le"] = ge(A[:, 1472:1472 + E3 * n])
    v["te"] = A[:, 1680:1680 + n]
    v["wrow"] = A[:, 1712:1712 + n].bitcast(U32)
    v["wrow_staged"] = [A[:, 1744 + j:1745 + j].bitcast(U32) for j in range(2)]
    return v


def clear_slots(k, sp):
    sp.wait_ge(*k.at("zeros_set", 1))
    sp.dma_start(k.slots.rearrange("t (s p) d -> p (t s) d", p=P), k.small[:, 640:896].unsqueeze(1).to_broadcast([P, 2 * TILES3, D])).then_inc(k.sem("slots_cleared"), 16)


def l3f_load(k, sp):
    v = moe3_views(k)
    sp.dma_start(k.small[:, 600:616], k.ins["l3f_gate"]).then_inc(k.sem("l3f_router"), 16)
    sp.wait_ge(*k.at("scattered", 16 * 2 * GROUPS))
    of = lambda buf, i: buf[bass.ds(i, 1)].rearrange("o (s p) d -> p (o s) d", p=P)
    for j in range(2):
        sp.dma_start(v["x"][j], of(k.slots, j)).then_inc(k.sem(f"x_in{j}"), 16)
    with sp.Fori(0, TILES3 // 2 - 1) as i:
        for j in range(2):
            sp.wait_ge(*k.at("slots_turned", 2 * i + j + 1))
            sp.dma_start(v["x"][j], of(k.slots, 2 * i + j + 2)).then_inc(k.sem(f"x_in{j}"), 16)
            sp.wait_ge(*k.at("o_copied", 2 * i + j + 1))
            sp.dma_start(of(k.results, 2 * i + j), v["o"][j]).then_inc(k.sem(f"o_out{j}"), 16)
    for j in range(2):
        sp.wait_ge(*k.at("o_copied", TILES3 - 1 + j))
        sp.dma_start(of(k.results, TILES3 - 2 + j), v["o"][j]).then_inc(k.sem(f"o_out{j}"), 16)


def store(k, sp):
    out = k.out.rearrange("(g p) d -> p g d", p=P)
    for q in range(4):
        sp.wait_ge(*k.at("l3f_done", 4 * q + 4))
        sp.dma_start(out[:, 4 * q:4 * q + 4], moe3_views(k)["out"][:, 4 * q:4 * q + 4]).then_inc(k.sem("stored"), 16)
    sp.wait_ge(*k.at("stored", 4 * 16))


def l3f_pool(k, pool):
    v = moe3_views(k)

    def row(idx, j):
        return bass.IndirectOffsetOnAxis(ap=idx[:, j:j + 1], axis=0)

    def weights(par, what, rows):
        pool.indirect_dma_start(v[what][par], None, k.ins["l3f_" + what], rows).then_inc(k.sem(f"expert_in{par}"), 16)
    def go():
        pool.sem_inc(k.sem("weights_go"), 1)
    pool.wait_ge(*k.at("slots_known", 1))
    weights(0, "gu", row(v["wrow"], 0))
    weights(0, "down", row(v["wrow"], 0))
    pool.wait_ge(*k.at("slots_cleared", 16))
    slots = k.slots.rearrange("t s d -> (t s) d")
    for g in range(GROUPS):
        if g % 2 == 0:
            pool.wait_ge(*k.at("rows_copied", g // 2 + 1))
        for j in range(2):
            pool.indirect_dma_start(slots, row(v["slot"][j], g), v["rows"][:, g], None).then_inc(k.sem("scattered"), 16)
    weights(1, "gu", row(v["wrow"], 1))
    weights(1, "down", row(v["wrow"], 1))
    with pool.Fori(1, TILES3 // 2) as i:
        for par in range(2):
            pool.wait_ge(*k.at("hact", 8 * (2 * i + par - 1)))
            pool.wait_ge(*k.at("row_staged", 2 * i + par - 1))
            go()
            weights(par, "gu", row(v["wrow_staged"][par], 0))
            pool.wait_ge(*k.at("down_ready", 2 * i + par - 1))
            go()
            weights(par, "down", row(v["wrow_staged"][par], 0))
    for j in range(2):
        pool.wait_ge(*k.at(f"o_out{j}", 16 * TILES3 // 2))
    results = k.results.rearrange("t s d -> (t s) d")
    for g in range(GROUPS):
        for j, dst in enumerate(("first", "second")):
            pool.indirect_dma_start(v[dst][:, g], None, results, row(v["slot"][j], g)).then_inc(k.sem(f"back{g // 4}"), 16)


def l3f_pe(k, pe):
    v = moe3_views(k)
    norm_pe(k, pe, "n12", k.H, "l3a_done", 2, free=(("ffv_read", 2 * TILES),))
    pe.wait_ge(*k.at("l3f_router", 16))
    logits_pe(k, pe, "l3f", "n12_scaled", blocks(k.small[:, 600:616], 2), E3, 1)
    pe.wait_ge(*k.at("l3f_chosen", 1))
    chosen = k.A[:, 768:768 + GROUPS * E3]
    pe.matmul(k.PS[:, 4, 0:P], k.causal, chosen, start=True, stop=True)
    pe.matmul(k.PS[:, 4, P:2 * P], k.mean_w[:, :], chosen, start=True, stop=True).then_inc(k.sem("ranks"), 1)
    for q in range(GROUPS // 2):
        if q >= 2:
            pe.wait_ge(*k.at("rows_copied", q - 1))
        for s in range(2):
            for h in range(NH):
                mm = pe.transpose(k.PS[:, 6 + q % 2, (2 * s + h) * P:(2 * s + h + 1) * P], k.Y[:, h, q, PAD + s * P:PAD + s * P + P], k.ident[:, :])
        mm.then_inc(k.sem("rows_turned"), 1)

    def turn(par, count):
        pe.wait_ge(*k.at(f"x_in{par}", count))
        for h in range(NH):
            for s in range(2):
                mm = pe.transpose(k.PS[:, 6 + par, h * TS + s * P:h * TS + (s + 1) * P], v["x"][par][:, s, h * P:(h + 1) * P], k.ident[:, :])
        mm.then_inc(k.sem("slots_turned"), 1)

    def products(i, par, last):
        j = 2 * i + par
        gu, down = blocks(v["gu"][par], 2), blocks(v["down"][par], 8)
        pe.wait_ge(*k.at(f"expert_in{par}", 32 * i + 32, positive=True))
        pe.wait_ge(*k.at("slots_copied", j + 1))
        for m in range(8):
            pe.wait_ge(*k.at("hact", 16 * i + max(8 * par + m - 3, 0)))
            for o in range(2):
                for h in range(NH):
                    mm = pe.matmul(k.PS[:, m % 4, o * TS:(o + 1) * TS], gu[:, h, FF3 * o + m * P:FF3 * o + (m + 1) * P], v["xt"][par][:, h], start=h == 0, stop=h == 1)
            mm.then_inc(k.sem("gu_ready"), 1)
        if not last:
            turn(1 - par, 16 * (i + par) + 16)
        pe.wait_ge(*k.at("o_copied", 2 * i))
        for s in range(2):
            for x in range(8):
                if s == 0:
                    pe.wait_ge(*k.at("hact", 8 * j + x + 1))
                mm = pe.matmul(k.PS[:, 4 + par, s * D:(s + 1) * D], v["f"][par][:, x, s * P:(s + 1) * P], down[:, x, :], start=x == 0, stop=x == 7)
        mm.then_inc(k.sem("down_ready"), 1)

    pe.wait_ge(*k.at("rows_copied", GROUPS // 2))
    turn(0, 16)
    with pe.Fori(0, TILES3 // 2 - 1) as i:
        for par in range(2):
            products(i, par, False)
    products(TILES3 // 2 - 1, 0, False)
    products(TILES3 // 2 - 1, 1, True)
    pe.wait_ge(*k.at("o_copied", TILES3))
    for q in range(GROUPS // 2):
        for s in range(2):
            for h in range(NH):
                mm = pe.transpose(k.PS[:, q, (2 * s + h) * P:(2 * s + h + 1) * P], k.H[:, h, q, s * P:(s + 1) * P], k.ident[:, :])
        mm.then_inc(k.sem("out_turned"), 1)


def l3f_act(k, act):
    v = moe3_views(k)
    norm_act(k, act, "n12")
    route_act(k, act, "l3f", E3, 0)
    for q in range(GROUPS // 2):
        act.wait_ge(*k.at("rows_turned", q + 1))
        act.activation(v["rows"][:, 2 * q:2 * q + 2], k.PS[:, 6 + q % 2, :].rearrange("p (g d) -> p g d", g=2), ACT.Copy).then_inc(k.sem("rows_copied"), 1)

    def turned(par, count):
        act.wait_ge(*k.at("slots_turned", count))
        act.activation(v["xt"][par], k.PS[:, 6 + par, :].rearrange("p (h t) -> p h t", h=NH), ACT.Copy).then_inc(k.sem("slots_copied"), 1)

    def gelus(i, par):
        for m in range(8):
            act.wait_ge(*k.at("gu_ready", 16 * i + 8 * par + m + 1))
            act.activation(v["gelu"][m % 4], k.PS[:, m % 4, 0:TS], ACT.Gelu).then_inc(k.sem("gelu3"), 1)
    turned(0, 1)
    with act.Fori(0, TILES3 // 2 - 1) as i:
        for par in range(2):
            gelus(i, par)
            turned(1 - par, 2 * i + par + 2)
    gelus(TILES3 // 2 - 1, 0)
    turned(1, TILES3)
    gelus(TILES3 // 2 - 1, 1)


def slots_dve(k, dve, chain):
    v = moe3_views(k)
    base, start, place = v["base"], v["start"], v["place"]
    wide = lambda ap: ap.unsqueeze(1).to_broadcast([P, GROUPS, E3])
    chain(dve.memset(base[:, 0], 0.0))
    chain(dve.memset(start[:, 0:1], 0.0))
    dve.wait_ge(*k.at("ranks", 1))
    for g in range(GROUPS):
        chain(dve.tensor_tensor(base[:, g + 1], base[:, g], k.PS[:, 4, P + E3 * g:P + E3 * (g + 1)], ALU.add))
    chain(dve.tensor_scalar(v["tiles"], base[:, GROUPS], 0.5 - 0.5 / TS, ROUND, ALU.add, ALU.add))
    chain(dve.tensor_scalar(v["tiles"], v["tiles"], -ROUND, None, ALU.add))
    for e in range(E3):
        chain(dve.tensor_tensor(start[:, e + 1:e + 2], start[:, e:e + 1], v["tiles"][:, e:e + 1], ALU.add))
    chain(dve.tensor_tensor(place, base[:, 0:GROUPS], wide(start[:, 0:E3]), ALU.add))
    chain(dve.scalar_tensor_tensor(place, place, float(TS), k.PS[:, 4, 0:P].rearrange("p (g e) -> p g e", e=E3), ALU.mult, ALU.add))
    for j, pick in enumerate((v["pick1"], v["pick2"])):
        chain(dve.tensor_tensor(v["tmp"], pick, place, ALU.mult))
        chain(dve.tensor_reduce(v["sum"], v["tmp"], AX.X, ALU.add))
        chain(dve.tensor_scalar(v["slot"][j], v["sum"], -1.0, None, ALU.add))
    number = k.attc[:, 4 * P + 28:4 * P + 54].unsqueeze(2).to_broadcast([P, TILES3 + 2, E3])
    chain(dve.tensor_tensor(v["le"], number, start[:, 1:E3 + 1].unsqueeze(1).to_broadcast([P, TILES3 + 2, E3]), ALU.is_ge))
    chain(dve.tensor_reduce(v["te"], v["le"], AX.X, ALU.add))
    chain(dve.tensor_scalar(v["te"], v["te"], float(E3 - 1), float(P), ALU.min, ALU.mult))
    dve.tensor_scalar(v["wrow"], v["te"], k.attc[:, 4 * P + 54:4 * P + 55], None, ALU.add).then_inc(k.sem("slots_known"), 1)


def l3f_dve(k, dve):
    v = moe3_views(k)
    norm_dve(k, dve, "n12", k.H, dst=lambda h, t: yt(k, h, t))
    chain = route_dve(k, dve, "l3f", E3, 1, 0.0, None, 0, sparse=True)
    slots_dve(k, dve, chain)

    def hidden(i, par):
        for m in range(8):
            dve.wait_ge(*k.at("gelu3", 16 * i + 8 * par + m + 1))
            dve.tensor_tensor(v["f"][par][:, m, :], v["gelu"][m % 4], k.PS[:, m % 4, TS:2 * TS], ALU.mult).then_inc(k.sem("hact"), 1)
            if m == 0:
                dve.tensor_copy(v["wrow_staged"][par], v["wrow"][:, bass.ds(2 * i + par + 2, 1)]).then_inc(k.sem("row_staged"), 1)
        dve.wait_ge(*k.at("down_ready", 2 * i + par + 1))
        dve.wait_ge(*k.at(f"o_out{par}", 16 * i))
        dve.tensor_copy(v["o"][par], k.PS[:, 4 + par, :].rearrange("p (s d) -> p s d", s=2)).then_inc(k.sem("o_copied"), 1)
    with dve.Fori(0, TILES3 // 2) as i:
        for par in range(2):
            hidden(i, par)
    for q in range(4):
        dve.wait_ge(*k.at(f"back{q}", 16 * 8))
        dve.wait_ge(*k.at("out_turned", 2 * q + 2))
        for g in range(4 * q, 4 * q + 4):
            dve.scalar_tensor_tensor(v["out"][:, g], v["second"][:, g], v["m2"][:, g:g + 1], k.PS[:, g // 2, g % 2 * D:(g % 2 + 1) * D], ALU.mult, ALU.add).then_inc(k.sem("second_in"), 1)
        for g in range(4 * q, 4 * q + 4):
            dve.wait_ge(*k.at("second_in", g + 1))
            dve.scalar_tensor_tensor(v["out"][:, g], v["first"][:, g], v["m1"][:, g:g + 1], v["out"][:, g], ALU.mult, ALU.add).then_inc(k.sem("l3f_done"), 1)


def more_inputs(ins, a):
    l0f_inputs(ins, a)
    l1a_inputs(ins, a)
    l1f_inputs(ins, a)
    l2a_inputs(ins, a)
    l2f_inputs(ins, a)
    l3a_inputs(ins, a)
    l3f_inputs(ins, a)
    return


SP_STAGES = [l0a_load, clear_slots, l0f_load, l1a_load, l1f_load, l2a_load, l2f_load, l3a_load, l3f_load]
POOL_STAGES = [l0a_pool, l1a_pool, l1f_pool, l2a_pool, l2f_pool, l3a_pool, l3f_pool]
PE_STAGES = [l0a_pe, l0f_pe, l1a_pe, l1f_pe, l2a_pe, l2f_pe, l3a_pe, l3f_pe]
ACT_STAGES = [l0a_act, l0f_act, l1a_act, l1f_act, l2a_act, l2f_act, l3a_act, l3f_act]
DVE_STAGES = [l0a_dve, l0f_dve, l1a_dve, l1f_dve, l2a_dve, l2f_dve, l3a_dve, l3f_dve]



def build(nc, ins, out):
    with ExitStack() as ctx:
        k = Kernel(nc, ctx, ins, out)
        allocate(k)
        k.slots = nc.dram_tensor("slots", (TILES3, TS, D), F32, kind="Internal").ap()
        k.results = nc.dram_tensor("results", (TILES3, TS, D), F32, kind="Internal").ap()
        block = ctx.enter_context(nc.Block())

        @block.sync
        def _(sp):
            for name in PRIMED:
                sp.sem_inc(k.sem(name), 1)
            load_constants(k, sp)
            tok_load(k, sp)
            for f in SP_STAGES:
                f(k, sp)
            store(k, sp)

        @block.gpsimd
        def _(pool):
            pool.memset(k.small[:, 640:896], 0.0).then_inc(k.sem("zeros_set"), 1)
            tok_pool(k, pool)
            for f in POOL_STAGES:
                f(k, pool)

        @block.tensor
        def _(pe):
            tok_pe(k, pe)
            for f in PE_STAGES:
                f(k, pe)

        @block.scalar
        def _(act):
            tok_act(k, act)
            for f in ACT_STAGES:
                f(k, act)

        @block.vector
        def _(dve):
            tok_dve(k, dve)
            for f in DVE_STAGES:
                f(k, dve)
        assert not k.unprimed, sorted(k.unprimed)



def halves(a):
    r, m = a.shape
    return a.reshape(r // P, P, m).transpose(1, 0, 2).reshape(P, -1)


def constants():
    f = np.float32
    c = {}
    c["c_ident"] = np.eye(P, dtype=f)
    c["c_mean"] = np.full((P, P), 1.0 / D, f)
    p = np.arange(P)
    theta = f(1.0) / np.power(f(10000.0), np.arange(8, dtype=f) / f(8))
    ang = np.outer(np.arange(T, dtype=f), theta).astype(f)
    cos, sin = np.cos(ang).astype(f), np.sin(ang).astype(f)
    sign = np.where(p % 16 < 8, f(-1), f(1))
    c["c_rope"] = np.concatenate([cos[:, p % 8].T, (sin[:, p % 8] * sign).T], axis=1).astype(f)
    perm = np.zeros((P, P), f)
    perm[p ^ 8, p] = 1.0
    q, key = np.arange(64)[:, None], np.arange(P)[None, :]
    first = np.where(key <= q, 0.0, -4e9)
    later = np.where((key - 64 <= q) & (q - (key - 64) < 64), 0.0, -4e9)
    band = np.concatenate([np.tile(first, (2, 1)), np.tile(later, (2, 1))], axis=1)
    causal = (p[:, None] <= p[None, :]).astype(f)
    gm = (p[:, None] // 16 % 4 == np.arange(4)[None, :]).astype(f)
    hm = (p[:, None] // 16 == np.arange(8)[None, :]).astype(f)
    rev = np.tile(16.0 - np.arange(16), (P, 1))
    slot_tile = np.concatenate([np.tile(np.arange(26), (P, 1)), p[:, None]], axis=1)
    c["c_att"] = np.concatenate([perm, band, causal, gm, hm, rev, slot_tile], axis=1).astype(f)
    fi = np.zeros((P, N // P), f)
    fi[0, ::2] = 1.0
    c["c_first"] = fi
    return c


def kernel(**x):
    import concourse.bacc as _bacc
    from concourse.bass_utils import run_bass_kernel_spmd as _run
    import ml_dtypes

    a = {n: np.ascontiguousarray(v) for n, v in x.items()}
    ins = constants()
    ins["c_identb"] = np.eye(P, dtype=ml_dtypes.bfloat16)
    tok = a["x"]
    ins["tok"] = tok.reshape(N // P, P).T
    ins["tok_prev"] = np.concatenate([np.zeros((B, 1), tok.dtype), tok[:, :-1]], axis=1).reshape(N // P, P).T
    ins["scale"] = a["L0_tok_scale"].reshape(1, 1)
    ins["embed"] = a["L0_tok_embed_weight"]
    ins["projT"] = a["L0_tok_proj_weight"].T
    jt, j2, g, d = np.meshgrid(np.arange(2), np.arange(2), np.arange(4), np.arange(16), indexing="ij")
    order = ((4 * g + 2 * jt + j2) * 16 + d).reshape(-1)
    dup = np.tile(np.arange(64), 2)
    v = {"bq": a["L0_attn_bq"][order], "bk": np.concatenate([a["L0_attn_bk"][dup], a["L0_attn_bk"][dup]]),
         "bo": a["L0_attn_bo"], "g1": a["L0_attn_g1"],
         "b1": a["L0_attn_b1"], "g2": a["L0_attn_g2"], "b2": a["L0_attn_b2"], "bf2": a["L0_attn_bf2"],
         "D": a["L1_attn_D"], "mu_r": a["L1_ffn_mu_r"], "mu_k": a["L1_ffn_mu_k"], "bgk2": a["L2_attn_bgk2"],
         "gamma": a["L2_attn_gamma"], "beta": a["L2_attn_beta"], "ln1_g": a["L3_attn_ln1_g"],
         "ln1_b": a["L3_attn_ln1_b"], "ln2_g": a["L3_attn_ln2_g"], "ln2_b": a["L3_attn_ln2_b"],
         "decay": a["L3_attn_time_decay"], "first": a["L3_attn_time_first"], "mix_k": a["L3_attn_time_mix_k"],
         "mix_v": a["L3_attn_time_mix_v"], "mix_r": a["L3_attn_time_mix_r"], "cm_k": a["L3_attn_cm_k"],
         "cm_r": a["L3_attn_cm_r"]}
    ins["vecs"] = np.concatenate([v[n].reshape(NH, P).T for n in VECS] + [a["L0_attn_bf1"].reshape(8, P).T], axis=1)
    ins["l0a_w"] = np.concatenate([halves(a["L0_attn_Wq"][:, order]), halves(a["L0_attn_Wk"][:, dup]), halves(a["L0_attn_Wv"]),
                                   halves(a["L0_attn_Wo"][order]), halves(a["L0_attn_Wf1"]), halves(a["L0_attn_Wf2"])], axis=1)
    ins["bv"] = a["L0_attn_bv"].reshape(1, 64)
    more_inputs(ins, a)

    nc = _bacc.Bacc("TRN2", target_bir_lowering=False, num_devices=1)
    arrays, aps = {}, {}
    for name, arr in ins.items():
        arr = np.ascontiguousarray(arr)
        arrays["in_" + name] = arr
        aps[name] = nc.dram_tensor("in_" + name, arr.shape, mybir.dt.from_np(arr.dtype), kind="ExternalInput").ap()
    out = nc.dram_tensor("out_0", (N, D), F32, kind="ExternalOutput").ap()
    build(nc, aps, out)
    r = _run(nc, [arrays], core_ids=[0])
    got = r.results[0]["out_0"]
    return got.reshape(B, T, D)
```

```python
from contextlib import ExitStack

import numpy as np
import concourse.bass as bass
from concourse import mybir

F32 = mybir.dt.float32
BF16 = mybir.dt.bfloat16
I32 = mybir.dt.int32
U32 = mybir.dt.uint32
ACT = mybir.ActivationFunctionType
ALU = mybir.AluOpType
AX = mybir.AxisListType

P = 128
D = 256
NH = D // P
B, T = 8, 256
N = B * T
TN = 512
TILES = N // TN
SPT = TN // T
PAD = 2
EPS = 1e-5
ROUND = 12582912.0

NORMS = {f"n{j}": j for j in range(13)}
WITH_BIAS = ["n1", "n2", "n7", "n10", "n11"]
NORM_COUNT = {"mean": TILES, "var": TILES, "std": TILES, "rstd": TILES, "centred": 2 * TILES, "squared": 2 * TILES,
              "scaled": 2 * TILES, "done": 2 * TILES}

VECS = ["bq", "bk", "bo", "g1", "b1", "g2", "b2", "bf2", "D", "mu_r", "mu_k", "bgk2", "gamma", "beta",
        "ln1_g", "ln1_b", "ln2_g", "ln2_b", "decay", "first", "mix_k", "mix_v", "mix_r", "cm_k", "cm_r"]
VCOL = {n: 2 * i for i, n in enumerate(VECS)}
NV = 2 * len(VECS)
BF1 = NV
NVEC = NV + 8


PRIMED = [
    "att+kv_turned+y_turned+l3f_rows_turned+l3f_ranks+l3f_slots_t",
    "att_out+l0f_rows_copied+softplus2+exps+cm_sig+l3f_rows_copie", "cos_done+moe_h+summed+gate_sums+x_clip+pp",
    "emb_copied+qk_copied+shared_silu+moe_silu+before+qkv_read+xq",
    "emb_proj+qk_ready+l0f_rows_turned+l0f_ranks+moe_in+fourier_i",
    "emb_turned+swapped+shared_in+moe_down+ssm_out+gate_ready+xq_", "exp_done+rk_read+gate_read+h_gelu+kvr_read",
    "factors", "ff1+shared_out+l0f_slots_turned+g_ready", "ff2+l0f_back_turned+l2a_ready",
    "ff_read+l2a_read+hid_127+ffv_read+l3f_done", "g_read", "gelu_done+l0f_slots_copied+softplus3+before4+gelu3",
    "h0_done", "h_quantised+l3a_done+l3f_o_copied", "h_shifted+x3_done+hact", "kv_copied", "l0a_done",
    "l0f_o_copied+ssm_read+gate_to_mid+x_scale+p_max", "l0f_o_out0+l3f_o_out0", "l0f_o_out1+l3f_o_out1",
    "l0f_o_out2+l3f_o_out2", "l0f_x_in0+l3f_x_in0", "l0f_x_in1+l3f_x_in1", "l0f_x_in2+l3f_x_in2",
    "mask_ready+keys_spread+state+hid_clip+ratio", "max_scaled+l0f_second+mixed+to_end+x_shifted+sums", "norm_centred",
    "norm_done", "norm_mean", "norm_rstd", "norm_scaled", "norm_squared", "norm_std", "norm_var",
    "probs+v_spread+hid_max+den_inv", "probs_copied+softplus1+hq_copied+ffk_relu+l3f_slots_copied",
    "probs_turned+v_ready+gla_att+hq_turned+ffk_ready+gu_ready", "rotated+shared_done+turned_out+to_mid+x_inv+pp_prev",
    "row_inv+l1f_done+gla_masked+h_scaled+den", "row_max+moe_out+l1a_done+clamped+x_127+exp_args",
    "row_sum+l0f_summed+v_read+decayed+x_quantised+num", "scores+rk_ready+gla_scores+h_ready+cm_ready",
    "seq_staged+sum_in+k_squared+keys_staged+tile_staged",
    "swap_used+shared_hid+l0f_row_staged+turned_in+log_gate+x_max", "values+v_turned+y_ready+ffv_ready+down_ready",
    "values_spread+gla_out+hid_inv+mixed4", "wo_done+gated+hid_scale+wkv+l3f_row_staged+second_in",
    "wo_ready+state_sum", "x3_added", "y_added", "y_scaled", "z_ready+q_spread+wkv_pool",
]

SHARED = [
    [("emb_proj", 8), ("qk_ready", 12), ("l0f_rows_turned", 8), ("l0f_ranks", 1), ("moe_in", 30), ("fourier_in", 8), ("qkv_ready", 28), ("x_turned", 16), ("mix_ready", 24)],
    [("emb_turned", 4), ("swapped", 12), ("shared_in", 4), ("moe_down", 30), ("ssm_out", 8), ("gate_ready", 8), ("xq_turned", 16), ("wkv_out", 8)],
    [("scores", 32), ("rk_ready", 16), ("gla_scores", 32), ("h_ready", 16), ("cm_ready", 8)],
    [("probs_turned", 64), ("v_ready", 8), ("gla_att", 32), ("hq_turned", 16), ("ffk_ready", 32), ("gu_ready", 192)],
    [("values", 8), ("v_turned", 8), ("y_ready", 16), ("ffv_ready", 8), ("down_ready", 24)],
    [("att", 32), ("kv_turned", 8), ("y_turned", 16), ("l3f_rows_turned", 8), ("l3f_ranks", 1), ("l3f_slots_turned", 24), ("out_turned", 8)],
    [("wo_ready", 8), ("state_sum", 8)],
    [("ff1", 32), ("shared_out", 4), ("l0f_slots_turned", 30), ("g_ready", 8)],
    [("ff2", 8), ("l0f_back_turned", 8), ("l2a_ready", 8)],
    [("emb_copied", 4), ("qk_copied", 12), ("shared_silu", 4), ("moe_silu", 30), ("before", 16), ("qkv_read", 28), ("xq_copied", 16), ("before3", 24)],
    [("exp_done", 32), ("rk_read", 16), ("gate_read", 8), ("h_gelu", 16), ("kvr_read", 24)],
    [("probs_copied", 64), ("softplus1", 8), ("hq_copied", 16), ("ffk_relu", 32), ("l3f_slots_copied", 24)],
    [("att_out", 32), ("l0f_rows_copied", 8), ("softplus2", 8), ("exps", 32), ("cm_sig", 8), ("l3f_rows_copied", 8)],
    [("gelu_done", 32), ("l0f_slots_copied", 30), ("softplus3", 8), ("before4", 16), ("gelu3", 192)],
    [("factors", 24)], [("kv_copied", 8)], [("g_read", 8)],
    [("swap_used", 12), ("shared_hid", 4), ("l0f_row_staged", 30), ("turned_in", 16), ("log_gate", 8), ("x_max", 16), ("mixed3", 24), ("ffk_squared", 32)],
    [("cos_done", 12), ("moe_h", 30), ("summed", 8), ("gate_sums", 8), ("x_clip", 16), ("pp", 8)],
    [("rotated", 12), ("shared_done", 8), ("turned_out", 16), ("to_mid", 8), ("x_inv", 16), ("pp_prev", 8)],
    [("l0f_o_copied", 30), ("ssm_read", 8), ("gate_to_mid", 8), ("x_scale", 16), ("p_max", 8)],
    [("row_max", 32), ("moe_out", 8), ("l1a_done", 8), ("clamped", 8), ("x_127", 16), ("exp_args", 32)],
    [("max_scaled", 32), ("l0f_second", 16), ("mixed", 16), ("to_end", 8), ("x_shifted", 16), ("sums", 16)],
    [("row_sum", 32), ("l0f_summed", 16), ("v_read", 8), ("decayed", 16), ("x_quantised", 16), ("num", 8)],
    [("row_inv", 32), ("l1f_done", 8), ("gla_masked", 32), ("h_scaled", 16), ("den", 8)],
    [("probs", 32), ("v_spread", 8), ("hid_max", 16), ("den_inv", 8)],
    [("mask_ready", 1), ("keys_spread", 8), ("state", 8), ("hid_clip", 16), ("ratio", 8)],
    [("values_spread", 16), ("gla_out", 32), ("hid_inv", 16), ("mixed4", 16)],
    [("wo_done", 8), ("gated", 8), ("hid_scale", 16), ("wkv", 8), ("l3f_row_staged", 24), ("second_in", 16)],
    [("ff_read", 8), ("l2a_read", 8), ("hid_127", 16), ("ffv_read", 8), ("l3f_done", 16)],
    [("h_shifted", 16), ("x3_done", 8), ("hact", 192)], [("h_quantised", 16), ("l3a_done", 8), ("l3f_o_copied", 24)],
    [("seq_staged", 16), ("sum_in", 8), ("k_squared", 8), ("keys_staged", 8), ("tile_staged", 4)],
    [("z_ready", 8), ("q_spread", 32), ("wkv_pool", 32)],
    [("l0f_scattered", 512), ("l3f_scattered", 512)],
] + [[(f"l0f_{what}{p}", 160), (f"l3f_{what}{p}", count)] for p in range(3) for what, count in (("x_in", 192), ("o_out", 192), ("expert_in", 384))
] + [[(f"l0f_back{q}", 128), (f"l3f_back{q}", 128)] for q in range(4)]
PLACE = {}
for _row in SHARED:
    _base = 0
    for _name, _count in _row:
        PLACE[_name] = ("+".join(n for n, _ in _row)[:60], _base)
        _base += _count


class Kernel:

    def __init__(self, nc, ctx, ins, out):
        self.nc, self.ctx, self.ins, self.out = nc, ctx, ins, out
        self.sems = {}
        self.unprimed = set()

    def sem(self, name):
        if name.split("_")[0] in NORMS:
            name = "norm_" + name.split("_")[1]
        name = PLACE.get(name, (name, 0))[0]
        if name not in self.sems:
            self.sems[name] = self.ctx.enter_context(self.nc.semaphore(name))
        return self.sems[name]

    def at(self, name, count, positive=False):
        norm, _, what = name.partition("_")
        if norm in NORMS:
            name = "norm_" + what
            count = count + NORM_COUNT[what] * (NORMS[norm] if what != "done" else WITH_BIAS.index(norm))
        name, before = PLACE.get(name, (name, 0))
        count = count + before
        if type(count) is not int and name not in PRIMED and not positive:
            self.unprimed.add(name)
        return self.sem(name), count + (1 if name in PRIMED else 0)

    def sb(self, name, cols, dt=F32, parts=P):
        return self.ctx.enter_context(self.nc.sbuf_tensor(name, [parts, cols], dt))


def seqs(buf):
    return buf[:, 0:NH * N].rearrange("p (h s t) -> p h s t", h=NH, s=B)


def tile(view, h, t):
    return view[:, h, bass.ds(t * SPT, SPT), :]


def blocks(ap, k):
    return ap.rearrange("p (k m) -> p k m", k=k)


def allocate(k):
    nc = k.nc
    k.H = seqs(k.sb("residual", NH * N))
    k.Ybuf = k.sb("normed", NH * B * (T + PAD))
    k.Y = k.Ybuf[:, :].rearrange("p (h s t) -> p h s t", h=NH, s=B)
    for n in "ABCDEQ":
        k.raw = k.sb("buf" + n, NH * N)
        if n == "A": k.A = k.raw
        if n == "B": k.B = k.raw
        if n == "C": k.C = k.raw
        if n == "D": k.D = k.raw
        if n == "E": k.E = k.raw
        if n == "Q": k.Q = k.raw
    k.R = k.sb("rstd", 2 * TN)
    k.W = k.sb("weights0", 9344)
    k.V = k.sb("weights1", 5504)
    k.ident = k.sb("ident", P)
    k.identb = k.sb("identb", P, BF16)
    k.mean_w = k.sb("mean_w", P)
    k.vec = k.sb("vec", NVEC)
    k.vec2 = k.sb("vec2", 24)
    k.rope = k.sb("rope", 2 * T)
    k.attc = k.sb("attc", 4 * P + 4 + 8 + 16 + 34)
    k.perm = k.attc[:, 0:P]
    k.band = k.attc[:, P:3 * P].rearrange("p (m k) -> p m k", m=2)
    k.causal = k.attc[:, 3 * P:4 * P]
    k.groupmask = k.attc[:, 4 * P:4 * P + 4]
    k.headmask = k.attc[:, 4 * P + 4:4 * P + 12]
    k.small = k.sb("small", 1024)
    k.PS = k.ctx.enter_context(nc.psum_tensor("banks", [P, 8, 512], F32))
    k.eps = k.small[:, 1023:1024]


def yt(k, h, t, shift=0):
    return k.Y[:, h, bass.ds(t * SPT, SPT), PAD - shift:PAD - shift + T]


def bank(k, b):
    return k.PS[:, b, :]


def bank_seq(k, b):
    return k.PS[:, b, :].rearrange("p (s t) -> p s t", s=SPT)


def rstd(k, p):
    return k.R[:, p * TN:(p + 1) * TN].rearrange("p (s t) -> p s t", s=SPT)


def vcol(k, name, h=0):
    return k.vec[:, VCOL[name] + h:VCOL[name] + h + 1]



def norm_pe(k, pe, n, src, ready, per_tile, free=()):
    for s, v in free:
        pe.wait_ge(*k.at(s, v))
    with pe.Fori(0, TILES // 2) as i:
        for par in range(2):
            t = 2 * i + par
            pe.wait_ge(*k.at(ready, per_tile * (t + 1)))
            pe.wait_ge(*k.at(n + "_centred", 4 * i))
            for h in range(NH):
                mm = pe.matmul(bank(k, par), k.mean_w[:, :], tile(src, h, t), start=h == 0, stop=h == 1)
            mm.then_inc(k.sem(n + "_mean"), 1)
    with pe.Fori(0, TILES // 2) as i:
        for par in range(2):
            t = 2 * i + par
            pe.wait_ge(*k.at(n + "_squared", 2 * (t + 1)))
            pe.wait_ge(*k.at(n + "_std", 2 * i))
            for h in range(NH):
                mm = pe.matmul(bank(k, 2 + par), k.mean_w[:, :], tile(seqs(k.Q), h, t), start=h == 0, stop=h == 1)
            mm.then_inc(k.sem(n + "_var"), 1)


def norm_act(k, act, n, bias=None, dst=None, free=()):
    for s, v in free:
        act.wait_ge(*k.at(s, v))
    with act.Fori(0, TILES) as t:
        for h in range(NH):
            act.wait_ge(*k.at(n + "_centred", 2 * t + h + 1))
            act.activation(tile(seqs(k.Q), h, t), tile(seqs(k.D), h, t), ACT.Square).then_inc(k.sem(n + "_squared"), 1)
    with act.Fori(0, TILES // 2) as i:
        for par in range(2):
            t = 2 * i + par
            act.wait_ge(*k.at(n + "_var", t + 1))
            act.wait_ge(*k.at(n + "_scaled", 4 * i))
            act.activation(k.R[:, par * TN:(par + 1) * TN], bank(k, 2 + par), ACT.Sqrt, bias=k.eps).then_inc(k.sem(n + "_std"), 1)
    if bias is not None:
        with act.Fori(0, TILES) as t:
            for h in range(NH):
                act.wait_ge(*k.at(n + "_scaled", 2 * t + h + 1))
                act.activation(dst(h, t), tile(seqs(k.D), h, t), ACT.Identity, bias=vcol(k, bias, h)).then_inc(k.sem(n + "_done"), 1)


def norm_dve(k, dve, n, src, gain=None, dst=None, free=()):
    for s, v in free:
        dve.wait_ge(*k.at(s, v))
    with dve.Fori(0, TILES // 2) as i:
        for par in range(2):
            t = 2 * i + par
            dve.wait_ge(*k.at(n + "_mean", t + 1))
            for h in range(NH):
                dve.tensor_tensor(tile(seqs(k.D), h, t), tile(src, h, t), bank_seq(k, par), ALU.subtract).then_inc(k.sem(n + "_centred"), 1)
    with dve.Fori(0, TILES // 2) as i:
        for par in range(2):
            t = 2 * i + par
            dve.wait_ge(*k.at(n + "_std", t + 1))
            dve.reciprocal(k.R[:, par * TN:(par + 1) * TN], k.R[:, par * TN:(par + 1) * TN]).then_inc(k.sem(n + "_rstd"), 1)
            dve.wait_ge(*k.at(n + "_rstd", t + 1))
            for h in range(NH):
                dve.wait_ge(*k.at(n + "_squared", 2 * t + h + 1))
                if gain is None:
                    dve.tensor_tensor(dst(h, t), tile(seqs(k.D), h, t), rstd(k, par), ALU.mult).then_inc(k.sem(n + "_scaled"), 1)
                else:
                    dve.scalar_tensor_tensor(tile(seqs(k.D), h, t), tile(seqs(k.D), h, t), vcol(k, gain, h), rstd(k, par), ALU.mult, ALU.mult).then_inc(k.sem(n + "_scaled"), 1)



def load_constants(k, sp):
    i = k.ins
    for dst, name in ((k.ident, "c_ident"), (k.mean_w, "c_mean"), (k.vec, "vecs"), (k.rope, "c_rope"), (k.attc, "c_att")):
        sp.dma_start(dst[:, :], i[name]).then_inc(k.sem("constants"), 16)
    sp.dma_start(k.identb[:, :], i["c_identb"]).then_inc(k.sem("constants"), 16)


CONST = 6 * 16


def load(k, sp, dst, src, sem):
    sp.dma_start(dst, src).then_inc(k.sem(sem), 16)



def hash_views(k):
    s = k.small[:, :].bitcast(I32)
    return [s[:, 16 * j:16 * j + 16] for j in range(20)]


def tok_load(k, sp):
    i = k.ins
    v = hash_views(k)
    sp.dma_start(v[0], i["tok"]).then_inc(k.sem("tok_in"), 16)
    sp.dma_start(v[1], i["tok_prev"]).then_inc(k.sem("tok_in"), 16)
    sp.dma_start(k.small[:, 320:336], i["c_first"]).then_inc(k.sem("tok_in"), 16)
    sp.dma_start(k.small[:, 336:337], i["scale"].to_broadcast([P, 1])).then_inc(k.sem("tok_in"), 16)
    sp.dma_start(k.W[0:64, 0:256], i["projT"]).then_inc(k.sem("tok_in"), 16)


def tok_dve(k, dve):
    v = hash_views(k)
    f = k.small
    done = [0]

    def chain(ins):
        done[0] += 1
        ins.then_inc(k.sem("hash_step"), 1)
        dve.wait_ge(*k.at("hash_step", done[0]))
    dve.memset(k.eps, EPS).then_inc(k.sem("eps_set"), 1)
    dve.memset(k.Y[:, :, :, 0:PAD], 0.0).then_inc(k.sem("pad_set"), 1)
    dve.wait_ge(*k.at("constants", CONST))
    for j, name in enumerate(["mu_r", "mu_k", "mix_k", "mix_v", "mix_r", "cm_k", "cm_r"]):
        dve.tensor_scalar(k.vec2[:, 2 * j:2 * j + 2], k.vec[:, VCOL[name]:VCOL[name] + 2], -1.0, 1.0, ALU.mult, ALU.add).then_inc(k.sem("rest_ready"), 1)
    dve.wait_ge(*k.at("tok_in", 80))
    limbs = []
    for src, mul, o in ((0, 36313, 2), (1, 27191, 9)):
        lo, hi, p0, p1, mid, a, b = v[o:o + 7]
        chain(dve.tensor_scalar(lo, v[src], 255, None, ALU.bitwise_and))
        chain(dve.tensor_scalar(hi, v[src], 8, None, ALU.logical_shift_right))
        chain(dve.tensor_scalar(p0, lo, float(mul), None, ALU.mult))
        chain(dve.tensor_scalar(p1, hi, float(mul), None, ALU.mult))
        chain(dve.tensor_scalar(mid, p1, 255, 8, ALU.bitwise_and, ALU.logical_shift_left))
        chain(dve.tensor_tensor(p0, p0, mid, ALU.add))
        chain(dve.tensor_scalar(a, p0, 65535, None, ALU.bitwise_and))
        chain(dve.tensor_scalar(b, p0, 16, None, ALU.logical_shift_right))
        chain(dve.tensor_scalar(p1, p1, 8, None, ALU.logical_shift_right))
        chain(dve.tensor_tensor(b, b, p1, ALU.add))
        limbs.append((a, b))
    (a0, b0), (a1, b1) = limbs
    chain(dve.tensor_tensor(a0, a0, a1, ALU.bitwise_xor))
    chain(dve.tensor_tensor(b0, b0, b1, ALU.bitwise_xor))
    sm, neg, big = f[:, 352:368], f[:, 368:384], f[:, 384:400]
    chain(dve.tensor_tensor(sm, a0, b0, ALU.add))
    chain(dve.tensor_scalar(neg, b0, 32768.0, None, ALU.is_ge))
    chain(dve.tensor_tensor(sm, sm, neg, ALU.subtract))
    chain(dve.tensor_scalar(big, sm, 65535.0, -65535.0, ALU.is_ge, ALU.mult))
    chain(dve.tensor_tensor(sm, sm, big, ALU.add))
    first = f[:, 320:336]
    chain(dve.scalar_tensor_tensor(neg, sm, -65535.0, first, ALU.add, ALU.mult))
    chain(dve.tensor_tensor(sm, sm, neg, ALU.subtract))
    dve.tensor_copy(f[:, 400:416].bitcast(U32), sm).then_inc(k.sem("rows_known"), 1)


def tok_pool(k, pool):
    pool.wait_ge(*k.at("rows_known", 1))
    idx = k.small[:, 400:416].bitcast(U32)
    for j in range(N // P):
        pool.indirect_dma_start(k.B[:, 64 * j:64 * j + 64], None, k.ins["embed"],
                                bass.IndirectOffsetOnAxis(ap=idx[:, j:j + 1], axis=0)).then_inc(k.sem("gathered"), 16)


def tok_pe(k, pe):
    pe.wait_ge(*k.at("constants", CONST))
    pe.wait_ge(*k.at("gathered", 16 * (N // P)))
    for t in range(TILES):
        if t >= 2:
            pe.wait_ge(*k.at("emb_copied", t - 1))
        for j in range(TN // P):
            mm = pe.transpose(k.PS[0:64, t % 2, j * P:(j + 1) * P], k.B[:, 64 * (4 * t + j):64 * (4 * t + j) + 64], k.ident[:, :])
        mm.then_inc(k.sem("emb_turned"), 1)
    pe.wait_ge(*k.at("tok_in", 80))
    for t in range(TILES):
        pe.wait_ge(*k.at("emb_copied", t + 1))
        if t >= 2:
            pe.wait_ge(*k.at("h0_done", 2 * (t - 1)))
        for m in range(NH):
            pe.matmul(bank(k, 2 + 2 * (t % 2) + m), k.W[0:64, m * P:(m + 1) * P],
                      k.A[0:64, t * TN:(t + 1) * TN], start=True, stop=True).then_inc(k.sem("emb_proj"), 1)


def tok_act(k, act):
    act.wait_ge(*k.at("tok_in", 80))
    for t in range(TILES):
        act.wait_ge(*k.at("emb_turned", t + 1))
        act.activation(k.A[0:64, t * TN:(t + 1) * TN], k.PS[0:64, t % 2, :], ACT.Copy).then_inc(k.sem("emb_copied"), 1)
    for t in range(TILES):
        for m in range(NH):
            act.wait_ge(*k.at("emb_proj", 2 * t + m + 1))
            act.activation(tile(k.H, m, t), bank_seq(k, 2 + 2 * (t % 2) + m), ACT.Copy, scale=k.small[:, 336:337]).then_inc(k.sem("h0_done"), 1)



QB = T // 64
WINDOW0 = [max(0, 64 * q - 64) for q in range(QB)]
L0 = {"wq": 0, "wk": 512, "wv": 768, "wo": 896, "wf1": 1408, "wf2": 3456}


def l0a_w(k, name, cols, nk=NH):
    return blocks(k.V[:, L0[name]:L0[name] + nk * cols], nk)


def l0a_load(k, sp):
    sp.dma_start(k.V[:, 0:5504], k.ins["l0a_w"]).then_inc(k.sem("l0a_weights"), 16)
    sp.dma_start(k.small[:, 448:512], k.ins["bv"].to_broadcast([P, 64])).then_inc(k.sem("l0a_weights"), 16)


def att_views(k):
    a = {}
    a["qs"] = k.E[:, 2048:2560]
    a["ys"] = k.E[:, 2560:3072].rearrange("p (h t) -> p h t", h=2)
    a["sm"] = [k.E[:, 3072:4096].rearrange("p (a k) -> p a k", a=8), k.C[:, 3072:4096].rearrange("p (a k) -> p a k", a=8)]
    a["pt"] = [k.E[:, 0:1024].rearrange("p (a k) -> p a k", a=8), k.E[:, 1024:2048].rearrange("p (a k) -> p a k", a=8)]
    a["kz"] = k.C[:, 2048:3072].rearrange("p (g t) -> p g t", g=4)
    a["k"] = k.C[:, 0:2048].rearrange("p (s t) -> p s t", s=B)
    a["vz"] = k.Q[:, :].rearrange("p (w a m) -> p w a m", w=4, a=8)
    a["mask"] = k.R[:, 0:P].bitcast(BF16).rearrange("p (m k) -> p m k", m=2)
    a["mx"] = k.small[:, 512:528]
    a["sum"] = k.small[:, 528:544]
    return a


QKB = [(0, 1, 4), (5, 6, 7)]


def l0a_pe(k, pe):
    a = att_views(k)
    norm_pe(k, pe, "n0", k.H, "h0_done", 2, free=(("h0_done", 2 * TILES),))
    norm_pe(k, pe, "n1", seqs(k.A), "n0_scaled", 2)
    pe.wait_ge(*k.at("l0a_weights", 32))
    wq, wk = l0a_w(k, "wq", D), l0a_w(k, "wk", P)
    with pe.Fori(0, TILES // 2) as i:
        for par in range(2):
            t = 2 * i + par
            pe.wait_ge(*k.at("n1_done", 2 * (t + 1)))
            pe.wait_ge(*k.at("qk_copied", 6 * i))
            for o in range(3):
                for h in range(NH):
                    w = wk[:, h, :] if o == 2 else wq[:, h, o * P:(o + 1) * P]
                    mm = pe.matmul(bank(k, QKB[par][o]), w, yt(k, h, t), start=h == 0, stop=h == 1)
                mm.then_inc(k.sem("qk_ready"), 1)
    with pe.Fori(0, TILES // 2) as i:
        for m in range(6):
            t = 2 * i + m // 3
            pe.wait_ge(*k.at("qk_copied", 6 * i + m + 1))
            pe.wait_ge(*k.at("swap_used", 6 * i + max(m - 1, 0)))
            src = a["k"][:, bass.ds(t * SPT, SPT), :] if m % 3 == 2 else tile(seqs(k.B), m % 3, t)
            pe.matmul(bank(k, 2 + m % 2), k.perm, src, start=True, stop=True).then_inc(k.sem("swapped"), 1)

    wv = l0a_w(k, "wv", 64)

    def scores(b, q, n):
        if q == 0:
            pe.wait_ge(*k.at("keys_spread", b + 1))
            pe.wait_ge(*k.at("seq_staged", 2 * b + 1))
        if type(n) is not int or n >= 2:
            pe.wait_ge(*k.at("exp_done", n - 1, positive=True))
        for j2 in range(2):
            out = bank(k, 1 + 2 * (q % 2) + j2)
            pe.matmul(out, k.identb[:, :], a["mask"][:, min(q, 1), :].unsqueeze(1).to_broadcast([P, 4, P]), start=True, stop=False)
            mm = pe.matmul(out, a["qs"][64 * j2:64 * j2 + 64, P * q:P * q + P],
                           a["kz"][64 * j2:64 * j2 + 64, :, WINDOW0[q]:WINDOW0[q] + P], start=False, stop=True)
        mm.then_inc(k.sem("scores"), 1)

    def turn_probs(b, q):
        pe.wait_ge(*k.at("probs", 4 * b + q + 1))
        for half in range(2):
            pe.wait_ge(*k.at("probs_copied", 8 * b + max(2 * q + half - 1, 0)))
            for x in range(4):
                mm = pe.transpose(k.PS[:, 5 + half, x * P:(x + 1) * P], a["sm"][q % 2][:, 4 * half + x, :], k.ident[:, :])
            mm.then_inc(k.sem("probs_turned"), 1)

    def attend(b, q):
        if q == 0:
            pe.wait_ge(*k.at("values_spread", 2 * b + 2))
        pe.wait_ge(*k.at("probs_copied", 8 * b + 2 * q + 2))
        pe.wait_ge(*k.at("att_out", 4 * b + q))
        for x in range(8):
            mm = pe.matmul(k.PS[:, 7, 0:P], a["vz"][:, q, x, :], a["pt"][q % 2][:, x, :], start=x == 0, stop=x == 7)
        mm.then_inc(k.sem("att"), 1)

    def values(b):
        pe.wait_ge(*k.at("seq_staged", 2 * b + 2))
        pe.wait_ge(*k.at("values_spread", 2 * b))
        for w in range(4):
            for h in range(NH):
                mm = pe.matmul(k.PS[:, 0, 64 * w:64 * w + 64], a["ys"][:, h, WINDOW0[w]:WINDOW0[w] + P], wv[:, h, :],
                               start=h == 0, stop=h == 1)
        mm.then_inc(k.sem("values"), 1)

    def sequence(b, last):
        for q in range(QB):
            if not last or q < 2:
                scores(b + (q + 2) // QB, (q + 2) % QB, 4 * b + q + 2)
            turn_probs(b, q)
            if q:
                attend(b, q - 1)
        if not last:
            values(b + 1)
        attend(b, QB - 1)

    pe.wait_ge(*k.at("mask_ready", 1))
    scores(0, 0, 0)
    scores(0, 1, 1)
    values(0)
    with pe.Fori(0, B - 1) as b:
        sequence(b, False)
    sequence(B - 1, True)

    wo = l0a_w(k, "wo", D)
    pe.wait_ge(*k.at("att_out", 4 * B))
    with pe.Fori(0, TILES // 2) as i:
        for par in range(2):
            t = 2 * i + par
            pe.wait_ge(*k.at("wo_done", 4 * i))
            for m in range(NH):
                for j in range(2):
                    mm = pe.matmul(bank(k, 4 + 2 * par + m), wo[:, j, m * P:(m + 1) * P], tile(seqs(k.D), j, t), start=j == 0, stop=j == 1)
                mm.then_inc(k.sem("wo_ready"), 1)
    norm_pe(k, pe, "n2", seqs(k.A), "wo_done", 2)
    wf1, wf2 = l0a_w(k, "wf1", 1024), l0a_w(k, "wf2", D, 8)
    with pe.Fori(0, TILES // 2) as i:
        for par in range(2):
            t = 2 * i + par
            pe.wait_ge(*k.at("n2_done", 2 * (t + 1)))
            for m in range(8):
                pe.wait_ge(*k.at("gelu_done", 16 * i + max(8 * par + m - 3, 0)))
                for h in range(NH):
                    mm = pe.matmul(bank(k, 4 + m % 4), wf1[:, h, m * P:(m + 1) * P], yt(k, h, t), start=h == 0, stop=h == 1)
                mm.then_inc(k.sem("ff1"), 1)
        for par in range(2):
            f = (k.B, k.C)[par][:, :].rearrange("p (m n) -> p m n", m=8)
            pe.wait_ge(*k.at("gelu_done", 16 * i + 8 * (par + 1)))
            pe.wait_ge(*k.at("ff_read", 4 * i))
            for m in range(NH):
                for x in range(8):
                    mm = pe.matmul(bank(k, 2 * par + m), wf2[:, x, m * P:(m + 1) * P], f[:, x, :], start=x == 0, stop=x == 7)
                mm.then_inc(k.sem("ff2"), 1)


def l0a_act(k, act):
    a = att_views(k)
    act.wait_ge(*k.at("constants", CONST))
    act.wait_ge(*k.at("eps_set", 1))
    norm_act(k, act, "n0")
    norm_act(k, act, "n1", "b1", lambda h, t: yt(k, h, t))
    with act.Fori(0, TILES // 2) as i:
        for par in range(2):
            t = 2 * i + par
            for o in range(3):
                act.wait_ge(*k.at("qk_ready", 6 * i + 3 * par + o + 1))
                dst = a["k"][:, bass.ds(t * SPT, SPT), :] if o == 2 else tile(seqs(k.B), o, t)
                bias = vcol(k, "bk") if o == 2 else vcol(k, "bq", o)
                act.activation(dst, bank_seq(k, QKB[par][o]), ACT.Identity, bias=bias).then_inc(k.sem("qk_copied"), 1)

    def exps(q, n):
        act.wait_ge(*k.at("max_scaled", n + 1))
        if type(n) is not int or n >= 2:
            act.wait_ge(*k.at("probs_turned", 2 * n - 2, positive=True))
        for x in range(8):
            ex = act.activation(a["sm"][q % 2][:, x, :], k.PS[:, 1 + 2 * (q % 2) + x // 4, x % 4 * P:x % 4 * P + P], ACT.Exp,
                                bias=a["mx"][:, 8 * (q % 2) + x:8 * (q % 2) + x + 1], scale=0.25)
        ex.then_inc(k.sem("exp_done"), 1)

    def copies(b, q):
        act.wait_ge(*k.at("att", 4 * b + max(q - 1, 0)))
        for half in range(2):
            act.wait_ge(*k.at("probs_turned", 8 * b + 2 * q + half + 1))
            act.activation(a["pt"][q % 2][:, 4 * half:4 * half + 4, :], bank(k, 5 + half).rearrange("p (x k) -> p x k", x=4), ACT.Copy).then_inc(k.sem("probs_copied"), 1)

    def output(b, q):
        act.wait_ge(*k.at("att", 4 * b + q + 1))
        act.activation(seqs(k.D)[:, :, b, 64 * q:64 * q + 64] if type(b) is int else seqs(k.D)[:, :, bass.ds(b, 1), 64 * q:64 * q + 64].rearrange("p j b q -> p j (b q)"),
                       k.PS[:, 7, 0:P].rearrange("p (j q) -> p j q", j=2), ACT.Copy).then_inc(k.sem("att_out"), 1)

    def sequence(b, last):
        for q in range(QB):
            if not last or q < 2:
                exps(q, 4 * b + q + 2)
            copies(b, q)
            if q:
                output(b, q - 1)
        output(b, QB - 1)

    exps(0, 0)
    exps(1, 1)
    with act.Fori(0, B - 1) as b:
        sequence(b, False)
    sequence(B - 1, True)
    norm_act(k, act, "n2", "b2", lambda h, t: yt(k, h, t))
    with act.Fori(0, TILES // 2) as i:
        for par in range(2):
            f = (k.B, k.C)[par][:, :].rearrange("p (m n) -> p m n", m=8)
            act.wait_ge(*k.at("ff2", 4 * i))
            for m in range(8):
                act.wait_ge(*k.at("ff1", 16 * i + 8 * par + m + 1))
                act.activation(f[:, m, :], bank(k, 4 + m % 4), ACT.Gelu, bias=k.vec[:, BF1 + m:BF1 + m + 1]).then_inc(k.sem("gelu_done"), 1)


def l0a_pool(k, pool):
    a = att_views(k)
    pool.wait_ge(*k.at("n1_var", TILES))
    pool.memset(k.Q[:, :], 0.0).then_inc(k.sem("vz_zero"), 1)
    with pool.Fori(0, B) as b:
        pool.wait_ge(*k.at("rotated", 3 * TILES))
        pool.wait_ge(*k.at("scores", 4 * b))
        pool.tensor_copy(a["qs"].rearrange("p (q j t) -> p j q t", q=QB, j=2),
                         seqs(k.B)[:, :, b, :].rearrange("p j (q t) -> p j q t", q=QB)).then_inc(k.sem("seq_staged"), 1)
        pool.wait_ge(*k.at("values", b))
        pool.tensor_copy(a["ys"], k.Y[:, :, b, PAD:PAD + T]).then_inc(k.sem("seq_staged"), 1)


def l0a_dve(k, dve):
    a = att_views(k)
    cos = k.rope[:, 0:T].unsqueeze(1).to_broadcast([P, SPT, T])
    sin = k.rope[:, T:2 * T].unsqueeze(1).to_broadcast([P, SPT, T])
    norm_dve(k, dve, "n0", k.H, dst=lambda h, t: tile(seqs(k.A), h, t))
    norm_dve(k, dve, "n1", seqs(k.A), gain="g1")
    tmp = k.E[:, 0:1024].rearrange("p (m s t) -> p m s t", m=2, s=SPT)
    with dve.Fori(0, TILES // 2) as i:
        for m in range(6):
            t = 2 * i + m // 3
            x = a["k"][:, bass.ds(t * SPT, SPT), :] if m % 3 == 2 else tile(seqs(k.B), m % 3, t)
            dve.wait_ge(*k.at("swapped", 6 * i + m + 1))
            dve.tensor_tensor(tmp[:, m % 2], bank_seq(k, 2 + m % 2), sin, ALU.mult).then_inc(k.sem("swap_used"), 1)
            dve.tensor_tensor(x, x, cos, ALU.mult).then_inc(k.sem("cos_done"), 1)
            dve.wait_ge(*k.at("swap_used", 6 * i + m + 1))
            dve.wait_ge(*k.at("cos_done", 6 * i + m + 1))
            dve.tensor_tensor(x, x, tmp[:, m % 2], ALU.add).then_inc(k.sem("rotated"), 1)
    dve.tensor_copy(a["mask"], k.band).then_inc(k.sem("mask_ready"), 1)
    bv = k.small[:, 448:512].rearrange("p (g d) -> p g d", g=4).unsqueeze(1).to_broadcast([P, 4, 4, 16])
    dve.wait_ge(*k.at("l0a_weights", 32))
    dve.wait_ge(*k.at("vz_zero", 1))

    def largest(q, n):
        mx = a["mx"][:, 8 * (q % 2):8 * (q % 2) + 8]
        dve.wait_ge(*k.at("scores", n + 1))
        src = k.PS[:, 1 + 2 * (q % 2):3 + 2 * (q % 2), :].rearrange("p b (g k) -> p (b g) k", g=4)
        dve.tensor_reduce(mx, src, AX.X, ALU.max).then_inc(k.sem("row_max"), 1)
        dve.wait_ge(*k.at("row_max", n + 1))
        dve.tensor_scalar(mx, mx, -0.25, None, ALU.mult).then_inc(k.sem("max_scaled"), 1)

    def normalise(q, n):
        sm = a["sm"][q % 2]
        s = a["sum"][:, 8 * (q % 2):8 * (q % 2) + 8]
        dve.wait_ge(*k.at("exp_done", n + 1))
        dve.tensor_reduce(s, sm, AX.X, ALU.add).then_inc(k.sem("row_sum"), 1)
        dve.wait_ge(*k.at("row_sum", n + 1))
        dve.reciprocal(s, s).then_inc(k.sem("row_inv"), 1)
        dve.wait_ge(*k.at("row_inv", n + 1))
        dve.tensor_tensor(sm, sm, s.unsqueeze(2).to_broadcast([P, 8, P]), ALU.mult).then_inc(k.sem("probs"), 1)

    def spread_keys(b):
        key = a["k"][:, b, :].unsqueeze(1) if type(b) is int else a["k"][:, bass.ds(b, 1), :]
        if type(b) is not int:
            dve.wait_ge(*k.at("scores", 4 * b, positive=True))
        dve.tensor_tensor(a["kz"], key.to_broadcast([P, 4, T]),
                          k.groupmask.unsqueeze(2).to_broadcast([P, 4, T]), ALU.mult).then_inc(k.sem("keys_spread"), 1)

    def spread_values(b):
        dve.wait_ge(*k.at("values", b + 1))
        dve.wait_ge(*k.at("att", 4 * b))
        for j2 in range(2):
            base = k.Q[:, 4 * j2 * 144:4 * j2 * 144 + 16]
            dst = bass.AP(tensor=base.tensor, offset=base.offset, ap=[base.ap[0], [1024, 4], [144, 4], [1, 16]])
            src = k.PS[:, 0, 0:256].rearrange("p (w g d) -> p w g d", w=4, g=4)
            dve.tensor_tensor(dst, src, bv, ALU.add).then_inc(k.sem("values_spread"), 1)

    def sequence(b, last):
        for q in range(QB):
            n = 4 * b + q
            if not last or q < 2:
                largest(q, n + 2)
            if not last or q < 3:
                normalise((q + 1) % QB, n + 1)
            if q == 0:
                spread_values(b)
            if q == 1 and not last:
                spread_keys(b + 1)

    spread_keys(0)
    largest(0, 0)
    largest(1, 1)
    normalise(0, 0)
    with dve.Fori(0, B - 1) as b:
        sequence(b, False)
    sequence(B - 1, True)
    with dve.Fori(0, TILES // 2) as i:
        for par in range(2):
            t = 2 * i + par
            for m in range(NH):
                dve.wait_ge(*k.at("wo_ready", 2 * t + m + 1))
                x = tile(seqs(k.A), m, t)
                dve.scalar_tensor_tensor(x, bank_seq(k, 4 + 2 * par + m), vcol(k, "bo", m), x, ALU.add, ALU.add).then_inc(k.sem("wo_done"), 1)
    norm_dve(k, dve, "n2", seqs(k.A), gain="g2")
    with dve.Fori(0, TILES // 2) as i:
        for par in range(2):
            t = 2 * i + par
            for m in range(NH):
                dve.wait_ge(*k.at("ff2", 2 * t + m + 1))
                x = tile(seqs(k.A), m, t)
                dve.scalar_tensor_tensor(x, bank_seq(k, 2 * par + m), vcol(k, "bf2", m), x, ALU.add, ALU.add).then_inc(k.sem("ff_read"), 1)
                dve.wait_ge(*k.at("ff_read", 2 * t + m + 1))
                dve.tensor_tensor(tile(k.H, m, t), tile(k.H, m, t), x, ALU.add).then_inc(k.sem("l0a_done"), 1)



def logits_pe(k, pe, n, ready, w, E, b):
    for g in range(N // P):
        if g % 4 == 0:
            pe.wait_ge(*k.at(ready, 2 * (g // 4 + 1)))
        for h in range(NH):
            mm = pe.matmul(k.PS[:, b, E * g:E * g + E], k.Y[:, h, g // 2, PAD + g % 2 * P:PAD + g % 2 * P + P], w[:, h, :],
                           start=h == 0, stop=h == 1)
    mm.then_inc(k.sem(n + "_logits"), 1)


def route_dve(k, dve, n, E, b, norm_eps, bias, lo, between=None):
    G = N // P
    buf = [k.A[:, lo + 256 * j:lo + 256 * j + G * E].rearrange("p (g e) -> p g e", g=G) for j in range(4)]
    col = [k.A[:, lo + 1024 + 16 * j:lo + 1040 + 16 * j] for j in range(4)]
    wide = lambda c: c.unsqueeze(2).to_broadcast([P, G, E])
    rev = k.attc[:, 4 * P + 12:4 * P + 12 + E].unsqueeze(1).to_broadcast([P, G, E])
    x, y, one, w = buf
    c, m1, m2, s = col
    done = [0]

    def chain(ins):
        done[0] += 1
        ins.then_inc(k.sem(n + "_route"), 1)
        dve.wait_ge(*k.at(n + "_route", done[0]))

    logits = k.PS[:, b, 0:G * E].rearrange("p (g e) -> p g e", g=G)
    dve.wait_ge(*k.at(n + "_logits", 1))
    if bias is not None:
        chain(dve.tensor_tensor(x, logits, bias.unsqueeze(1).to_broadcast([P, G, E]), ALU.add))
    else:
        chain(dve.tensor_copy(x, logits))
    chain(dve.tensor_reduce(c, x, AX.X, ALU.max))
    chain(dve.tensor_tensor(x, x, wide(c), ALU.subtract))
    dve.sem_inc(k.sem(n + "_exp_in"), 1)
    dve.wait_ge(*k.at(n + "_exp", 1))
    chain(dve.tensor_reduce(s, x, AX.X, ALU.add))
    chain(dve.reciprocal(s, s))
    chain(dve.tensor_tensor(x, x, wide(s), ALU.mult))
    for step, m in ((0, m1), (1, m2)):
        pick = one if step == 0 else y
        chain(dve.tensor_reduce(m, x, AX.X, ALU.max))
        chain(dve.tensor_tensor(pick, x, wide(m), ALU.is_equal))
        chain(dve.tensor_tensor(pick, pick, rev, ALU.mult))
        chain(dve.tensor_reduce(c, pick, AX.X, ALU.max))
        chain(dve.tensor_tensor(pick, pick, wide(c), ALU.is_equal))
        if step == 0:
            chain(dve.scalar_tensor_tensor(x, pick, -2.0, x, ALU.mult, ALU.add))
    dve.tensor_tensor(w, one, y, ALU.add).then_inc(k.sem(n + "_chosen"), 1)
    if between:
        between()
    chain(dve.tensor_tensor(s, m1, m2, ALU.add))
    if norm_eps:
        chain(dve.tensor_scalar(s, s, norm_eps, None, ALU.add))
    chain(dve.reciprocal(s, s))
    chain(dve.tensor_tensor(m1, m1, s, ALU.mult))
    chain(dve.tensor_tensor(m2, m2, s, ALU.mult))
    return chain


def route_act(k, act, n, E, lo):
    x = k.A[:, lo:lo + N // P * E]
    act.wait_ge(*k.at(n + "_exp_in", 1))
    act.activation(x, x, ACT.Exp).then_inc(k.sem(n + "_exp"), 1)



TS = 256
GROUPS = N // P
E0, E3 = 16, 8
RING0, RING3 = 3, 2


def tiles_for(experts, ring):
    most = (2 * N + experts * (TS - 1)) // TS
    return -(-most // ring) * ring


TILES0, TILES3 = tiles_for(E0 - 1, RING0), tiles_for(E3, RING3)
TILE_NUMBER = 4 * P + 28
NUMBERS = max(TILES0 + RING0, TILES3 + RING3)


def slot_views(k, E, tiles, ring):
    area = [1088]

    def take(cols):
        area[0] += cols
        return k.A[:, area[0] - cols:area[0]]
    ge = lambda ap: ap.rearrange("p (g e) -> p g e", e=E)
    n = tiles + ring
    return {"tmp": ge(k.A[:, 0:GROUPS * E]), "pick2": ge(k.A[:, 256:256 + GROUPS * E]), "pick1": ge(k.A[:, 512:512 + GROUPS * E]),
            "chosen": k.A[:, 768:768 + GROUPS * E], "m1": k.A[:, 1040:1056], "m2": k.A[:, 1056:1072],
            "base": ge(take((GROUPS + 1) * E)),
            "tiles": take(E), "start": take(E + 1),
            "place": ge(take(GROUPS * E)), "sum": take(GROUPS), "slot": [take(GROUPS).bitcast(U32) for j in range(2)],
            "before": ge(take(n * E)), "expert": take(n),
            "row": take(n).bitcast(U32),
            "row_staged": [take(1).bitcast(U32) for j in range(ring)]}


def tile_of(slots, j):
    return slots[bass.ds(j, 1)].rearrange("o (s p) d -> p (o s) d", p=P)


def row_of(idx, j=0):
    return bass.IndirectOffsetOnAxis(ap=idx[:, j:j + 1], axis=0)


def clear_slots(k, sp):
    sp.wait_ge(*k.at("zeros_set", 1))
    sp.dma_start(k.slots.rearrange("t (s p) d -> p (t s) d", p=P),
                 k.small[:, 640:896].unsqueeze(1).to_broadcast([P, 2 * (TILES0 + N // TS), D])).then_inc(k.sem("slots_cleared"), 16)


def ranks_pe(k, pe, n, E, v):
    pe.wait_ge(*k.at(n + "_chosen", 1))
    c = GROUPS * E
    pe.matmul(k.PS[:, 4, 0:c], k.causal, v["chosen"], start=True, stop=True)
    pe.matmul(k.PS[:, 4, c:2 * c], k.mean_w[:, :], v["chosen"], start=True, stop=True).then_inc(k.sem(n + "_ranks"), 1)


def rows_pe(k, pe, n):
    for q in range(GROUPS // 2):
        if q >= 2:
            pe.wait_ge(*k.at(n + "_rows_copied", q - 1))
        for s in range(2):
            for h in range(NH):
                mm = pe.transpose(k.PS[:, 6 + q % 2, (2 * s + h) * P:(2 * s + h + 1) * P], k.Y[:, h, q, PAD + s * P:PAD + s * P + P], k.ident[:, :])
        mm.then_inc(k.sem(n + "_rows_turned"), 1)


def rows_act(k, act, n, rows):
    for q in range(GROUPS // 2):
        act.wait_ge(*k.at(n + "_rows_turned", q + 1))
        act.activation(rows[:, 2 * q:2 * q + 2], k.PS[:, 6 + q % 2, :].rearrange("p (g d) -> p g d", g=2), ACT.Copy).then_inc(k.sem(n + "_rows_copied"), 1)


def slots_dve(k, dve, n, chain, v, E, tiles, ring, experts):
    base, start, place = v["base"], v["start"], v["place"]
    chain(dve.memset(base[:, 0], 0.0))
    chain(dve.memset(start[:, 0:1], 0.0))
    dve.wait_ge(*k.at(n + "_ranks", 1))
    c = GROUPS * E
    for g in range(GROUPS):
        chain(dve.tensor_tensor(base[:, g + 1], base[:, g], k.PS[:, 4, c + E * g:c + E * (g + 1)], ALU.add))
    chain(dve.tensor_scalar(v["tiles"], base[:, GROUPS], 0.5 - 0.5 / TS, ROUND, ALU.add, ALU.add))
    chain(dve.tensor_scalar(v["tiles"], v["tiles"], -ROUND, None, ALU.add))
    for e in range(experts):
        chain(dve.tensor_tensor(start[:, e + 1:e + 2], start[:, e:e + 1], v["tiles"][:, e:e + 1], ALU.add))
    chain(dve.tensor_tensor(place, base[:, 0:GROUPS], start[:, 0:E].unsqueeze(1).to_broadcast([P, GROUPS, E]), ALU.add))
    if experts < E:
        chain(dve.tensor_scalar(place[:, :, experts:E], base[:, 0:GROUPS, experts:E], float(tiles), None, ALU.add))
    chain(dve.scalar_tensor_tensor(place, place, float(TS), k.PS[:, 4, 0:c].rearrange("p (g e) -> p g e", e=E), ALU.mult, ALU.add))
    for j, pick in enumerate((v["pick1"], v["pick2"])):
        chain(dve.tensor_tensor(v["tmp"], pick, place, ALU.mult))
        chain(dve.tensor_reduce(v["sum"], v["tmp"], AX.X, ALU.add))
        chain(dve.tensor_scalar(v["slot"][j], v["sum"], -1.0, None, ALU.add))
    shape = [P, tiles + ring, experts]
    number = k.attc[:, TILE_NUMBER:TILE_NUMBER + tiles + ring].unsqueeze(2).to_broadcast(shape)
    before = v["before"][:, :, 0:experts]
    chain(dve.tensor_tensor(before, number, start[:, 1:experts + 1].unsqueeze(1).to_broadcast(shape), ALU.is_ge))
    chain(dve.tensor_reduce(v["expert"], before, AX.X, ALU.add))
    chain(dve.tensor_scalar(v["expert"], v["expert"], float(experts - 1), float(P), ALU.min, ALU.mult))
    partition = k.attc[:, TILE_NUMBER + NUMBERS:TILE_NUMBER + NUMBERS + 1]
    dve.tensor_scalar(v["row"], v["expert"], partition, None, ALU.add).then_inc(k.sem(n + "_slots_known"), 1)


def scatter_pool(k, pool, n, v, rows):
    for g in range(GROUPS):
        if g % 2 == 0:
            pool.wait_ge(*k.at(n + "_rows_copied", g // 2 + 1))
        for j in range(2):
            pool.indirect_dma_start(k.slots.rearrange("t s d -> (t s) d"), row_of(v["slot"][j], g), rows[:, g], None).then_inc(k.sem(n + "_scattered"), 16)


def gather_pool(k, pool, n, v, dsts):
    for g in range(GROUPS):
        for j, dst in enumerate(dsts):
            pool.indirect_dma_start(dst[:, g], None, k.slots.rearrange("t s d -> (t s) d"), row_of(v["slot"][j], g)).then_inc(k.sem(f"{n}_back{g // 4}"), 16)



W0 = {"conv": 0, "sup": 768, "sdown": 1024, "router": 1280}
N0 = "l0f"


def l0f_inputs(ins, a):
    gate, up, down = a["L0_ffn_expert_gate_w"], a["L0_ffn_expert_up_w"], a["L0_ffn_expert_down_w"]
    ins["l0f_experts"] = np.concatenate([np.concatenate([halves(gate[e]), halves(up[e]), down[e]], axis=1) for e in range(E0 - 1)])
    conv = a["L0_ffn_conv_w"].transpose(2, 1, 0)
    ins["l0f_w"] = np.concatenate([halves(conv[j]) for j in range(3)]
                                  + [halves(a["L0_ffn_shared_up_w"]), a["L0_ffn_shared_down_w"], halves(a["L0_ffn_router_w"])], axis=1)
    ins["router_bias"] = a["L0_ffn_router_bias"].reshape(1, E0)


def moe0_views(k):
    v = slot_views(k, E0, TILES0, RING0)
    ring = lambda ap, cols: [ap[:, cols * j:cols * j + cols] for j in range(RING0)]
    two = lambda aps: [ap.rearrange("p (s d) -> p s d", s=2) for ap in aps]
    group = lambda buf: buf[:, :].rearrange("p (g d) -> p g d", g=GROUPS)
    v["weights"] = ring(k.D[:, 512:2816], 768)
    v["x"], v["xt"] = two(ring(k.C[:, 0:1536], 512)), two(ring(k.C[:, 1536:3072], 512))
    v["o"], v["f"], v["silu"] = two(ring(k.E[:, 0:1536], 512)), ring(k.E[:, 1536:2304], TS), ring(k.E[:, 2304:3072], TS)
    v["rows"], v["first"], v["second"] = group(k.B), group(k.Q), group(k.B)
    v["shared"] = [k.Q[:, 1024 * j:1024 * j + TN] for j in range(2)], [k.Q[:, 1024 * j + TN:1024 * j + 2 * TN] for j in range(2)]
    return v


def l0f_load(k, sp):
    v = moe0_views(k)
    sp.wait_ge(*k.at("emb_proj", 8))
    sp.dma_start(k.W[:, 0:1312], k.ins["l0f_w"]).then_inc(k.sem("l0f_weights"), 16)
    sp.dma_start(k.small[:, 544:560], k.ins["router_bias"].to_broadcast([P, E0])).then_inc(k.sem("l0f_weights"), 16)
    l1a_weights(k, sp)
    sp.wait_ge(*k.at("l0f_scattered", 16 * 2 * GROUPS))
    for j in range(RING0):
        sp.dma_start(v["x"][j], tile_of(k.slots, j)).then_inc(k.sem(f"l0f_x_in{j}"), 16)
    with sp.Fori(0, TILES0 // RING0 - 1) as i:
        for p in range(RING0):
            sp.wait_ge(*k.at("l0f_slots_turned", RING0 * i + p + 1))
            sp.dma_start(v["x"][p], tile_of(k.slots, RING0 * i + p + RING0)).then_inc(k.sem(f"l0f_x_in{p}"), 16)
            sp.wait_ge(*k.at("l0f_o_copied", RING0 * i + p + 1))
            sp.dma_start(tile_of(k.slots, RING0 * i + p), v["o"][p]).then_inc(k.sem(f"l0f_o_out{p}"), 16)
    for p in range(RING0):
        sp.wait_ge(*k.at("l0f_o_copied", TILES0 - RING0 + p + 1))
        sp.dma_start(tile_of(k.slots, TILES0 - RING0 + p), v["o"][p]).then_inc(k.sem(f"l0f_o_out{p}"), 16)


def l0f_pool(k, pool):
    v = moe0_views(k)

    def weights(p, row):
        pool.indirect_dma_start(v["weights"][p], None, k.ins["l0f_experts"], row).then_inc(k.sem(f"l0f_expert_in{p}"), 16)
    l1a_tables_pool(k, pool)
    pool.wait_ge(*k.at("l0f_slots_known", 1))
    pool.wait_ge(*k.at("slots_cleared", 16))
    scatter_pool(k, pool, N0, v, v["rows"])
    for p in range(RING0):
        weights(p, row_of(v["row"], p))
    with pool.Fori(1, TILES0 // RING0) as i:
        for p in range(RING0):
            j = RING0 * i + p
            pool.wait_ge(*k.at("l0f_row_staged", j - RING0 + 1))
            pool.wait_ge(*k.at("moe_down", j - RING0 + 1))
            pool.sem_inc(k.sem("weights_go"), 1)
            weights(p, row_of(v["row_staged"][p]))
    for p in range(RING0):
        pool.wait_ge(*k.at(f"l0f_o_out{p}", 16 * TILES0 // RING0))
    gather_pool(k, pool, N0, v, (v["first"], v["second"]))


def l0f_pe(k, pe):
    v = moe0_views(k)
    wt = lambda name, i, n: blocks(k.W[:, W0[name] + i * n:W0[name] + (i + 1) * n], 2)
    norm_pe(k, pe, "n3", k.H, "l0a_done", 2, free=(("ff_read", 2 * TILES),))
    pe.wait_ge(*k.at("l0f_weights", 32))
    logits_pe(k, pe, "l0f", "n3_scaled", wt("router", 0, 32), E0, 1)
    l1_prep_pe(k, pe)
    rows_pe(k, pe, N0)
    ranks_pe(k, pe, N0, E0, v)
    pe.wait_ge(*k.at("folded_copied", 2))
    pe.wait_ge(*k.at("eigen", 1))
    with pe.Fori(0, TILES // 2) as i:
        for par in range(2):
            t = 2 * i + par
            pe.wait_ge(*k.at("shared_hid", t))
            for j in range(3):
                for h in range(NH):
                    pe.matmul(bank(k, 2), wt("conv", j, 256)[:, h, :], yt(k, h, t, 2 - j), start=j + h == 0, stop=j + h == 3)
            for h in range(NH):
                mm = pe.matmul(bank(k, 3), wt("sup", 0, 256)[:, h, :], yt(k, h, t), start=h == 0, stop=h == 1)
            mm.then_inc(k.sem("shared_in"), 1)
            pe.wait_ge(*k.at("shared_hid", t + 1))
            pe.wait_ge(*k.at("shared_done", 2 * t))
            for m in range(NH):
                mm = pe.matmul(bank(k, (5, 0)[m]), k.W[:, W0["sdown"] + m * P:W0["sdown"] + (m + 1) * P], v["shared"][1][par], start=True, stop=True)
            mm.then_inc(k.sem("shared_out"), 1)

    def turn(j, p, count):
        pe.wait_ge(*k.at(f"l0f_x_in{p}", count))
        for h in range(NH):
            for s in range(2):
                mm = pe.transpose(k.PS[:, p, h * TS + s * P:h * TS + (s + 1) * P], v["x"][p][:, s, h * P:(h + 1) * P], k.ident[:, :])
        mm.then_inc(k.sem("l0f_slots_turned"), 1)

    def gate_up(j, p, count):
        w = v["weights"][p]
        pe.wait_ge(*k.at(f"l0f_expert_in{p}", count, positive=True))
        pe.wait_ge(*k.at("l0f_slots_copied", j + 1))
        for o in range(2):
            for h in range(NH):
                mm = pe.matmul(k.PS[:, p, o * TS:(o + 1) * TS], w[:, 256 * o + P * h:256 * o + P * (h + 1)], v["xt"][p][:, h], start=h == 0, stop=h == 1)
        mm.then_inc(k.sem("moe_in"), 1)

    def down(j, p, i):
        pe.wait_ge(*k.at("moe_h", j + 1))
        pe.wait_ge(*k.at("l0f_o_copied", RING0 * i + max(p - 2, 0) if type(i) is not int else j - 2))
        for s in range(2):
            mm = pe.matmul(k.PS[:, 3 + p, s * D:(s + 1) * D], v["f"][p][:, s * P:(s + 1) * P], v["weights"][p][:, 512:768], start=True, stop=True)
        mm.then_inc(k.sem("moe_down"), 1)

    pe.wait_ge(*k.at("shared_done", 2 * TILES))
    pe.wait_ge(*k.at("l0f_rows_copied", GROUPS // 2))
    turn(0, 0, 16)
    turn(1, 1, 16)
    gate_up(0, 0, 16)

    def round_of_tiles(i, last):
        for p in range(RING0):
            j = RING0 * i + p
            if not last or p < 1:
                pe.wait_ge(*k.at("moe_h", j))
                turn(j + 2, (p + 2) % RING0, 16 * (i + (p + 2) // RING0) + 16)
            if not last or p < 2:
                gate_up(j + 1, (p + 1) % RING0, 16 * (i + (p + 1) // RING0) + 16)
            down(j, p, i)
    with pe.Fori(0, TILES0 // RING0 - 1) as i:
        round_of_tiles(i, False)
    round_of_tiles(TILES0 // RING0 - 1, True)
    pe.wait_ge(*k.at("l0f_o_copied", TILES0))
    for q in range(GROUPS // 2):
        pe.wait_ge(*k.at("l0f_summed", 2 * q + 2))
        for h in range(NH):
            for s in range(2):
                mm = pe.transpose(k.PS[:, q, h * T + s * P:h * T + (s + 1) * P], v["first"][:, 2 * q + s, h * P:(h + 1) * P], k.ident[:, :])
        mm.then_inc(k.sem("l0f_back_turned"), 1)


def l0f_act(k, act):
    v = moe0_views(k)
    norm_act(k, act, "n3")
    route_act(k, act, "l0f", E0, 0)
    rows_act(k, act, N0, v["rows"])
    l1_prep_act(k, act)
    with act.Fori(0, TILES // 2) as i:
        for par in range(2):
            act.wait_ge(*k.at("shared_in", 2 * i + par + 1))
            act.activation(v["shared"][0][par], bank(k, 2), ACT.Silu).then_inc(k.sem("shared_silu"), 1)

    def turned(j, p):
        act.wait_ge(*k.at("l0f_slots_turned", j + 1))
        act.activation(v["xt"][p], k.PS[:, p, :].rearrange("p (h t) -> p h t", h=NH), ACT.Copy).then_inc(k.sem("l0f_slots_copied"), 1)

    def silu(j, p):
        act.wait_ge(*k.at("moe_in", j + 1))
        act.activation(v["silu"][p], k.PS[:, p, 0:TS], ACT.Silu).then_inc(k.sem("moe_silu"), 1)
    turned(0, 0)
    turned(1, 1)
    silu(0, 0)

    def round_of_tiles(i, last):
        for p in range(RING0):
            if not last or p < 1:
                turned(RING0 * i + p + 2, (p + 2) % RING0)
            if not last or p < 2:
                silu(RING0 * i + p + 1, (p + 1) % RING0)
    with act.Fori(0, TILES0 // RING0 - 1) as i:
        round_of_tiles(i, False)
    round_of_tiles(TILES0 // RING0 - 1, True)


def l0f_dve(k, dve):
    v = moe0_views(k)
    norm_dve(k, dve, "n3", k.H, dst=lambda h, t: yt(k, h, t))
    chain = route_dve(k, dve, "l0f", E0, 1, 1e-6, k.small[:, 544:560], 0, between=lambda: l1_prep_dve(k, dve))
    slots_dve(k, dve, N0, chain, v, E0, TILES0, RING0, E0 - 1)
    with dve.Fori(0, TILES // 2) as i:
        for par in range(2):
            t = 2 * i + par
            dve.wait_ge(*k.at("shared_silu", t + 1))
            dve.tensor_tensor(v["shared"][1][par], v["shared"][0][par], bank(k, 3), ALU.mult).then_inc(k.sem("shared_hid"), 1)
            dve.wait_ge(*k.at("shared_out", t + 1))
            for m in range(NH):
                dve.tensor_tensor(tile(k.H, m, t), tile(k.H, m, t), bank_seq(k, (5, 0)[m]), ALU.add).then_inc(k.sem("shared_done"), 1)

    def hidden(j, p):
        dve.wait_ge(*k.at("moe_silu", j + 1))
        dve.tensor_tensor(v["f"][p], v["silu"][p], k.PS[:, p, TS:2 * TS], ALU.mult).then_inc(k.sem("moe_h"), 1)
        dve.tensor_copy(v["row_staged"][p], v["row"][:, bass.ds(j + RING0, 1)]).then_inc(k.sem("l0f_row_staged"), 1)

    def out(j, p, i):
        dve.wait_ge(*k.at("moe_down", j + 1))
        dve.wait_ge(*k.at(f"l0f_o_out{p}", 16 * i))
        dve.tensor_copy(v["o"][p], k.PS[:, 3 + p, :].rearrange("p (s d) -> p s d", s=2)).then_inc(k.sem("l0f_o_copied"), 1)
    hidden(0, 0)

    def round_of_tiles(i, last):
        for p in range(RING0):
            if not last or p < 2:
                hidden(RING0 * i + p + 1, (p + 1) % RING0)
            out(RING0 * i + p, p, i)
    with dve.Fori(0, TILES0 // RING0 - 1) as i:
        round_of_tiles(i, False)
    round_of_tiles(TILES0 // RING0 - 1, True)
    for q in range(4):
        dve.wait_ge(*k.at(f"l0f_back{q}", 16 * 8))
        for g in range(4 * q, 4 * q + 4):
            dve.tensor_scalar(v["second"][:, g], v["second"][:, g], v["m2"][:, g:g + 1], None, ALU.mult).then_inc(k.sem("l0f_second"), 1)
        for g in range(4 * q, 4 * q + 4):
            dve.wait_ge(*k.at("l0f_second", g + 1))
            dve.scalar_tensor_tensor(v["first"][:, g], v["first"][:, g], v["m1"][:, g:g + 1], v["second"][:, g], ALU.mult, ALU.add).then_inc(k.sem("l0f_summed"), 1)
        for s in (2 * q, 2 * q + 1):
            dve.wait_ge(*k.at("l0f_back_turned", s + 1))
            dve.tensor_tensor(k.H[:, :, s, :], k.H[:, :, s, :], bank(k, s).rearrange("p (h t) -> p h t", h=NH), ALU.add).then_inc(k.sem("moe_out"), 1)



V1 = {"B": 0, "F": 512, "G": 1024, "C": 1536, "S": 2048, "a": 2176, "ER": 2304, "EI": 2560, "keep": 2816, "BF": 3328, "CG": 3840}


def l1a_inputs(ins, a):
    n, f = np.arange(D)[:, None].astype(np.float64), np.arange(P)[None, :]
    w = 2 * np.pi / D
    ft = np.concatenate([np.cos(w * n * f), -np.sin(w * n * f)], axis=1)
    ft[:, P] = np.cos(np.pi * n[:, 0])
    g = 2 * ft / D
    g[:, 0] /= 2
    g[:, P] /= 2
    s = -2 * np.sin(w * (np.arange(P)[:, None] + 1) * f)
    s[P - 1] = 0.0
    ft, g, s = (x.astype(np.float32) for x in (ft, g, s))
    ins["l1_w"] = np.concatenate([halves(a["L1_attn_B_w"]), halves(ft), halves(g), halves(a["L1_attn_C_w"].T), s,
                                  a["L1_attn_a_params"].reshape(P, 1)], axis=1)


def l1a_weights(k, sp):
    sp.wait_ge(*k.at("ff2", 2 * TILES))
    sp.dma_start(k.V[:, 0:2177], k.ins["l1_w"]).then_inc(k.sem("l1_weights"), 16)


def l1w(k, name):
    return blocks(k.V[:, V1[name]:V1[name] + 512], 2)


def l1_prep_pe(k, pe):
    pe.wait_ge(*k.at("l1_weights", 16))
    pe.matmul(k.PS[:, 0, 0:1], k.V[:, V1["S"]:V1["S"] + P], k.V[:, V1["a"]:V1["a"] + 1], start=True, stop=True).then_inc(k.sem("omega"), 1)
    for b, lhs, rhs in ((2, "B", "F"), (3, "G", "C")):
        for m in range(NH):
            for h in range(NH):
                mm = pe.matmul(k.PS[:, b, m * D:(m + 1) * D], l1w(k, lhs)[:, h, m * P:(m + 1) * P], l1w(k, rhs)[:, h, :], start=h == 0, stop=h == 1)
        mm.then_inc(k.sem("folded"), 1)


def l1_prep_act(k, act):
    for j, name in enumerate(("BF", "CG")):
        act.wait_ge(*k.at("folded", j + 1))
        act.activation(k.V[:, V1[name]:V1[name] + 512], bank(k, 2 + j), ACT.Copy).then_inc(k.sem("folded_copied"), 1)


def l1_prep_dve(k, dve):
    s = k.vec2
    done = [0]

    def chain(ins):
        done[0] += 1
        ins.then_inc(k.sem("eigen_step"), 1)
        dve.wait_ge(*k.at("eigen_step", done[0]))
    w, w2, den, lr, li = (s[:, 14 + j:15 + j] for j in range(5))
    dve.wait_ge(*k.at("omega", 1))
    chain(dve.tensor_copy(w, k.PS[:, 0, 0:1]))
    chain(dve.tensor_tensor(w2, w, w, ALU.mult))
    chain(dve.tensor_scalar(den, w2, 1.0, None, ALU.add))
    chain(dve.reciprocal(den, den))
    chain(dve.tensor_scalar(w2, w2, -1.0, 1.0, ALU.mult, ALU.add))
    chain(dve.tensor_tensor(lr, w2, den, ALU.mult))
    chain(dve.tensor_scalar(w, w, -2.0, None, ALU.mult))
    dve.tensor_tensor(li, w, den, ALU.mult).then_inc(k.sem("eigen"), 1)
    keep = k.V[:, V1["keep"]:V1["keep"] + TN]
    chain(dve.memset(keep, 1.0))
    dve.memset(keep.rearrange("p (s t) -> p s t", s=SPT)[:, :, 0:1], 0.0).then_inc(k.sem("keep_set"), 1)


def l1a_tables_pool(k, pool):
    s = k.vec2
    lr, li, sq, c0 = (s[:, 17 + j:18 + j] for j in range(4))
    done = [0]

    def chain(ins):
        done[0] += 1
        ins.then_inc(k.sem("power_step"), 1)
        pool.wait_ge(*k.at("power_step", done[0]))
    ER, EI = k.V[:, V1["ER"]:V1["ER"] + T], k.V[:, V1["EI"]:V1["EI"] + T]
    tmp = k.D[:, 0:2 * P]
    pool.wait_ge(*k.at("n3_scaled", 2 * TILES))
    pool.wait_ge(*k.at("eigen", 1))
    chain(pool.memset(ER[:, 0:1], 1.0))
    chain(pool.memset(EI[:, 0:1], 0.0))
    n = 1
    while n < T:
        a, b = tmp[:, 0:n], tmp[:, P:P + n]
        chain(pool.tensor_scalar(a, ER[:, 0:n], lr, None, ALU.mult))
        chain(pool.tensor_scalar(b, EI[:, 0:n], li, None, ALU.mult))
        chain(pool.tensor_tensor(ER[:, n:2 * n], a, b, ALU.subtract))
        chain(pool.tensor_scalar(a, ER[:, 0:n], li, None, ALU.mult))
        chain(pool.tensor_scalar(b, EI[:, 0:n], lr, None, ALU.mult))
        chain(pool.tensor_tensor(EI[:, n:2 * n], a, b, ALU.add))
        chain(pool.tensor_tensor(sq, lr, lr, ALU.mult))
        chain(pool.tensor_tensor(c0, li, li, ALU.mult))
        chain(pool.tensor_tensor(li, li, lr, ALU.mult))
        chain(pool.tensor_tensor(li, li, li, ALU.add))
        chain(pool.tensor_tensor(lr, sq, c0, ALU.subtract))
        n *= 2
    pool.sem_inc(k.sem("powers"), 1)


def l1a_pe(k, pe):
    norm_pe(k, pe, "n4", k.H, "moe_out", 2)
    bf, cg = l1w(k, "BF"), l1w(k, "CG")
    with pe.Fori(0, TILES // 2) as i:
        for par in range(2):
            t = 2 * i + par
            pe.wait_ge(*k.at("n4_scaled", 2 * (t + 1)))
            pe.wait_ge(*k.at("turned_in", 8 * i))
            for m in range(NH):
                for h in range(NH):
                    mm = pe.matmul(bank(k, 4 + 2 * par + m), bf[:, h, m * P:(m + 1) * P], yt(k, h, t), start=h == 0, stop=h == 1)
                mm.then_inc(k.sem("fourier_in"), 1)
    with pe.Fori(0, TILES // 2) as i:
        for par in range(2):
            t = 2 * i + par
            pe.wait_ge(*k.at("z_ready", 2 * (t + 1)))
            pe.wait_ge(*k.at("ssm_read", 4 * i))
            for m in range(NH):
                for h in range(NH):
                    mm = pe.matmul(bank(k, 2 * par + m), cg[:, h, m * P:(m + 1) * P], tile(seqs(k.C), h, t), start=h == 0, stop=h == 1)
                mm.then_inc(k.sem("ssm_out"), 1)


def l1a_act(k, act):
    norm_act(k, act, "n4")


def powers(k, name):
    return k.V[:, V1[name]:V1[name] + T].unsqueeze(1).to_broadcast([P, SPT, T])


def l1a_pool(k, pool):
    A, Bv, C, Dv = seqs(k.A), seqs(k.B), seqs(k.C), seqs(k.D)
    pool.wait_ge(*k.at("ff2", 2 * TILES))
    with pool.Fori(0, TILES) as t:
        pool.wait_ge(*k.at("turned_in", 4 * t + 2))
        pool.tensor_tensor(tile(C, 0, t), tile(A, 0, t), tile(A, 1, t), ALU.add).then_inc(k.sem("sum_in"), 1)
        pool.wait_ge(*k.at("turned_in", 4 * t + 4))
        pool.tensor_tensor(tile(C, 1, t), tile(Bv, 0, t), tile(Bv, 1, t), ALU.subtract).then_inc(k.sem("sum_in"), 1)
    with pool.Fori(0, TILES) as t:
        pool.wait_ge(*k.at("turned_out", 4 * t + 2))
        pool.tensor_tensor(tile(C, 0, t), tile(A, 0, t), tile(A, 1, t), ALU.subtract).then_inc(k.sem("z_ready"), 1)
        pool.wait_ge(*k.at("turned_out", 4 * t + 4))
        pool.tensor_tensor(tile(C, 1, t), tile(Bv, 0, t), tile(Bv, 1, t), ALU.add).then_inc(k.sem("z_ready"), 1)


def flat(buf, h, t):
    return buf[:, bass.ds(t * TN + h * N, TN)]


def l1a_dve(k, dve):
    A, Bv, Dv = seqs(k.A), seqs(k.B), seqs(k.D)
    norm_dve(k, dve, "n4", k.H, dst=lambda h, t: yt(k, h, t), free=(("powers", 1),))
    dve.wait_ge(*k.at("powers", 1))
    dve.wait_ge(*k.at("keep_set", 1))
    with dve.Fori(0, TILES // 2) as i:
        for par in range(2):
            t = 2 * i + par
            re, im = bank_seq(k, 4 + 2 * par), bank_seq(k, 5 + 2 * par)
            dve.wait_ge(*k.at("fourier_in", 2 * t + 2))
            for dst, src, e in ((tile(A, 0, t), re, "ER"), (tile(A, 1, t), im, "EI"), (tile(Bv, 0, t), im, "ER"), (tile(Bv, 1, t), re, "EI")):
                dve.tensor_tensor(dst, src, powers(k, e), ALU.mult).then_inc(k.sem("turned_in"), 1)
    with dve.Fori(0, TILES) as t:
        for h in range(NH):
            dve.wait_ge(*k.at("sum_in", 2 * t + h + 1))
            dve.tensor_tensor_scan(flat(k.D, h, t), k.V[:, V1["keep"]:V1["keep"] + TN], flat(k.C, h, t), 0.0, ALU.mult, ALU.add).then_inc(k.sem("summed"), 1)
        dve.wait_ge(*k.at("summed", 2 * t + 2))
        for dst, h, e in ((tile(A, 0, t), 0, "ER"), (tile(A, 1, t), 1, "EI"), (tile(Bv, 0, t), 1, "ER"), (tile(Bv, 1, t), 0, "EI")):
            dve.tensor_tensor(dst, tile(Dv, h, t), powers(k, e), ALU.mult).then_inc(k.sem("turned_out"), 1)
    with dve.Fori(0, TILES // 2) as i:
        for par in range(2):
            t = 2 * i + par
            dve.wait_ge(*k.at("z_ready", 2 * t + 2))
            for m in range(NH):
                dve.wait_ge(*k.at("ssm_out", 2 * t + m + 1))
                dve.scalar_tensor_tensor(tile(A, m, t), yt(k, m, t), vcol(k, "D", m), bank_seq(k, 2 * par + m), ALU.mult, ALU.add).then_inc(k.sem("ssm_read"), 1)
                dve.wait_ge(*k.at("ssm_read", 2 * t + m + 1))
                dve.tensor_tensor(tile(k.H, m, t), tile(k.H, m, t), tile(A, m, t), ALU.add).then_inc(k.sem("l1a_done"), 1)



def l1f_inputs(ins, a):
    ins["l1f_w"] = np.concatenate([halves(a["L1_ffn_W_" + n].T) for n in "rkv"], axis=1)


def l1f_load(k, sp):
    sp.wait_ge(*k.at("shared_out", TILES))
    sp.dma_start(k.W[:, 0:1536], k.ins["l1f_w"]).then_inc(k.sem("l1f_weights"), 16)


def l1f_pe(k, pe):
    wr, wk, wv = (blocks(k.W[:, 512 * j:512 * j + 512], 2) for j in range(3))
    norm_pe(k, pe, "n5", k.H, "l1a_done", 2, free=(("ssm_read", 2 * TILES),))
    pe.wait_ge(*k.at("l1f_weights", 16))
    pe.wait_ge(*k.at("n5_std", TILES))
    with pe.Fori(0, TILES // 2) as i:
        for par in range(2):
            t = 2 * i + par
            pe.wait_ge(*k.at("rk_read", 8 * i))
            pe.wait_ge(*k.at("mixed", 4 * t + 4))
            for o, (w, x) in enumerate(((wr, k.B), (wk, k.C))):
                for m in range(NH):
                    for h in range(NH):
                        mm = pe.matmul(bank(k, 4 * par + 2 * o + m), w[:, h, m * P:(m + 1) * P], tile(seqs(x), h, t), start=h == 0, stop=h == 1)
                    mm.then_inc(k.sem("rk_ready"), 1)
    with pe.Fori(0, TILES // 2) as i:
        for par in range(2):
            t = 2 * i + par
            pe.wait_ge(*k.at("k_squared", 2 * t + 2))
            pe.wait_ge(*k.at("rk_read", 4 * TILES))
            pe.wait_ge(*k.at("v_read", 4 * i))
            for m in range(NH):
                for h in range(NH):
                    mm = pe.matmul(bank(k, 4 * par + m), wv[:, h, m * P:(m + 1) * P], tile(seqs(k.D), h, t), start=h == 0, stop=h == 1)
                mm.then_inc(k.sem("v_ready"), 1)


def l1f_act(k, act):
    norm_act(k, act, "n5")
    act.wait_ge(*k.at("rest_ready", 7))
    with act.Fori(0, TILES) as t:
        act.wait_ge(*k.at("n5_scaled", 2 * t + 2))
        for o, x in enumerate((k.B, k.C)):
            for h in range(NH):
                act.activation(tile(seqs(x), h, t), yt(k, h, t, 1), ACT.Copy, scale=k.vec2[:, 2 * o + h:2 * o + h + 1]).then_inc(k.sem("before"), 1)
    with act.Fori(0, TILES // 2) as i:
        for par in range(2):
            t = 2 * i + par
            for m in range(NH):
                act.wait_ge(*k.at("rk_ready", 4 * t + m + 1))
                act.activation(tile(seqs(k.A), m, t), bank_seq(k, 4 * par + m), ACT.Sigmoid).then_inc(k.sem("rk_read"), 1)
            for m in range(NH):
                act.wait_ge(*k.at("rk_ready", 4 * t + 2 + m + 1))
                act.activation(tile(seqs(k.D), m, t), bank_seq(k, 4 * par + 2 + m), ACT.Relu).then_inc(k.sem("rk_read"), 1)


def l1f_pool(k, pool):
    with pool.Fori(0, TILES) as t:
        for h in range(NH):
            pool.wait_ge(*k.at("rk_read", 4 * t + 2 + h + 1))
            pool.tensor_tensor(tile(seqs(k.D), h, t), tile(seqs(k.D), h, t), tile(seqs(k.D), h, t), ALU.mult).then_inc(k.sem("k_squared"), 1)


def l1f_dve(k, dve):
    norm_dve(k, dve, "n5", k.H, dst=lambda h, t: yt(k, h, t))
    with dve.Fori(0, TILES) as t:
        for o, (x, mu) in enumerate(((k.B, "mu_r"), (k.C, "mu_k"))):
            for h in range(NH):
                dve.wait_ge(*k.at("before", 4 * t + 2 * o + h + 1))
                v = tile(seqs(x), h, t)
                dve.scalar_tensor_tensor(v, yt(k, h, t), vcol(k, mu, h), v, ALU.mult, ALU.add).then_inc(k.sem("mixed"), 1)
    with dve.Fori(0, TILES // 2) as i:
        for par in range(2):
            t = 2 * i + par
            for m in range(NH):
                a = tile(seqs(k.A), m, t)
                dve.wait_ge(*k.at("v_ready", 2 * t + m + 1))
                dve.tensor_tensor(a, a, bank_seq(k, 4 * par + m), ALU.mult).then_inc(k.sem("v_read"), 1)
                dve.wait_ge(*k.at("v_read", 2 * t + m + 1))
                dve.tensor_tensor(tile(k.H, m, t), tile(k.H, m, t), a, ALU.add).then_inc(k.sem("l1f_done"), 1)



CH = 128
W2 = {"q": 1536, "k": 2048, "g": 2560, "out": 3072, "v": 3584, "gk1": 4096, "gk2": 4352}
FAR = 16 * 85.0


def l2a_inputs(ins, a):
    w = {n: a["L2_attn_" + n] for n in ("Wq", "Wk", "Wg", "Wout", "Wv", "Wgk1")}
    w["Wgk1"] = np.pad(w["Wgk1"], ((0, 0), (0, P - 16)))
    ins["l2a_w"] = np.concatenate([halves(w[n]) for n in ("Wq", "Wk", "Wg", "Wout", "Wv", "Wgk1")], axis=1)
    ins["gk2"] = np.pad(a["L2_attn_Wgk2"], ((0, P - 16), (0, 0)))


def l2a_load(k, sp):
    sp.dma_start(k.W[:, 1536:4352], k.ins["l2a_w"]).then_inc(k.sem("l2a_weights"), 16)
    sp.dma_start(k.W[:, 4352:4608], k.ins["gk2"]).then_inc(k.sem("l2a_weights"), 16)


def l2w(k, name):
    return blocks(k.W[:, W2[name]:W2[name] + 512], 2)


def gla_views(k):
    v = {"keep": k.V[:, 0:512], "gsum": k.V[:, 4096:4098]}
    for name, a in (("dm", 512), ("eo", 1024), ("vi", 1536)):
        v[name] = k.V[:, a:a + 512].rearrange("p (h c t) -> p h c t", h=2, c=2)
    v["ve"] = k.V[:, 2048:2304].rearrange("p (h t) -> p h t", h=2)
    v["ks"] = k.V[:, 2560:3072].rearrange("p (h t) -> p h t", h=2)
    v["turned"] = k.V[:, 3072:3584]
    v["veT"] = k.V[:, 3072:3328].rearrange("p (h m) -> p h m", h=2)
    v["kT"] = k.V[:, 3328:3584].rearrange("p (h m) -> p h m", h=2)
    v["st"] = k.V[:, 3584:3840].rearrange("p (h m) -> p h m", h=2)
    v["qz"] = [k.A[:, 1024 * j:1024 * j + 1024].rearrange("p (a t) -> p a t", a=8) for j in range(2)]
    v["am"] = [k.A[:, 2048 + 1024 * j:3072 + 1024 * j].rearrange("p (a t) -> p a t", a=8) for j in range(2)]
    v["vz"] = k.Q[:, :].rearrange("p (u a m) -> p u a m", u=4, a=8)
    return v


def l2a_pe(k, pe):
    v = gla_views(k)
    norm_pe(k, pe, "n6", k.H, "l1f_done", 2, free=(("v_read", 2 * TILES),))
    pe.wait_ge(*k.at("l2a_weights", 32))
    pe.wait_ge(*k.at("n6_std", TILES))
    with pe.Fori(0, TILES // 2) as i:
        for par in range(2):
            t = 2 * i + par
            pe.wait_ge(*k.at("n6_scaled", 2 * t + 2))
            for n in range(7):
                pe.wait_ge(*k.at("qkv_read", 14 * i + (par and n + 1)))
                w = l2w(k, "qkv"[n // 2])[:, :, (n % 2) * P:(n % 2 + 1) * P] if n < 6 else blocks(k.W[:, W2["gk1"]:W2["gk1"] + 256], 2)
                for h in range(NH):
                    mm = pe.matmul(bank(k, n), w[:, h, :], yt(k, h, t), start=h == 0, stop=h == 1)
                mm.then_inc(k.sem("qkv_ready"), 1)
    pe.wait_ge(*k.at("qkv_read", 7 * TILES))
    with pe.Fori(0, TILES // 2) as i:
        for par in range(2):
            pe.wait_ge(*k.at("gate_read", 4 * i))
            for m in range(NH):
                pe.matmul(bank(k, 2 * par + m), k.W[:, W2["gk2"] + m * P:W2["gk2"] + (m + 1) * P], k.Q[:, bass.ds((2 * i + par) * TN, TN)],
                          start=True, stop=True).then_inc(k.sem("gate_ready"), 1)
    pe.wait_ge(*k.at("gate_read", 2 * TILES))
    with pe.Fori(0, B) as b:

        def scores(u):
            c, h = u // 2, u % 2
            pe.wait_ge(*k.at("q_spread", 4 * b + u + 1))
            pe.wait_ge(*k.at("gla_masked", 4 * b + max(u - 1, 0)))
            for x in range(2):
                mm = pe.matmul(bank(k, 2 + 2 * (u % 2) + x), v["ks"][:, h, CH * c:CH * c + CH], v["qz"][u % 2][:, 4 * x:4 * x + 4, :], start=True, stop=True)
            mm.then_inc(k.sem("gla_scores"), 1)

        def outputs(u):
            c, h = u // 2, u % 2
            pe.wait_ge(*k.at("gla_masked", 4 * b + u + 1))
            pe.wait_ge(*k.at("gla_out", 4 * b + max(u - 1, 0)))
            for x in range(8):
                mm = pe.matmul(k.PS[:, 6 + u % 2, 0:P], v["vz"][:, u, x, :], v["am"][u % 2][:, x, :], start=x == 0, stop=x == 7 and c == 0)
            if c:
                if u == 2:
                    pe.wait_ge(*k.at("state", b + 1))
                mm = pe.matmul(k.PS[:, 6 + u % 2, 0:P], v["st"][:, h, :], seqs(k.B)[:, h, b, CH:2 * CH], start=False, stop=True)
            mm.then_inc(k.sem("gla_att"), 1)

        pe.wait_ge(*k.at("keys_staged", b + 1))
        scores(0)
        scores(1)
        pe.wait_ge(*k.at("decayed", 2 * b + 2))
        pe.wait_ge(*k.at("v_spread", b))
        pe.wait_ge(*k.at("state", b))
        for u in range(4):
            mm = pe.transpose(k.PS[:, 0, P * u:P * u + P], v["vi"][:, u % 2, u // 2, :], k.ident[:, :])
        mm.then_inc(k.sem("v_turned"), 1)
        for h in range(NH):
            pe.transpose(k.PS[:, 1, P * h:P * h + P], v["ve"][:, h, :], k.ident[:, :])
            mm = pe.transpose(k.PS[:, 1, D + P * h:D + P * h + P], v["ks"][:, h, 0:CH], k.ident[:, :])
        mm.then_inc(k.sem("kv_turned"), 1)
        pe.wait_ge(*k.at("v_spread", b + 1))
        outputs(0)
        scores(2)
        pe.wait_ge(*k.at("kv_copied", b + 1))
        for h in range(NH):
            mm = pe.matmul(k.PS[:, 1, P * h:P * h + P], v["kT"][:, h, :], v["veT"][:, h, :], start=True, stop=True)
        mm.then_inc(k.sem("state_sum"), 1)
        outputs(1)
        scores(3)
        outputs(2)
        outputs(3)
    norm_pe(k, pe, "n7", seqs(k.E), "gla_out", 8, free=(("gla_out", 4 * B),))
    pe.wait_ge(*k.at("n7_std", TILES))
    with pe.Fori(0, TILES // 2) as i:
        for par in range(2):
            pe.wait_ge(*k.at("g_read", 4 * i))
            for m in range(NH):
                for h in range(NH):
                    mm = pe.matmul(bank(k, 2 * par + m), l2w(k, "g")[:, h, m * P:(m + 1) * P], yt(k, h, 2 * i + par), start=h == 0, stop=h == 1)
                mm.then_inc(k.sem("g_ready"), 1)
    with pe.Fori(0, TILES // 2) as i:
        for par in range(2):
            t = 2 * i + par
            pe.wait_ge(*k.at("gated", 2 * t + 2))
            pe.wait_ge(*k.at("l2a_read", 4 * i))
            for m in range(NH):
                for h in range(NH):
                    mm = pe.matmul(bank(k, 4 + 2 * par + m), l2w(k, "out")[:, h, m * P:(m + 1) * P], tile(seqs(k.A), h, t), start=h == 0, stop=h == 1)
                mm.then_inc(k.sem("l2a_ready"), 1)


def l2a_act(k, act):
    v = gla_views(k)
    norm_act(k, act, "n6")
    with act.Fori(0, TILES // 2) as i:
        for par in range(2):
            t = 2 * i + par
            for n in range(7):
                dst = tile(seqs((k.B, k.C, k.E)[n // 2]), n % 2, t) if n < 6 else tile(seqs(k.Q), 0, t)
                act.wait_ge(*k.at("qkv_ready", 7 * t + n + 1))
                act.activation(dst, bank_seq(k, n), ACT.Copy).then_inc(k.sem("qkv_read"), 1)
    with act.Fori(0, TILES // 2) as i:
        for par in range(2):
            t = 2 * i + par
            for m in range(NH):
                act.wait_ge(*k.at("gate_ready", 2 * t + m + 1))
                act.activation(tile(seqs(k.A), m, t), bank_seq(k, 2 * par + m), ACT.Identity, bias=vcol(k, "bgk2", m)).then_inc(k.sem("gate_read"), 1)
    for n, (f, src, dst) in enumerate(((ACT.Abs, k.A, k.Q), (ACT.Exp, k.Q, k.Q), (ACT.Ln, k.Q, k.Q))):
        with act.Fori(0, TILES) as t:
            for m in range(NH):
                act.wait_ge(*k.at("gate_read" if n == 0 else f"softplus{n}", 2 * t + m + 1))
                act.activation(tile(seqs(dst), m, t), tile(seqs(src), m, t), f, bias=1.0 if n == 2 else 0.0, scale=-1.0 if n == 1 else 1.0).then_inc(k.sem(f"softplus{n + 1}"), 1)
    with act.Fori(0, B) as b:
        act.wait_ge(*k.at("clamped", b + 1))
        act.wait_ge(*k.at("gla_out", 4 * b))
        act.activation(v["vi"], v["dm"], ACT.Exp, scale=-1 / 16).then_inc(k.sem("factors"), 1)
        act.wait_ge(*k.at("to_end", b + 1))
        act.activation(v["ve"], v["ve"], ACT.Exp, scale=1 / 16).then_inc(k.sem("factors"), 1)
        act.activation(v["eo"], v["dm"], ACT.Exp, scale=1 / 16).then_inc(k.sem("factors"), 1)
        act.wait_ge(*k.at("kv_turned", b + 1))
        act.wait_ge(*k.at("state_sum", b))
        act.activation(v["turned"], bank(k, 1), ACT.Copy).then_inc(k.sem("kv_copied"), 1)
    norm_act(k, act, "n7", "beta", lambda h, t: tile(seqs(k.A), h, t))
    with act.Fori(0, TILES // 2) as i:
        for par in range(2):
            for m in range(NH):
                act.wait_ge(*k.at("g_ready", 4 * i + 2 * par + m + 1))
                act.activation(tile(seqs(k.B), m, 2 * i + par), bank_seq(k, 2 * par + m), ACT.Silu).then_inc(k.sem("g_read"), 1)


def l2a_pool(k, pool):
    v = gla_views(k)
    pool.wait_ge(*k.at("gate_sums", 2 * TILES))
    pool.memset(k.Q[:, :], 0.0).then_inc(k.sem("vz2_zero"), 1)
    pool.wait_ge(*k.at("qkv_read", 7 * TILES))
    with pool.Fori(0, B) as b:
        pool.wait_ge(*k.at("state_sum", b))
        pool.wait_ge(*k.at("gla_scores", 4 * b))
        pool.tensor_copy(v["ks"], seqs(k.C)[:, :, b, :]).then_inc(k.sem("keys_staged"), 1)
        for u in range(4):
            pool.wait_ge(*k.at("gla_scores", 4 * b + max(u - 1, 0)))
            pool.tensor_tensor(v["qz"][u % 2], seqs(k.B)[:, u % 2, b, CH * (u // 2):CH * (u // 2) + CH].unsqueeze(1).to_broadcast([P, 8, CH]),
                               k.headmask.unsqueeze(2).to_broadcast([P, 8, CH]), ALU.mult).then_inc(k.sem("q_spread"), 1)


def l2a_dve(k, dve):
    v = gla_views(k)
    norm_dve(k, dve, "n6", k.H, dst=lambda h, t: yt(k, h, t))
    dve.wait_ge(*k.at("ssm_out", 2 * TILES))
    dve.memset(v["keep"], 1.0).then_inc(k.sem("keep2"), 1)
    dve.wait_ge(*k.at("keep2", 1))
    dve.memset(v["keep"].rearrange("p (c t) -> p c t", t=CH)[:, :, 0:1], 0.0).then_inc(k.sem("keep2"), 1)
    dve.wait_ge(*k.at("keep2", 2))
    with dve.Fori(0, TILES) as t:
        for m in range(NH):
            dve.wait_ge(*k.at("softplus3", 2 * t + m + 1))
            g = tile(seqs(k.A), m, t)
            dve.scalar_tensor_tensor(g, g, 0.0, tile(seqs(k.Q), m, t), ALU.min, ALU.subtract).then_inc(k.sem("log_gate"), 1)
            dve.wait_ge(*k.at("log_gate", 2 * t + m + 1))
            dve.tensor_tensor_scan(flat(k.D, m, t), v["keep"], flat(k.A, m, t), 0.0, ALU.mult, ALU.add).then_inc(k.sem("gate_sums"), 1)
    dve.wait_ge(*k.at("gate_sums", 2 * TILES))
    dve.wait_ge(*k.at("vz2_zero", 1))
    G = seqs(k.D)
    with dve.Fori(0, B) as b:
        g = G[:, :, b, :].rearrange("p h (c t) -> p h c t", c=2)
        dve.wait_ge(*k.at("factors", 3 * b))
        dve.wait_ge(*k.at("kv_turned", b))
        dve.tensor_tensor(v["dm"], g, g[:, :, :, CH // 2 - 1:CH // 2].to_broadcast([P, 2, 2, CH]), ALU.subtract).then_inc(k.sem("to_mid"), 1)
        dve.tensor_tensor(v["gsum"].unsqueeze(2), g[:, :, 0, CH - 1:CH], g[:, :, 1, CH // 2 - 1:CH // 2], ALU.add).then_inc(k.sem("gate_to_mid"), 1)
        dve.wait_ge(*k.at("to_mid", b + 1))
        dve.tensor_scalar(v["dm"], v["dm"], FAR, -FAR, ALU.min, ALU.max).then_inc(k.sem("clamped"), 1)
        dve.wait_ge(*k.at("gate_to_mid", b + 1))
        dve.tensor_tensor(v["ve"], v["gsum"].unsqueeze(2).to_broadcast([P, 2, CH]), g[:, :, 0, :], ALU.subtract).then_inc(k.sem("to_end"), 1)
        vals = seqs(k.E)[:, :, b, :]
        dve.wait_ge(*k.at("factors", 3 * b + 1))
        dve.tensor_tensor(v["vi"], v["vi"], vals.rearrange("p h (c t) -> p h c t", c=2), ALU.mult).then_inc(k.sem("decayed"), 1)
        dve.wait_ge(*k.at("factors", 3 * b + 2))
        dve.tensor_tensor(v["ve"], v["ve"], vals[:, :, 0:CH], ALU.mult).then_inc(k.sem("decayed"), 1)

        def mask(u):
            dve.wait_ge(*k.at("gla_scores", 4 * b + u + 1))
            dve.wait_ge(*k.at("gla_att", 4 * b + max(u - 1, 0)))
            src = k.PS[:, 2 + 2 * (u % 2):4 + 2 * (u % 2), :].rearrange("p b (a t) -> p (b a) t", a=4)
            dve.tensor_tensor(v["am"][u % 2], src, k.causal.unsqueeze(1).to_broadcast([P, 8, CH]), ALU.mult).then_inc(k.sem("gla_masked"), 1)

        def output(u):
            c, h = u // 2, u % 2
            dve.wait_ge(*k.at("gla_att", 4 * b + u + 1))
            dve.tensor_tensor(seqs(k.E)[:, h, b, CH * c:CH * c + CH], k.PS[:, 6 + u % 2, 0:P], v["eo"][:, h, c, :], ALU.mult).then_inc(k.sem("gla_out"), 1)

        mask(0)
        mask(1)
        dve.wait_ge(*k.at("v_turned", b + 1))
        base = k.Q[:, 0:16]
        dst = bass.AP(tensor=base.tensor, offset=base.offset, ap=[base.ap[0], [1024, 4], [144, 8], [1, 16]])
        dve.tensor_copy(dst, k.PS[:, 0, :].rearrange("p (u a d) -> p u a d", u=4, a=8)).then_inc(k.sem("v_spread"), 1)
        dve.wait_ge(*k.at("factors", 3 * b + 3))
        dve.wait_ge(*k.at("decayed", 2 * b + 2))
        output(0)
        mask(2)
        dve.wait_ge(*k.at("state_sum", b + 1))
        dve.tensor_tensor(v["st"].rearrange("p h (a d) -> p h a d", a=8), k.PS[:, 1, 0:D].rearrange("p (h a d) -> p h a d", h=2, a=8),
                          k.headmask.unsqueeze(1).unsqueeze(3).to_broadcast([P, 2, 8, 16]), ALU.mult).then_inc(k.sem("state"), 1)
        output(1)
        mask(3)
        output(2)
        output(3)
    norm_dve(k, dve, "n7", seqs(k.E), gain="gamma")
    with dve.Fori(0, TILES) as t:
        for m in range(NH):
            dve.wait_ge(*k.at("g_read", 2 * t + m + 1))
            dve.wait_ge(*k.at("n7_done", 2 * t + m + 1))
            x = tile(seqs(k.A), m, t)
            dve.tensor_tensor(x, x, tile(seqs(k.B), m, t), ALU.mult).then_inc(k.sem("gated"), 1)
    with dve.Fori(0, TILES // 2) as i:
        for par in range(2):
            t = 2 * i + par
            for m in range(NH):
                dve.wait_ge(*k.at("l2a_ready", 2 * t + m + 1))
                dve.tensor_tensor(tile(k.H, m, t), tile(k.H, m, t), bank_seq(k, 4 + 2 * par + m), ALU.add).then_inc(k.sem("l2a_read"), 1)



W6 = {"b1": 6656, "b2": 7680}
GPT = TN // P


def l2f_inputs(ins, a):
    ins["l2f_w"] = np.concatenate([halves(a["L2_ffn_W1"].T), halves(a["L2_ffn_W2"].T)], axis=1)
    ins["l2f_b"] = np.concatenate([a["L2_ffn_b1"], a["L2_ffn_b2"]]).reshape(1, 1280)


def l2f_load(k, sp):
    sp.dma_start(k.W[:, 6656:7936], k.ins["l2f_b"].to_broadcast([P, 1280])).then_inc(k.sem("l2f_bias"), 16)
    sp.wait_ge(*k.at("state_sum", B))
    sp.dma_start(k.C[:, :], k.ins["l2f_w"]).then_inc(k.sem("l2f_weights"), 16)


def ffq_views(k):
    v = {"w1": k.W[:, 4608:5632].bitcast(BF16).rearrange("p (k m) -> p k m", k=2),
         "w2": k.W[:, 5632:6656].bitcast(BF16).rearrange("p (k m) -> p k m", k=8),
         "b1": k.W[:, 6656:7680], "b2": k.W[:, 7680:7936], "wsum": k.vec2[:, 22:24], "wscale": k.vec2[:, 20:22], "winv": k.vec2[:, 14:16],
         "xs": k.A[:, 0:1024].rearrange("p (h t) -> p h t", h=2),
         "out": k.B[:, 3072:3328], "hq": k.B[:, 2048:2560].bitcast(BF16), "ht": k.B[:, 2560:3072].bitcast(BF16).rearrange("p (k t) -> p k t", k=8)}
    for j in range(2):
        v["x", j] = k.A[:, 1024 + 256 * j:1280 + 256 * j]
        v["xq", j] = k.A[:, 1536 + 128 * j:1664 + 128 * j].bitcast(BF16)
        v["xt", j] = k.A[:, 1792 + 128 * j:1920 + 128 * j].bitcast(BF16).rearrange("p (k t) -> p k t", k=2)
        v["h", j] = k.B[:, 1024 * j:1024 * j + 1024]
        v["sx", j] = k.small[:, 560 + 4 * j:564 + 4 * j]
        v["sh", j] = k.small[:, 568 + 4 * j:572 + 4 * j]
    return v


def over_groups(engine, work):
    def steps(tile_of_step):
        for u in range(GPT):
            for f, lag in work:
                t, g = tile_of_step + (u - lag) // GPT, (u - lag) % GPT
                if type(t) is not int or 0 <= t < TILES:
                    f(t, GPT * t + g, g)
    steps(0)
    with engine.Fori(1, TILES) as t:
        steps(t)
    steps(TILES)


def two_back(n):
    return n - 1 if type(n) is not int else max(n - 1, 0)


def l2f_pe(k, pe):
    v = ffq_views(k)
    norm_pe(k, pe, "n8", k.H, "l2a_read", 2, free=(("gated", 2 * TILES),))
    pe.wait_ge(*k.at("w_sums", 2))
    pe.matmul(k.PS[:, 4, 0:2], k.mean_w[:, :], v["wsum"], start=True, stop=True).then_inc(k.sem("w_means"), 1)
    pe.wait_ge(*k.at("w_quantised", 2))

    def turn_x(t, n, g):
        if g == 0:
            pe.wait_ge(*k.at("tile_staged", t + 1))
        pe.wait_ge(*k.at("x_shifted", n))
        for h in range(NH):
            mm = pe.transpose(k.PS[:, 0, P * h:P * h + P], v["xs"][:, h, P * g:P * g + P], k.ident[:, :])
        mm.then_inc(k.sem("x_turned"), 1)

    def turn_xq(t, n, g):
        pe.wait_ge(*k.at("x_quantised", n + 1, positive=True))
        pe.wait_ge(*k.at("xq_copied", n))
        for h in range(NH):
            mm = pe.transpose(k.PS[:, 2, 64 * h:64 * h + 64].bitcast(BF16), v["xq", g % 2][:, P * h:P * h + P], k.identb[:, :])
        mm.then_inc(k.sem("xq_turned"), 1)

    def turn_hidden(t, n, g):
        pe.wait_ge(*k.at("h_quantised", n + 1))
        pe.wait_ge(*k.at("hq_copied", n))
        for x in range(8):
            mm = pe.transpose(k.PS[:, 5, 64 * x:64 * x + 64].bitcast(BF16), v["hq"][:, P * x:P * x + P], k.identb[:, :])
        mm.then_inc(k.sem("hq_turned"), 1)

    def first_product(t, n, g):
        pe.wait_ge(*k.at("xq_copied", n + 1))
        pe.wait_ge(*k.at("h_scaled", n))
        for c in range(2):
            for h in range(NH):
                mm = pe.matmul(bank(k, 3 + c), v["xt", g % 2][:, h, :], v["w1"][:, h, TN * c:TN * c + TN], start=h == 0, stop=h == 1)
        mm.then_inc(k.sem("h_ready"), 1)

    def turn_out(t, n, g):
        pe.wait_ge(*k.at("y_scaled", n + 1))
        pe.wait_ge(*k.at("y_added", n))
        for h in range(NH):
            mm = pe.transpose(k.PS[:, 7, P * h:P * h + P], v["out"][:, P * h:P * h + P], k.ident[:, :])
        mm.then_inc(k.sem("y_turned"), 1)

    def second_product(t, n, g):
        pe.wait_ge(*k.at("hq_copied", n + 1))
        pe.wait_ge(*k.at("y_scaled", n))
        for x in range(8):
            mm = pe.matmul(k.PS[:, 6, 0:D], v["ht"][:, x, :], v["w2"][:, x, :], start=x == 0, stop=x == 7)
        mm.then_inc(k.sem("y_ready"), 1)

    over_groups(pe, [(turn_x, 0), (turn_xq, 1), (turn_hidden, 3), (turn_out, 4), (first_product, 1), (second_product, 3)])


def l2f_act(k, act):
    v = ffq_views(k)
    norm_act(k, act, "n8")

    def copy_x(t, n, g):
        act.wait_ge(*k.at("xq_turned", n + 1))
        act.wait_ge(*k.at("h_ready", two_back(n)))
        act.activation(v["xt", g % 2], k.PS[:, 2, 0:P].bitcast(BF16).rearrange("p (k t) -> p k t", k=2), ACT.Copy).then_inc(k.sem("xq_copied"), 1)

    def copy_hidden(t, n, g):
        act.wait_ge(*k.at("hq_turned", n + 1))
        act.wait_ge(*k.at("y_ready", n))
        act.activation(v["ht"], bank(k, 5).bitcast(BF16).rearrange("p (k t) -> p k t", k=8), ACT.Copy).then_inc(k.sem("hq_copied"), 1)

    def gelu(t, n, g):
        act.wait_ge(*k.at("h_scaled", n + 1))
        act.activation(v["h", g % 2], v["h", g % 2], ACT.Gelu).then_inc(k.sem("h_gelu"), 1)

    over_groups(act, [(copy_x, 1), (copy_hidden, 3), (gelu, 1)])


def l2f_pool(k, pool):
    v = ffq_views(k)
    pool.wait_ge(*k.at("l2a_ready", 2 * TILES))
    with pool.Fori(0, TILES) as t:
        pool.wait_ge(*k.at("n8_scaled", 2 * t + 2))
        pool.wait_ge(*k.at("x_turned", GPT * t))
        pool.tensor_copy(v["xs"].rearrange("p h (s t) -> p h s t", s=SPT), k.Y[:, :, bass.ds(SPT * t, SPT), PAD:PAD + T]).then_inc(k.sem("tile_staged"), 1)


def l2f_dve(k, dve):
    v = ffq_views(k)
    norm_dve(k, dve, "n8", k.H, dst=lambda h, t: yt(k, h, t))
    done = [0]

    def chain(ins):
        done[0] += 1
        ins.then_inc(k.sem("w_step"), 1)
        dve.wait_ge(*k.at("w_step", done[0]))
    raw = [k.C[:, 0:2048], k.C[:, 2048:4096]]
    dve.wait_ge(*k.at("l2f_weights", 16))
    for j in range(2):
        dve.tensor_reduce(v["wsum"][:, j:j + 1], raw[j], AX.X, ALU.add, apply_absolute_value=True).then_inc(k.sem("w_sums"), 1)
    dve.wait_ge(*k.at("w_means", 1))
    chain(dve.tensor_scalar(v["wscale"], k.PS[:, 4, 0:2], 1 / 1024, EPS, ALU.mult, ALU.max))
    chain(dve.reciprocal(v["winv"], v["wscale"]))
    chain(dve.tensor_scalar(v["wscale"], v["wscale"], 1 / 127, None, ALU.mult))
    for j, w in enumerate(("w1", "w2")):
        flatw = v[w].rearrange("p k m -> p (k m)")
        chain(dve.tensor_scalar(raw[j], raw[j], v["winv"][:, j:j + 1], ROUND, ALU.mult, ALU.add))
        chain(dve.tensor_scalar(raw[j], raw[j], ROUND, 1.0, ALU.subtract, ALU.min))
        dve.tensor_scalar(flatw, raw[j], -1.0, None, ALU.max).then_inc(k.sem("w_quantised"), 1)
    dve.wait_ge(*k.at("l2f_bias", 16))

    def row_scale(src, s, n, what, j):
        dve.tensor_reduce(s[:, 0:1], src, AX.X, ALU.max, apply_absolute_value=True).then_inc(k.sem(what + "_max"), 1)
        dve.wait_ge(*k.at(what + "_max", n + 1))
        dve.tensor_scalar(s[:, 0:1], s[:, 0:1], EPS, None, ALU.max).then_inc(k.sem(what + "_clip"), 1)
        dve.wait_ge(*k.at(what + "_clip", n + 1))
        dve.reciprocal(s[:, 1:2], s[:, 0:1]).then_inc(k.sem(what + "_inv"), 1)
        dve.tensor_scalar(s[:, 2:3], s[:, 0:1], v["wscale"][:, j:j + 1], None, ALU.mult).then_inc(k.sem(what + "_scale"), 1)
        dve.wait_ge(*k.at(what + "_inv", n + 1))
        dve.tensor_scalar(s[:, 1:2], s[:, 1:2], 127.0, None, ALU.mult).then_inc(k.sem(what + "_127"), 1)
        dve.wait_ge(*k.at(what + "_127", n + 1))

    def quantise_x(t, n, g):
        x, s = v["x", g % 2], v["sx", g % 2]
        dve.wait_ge(*k.at("x_turned", n + 1))
        row_scale(k.PS[:, 0, 0:D], s, n, "x", 0)
        dve.tensor_scalar(x, k.PS[:, 0, 0:D], s[:, 1:2], ROUND, ALU.mult, ALU.add).then_inc(k.sem("x_shifted"), 1)
        dve.wait_ge(*k.at("x_shifted", n + 1))
        dve.wait_ge(*k.at("xq_turned", two_back(n)))
        dve.tensor_scalar(v["xq", g % 2], x, ROUND, 127.0, ALU.subtract, ALU.min).then_inc(k.sem("x_quantised"), 1)

    def scale_hidden(t, n, g):
        dve.wait_ge(*k.at("h_ready", n + 1))
        dve.wait_ge(*k.at("x_scale", n + 1))
        dve.wait_ge(*k.at("h_quantised", two_back(n)))
        dve.scalar_tensor_tensor(v["h", g % 2], k.PS[:, 3:5, :].rearrange("p b n -> p (b n)"), v["sx", g % 2][:, 2:3], v["b1"],
                                 ALU.mult, ALU.add).then_inc(k.sem("h_scaled"), 1)

    def quantise_hidden(t, n, g):
        x, s = v["h", g % 2], v["sh", g % 2]
        dve.wait_ge(*k.at("h_gelu", n + 1))
        row_scale(x, s, n, "hid", 1)
        dve.tensor_scalar(x, x, s[:, 1:2], ROUND, ALU.mult, ALU.add).then_inc(k.sem("h_shifted"), 1)
        dve.wait_ge(*k.at("h_shifted", n + 1))
        dve.wait_ge(*k.at("hq_turned", n))
        dve.tensor_scalar(v["hq"], x, ROUND, 127.0, ALU.subtract, ALU.min).then_inc(k.sem("h_quantised"), 1)

    def add_out(t, n, g):
        dve.wait_ge(*k.at("y_turned", n + 1))
        seq = bass.ds(SPT * t + g // 2, 1)
        dst = k.H[:, :, seq, P * (g % 2):P * (g % 2) + P].rearrange("p h s t -> p h (s t)")
        dve.tensor_tensor(dst, dst, k.PS[:, 7, 0:D].rearrange("p (h t) -> p h t", h=2), ALU.add).then_inc(k.sem("y_added"), 1)

    def scale_out(t, n, g):
        dve.wait_ge(*k.at("y_ready", n + 1))
        dve.wait_ge(*k.at("y_turned", n))
        dve.wait_ge(*k.at("hid_scale", n + 1))
        dve.scalar_tensor_tensor(v["out"], k.PS[:, 6, 0:D], v["sh", g % 2][:, 2:3], v["b2"], ALU.mult, ALU.add).then_inc(k.sem("y_scaled"), 1)

    over_groups(dve, [(quantise_x, 0), (scale_hidden, 1), (add_out, 4), (quantise_hidden, 2), (scale_out, 3)])



V3 = {"k": 0, "v": 512, "r": 1024, "o": 1536}
FIRST = -1e38


def l3a_inputs(ins, a):
    w = {n: a["L3_attn_" + n].T for n in ("att_Wk", "att_Wv", "att_Wr", "att_Wo", "ffn_Wk", "ffn_Wr", "ffn_Wv")}
    ins["l3a_w"] = np.concatenate([halves(w[n]) for n in ("att_Wk", "att_Wv", "att_Wr", "att_Wo", "ffn_Wk")], axis=1)
    ins["l3a_w2"] = np.concatenate([halves(w["ffn_Wv"]), halves(w["ffn_Wr"])], axis=1)


def l3a_load(k, sp):
    sp.wait_ge(*k.at("gla_out", 4 * B))
    sp.dma_start(k.V[:, 0:4096], k.ins["l3a_w"]).then_inc(k.sem("l3a_weights"), 16)
    sp.wait_ge(*k.at("y_ready", N // P))
    sp.wait_ge(*k.at("y_scaled", N // P))
    sp.dma_start(k.W[:, 6144:8704], k.ins["l3a_w2"]).then_inc(k.sem("l3a_weights"), 16)


def wkv_views(k, h):
    s = (k.B, k.C)[h]
    v = {"pp": s[:, 0:513], "aa": s[:, 520:1033], "bb": s[:, 1040:1553], "p": k.R[:, TN * h:TN * h + TN],
         "step": (k.W[:, 8704:9216], k.rope[:, :])[h], "first": k.V[:, 4608:5120]}
    for j, name in enumerate(("e1b", "e2b", "e1", "e2")):
        v[name] = s[:, 2048 + TN * j:2560 + TN * j]
    return v


def l3a_pe(k, pe):
    norm_pe(k, pe, "n9", k.H, "y_added", 4, free=(("y_added", N // P), ("h_scaled", N // P)))
    norm_pe(k, pe, "n10", seqs(k.A), "n9_scaled", 2)
    pe.wait_ge(*k.at("l3a_weights", 32))
    pe.wait_ge(*k.at("n10_std", TILES))
    wb = lambda name: blocks(k.V[:, V3[name]:V3[name] + 512], 2)
    with pe.Fori(0, TILES // 2) as i:
        for par in range(2):
            t = 2 * i + par
            for n in range(6):
                pe.wait_ge(*k.at("mixed3", 6 * t + 2 * (n // 2) + 2))
                pe.wait_ge(*k.at("kvr_read", 12 * i + (par and n + 1)))
                for h in range(NH):
                    mm = pe.matmul(bank(k, n), wb("kvr"[n // 2])[:, h, (n % 2) * P:(n % 2 + 1) * P], tile(seqs((k.B, k.C, k.E)[n // 2]), h, t), start=h == 0, stop=h == 1)
                mm.then_inc(k.sem("mix_ready"), 1)
    pe.wait_ge(*k.at("kvr_read", 6 * TILES))
    with pe.Fori(0, TILES // 2) as i:
        for par in range(2):
            t = 2 * i + par
            pe.wait_ge(*k.at("wkv", 2 * t + 2))
            pe.wait_ge(*k.at("x3_done", 4 * i))
            for m in range(NH):
                for h in range(NH):
                    mm = pe.matmul(bank(k, 4 + 2 * par + m), wb("o")[:, h, m * P:(m + 1) * P], tile(seqs(k.E), h, t), start=h == 0, stop=h == 1)
                mm.then_inc(k.sem("wkv_out"), 1)
    norm_pe(k, pe, "n11", seqs(k.A), "x3_done", 2)
    pe.wait_ge(*k.at("n11_std", TILES))
    wr = blocks(k.W[:, 8192:8704], 2)
    with pe.Fori(0, TILES // 2) as i:
        for par in range(2):
            t = 2 * i + par
            pe.wait_ge(*k.at("mixed4", 4 * t + 4))
            pe.wait_ge(*k.at("cm_sig", 4 * i))
            for m in range(NH):
                for h in range(NH):
                    mm = pe.matmul(bank(k, 2 * par + m), wr[:, h, m * P:(m + 1) * P], tile(seqs(k.C), h, t), start=h == 0, stop=h == 1)
                mm.then_inc(k.sem("cm_ready"), 1)
    pe.wait_ge(*k.at("cm_sig", 2 * TILES))
    wk, wv = blocks(k.V[:, 2048:4096], 2), blocks(k.W[:, 6144:8192], 8)
    with pe.Fori(0, TILES // 2) as i:
        for par in range(2):
            t = 2 * i + par
            for m in range(8):
                pe.wait_ge(*k.at("ffk_relu", 16 * i + max(8 * par + m - 3, 0)))
                for h in range(NH):
                    mm = pe.matmul(bank(k, 4 + m % 4), wk[:, h, m * P:(m + 1) * P], tile(seqs(k.B), h, t), start=h == 0, stop=h == 1)
                mm.then_inc(k.sem("ffk_ready"), 1)
        for par in range(2):
            f = (k.E, k.Q)[par][:, :].rearrange("p (m n) -> p m n", m=8)
            pe.wait_ge(*k.at("ffk_squared", 16 * i + 8 * (par + 1)))
            pe.wait_ge(*k.at("ffv_read", 4 * i))
            for m in range(NH):
                for x in range(8):
                    mm = pe.matmul(bank(k, 2 * par + m), wv[:, x, m * P:(m + 1) * P], f[:, x, :], start=x == 0, stop=x == 7)
                mm.then_inc(k.sem("ffv_ready"), 1)


def l3a_act(k, act):
    norm_act(k, act, "n9")
    act.activation(k.small[:, 576:578], k.vec[:, VCOL["decay"]:VCOL["decay"] + 2], ACT.Exp).then_inc(k.sem("decay_exp"), 1)
    norm_act(k, act, "n10", "ln1_b", lambda h, t: yt(k, h, t))
    with act.Fori(0, TILES) as t:
        act.wait_ge(*k.at("n10_done", 2 * t + 2))
        for o, x in enumerate((k.B, k.C, k.E)):
            for h in range(NH):
                act.activation(tile(seqs(x), h, t), yt(k, h, t, 1), ACT.Copy, scale=k.vec2[:, 4 + 2 * o + h:5 + 2 * o + h]).then_inc(k.sem("before3"), 1)
    with act.Fori(0, TILES) as t:
        for n in range(6):
            act.wait_ge(*k.at("mix_ready", 6 * t + max(n, 5 if n == 4 else 0) + 1))
            dst = tile(seqs((k.D, k.Q, k.E)[n // 2]), n % 2, t)
            act.activation(dst, bank_seq(k, n), ACT.Sigmoid if n >= 4 else ACT.Copy).then_inc(k.sem("kvr_read"), 1)
    with act.Fori(0, TILES) as t:
        for h in range(NH):
            v = wkv_views(k, h)
            for j, name in enumerate(("e1b", "e2b", "e1", "e2")):
                act.wait_ge(*k.at("exp_args", 8 * t + 4 * h + j + 1))
                act.activation(v[name], v[name], ACT.Exp).then_inc(k.sem("exps"), 1)
    norm_act(k, act, "n11", "ln2_b", lambda h, t: yt(k, h, t))
    with act.Fori(0, TILES) as t:
        act.wait_ge(*k.at("n11_done", 2 * t + 2))
        for o, x in enumerate((k.B, k.C)):
            for h in range(NH):
                act.activation(tile(seqs(x), h, t), yt(k, h, t, 1), ACT.Copy, scale=k.vec2[:, 10 + 2 * o + h:11 + 2 * o + h]).then_inc(k.sem("before4"), 1)
    with act.Fori(0, TILES // 2) as i:
        for par in range(2):
            t = 2 * i + par
            act.wait_ge(*k.at("cm_ready", 2 * t + 2))
            for m in range(NH):
                act.activation(tile(seqs(k.C), m, t), bank_seq(k, 2 * par + m), ACT.Sigmoid).then_inc(k.sem("cm_sig"), 1)
    with act.Fori(0, TILES // 2) as i:
        for par in range(2):
            f = (k.E, k.Q)[par][:, :].rearrange("p (m n) -> p m n", m=8)
            act.wait_ge(*k.at("ffv_ready", 4 * i))
            for m in range(8):
                act.wait_ge(*k.at("ffk_ready", 16 * i + 8 * par + m + 1))
                act.activation(f[:, m, :], bank(k, 4 + m % 4), ACT.Relu).then_inc(k.sem("ffk_relu"), 1)


def l3a_pool(k, pool):
    with pool.Fori(0, TILES) as t:
        for h in range(NH):
            v = wkv_views(k, h)
            val = flat(k.Q, h, t)
            pool.wait_ge(*k.at("exps", 8 * t + 4 * h + 4))
            pool.tensor_tensor(v["pp"][:, 1:TN + 1], v["e2b"], val, ALU.mult).then_inc(k.sem("wkv_pool"), 1)
            pool.tensor_tensor(v["p"], v["e2"], val, ALU.mult).then_inc(k.sem("wkv_pool"), 1)
            pool.wait_ge(*k.at("sums", 4 * t + 2 * h + 2))
            pool.tensor_tensor(v["e1b"], v["e1"], v["aa"][:, 0:TN], ALU.mult).then_inc(k.sem("wkv_pool"), 1)
            pool.wait_ge(*k.at("wkv_pool", 8 * t + 4 * h + 3))
            pool.tensor_tensor(v["e1"], v["e1"], v["bb"][:, 0:TN], ALU.mult).then_inc(k.sem("wkv_pool"), 1)


def l3a_dve(k, dve):
    norm_dve(k, dve, "n9", k.H, dst=lambda h, t: tile(seqs(k.A), h, t))
    done = [0]

    def chain(ins):
        done[0] += 1
        ins.then_inc(k.sem("wkv_step"), 1)
        dve.wait_ge(*k.at("wkv_step", done[0]))
    vs = [wkv_views(k, h) for h in range(NH)]
    w = k.small[:, 576:578]
    first = vs[0]["first"]
    dve.wait_ge(*k.at("decay_exp", 1))
    chain(dve.tensor_scalar(w, w, -1.0, None, ALU.mult))
    chain(dve.memset(first, 0.0))
    chain(dve.memset(first.rearrange("p (s t) -> p s t", s=SPT)[:, :, 0:1], FIRST))
    for h in range(NH):
        chain(dve.tensor_scalar(vs[h]["step"], first, w[:, h:h + 1], None, ALU.add))
    norm_dve(k, dve, "n10", seqs(k.A), gain="ln1_g")
    with dve.Fori(0, TILES) as t:
        for o, (x, mu) in enumerate(((k.B, "mix_k"), (k.C, "mix_v"), (k.E, "mix_r"))):
            for h in range(NH):
                dve.wait_ge(*k.at("before3", 6 * t + 2 * o + h + 1))
                y = tile(seqs(x), h, t)
                dve.scalar_tensor_tensor(y, yt(k, h, t), vcol(k, mu, h), y, ALU.mult, ALU.add).then_inc(k.sem("mixed3"), 1)
    dve.wait_ge(*k.at("mix_ready", 6 * TILES))
    for h in range(NH):
        for name in ("pp", "aa", "bb"):
            chain(dve.memset(vs[h][name][:, 0:1], 0.0))
    with dve.Fori(0, TILES) as t:
        for h in range(NH):
            v, n = vs[h], 2 * t + h
            key, u = flat(k.D, h, t), vcol(k, "first", h)
            dve.wait_ge(*k.at("kvr_read", 6 * t + 6))
            dve.wait_ge(*k.at("wkv", 2 * t))
            dve.tensor_tensor_scan(v["pp"][:, 1:TN + 1], v["step"], key, 0.0, ALU.add, ALU.max).then_inc(k.sem("pp"), 1)
            dve.wait_ge(*k.at("pp", n + 1))
            dve.tensor_tensor(v["e1"], v["pp"][:, 0:TN], v["first"], ALU.add).then_inc(k.sem("pp_prev"), 1)
            dve.wait_ge(*k.at("pp_prev", n + 1))
            dve.scalar_tensor_tensor(v["p"], key, u, v["e1"], ALU.add, ALU.max).then_inc(k.sem("p_max"), 1)
            dve.scalar_tensor_tensor(v["e1b"], v["e1"], w[:, h:h + 1], v["pp"][:, 1:TN + 1], ALU.add, ALU.subtract).then_inc(k.sem("exp_args"), 1)
            dve.tensor_tensor(v["e2b"], key, v["pp"][:, 1:TN + 1], ALU.subtract).then_inc(k.sem("exp_args"), 1)
            dve.wait_ge(*k.at("p_max", n + 1))
            dve.tensor_tensor(v["e1"], v["e1"], v["p"], ALU.subtract).then_inc(k.sem("exp_args"), 1)
            dve.scalar_tensor_tensor(v["e2"], key, u, v["p"], ALU.add, ALU.subtract).then_inc(k.sem("exp_args"), 1)
        for h in range(NH):
            v = vs[h]
            dve.wait_ge(*k.at("exps", 8 * t + 4 * h + 2))
            dve.tensor_tensor_scan(v["bb"][:, 1:TN + 1], v["e1b"], v["e2b"], 0.0, ALU.mult, ALU.add).then_inc(k.sem("sums"), 1)
            dve.wait_ge(*k.at("wkv_pool", 8 * t + 4 * h + 1))
            dve.tensor_tensor_scan(v["aa"][:, 1:TN + 1], v["e1b"], v["pp"][:, 1:TN + 1], 0.0, ALU.mult, ALU.add).then_inc(k.sem("sums"), 1)
        for h in range(NH):
            v, n = vs[h], 2 * t + h
            dve.wait_ge(*k.at("wkv_pool", 8 * t + 4 * h + 3))
            dve.tensor_tensor(v["e1b"], v["e1b"], v["p"], ALU.add).then_inc(k.sem("num"), 1)
            dve.wait_ge(*k.at("wkv_pool", 8 * t + 4 * h + 4))
            dve.tensor_tensor(v["e1"], v["e1"], v["e2"], ALU.add).then_inc(k.sem("den"), 1)
            dve.wait_ge(*k.at("den", n + 1))
            dve.reciprocal(v["e1"], v["e1"]).then_inc(k.sem("den_inv"), 1)
            dve.wait_ge(*k.at("num", n + 1))
            dve.wait_ge(*k.at("den_inv", n + 1))
            dve.tensor_tensor(v["e1"], v["e1"], v["e1b"], ALU.mult).then_inc(k.sem("ratio"), 1)
            dve.wait_ge(*k.at("ratio", n + 1))
            dve.tensor_tensor(flat(k.E, h, t), flat(k.E, h, t), v["e1"], ALU.mult).then_inc(k.sem("wkv"), 1)
    with dve.Fori(0, TILES // 2) as i:
        for par in range(2):
            t = 2 * i + par
            for m in range(NH):
                dve.wait_ge(*k.at("wkv_out", 2 * t + m + 1))
                dve.tensor_tensor(tile(seqs(k.A), m, t), tile(seqs(k.A), m, t), bank_seq(k, 4 + 2 * par + m), ALU.add).then_inc(k.sem("x3_done"), 1)
    norm_dve(k, dve, "n11", seqs(k.A), gain="ln2_g")
    with dve.Fori(0, TILES) as t:
        for o, (x, mu) in enumerate(((k.B, "cm_k"), (k.C, "cm_r"))):
            for h in range(NH):
                dve.wait_ge(*k.at("before4", 4 * t + 2 * o + h + 1))
                y = tile(seqs(x), h, t)
                dve.scalar_tensor_tensor(y, yt(k, h, t), vcol(k, mu, h), y, ALU.mult, ALU.add).then_inc(k.sem("mixed4"), 1)
    with dve.Fori(0, TILES // 2) as i:
        for par in range(2):
            f = (k.E, k.Q)[par][:, :].rearrange("p (m n) -> p m n", m=8)
            for m in range(8):
                dve.wait_ge(*k.at("ffk_relu", 16 * i + 8 * par + m + 1))
                dve.tensor_tensor(f[:, m, :], f[:, m, :], f[:, m, :], ALU.mult).then_inc(k.sem("ffk_squared"), 1)
        for par in range(2):
            t = 2 * i + par
            for m in range(NH):
                c, x = tile(seqs(k.C), m, t), tile(seqs(k.A), m, t)
                dve.wait_ge(*k.at("ffv_ready", 2 * t + m + 1))
                dve.tensor_tensor(c, c, bank_seq(k, 2 * par + m), ALU.mult).then_inc(k.sem("ffv_read"), 1)
                dve.tensor_tensor(tile(k.H, m, t), tile(k.H, m, t), x, ALU.add).then_inc(k.sem("x3_added"), 1)
                dve.wait_ge(*k.at("ffv_read", 2 * t + m + 1))
                dve.wait_ge(*k.at("x3_added", 2 * t + m + 1))
                dve.tensor_tensor(tile(k.H, m, t), tile(k.H, m, t), c, ALU.add).then_inc(k.sem("l3a_done"), 1)



FF3 = 1024
N3 = "l3f"


def l3f_inputs(ins, a):
    gu, down = a["L3_ffn_gate_up_w"], a["L3_ffn_down_w"]
    ins["l3f_gu"] = gu.transpose(0, 2, 1).reshape(E3, 2, P, 2 * FF3).transpose(0, 2, 1, 3).reshape(E3 * P, 4 * FF3)
    ins["l3f_down"] = down.transpose(0, 2, 1).reshape(E3, 8, P, D).transpose(0, 2, 1, 3).reshape(E3 * P, 8 * D)
    ins["l3f_gate"] = halves(a["L3_ffn_gate_w"].T)


def moe3_views(k):
    two = lambda ap: [ap[:, 512 * j:512 * j + 512].rearrange("p (s d) -> p s d", s=2) for j in range(2)]
    v = slot_views(k, E3, TILES3, RING3)
    v |= {"gu": [k.W[:, 0:4096], k.B[:, :]], "down": [k.W[:, 4096:6144], k.C[:, 0:2048]],
         "rows": k.Q[:, :].rearrange("p (g d) -> p g d", g=GROUPS),
         "x": two(k.C[:, 2048:3072]), "xt": two(k.C[:, 3072:4096]), "o": two(k.V[:, 1024:2048]),
         "f": [k.D[:, 2048 * j:2048 * j + 2048].rearrange("p (m n) -> p m n", m=8) for j in range(2)],
         "gelu": [k.V[:, TS * j:TS * j + TS] for j in range(4)],
         "first": k.E[:, :].rearrange("p (g d) -> p g d", g=GROUPS), "second": k.Q[:, :].rearrange("p (g d) -> p g d", g=GROUPS),
         "out": k.B[:, :].rearrange("p (g d) -> p g d", g=GROUPS)}
    return v


def l3f_load(k, sp):
    v = moe3_views(k)
    sp.dma_start(k.small[:, 600:616], k.ins["l3f_gate"]).then_inc(k.sem("l3f_router"), 16)
    sp.wait_ge(*k.at("l3f_scattered", 16 * 2 * GROUPS))
    for j in range(2):
        sp.dma_start(v["x"][j], tile_of(k.slots, j)).then_inc(k.sem(f"l3f_x_in{j}"), 16)
    with sp.Fori(0, TILES3 // 2 - 1) as i:
        for j in range(2):
            sp.wait_ge(*k.at("l3f_slots_turned", 2 * i + j + 1))
            sp.dma_start(v["x"][j], tile_of(k.slots, 2 * i + j + 2)).then_inc(k.sem(f"l3f_x_in{j}"), 16)
            sp.wait_ge(*k.at("l3f_o_copied", 2 * i + j + 1))
            sp.dma_start(tile_of(k.slots, 2 * i + j), v["o"][j]).then_inc(k.sem(f"l3f_o_out{j}"), 16)
    for j in range(2):
        sp.wait_ge(*k.at("l3f_o_copied", TILES3 - 1 + j))
        sp.dma_start(tile_of(k.slots, TILES3 - 2 + j), v["o"][j]).then_inc(k.sem(f"l3f_o_out{j}"), 16)


def store(k, sp):
    out = k.out.rearrange("(g p) d -> p g d", p=P)
    for q in range(4):
        sp.wait_ge(*k.at("l3f_done", 4 * q + 4))
        sp.dma_start(out[:, 4 * q:4 * q + 4], moe3_views(k)["out"][:, 4 * q:4 * q + 4]).then_inc(k.sem("stored"), 16)
    sp.wait_ge(*k.at("stored", 4 * 16))


def l3f_pool(k, pool):
    v = moe3_views(k)

    def weights(par, what, rows):
        pool.indirect_dma_start(v[what][par], None, k.ins["l3f_" + what], rows).then_inc(k.sem(f"l3f_expert_in{par}"), 16)
    def go():
        pool.sem_inc(k.sem("weights_go"), 1)
    pool.wait_ge(*k.at("l3f_slots_known", 1))
    weights(0, "gu", row_of(v["row"], 0))
    weights(0, "down", row_of(v["row"], 0))
    scatter_pool(k, pool, N3, v, v["rows"])
    weights(1, "gu", row_of(v["row"], 1))
    weights(1, "down", row_of(v["row"], 1))
    with pool.Fori(1, TILES3 // 2) as i:
        for par in range(2):
            pool.wait_ge(*k.at("hact", 8 * (2 * i + par - 1)))
            pool.wait_ge(*k.at("l3f_row_staged", 2 * i + par - 1))
            go()
            weights(par, "gu", row_of(v["row_staged"][par]))
            pool.wait_ge(*k.at("down_ready", 2 * i + par - 1))
            go()
            weights(par, "down", row_of(v["row_staged"][par]))
    for j in range(2):
        pool.wait_ge(*k.at(f"l3f_o_out{j}", 16 * TILES3 // 2))
    gather_pool(k, pool, N3, v, (v["first"], v["second"]))


def l3f_pe(k, pe):
    v = moe3_views(k)
    norm_pe(k, pe, "n12", k.H, "l3a_done", 2, free=(("ffv_read", 2 * TILES),))
    pe.wait_ge(*k.at("l3f_router", 16))
    logits_pe(k, pe, "l3f", "n12_scaled", blocks(k.small[:, 600:616], 2), E3, 1)
    rows_pe(k, pe, N3)
    ranks_pe(k, pe, N3, E3, v)

    def turn(par, count):
        pe.wait_ge(*k.at(f"l3f_x_in{par}", count))
        for h in range(NH):
            for s in range(2):
                mm = pe.transpose(k.PS[:, 6 + par, h * TS + s * P:h * TS + (s + 1) * P], v["x"][par][:, s, h * P:(h + 1) * P], k.ident[:, :])
        mm.then_inc(k.sem("l3f_slots_turned"), 1)

    def products(i, par, last):
        j = 2 * i + par
        gu, down = blocks(v["gu"][par], 2), blocks(v["down"][par], 8)
        pe.wait_ge(*k.at(f"l3f_expert_in{par}", 32 * i + 32, positive=True))
        pe.wait_ge(*k.at("l3f_slots_copied", j + 1))
        for m in range(8):
            pe.wait_ge(*k.at("hact", 16 * i + max(8 * par + m - 3, 0)))
            for o in range(2):
                for h in range(NH):
                    mm = pe.matmul(k.PS[:, m % 4, o * TS:(o + 1) * TS], gu[:, h, FF3 * o + m * P:FF3 * o + (m + 1) * P], v["xt"][par][:, h], start=h == 0, stop=h == 1)
            mm.then_inc(k.sem("gu_ready"), 1)
        if not last:
            turn(1 - par, 16 * (i + par) + 16)
        pe.wait_ge(*k.at("l3f_o_copied", 2 * i))
        for s in range(2):
            for x in range(8):
                if s == 0:
                    pe.wait_ge(*k.at("hact", 8 * j + x + 1))
                mm = pe.matmul(k.PS[:, 4 + par, s * D:(s + 1) * D], v["f"][par][:, x, s * P:(s + 1) * P], down[:, x, :], start=x == 0, stop=x == 7)
        mm.then_inc(k.sem("down_ready"), 1)

    pe.wait_ge(*k.at("l3f_rows_copied", GROUPS // 2))
    turn(0, 16)
    with pe.Fori(0, TILES3 // 2 - 1) as i:
        for par in range(2):
            products(i, par, False)
    products(TILES3 // 2 - 1, 0, False)
    products(TILES3 // 2 - 1, 1, True)
    pe.wait_ge(*k.at("l3f_o_copied", TILES3))
    for q in range(GROUPS // 2):
        for s in range(2):
            for h in range(NH):
                mm = pe.transpose(k.PS[:, q, (2 * s + h) * P:(2 * s + h + 1) * P], k.H[:, h, q, s * P:(s + 1) * P], k.ident[:, :])
        mm.then_inc(k.sem("out_turned"), 1)


def l3f_act(k, act):
    v = moe3_views(k)
    norm_act(k, act, "n12")
    route_act(k, act, "l3f", E3, 0)
    rows_act(k, act, N3, v["rows"])

    def turned(par, count):
        act.wait_ge(*k.at("l3f_slots_turned", count))
        act.activation(v["xt"][par], k.PS[:, 6 + par, :].rearrange("p (h t) -> p h t", h=NH), ACT.Copy).then_inc(k.sem("l3f_slots_copied"), 1)

    def gelus(i, par):
        for m in range(8):
            act.wait_ge(*k.at("gu_ready", 16 * i + 8 * par + m + 1))
            act.activation(v["gelu"][m % 4], k.PS[:, m % 4, 0:TS], ACT.Gelu).then_inc(k.sem("gelu3"), 1)
    turned(0, 1)
    with act.Fori(0, TILES3 // 2 - 1) as i:
        for par in range(2):
            gelus(i, par)
            turned(1 - par, 2 * i + par + 2)
    gelus(TILES3 // 2 - 1, 0)
    turned(1, TILES3)
    gelus(TILES3 // 2 - 1, 1)


def l3f_dve(k, dve):
    v = moe3_views(k)
    norm_dve(k, dve, "n12", k.H, dst=lambda h, t: yt(k, h, t))
    chain = route_dve(k, dve, "l3f", E3, 1, 0.0, None, 0)
    slots_dve(k, dve, N3, chain, v, E3, TILES3, RING3, E3)

    def hidden(i, par):
        for m in range(8):
            dve.wait_ge(*k.at("gelu3", 16 * i + 8 * par + m + 1))
            dve.tensor_tensor(v["f"][par][:, m, :], v["gelu"][m % 4], k.PS[:, m % 4, TS:2 * TS], ALU.mult).then_inc(k.sem("hact"), 1)
            if m == 0:
                dve.tensor_copy(v["row_staged"][par], v["row"][:, bass.ds(2 * i + par + 2, 1)]).then_inc(k.sem("l3f_row_staged"), 1)
        dve.wait_ge(*k.at("down_ready", 2 * i + par + 1))
        dve.wait_ge(*k.at(f"l3f_o_out{par}", 16 * i))
        dve.tensor_copy(v["o"][par], k.PS[:, 4 + par, :].rearrange("p (s d) -> p s d", s=2)).then_inc(k.sem("l3f_o_copied"), 1)
    with dve.Fori(0, TILES3 // 2) as i:
        for par in range(2):
            hidden(i, par)
    for q in range(4):
        dve.wait_ge(*k.at(f"l3f_back{q}", 16 * 8))
        dve.wait_ge(*k.at("out_turned", 2 * q + 2))
        for g in range(4 * q, 4 * q + 4):
            dve.scalar_tensor_tensor(v["out"][:, g], v["second"][:, g], v["m2"][:, g:g + 1], k.PS[:, g // 2, g % 2 * D:(g % 2 + 1) * D], ALU.mult, ALU.add).then_inc(k.sem("second_in"), 1)
        for g in range(4 * q, 4 * q + 4):
            dve.wait_ge(*k.at("second_in", g + 1))
            dve.scalar_tensor_tensor(v["out"][:, g], v["first"][:, g], v["m1"][:, g:g + 1], v["out"][:, g], ALU.mult, ALU.add).then_inc(k.sem("l3f_done"), 1)


def more_inputs(ins, a):
    l0f_inputs(ins, a)
    l1a_inputs(ins, a)
    l1f_inputs(ins, a)
    l2a_inputs(ins, a)
    l2f_inputs(ins, a)
    l3a_inputs(ins, a)
    l3f_inputs(ins, a)
    return


SP_STAGES = [l0a_load, clear_slots, l0f_load, l1f_load, l2a_load, l2f_load, l3a_load, l3f_load]
POOL_STAGES = [l0a_pool, l0f_pool, l1a_pool, l1f_pool, l2a_pool, l2f_pool, l3a_pool, l3f_pool]
PE_STAGES = [l0a_pe, l0f_pe, l1a_pe, l1f_pe, l2a_pe, l2f_pe, l3a_pe, l3f_pe]
ACT_STAGES = [l0a_act, l0f_act, l1a_act, l1f_act, l2a_act, l2f_act, l3a_act, l3f_act]
DVE_STAGES = [l0a_dve, l0f_dve, l1a_dve, l1f_dve, l2a_dve, l2f_dve, l3a_dve, l3f_dve]



def build(nc, ins, out):
    with ExitStack() as ctx:
        k = Kernel(nc, ctx, ins, out)
        allocate(k)
        k.slots = nc.dram_tensor("slots", (TILES0 + N // TS, TS, D), F32, kind="Internal").ap()
        block = ctx.enter_context(nc.Block())

        @block.sync
        def _(sp):
            for name in PRIMED:
                sp.sem_inc(k.sem(name), 1)
            load_constants(k, sp)
            tok_load(k, sp)
            for f in SP_STAGES:
                f(k, sp)
            store(k, sp)

        @block.gpsimd
        def _(pool):
            pool.memset(k.small[:, 640:896], 0.0).then_inc(k.sem("zeros_set"), 1)
            tok_pool(k, pool)
            for f in POOL_STAGES:
                f(k, pool)

        @block.tensor
        def _(pe):
            tok_pe(k, pe)
            for f in PE_STAGES:
                f(k, pe)

        @block.scalar
        def _(act):
            tok_act(k, act)
            for f in ACT_STAGES:
                f(k, act)

        @block.vector
        def _(dve):
            tok_dve(k, dve)
            for f in DVE_STAGES:
                f(k, dve)
        assert not k.unprimed, sorted(k.unprimed)



def halves(a):
    r, m = a.shape
    return a.reshape(r // P, P, m).transpose(1, 0, 2).reshape(P, -1)


def constants():
    f = np.float32
    c = {}
    c["c_ident"] = np.eye(P, dtype=f)
    c["c_mean"] = np.full((P, P), 1.0 / D, f)
    p = np.arange(P)
    theta = f(1.0) / np.power(f(10000.0), np.arange(8, dtype=f) / f(8))
    ang = np.outer(np.arange(T, dtype=f), theta).astype(f)
    cos, sin = np.cos(ang).astype(f), np.sin(ang).astype(f)
    sign = np.where(p % 16 < 8, f(-1), f(1))
    c["c_rope"] = np.concatenate([cos[:, p % 8].T, (sin[:, p % 8] * sign).T], axis=1).astype(f)
    perm = np.zeros((P, P), f)
    perm[p ^ 8, p] = 1.0
    q, key = np.arange(64)[:, None], np.arange(P)[None, :]
    first = np.where(key <= q, 0.0, -4e9)
    later = np.where((key - 64 <= q) & (q - (key - 64) < 64), 0.0, -4e9)
    band = np.concatenate([np.tile(first, (2, 1)), np.tile(later, (2, 1))], axis=1)
    causal = (p[:, None] <= p[None, :]).astype(f)
    gm = (p[:, None] // 16 % 4 == np.arange(4)[None, :]).astype(f)
    hm = (p[:, None] // 16 == np.arange(8)[None, :]).astype(f)
    rev = np.tile(16.0 - np.arange(16), (P, 1))
    slot_tile = np.concatenate([np.tile(np.arange(NUMBERS), (P, 1)), p[:, None]], axis=1)
    c["c_att"] = np.concatenate([perm, band, causal, gm, hm, rev, slot_tile], axis=1).astype(f)
    fi = np.zeros((P, N // P), f)
    fi[0, ::2] = 1.0
    c["c_first"] = fi
    return c


def kernel(**x):
    import concourse.bacc as _bacc
    from concourse.bass_utils import run_bass_kernel_spmd as _run
    import ml_dtypes

    a = {n: np.ascontiguousarray(v) for n, v in x.items()}
    ins = constants()
    ins["c_identb"] = np.eye(P, dtype=ml_dtypes.bfloat16)
    tok = a["x"]
    ins["tok"] = tok.reshape(N // P, P).T
    ins["tok_prev"] = np.concatenate([np.zeros((B, 1), tok.dtype), tok[:, :-1]], axis=1).reshape(N // P, P).T
    ins["scale"] = a["L0_tok_scale"].reshape(1, 1)
    ins["embed"] = a["L0_tok_embed_weight"]
    ins["projT"] = a["L0_tok_proj_weight"].T
    jt, j2, g, d = np.meshgrid(np.arange(2), np.arange(2), np.arange(4), np.arange(16), indexing="ij")
    order = ((4 * g + 2 * jt + j2) * 16 + d).reshape(-1)
    dup = np.tile(np.arange(64), 2)
    v = {"bq": a["L0_attn_bq"][order], "bk": np.concatenate([a["L0_attn_bk"][dup], a["L0_attn_bk"][dup]]),
         "bo": a["L0_attn_bo"], "g1": a["L0_attn_g1"],
         "b1": a["L0_attn_b1"], "g2": a["L0_attn_g2"], "b2": a["L0_attn_b2"], "bf2": a["L0_attn_bf2"],
         "D": a["L1_attn_D"], "mu_r": a["L1_ffn_mu_r"], "mu_k": a["L1_ffn_mu_k"], "bgk2": a["L2_attn_bgk2"],
         "gamma": a["L2_attn_gamma"], "beta": a["L2_attn_beta"], "ln1_g": a["L3_attn_ln1_g"],
         "ln1_b": a["L3_attn_ln1_b"], "ln2_g": a["L3_attn_ln2_g"], "ln2_b": a["L3_attn_ln2_b"],
         "decay": a["L3_attn_time_decay"], "first": a["L3_attn_time_first"], "mix_k": a["L3_attn_time_mix_k"],
         "mix_v": a["L3_attn_time_mix_v"], "mix_r": a["L3_attn_time_mix_r"], "cm_k": a["L3_attn_cm_k"],
         "cm_r": a["L3_attn_cm_r"]}
    ins["vecs"] = np.concatenate([v[n].reshape(NH, P).T for n in VECS] + [a["L0_attn_bf1"].reshape(8, P).T], axis=1)
    ins["l0a_w"] = np.concatenate([halves(a["L0_attn_Wq"][:, order]), halves(a["L0_attn_Wk"][:, dup]), halves(a["L0_attn_Wv"]),
                                   halves(a["L0_attn_Wo"][order]), halves(a["L0_attn_Wf1"]), halves(a["L0_attn_Wf2"])], axis=1)
    ins["bv"] = a["L0_attn_bv"].reshape(1, 64)
    more_inputs(ins, a)

    nc = _bacc.Bacc("TRN2", target_bir_lowering=False, num_devices=1)
    arrays, aps = {}, {}
    for name, arr in ins.items():
        arr = np.ascontiguousarray(arr)
        arrays["in_" + name] = arr
        aps[name] = nc.dram_tensor("in_" + name, arr.shape, mybir.dt.from_np(arr.dtype), kind="ExternalInput").ap()
    out = nc.dram_tensor("out_0", (N, D), F32, kind="ExternalOutput").ap()
    build(nc, aps, out)
    r = _run(nc, [arrays], core_ids=[0])
    got = r.results[0]["out_0"]
    return got.reshape(B, T, D)
```
